# Optimizing a Trainium2 kernel written in Bass

```python
import numpy as np
import jax
import jax.numpy as jnp

def _softmax(x, axis=-1):
    return jax.nn.softmax(x, axis=axis)

def _gelu(x):
    return jax.nn.gelu(x, approximate=True)

def _silu(x):
    return jax.nn.silu(x)

def _sigmoid(x):
    return jax.nn.sigmoid(x)

def _layernorm(x, axis=-1, eps=1e-05):
    m = jnp.mean(x, axis=axis, keepdims=True)
    v = jnp.var(x, axis=axis, keepdims=True)
    return (x - m) / jnp.sqrt(v + eps)

def _scatter_add(tgt, idx, src, axis=0):
    return tgt.at[idx].add(src)

def _segment_sum(src, seg, n):
    return jax.ops.segment_sum(src, seg, n)
kernel_name = 'mk_decoder_postln_d4_seqx_r8_1d925d'

def setup_inputs(seed: int=0):
    np.random.seed(seed)
    _w = jnp.asarray

    def _rec_inputs():
        import jax
        import jax.numpy as jnp
        _rk = jax.random.key(seed)
        x = 7.22e-05 + 1 * jax.random.normal(jax.random.fold_in(_rk, 1), (32, 128, 128), jnp.float32)
        _lenS = 128 - jax.random.randint(jax.random.fold_in(_rk, 7), (32,), 0, max(1, 128 // 4) + 1, jnp.int32)
        _lenS2 = 120 - jax.random.randint(jax.random.fold_in(_rk, 8), (32,), 0, max(1, 120 // 4) + 1, jnp.int32)
        _ctx_768P = jax.random.normal(jax.random.fold_in(_rk, 11), (32, 16, 96), jnp.float32)
        _ctx_768c = jax.random.dirichlet(jax.random.fold_in(_rk, 511), 0.3 * jnp.ones((16,), jnp.float32), (32, 120))
        _ctx_768t = jnp.einsum('bsk,bkd->bsd', _ctx_768c, _ctx_768P)
        _ctx_768t = _ctx_768t * jax.lax.rsqrt(jnp.mean(jnp.square(_ctx_768t)) + 1e-12) * 0.953939
        ctx_768 = 3.88148e-05 + 0.999967 * (_ctx_768t + 0.3 * jax.random.normal(jax.random.fold_in(_rk, 611), (32, 120, 96), jnp.float32))
        _validS = jnp.arange(128)[None, :] < _lenS[:, None]
        _validS2 = jnp.arange(120)[None, :] < _lenS2[:, None]
        _causal = jnp.tril(jnp.ones((128, 128), dtype=bool))
        mask_BxS_bf1 = jnp.ones((32, 128), dtype=bool)
        mask_BxS2_bf1 = jnp.ones((32, 120), dtype=bool)
        return (x, ctx_768, mask_BxS_bf1, mask_BxS2_bf1)
    x, ctx_768, mask_BxS_bf1, mask_BxS2_bf1 = _rec_inputs()

    def _L0_attn_setup():
        import jax, jax.numpy as jnp
        import numpy as np
        HIDDEN = 128
        HEADS = 16
        HEAD_DIM = HIDDEN // HEADS
        EPS = 1e-05
        key = jax.random.key(seed)
        ks = jax.random.split(key, 12)
        B, S, H = (2, 256, HIDDEN)
        s = 1.0 / np.sqrt(H)
        x = jax.random.normal(ks[0], (B, S, H), dtype=jnp.float32)
        Wq = jax.random.normal(ks[1], (H, H), dtype=jnp.float32) * s
        bq = jnp.zeros((H,), dtype=jnp.float32)
        Wk = jax.random.normal(ks[2], (H, H), dtype=jnp.float32) * s
        bk = jnp.zeros((H,), dtype=jnp.float32)
        Wv = jax.random.normal(ks[3], (H, H), dtype=jnp.float32) * s
        bv = jnp.zeros((H,), dtype=jnp.float32)
        Wg = jax.random.normal(ks[4], (2 * H, H), dtype=jnp.float32) * (1.0 / np.sqrt(2 * H))
        bg = jnp.zeros((H,), dtype=jnp.float32)
        gamma = jnp.ones((H,), dtype=jnp.float32)
        beta = jnp.zeros((H,), dtype=jnp.float32)
        return {'x': x, 'Wq': Wq, 'bq': bq, 'Wk': Wk, 'bk': bk, 'Wv': Wv, 'bv': bv, 'Wg': Wg, 'bg': bg, 'gamma': gamma, 'beta': beta}
    _L0_attn_all = _L0_attn_setup()
    _L0_attn_in = {k: v for k, v in _L0_attn_all.items() if k in ('Wq', 'bq', 'Wk', 'bk', 'Wv', 'bv', 'Wg', 'bg', 'gamma', 'beta')}
    del _L0_attn_all

    def _L0_xattn_setup():
        import jax, jax.numpy as jnp
        import numpy as np
        B, T, DT, G, DV = (16, 64, 128, 72, 96)
        H, DH = (4, 32)
        INNER = H * DH
        HID = 4 * DT
        N_STATE = 64
        K_TOP = 32

        def layernorm(x, g, b, eps=1e-05):
            m = x.mean(-1, keepdims=True)
            v = x.var(-1, keepdims=True)
            return (x - m) * jax.lax.rsqrt(v + eps) * g + b

        def s4d(x, log_dt, A_re, A_im, C_re, C_im, D_skip):
            Bb, L, D = x.shape
            dt = jnp.exp(log_dt)
            A = A_re + 1j * A_im
            C = C_re + 1j * C_im
            dtA = dt[:, None] * A
            dC = C * (jnp.exp(dtA) - 1.0) / A
            powers = jnp.exp(dtA[:, :, None] * jnp.arange(L))
            K = 2.0 * jnp.einsum('dn,dnl->dl', dC, powers).real
            n = 2 * L
            Kf = jnp.fft.rfft(K, n=n, axis=-1)
            xf = jnp.fft.rfft(x, n=n, axis=1)
            y = jnp.fft.irfft(xf * Kf.T[None], n=n, axis=1)[:, :L]
            return y + x * D_skip
        key = jax.random.key(seed)
        ks = jax.random.split(key, 16)
        s = 0.02
        inp = {'x_text': jax.random.normal(ks[0], (B, T, DT), jnp.float32), 'x_vision': jax.random.normal(ks[1], (B, G, DV), jnp.float32), 'text_mask': jnp.ones((B, T), bool), 'vision_mask': jnp.ones((B, G), bool), 'Wq': jax.random.normal(ks[2], (DT, INNER), jnp.float32) * s, 'Wk': jax.random.normal(ks[3], (DV, INNER), jnp.float32) * s, 'Wv': jax.random.normal(ks[4], (DV, DT), jnp.float32) * s, 'W_film_in': jax.random.normal(ks[5], (DT, 2 * DT), jnp.float32) * s, 'b_film_in': jnp.zeros((2 * DT,), jnp.float32), 'W_film_out': jax.random.normal(ks[6], (DT, 2 * DT), jnp.float32) * s, 'b_film_out': jnp.zeros((2 * DT,), jnp.float32), 'g_norm_in': jnp.ones((DT,), jnp.float32), 'b_norm_in': jnp.zeros((DT,), jnp.float32), 'g_norm_out': jnp.ones((DT,), jnp.float32), 'b_norm_out': jnp.zeros((DT,), jnp.float32), 'g_ffn': jnp.ones((DT,), jnp.float32), 'b_ffn': jnp.zeros((DT,), jnp.float32), 'W1': jax.random.normal(ks[7], (DT, HID), jnp.float32) * s, 'b1': jnp.zeros((HID,), jnp.float32), 'W2': jax.random.normal(ks[8], (HID, DT), jnp.float32) * s, 'b2': jnp.zeros((DT,), jnp.float32), 'log_dt': jnp.log(0.001) + jax.random.uniform(ks[9], (DT,), jnp.float32) * (jnp.log(0.1) - jnp.log(0.001)), 'A_re': -0.5 * jnp.ones((DT, N_STATE), jnp.float32), 'A_im': jnp.tile(jnp.pi * jnp.arange(N_STATE, dtype=jnp.float32), (DT, 1)), 'C_re': jax.random.normal(ks[10], (DT, N_STATE), jnp.float32) * 0.5 ** 0.5, 'C_im': jax.random.normal(ks[11], (DT, N_STATE), jnp.float32) * 0.5 ** 0.5, 'D_skip': jax.random.normal(ks[12], (DT,), jnp.float32), 'mod_gate': jnp.array(0.5, jnp.float32)}
        return inp
    _L0_xattn_all = _L0_xattn_setup()
    _L0_xattn_in = {k: v for k, v in _L0_xattn_all.items() if k in ('Wq', 'Wk', 'Wv', 'W_film_in', 'b_film_in', 'W_film_out', 'b_film_out', 'g_norm_in', 'b_norm_in', 'g_norm_out', 'b_norm_out', 'g_ffn', 'b_ffn', 'W1', 'b1', 'W2', 'b2', 'log_dt', 'A_re', 'A_im', 'C_re', 'C_im', 'D_skip', 'mod_gate')}
    del _L0_xattn_all

    def _L0_ffn_setup():
        import jax, jax.numpy as jnp
        import numpy as np
        E, D, F, GATE_DIM = (8, 128, 512, 16)
        B, T = (2, 256)
        key = jax.random.key(seed)
        ks = jax.random.split(key, 7)
        s = 0.02
        return {'hidden_states': jax.random.normal(ks[0], (B, T, D), dtype=jnp.float32), 'w_red': jax.random.normal(ks[1], (D, GATE_DIM), dtype=jnp.float32) * s, 'wg': jax.random.normal(ks[2], (E, GATE_DIM), dtype=jnp.float32), 'w1': jax.random.normal(ks[3], (E, D, F), dtype=jnp.float32) * s, 'b1': jax.random.normal(ks[4], (E, F), dtype=jnp.float32) * s, 'w2': jax.random.normal(ks[5], (E, F, D), dtype=jnp.float32) * s, 'b2': jax.random.normal(ks[6], (E, D), dtype=jnp.float32) * s}
    _L0_ffn_all = _L0_ffn_setup()
    _L0_ffn_in = {k: v for k, v in _L0_ffn_all.items() if k in ('w_red', 'wg', 'w1', 'b1', 'w2', 'b2')}
    del _L0_ffn_all

    def _L1_attn_setup():
        import jax, jax.numpy as jnp
        import numpy as np
        B, T, C = (8, 128, 128)

        def wkv(w_param, u, k, v):
            w = -jnp.exp(w_param.astype(jnp.float32))
            kf = k.astype(jnp.float32)
            vf = v.astype(jnp.float32)
            Bn, Tn, Cn = kf.shape
            aa0 = jnp.zeros((Bn, Cn), jnp.float32)
            bb0 = jnp.zeros((Bn, Cn), jnp.float32)
            pp0 = jnp.full((Bn, Cn), -1e+38, jnp.float32)

            def step(carry, kv_t):
                aa, bb, pp = carry
                kt, vt = kv_t
                ww = u + kt
                p = jnp.maximum(pp, ww)
                e1 = jnp.exp(pp - p)
                e2 = jnp.exp(ww - p)
                y = (e1 * aa + e2 * vt) / (e1 * bb + e2)
                ww2 = pp + w
                p2 = jnp.maximum(ww2, kt)
                e1b = jnp.exp(ww2 - p2)
                e2b = jnp.exp(kt - p2)
                return ((e1b * aa + e2b * vt, e1b * bb + e2b, p2), y)
            kT = jnp.swapaxes(kf, 0, 1)
            vT = jnp.swapaxes(vf, 0, 1)
            _, ys = jax.lax.scan(step, (aa0, bb0, pp0), (kT, vT))
            return jnp.swapaxes(ys, 0, 1).astype(k.dtype)
        key = jax.random.key(seed)
        ks = jax.random.split(key, 10)
        s = 1.0 / np.sqrt(C)
        return {'x': jax.random.normal(ks[0], (B, T, C), jnp.float32), 'time_decay': jax.random.normal(ks[1], (C,), jnp.float32) * 0.5, 'time_first': jax.random.normal(ks[2], (C,), jnp.float32) * 0.5, 'time_mix_k': jax.random.uniform(ks[3], (1, 1, C), jnp.float32), 'time_mix_v': jax.random.uniform(ks[4], (1, 1, C), jnp.float32), 'time_mix_r': jax.random.uniform(ks[5], (1, 1, C), jnp.float32), 'Wk': jax.random.normal(ks[6], (C, C), jnp.float32) * s, 'Wv': jax.random.normal(ks[7], (C, C), jnp.float32) * s, 'Wr': jax.random.normal(ks[8], (C, C), (jnpp := jnp.float32)) * s, 'Wo': jax.random.normal(ks[9], (C, C), jnp.float32) * s}
    _L1_attn_all = _L1_attn_setup()
    _L1_attn_in = {k: v for k, v in _L1_attn_all.items() if k in ('time_decay', 'time_first', 'time_mix_k', 'time_mix_v', 'time_mix_r', 'Wk', 'Wv', 'Wr', 'Wo')}
    del _L1_attn_all

    def _L1_xattn_setup():
        import jax, jax.numpy as jnp
        import numpy as np
        QUERY_DIM, KV_DIM, EMBED_DIM, NUM_HEADS = (128, 96, 128, 16)
        HEAD_DIM = EMBED_DIM // NUM_HEADS
        SCALE = HEAD_DIM ** (-0.5)
        LN_EPS = 1e-05

        def _l2norm(x, eps=1e-12):
            n = jnp.sqrt(jnp.sum(x * x, axis=-1, keepdims=True))
            return x / jnp.maximum(n, eps)
        key = jax.random.key(seed)
        ks = jax.random.split(key, 12)
        B, Nq, Nk = (2, 256, 256)
        s = lambda d: 1.0 / np.sqrt(d)
        return {'query': jax.random.normal(ks[0], (B, Nq, QUERY_DIM), jnp.float32), 'key': jax.random.normal(ks[1], (B, Nk, KV_DIM), jnp.float32), 'value': jax.random.normal(ks[2], (B, Nk, KV_DIM), jnp.float32), 'Wq': jax.random.normal(ks[3], (QUERY_DIM, EMBED_DIM), jnp.float32) * s(QUERY_DIM), 'bq': jnp.zeros((EMBED_DIM,), jnp.float32), 'Wk': jax.random.normal(ks[4], (KV_DIM, EMBED_DIM), jnp.float32) * s(KV_DIM), 'bk': jnp.zeros((EMBED_DIM,), jnp.float32), 'Wv': jax.random.normal(ks[5], (KV_DIM, EMBED_DIM), jnp.float32) * s(KV_DIM), 'bv': jnp.zeros((EMBED_DIM,), jnp.float32), 'Wo': jax.random.normal(ks[6], (EMBED_DIM, EMBED_DIM), jnp.float32) * s(EMBED_DIM), 'bo': jnp.zeros((EMBED_DIM,), jnp.float32), 'ln_gamma': jnp.ones((EMBED_DIM,), jnp.float32), 'ln_beta': jnp.zeros((EMBED_DIM,), jnp.float32)}
    _L1_xattn_all = _L1_xattn_setup()
    _L1_xattn_in = {k: v for k, v in _L1_xattn_all.items() if k in ('Wq', 'bq', 'Wk', 'bk', 'Wv', 'bv', 'Wo', 'bo', 'ln_gamma', 'ln_beta')}
    del _L1_xattn_all

    def _L1_ffn_setup():
        import jax, jax.numpy as jnp
        import numpy as np
        B, S, D, F, E = (4, 256, 128, 512, 8)
        LN_EPS = 1e-05
        key = jax.random.key(seed)
        ks = jax.random.split(key, 6)
        sc = 0.02
        return {'x': jax.random.normal(ks[0], (B, S, D), dtype=jnp.float32), 'Wr': jax.random.normal(ks[1], (D, E), dtype=jnp.float32) * sc, 'br': jnp.zeros((E,), jnp.float32), 'ln_g': jnp.ones((D,), jnp.float32), 'ln_b': jnp.zeros((D,), jnp.float32), 'W1': jax.random.normal(ks[2], (E, D, F), dtype=jnp.float32) * sc, 'b1': jnp.zeros((E, F), jnp.float32), 'W2': jax.random.normal(ks[3], (E, F, D), dtype=jnp.float32) * sc, 'b2': jnp.zeros((E, D), jnp.float32)}
    _L1_ffn_all = _L1_ffn_setup()
    _L1_ffn_in = {k: v for k, v in _L1_ffn_all.items() if k in ('Wr', 'br', 'ln_g', 'ln_b', 'W1', 'b1', 'W2', 'b2')}
    del _L1_ffn_all

    def _L2_attn_setup():
        import jax, jax.numpy as jnp
        import numpy as np
        S, B, E, H = (256, 2, 128, 16)
        D = E // H
        key = jax.random.key(seed)
        ks = jax.random.split(key, 8)
        x = jax.random.normal(ks[0], (S, B, E), dtype=jnp.float32)
        in_proj_weight = jax.random.normal(ks[1], (3 * E, E), dtype=jnp.float32) * 0.02
        in_proj_bias = jax.random.normal(ks[2], (3 * E,), dtype=jnp.float32) * 0.02
        gamma = 1.0 + jax.random.normal(ks[3], (1, 1, 3 * E), dtype=jnp.float32) * 0.1
        linear_alpha = 1.0 + jax.random.normal(ks[4], (1, 1, E), dtype=jnp.float32) * 0.1
        linear_gamma = 1.0 + jax.random.normal(ks[5], (1, 1, E), dtype=jnp.float32) * 0.1
        out_proj_weight = jax.random.normal(ks[6], (E, E), dtype=jnp.float32) * 0.02
        out_proj_bias = jax.random.normal(ks[7], (E,), dtype=jnp.float32) * 0.02
        return {'x': x, 'in_proj_weight': in_proj_weight, 'in_proj_bias': in_proj_bias, 'gamma': gamma, 'linear_alpha': linear_alpha, 'linear_gamma': linear_gamma, 'out_proj_weight': out_proj_weight, 'out_proj_bias': out_proj_bias}
    _L2_attn_all = _L2_attn_setup()
    _L2_attn_in = {k: v for k, v in _L2_attn_all.items() if k in ('in_proj_weight', 'in_proj_bias', 'gamma', 'linear_alpha', 'linear_gamma', 'out_proj_weight', 'out_proj_bias')}
    del _L2_attn_all

    def _L2_xattn_setup():
        import jax, jax.numpy as jnp
        import numpy as np
        N_HEADS = 16
        D_EMBED = 128
        D_CROSS = 96
        D_HEAD = D_EMBED // N_HEADS
        key = jax.random.key(seed)
        ks = jax.random.split(key, 10)
        B, SQ, SKV = (8, 512, 77)
        s_e = 1.0 / np.sqrt(D_EMBED)
        s_c = 1.0 / np.sqrt(D_CROSS)
        return {'x': jax.random.normal(ks[0], (B, SQ, D_EMBED), jnp.float32), 'y': jax.random.normal(ks[1], (B, SKV, D_CROSS), jnp.float32), 'wq': jax.random.normal(ks[2], (D_EMBED, D_EMBED), jnp.float32) * s_e, 'bq': jnp.zeros((D_EMBED,), jnp.float32), 'wk': jax.random.normal(ks[3], (D_CROSS, D_EMBED), jnp.float32) * s_c, 'bk': jnp.zeros((D_EMBED,), jnp.float32), 'wv': jax.random.normal(ks[4], (D_CROSS, D_EMBED), jnp.float32) * s_c, 'bv': jnp.zeros((D_EMBED,), jnp.float32), 'wo': jax.random.normal(ks[5], (D_EMBED, D_EMBED), jnp.float32) * s_e, 'bo': jnp.zeros((D_EMBED,), jnp.float32)}
    _L2_xattn_all = _L2_xattn_setup()
    _L2_xattn_in = {k: v for k, v in _L2_xattn_all.items() if k in ('wq', 'bq', 'wk', 'bk', 'wv', 'bv', 'wo', 'bo')}
    del _L2_xattn_all

    def _L2_ffn_setup():
        import jax, jax.numpy as jnp
        import numpy as np
        B, SEQ, DIM = (2, 512, 128)
        E, S = (8, 64)
        HID = 4 * DIM
        SCALE = DIM ** 0.5

        def rmsnorm(x, gamma):
            n = jnp.linalg.norm(x, axis=-1, keepdims=True)
            return x / jnp.maximum(n, 1e-12) * SCALE * gamma
        key = jax.random.key(seed)
        ks = jax.random.split(key, 4)
        w_init = lambda k, shape: jax.random.normal(k, shape, dtype=jnp.float32) * 0.02
        return {'x': jax.random.normal(ks[0], (B, SEQ, DIM), dtype=jnp.float32), 'norm_gamma': jnp.ones((DIM,), jnp.float32), 'slot_norm_gamma': jnp.ones((DIM,), jnp.float32), 'slot_embeds': jax.random.normal(ks[1], (E, S, DIM), dtype=jnp.float32), 'w1': w_init(ks[2], (E, DIM, HID)), 'b1': jnp.zeros((E, HID), jnp.float32), 'w2': w_init(ks[3], (E, HID, DIM)), 'b2': jnp.zeros((E, DIM), jnp.float32)}
    _L2_ffn_all = _L2_ffn_setup()
    _L2_ffn_in = {k: v for k, v in _L2_ffn_all.items() if k in ('norm_gamma', 'slot_norm_gamma', 'slot_embeds', 'w1', 'b1', 'w2', 'b2')}
    del _L2_ffn_all

    def _L3_attn_setup():
        import jax, jax.numpy as jnp
        import numpy as np
        NUM_HEADS = 16

        def _feature(x):
            return jax.nn.elu(x) + 1.0
        key = jax.random.key(seed)
        ks = jax.random.split(key, 9)
        B, N, E = (2, 256, 128)
        s = 1.0 / np.sqrt(E).astype(np.float32)
        inp = {'x': jax.random.normal(ks[0], (B, N, E), jnp.float32)}
        names = ['q', 'k', 'v', 'o']
        for i, n in enumerate(names):
            inp[f'W{n}'] = jax.random.normal(ks[1 + 2 * i], (E, E), jnp.float32) * s
            inp[f'b{n}'] = jax.random.normal(ks[2 + 2 * i], (E,), jnp.float32) * 0.01
        return inp
    _L3_attn_all = _L3_attn_setup()
    _L3_attn_in = {k: v for k, v in _L3_attn_all.items() if k in ('Wq', 'bq', 'Wk', 'bk', 'Wv', 'bv', 'Wo', 'bo')}
    del _L3_attn_all

    def _L3_xattn_setup():
        import jax, jax.numpy as jnp
        import numpy as np
        H = 8
        D = 64
        SCALE = D ** (-0.5)
        key = jax.random.key(seed)
        ks = jax.random.split(key, 7)
        B, Nq, Nkv = (2, 256, 256)
        Cq, Ck, I = (128, 96, H * D)
        return {'x': jax.random.normal(ks[0], (B, Nq, Cq), jnp.float32), 'context': jax.random.normal(ks[1], (B, Nkv, Ck), jnp.float32), 'Wq': jax.random.normal(ks[2], (Cq, I), jnp.float32) * Cq ** (-0.5), 'Wk': jax.random.normal(ks[3], (Ck, I), jnp.float32) * Ck ** (-0.5), 'Wv': jax.random.normal(ks[4], (Ck, I), jnp.float32) * Ck ** (-0.5), 'Wo': jax.random.normal(ks[5], (I, Cq), jnp.float32) * I ** (-0.5), 'bo': jnp.zeros((Cq,), jnp.float32)}
    _L3_xattn_all = _L3_xattn_setup()
    _L3_xattn_in = {k: v for k, v in _L3_xattn_all.items() if k in ('Wq', 'Wk', 'Wv', 'Wo', 'bo')}
    del _L3_xattn_all

    def _L3_ffn_setup():
        import jax, jax.numpy as jnp
        import numpy as np
        D_MODEL = 128
        N_HEADS = 16
        HEAD_DIM = D_MODEL // N_HEADS
        FFN_DIM = 512
        N_EXPERTS = 8
        TOP_K = 2
        BATCH = 4
        SEQ = 128

        def _layernorm(x, w, b, eps=1e-05):
            mu = jnp.mean(x, axis=-1, keepdims=True)
            var = jnp.mean(jnp.square(x - mu), axis=-1, keepdims=True)
            return (x - mu) * jax.lax.rsqrt(var + eps) * w + b

        def _causal_attention(nx, Wqkv, bqkv, Wo, bo):
            B, S, D = nx.shape
            qkv = nx @ Wqkv + bqkv
            q, k, v = jnp.split(qkv, 3, axis=-1)
            q = q.reshape(B, S, N_HEADS, HEAD_DIM)
            k = k.reshape(B, S, N_HEADS, HEAD_DIM)
            v = v.reshape(B, S, N_HEADS, HEAD_DIM)
            scores = jnp.einsum('bqhd,bkhd->bhqk', q, k) / jnp.sqrt(jnp.float32(HEAD_DIM))
            causal = jnp.tril(jnp.ones((S, S), bool))
            scores = jnp.where(causal, scores, jnp.finfo(scores.dtype).min)
            attn = jax.nn.softmax(scores, axis=-1)
            out = jnp.einsum('bhqk,bkhd->bqhd', attn, v).reshape(B, S, D)
            return out @ Wo + bo

        def _moe_ffn(nx, gate_W, fc1_w, fc1_b, fc2_w, fc2_b):
            gate_logits = nx @ gate_W
            topk_vals, topk_idx = jax.lax.top_k(gate_logits, TOP_K)
            gate_w = jax.nn.softmax(topk_vals, axis=-1)
            dense_gates = jnp.sum(jax.nn.one_hot(topk_idx, N_EXPERTS, dtype=nx.dtype) * gate_w[..., None], axis=-2)
            moe_out = jnp.zeros_like(nx)
            for e in range(N_EXPERTS):
                h = jax.nn.gelu(jnp.einsum('bsd,fd->bsf', nx, fc1_w[e]) + fc1_b[e], approximate=False)
                y = jnp.einsum('bsf,df->bsd', h, fc2_w[e]) + fc2_b[e]
                moe_out = moe_out + y * dense_gates[..., e:e + 1]
            return moe_out
        key = jax.random.key(seed)
        ks = jax.random.split(key, 12)
        s = lambda k, shape, scale: jax.random.normal(k, shape, dtype=jnp.float32) * scale
        inp = {'x': s(ks[0], (BATCH, SEQ, D_MODEL), 1.0), 'ln1_w': jnp.ones((D_MODEL,), jnp.float32), 'ln1_b': jnp.zeros((D_MODEL,), jnp.float32), 'ln2_w': jnp.ones((D_MODEL,), jnp.float32), 'ln2_b': jnp.zeros((D_MODEL,), jnp.float32), 'Wqkv': s(ks[1], (D_MODEL, 3 * D_MODEL), 0.02), 'bqkv': jnp.zeros((3 * D_MODEL,), jnp.float32), 'Wo': s(ks[2], (D_MODEL, D_MODEL), 0.02), 'bo': jnp.zeros((D_MODEL,), jnp.float32), 'gate_W': s(ks[3], (D_MODEL, N_EXPERTS), 0.02), 'fc1_w': s(ks[4], (N_EXPERTS, FFN_DIM, D_MODEL), (2.0 / D_MODEL) ** 0.5), 'fc1_b': jnp.zeros((N_EXPERTS, FFN_DIM), jnp.float32), 'fc2_w': s(ks[5], (N_EXPERTS, D_MODEL, FFN_DIM), (1.0 / FFN_DIM) ** 0.5), 'fc2_b': jnp.zeros((N_EXPERTS, D_MODEL), jnp.float32)}
        return inp
    _L3_ffn_all = _L3_ffn_setup()
    _L3_ffn_in = {k: v for k, v in _L3_ffn_all.items() if k in ('ln1_w', 'ln1_b', 'ln2_w', 'ln2_b', 'Wqkv', 'bqkv', 'Wo', 'bo', 'gate_W', 'fc1_w', 'fc1_b', 'fc2_w', 'fc2_b')}
    del _L3_ffn_all
    return {'x': x, 'ctx_768': ctx_768, 'mask_BxS_bf1': mask_BxS_bf1, 'mask_BxS2_bf1': mask_BxS2_bf1, 'L0_attn_Wq': _L0_attn_in['Wq'], 'L0_attn_bq': _L0_attn_in['bq'], 'L0_attn_Wk': _L0_attn_in['Wk'], 'L0_attn_bk': _L0_attn_in['bk'], 'L0_attn_Wv': _L0_attn_in['Wv'], 'L0_attn_bv': _L0_attn_in['bv'], 'L0_attn_Wg': _L0_attn_in['Wg'], 'L0_attn_bg': _L0_attn_in['bg'], 'L0_attn_gamma': _L0_attn_in['gamma'], 'L0_attn_beta': _L0_attn_in['beta'], 'L0_xattn_Wq': _L0_xattn_in['Wq'], 'L0_xattn_Wk': _L0_xattn_in['Wk'], 'L0_xattn_Wv': _L0_xattn_in['Wv'], 'L0_xattn_W_film_in': _L0_xattn_in['W_film_in'], 'L0_xattn_b_film_in': _L0_xattn_in['b_film_in'], 'L0_xattn_W_film_out': _L0_xattn_in['W_film_out'], 'L0_xattn_b_film_out': _L0_xattn_in['b_film_out'], 'L0_xattn_g_norm_in': _L0_xattn_in['g_norm_in'], 'L0_xattn_b_norm_in': _L0_xattn_in['b_norm_in'], 'L0_xattn_g_norm_out': _L0_xattn_in['g_norm_out'], 'L0_xattn_b_norm_out': _L0_xattn_in['b_norm_out'], 'L0_xattn_g_ffn': _L0_xattn_in['g_ffn'], 'L0_xattn_b_ffn': _L0_xattn_in['b_ffn'], 'L0_xattn_W1': _L0_xattn_in['W1'], 'L0_xattn_b1': _L0_xattn_in['b1'], 'L0_xattn_W2': _L0_xattn_in['W2'], 'L0_xattn_b2': _L0_xattn_in['b2'], 'L0_xattn_log_dt': _L0_xattn_in['log_dt'], 'L0_xattn_A_re': _L0_xattn_in['A_re'], 'L0_xattn_A_im': _L0_xattn_in['A_im'], 'L0_xattn_C_re': _L0_xattn_in['C_re'], 'L0_xattn_C_im': _L0_xattn_in['C_im'], 'L0_xattn_D_skip': _L0_xattn_in['D_skip'], 'L0_xattn_mod_gate': _L0_xattn_in['mod_gate'], 'L0_ffn_w_red': _L0_ffn_in['w_red'], 'L0_ffn_wg': _L0_ffn_in['wg'], 'L0_ffn_w1': _L0_ffn_in['w1'], 'L0_ffn_b1': _L0_ffn_in['b1'], 'L0_ffn_w2': _L0_ffn_in['w2'], 'L0_ffn_b2': _L0_ffn_in['b2'], 'L1_attn_time_decay': _L1_attn_in['time_decay'], 'L1_attn_time_first': _L1_attn_in['time_first'], 'L1_attn_time_mix_k': _L1_attn_in['time_mix_k'], 'L1_attn_time_mix_v': _L1_attn_in['time_mix_v'], 'L1_attn_time_mix_r': _L1_attn_in['time_mix_r'], 'L1_attn_Wk': _L1_attn_in['Wk'], 'L1_attn_Wv': _L1_attn_in['Wv'], 'L1_attn_Wr': _L1_attn_in['Wr'], 'L1_attn_Wo': _L1_attn_in['Wo'], 'L1_xattn_Wq': _L1_xattn_in['Wq'], 'L1_xattn_bq': _L1_xattn_in['bq'], 'L1_xattn_Wk': _L1_xattn_in['Wk'], 'L1_xattn_bk': _L1_xattn_in['bk'], 'L1_xattn_Wv': _L1_xattn_in['Wv'], 'L1_xattn_bv': _L1_xattn_in['bv'], 'L1_xattn_Wo': _L1_xattn_in['Wo'], 'L1_xattn_bo': _L1_xattn_in['bo'], 'L1_xattn_ln_gamma': _L1_xattn_in['ln_gamma'], 'L1_xattn_ln_beta': _L1_xattn_in['ln_beta'], 'L1_ffn_Wr': _L1_ffn_in['Wr'], 'L1_ffn_br': _L1_ffn_in['br'], 'L1_ffn_ln_g': _L1_ffn_in['ln_g'], 'L1_ffn_ln_b': _L1_ffn_in['ln_b'], 'L1_ffn_W1': _L1_ffn_in['W1'], 'L1_ffn_b1': _L1_ffn_in['b1'], 'L1_ffn_W2': _L1_ffn_in['W2'], 'L1_ffn_b2': _L1_ffn_in['b2'], 'L2_attn_in_proj_weight': _L2_attn_in['in_proj_weight'], 'L2_attn_in_proj_bias': _L2_attn_in['in_proj_bias'], 'L2_attn_gamma': _L2_attn_in['gamma'], 'L2_attn_linear_alpha': _L2_attn_in['linear_alpha'], 'L2_attn_linear_gamma': _L2_attn_in['linear_gamma'], 'L2_attn_out_proj_weight': _L2_attn_in['out_proj_weight'], 'L2_attn_out_proj_bias': _L2_attn_in['out_proj_bias'], 'L2_xattn_wq': _L2_xattn_in['wq'], 'L2_xattn_bq': _L2_xattn_in['bq'], 'L2_xattn_wk': _L2_xattn_in['wk'], 'L2_xattn_bk': _L2_xattn_in['bk'], 'L2_xattn_wv': _L2_xattn_in['wv'], 'L2_xattn_bv': _L2_xattn_in['bv'], 'L2_xattn_wo': _L2_xattn_in['wo'], 'L2_xattn_bo': _L2_xattn_in['bo'], 'L2_ffn_norm_gamma': _L2_ffn_in['norm_gamma'], 'L2_ffn_slot_norm_gamma': _L2_ffn_in['slot_norm_gamma'], 'L2_ffn_slot_embeds': _L2_ffn_in['slot_embeds'], 'L2_ffn_w1': _L2_ffn_in['w1'], 'L2_ffn_b1': _L2_ffn_in['b1'], 'L2_ffn_w2': _L2_ffn_in['w2'], 'L2_ffn_b2': _L2_ffn_in['b2'], 'L3_attn_Wq': _L3_attn_in['Wq'], 'L3_attn_bq': _L3_attn_in['bq'], 'L3_attn_Wk': _L3_attn_in['Wk'], 'L3_attn_bk': _L3_attn_in['bk'], 'L3_attn_Wv': _L3_attn_in['Wv'], 'L3_attn_bv': _L3_attn_in['bv'], 'L3_attn_Wo': _L3_attn_in['Wo'], 'L3_attn_bo': _L3_attn_in['bo'], 'L3_xattn_Wq': _L3_xattn_in['Wq'], 'L3_xattn_Wk': _L3_xattn_in['Wk'], 'L3_xattn_Wv': _L3_xattn_in['Wv'], 'L3_xattn_Wo': _L3_xattn_in['Wo'], 'L3_xattn_bo': _L3_xattn_in['bo'], 'L3_ffn_ln1_w': _L3_ffn_in['ln1_w'], 'L3_ffn_ln1_b': _L3_ffn_in['ln1_b'], 'L3_ffn_ln2_w': _L3_ffn_in['ln2_w'], 'L3_ffn_ln2_b': _L3_ffn_in['ln2_b'], 'L3_ffn_Wqkv': _L3_ffn_in['Wqkv'], 'L3_ffn_bqkv': _L3_ffn_in['bqkv'], 'L3_ffn_Wo': _L3_ffn_in['Wo'], 'L3_ffn_bo': _L3_ffn_in['bo'], 'L3_ffn_gate_W': _L3_ffn_in['gate_W'], 'L3_ffn_fc1_w': _L3_ffn_in['fc1_w'], 'L3_ffn_fc1_b': _L3_ffn_in['fc1_b'], 'L3_ffn_fc2_w': _L3_ffn_in['fc2_w'], 'L3_ffn_fc2_b': _L3_ffn_in['fc2_b']}

def reference(x, ctx_768, mask_BxS_bf1, mask_BxS2_bf1, L0_attn_Wq, L0_attn_bq, L0_attn_Wk, L0_attn_bk, L0_attn_Wv, L0_attn_bv, L0_attn_Wg, L0_attn_bg, L0_attn_gamma, L0_attn_beta, L0_xattn_Wq, L0_xattn_Wk, L0_xattn_Wv, L0_xattn_W_film_in, L0_xattn_b_film_in, L0_xattn_W_film_out, L0_xattn_b_film_out, L0_xattn_g_norm_in, L0_xattn_b_norm_in, L0_xattn_g_norm_out, L0_xattn_b_norm_out, L0_xattn_g_ffn, L0_xattn_b_ffn, L0_xattn_W1, L0_xattn_b1, L0_xattn_W2, L0_xattn_b2, L0_xattn_log_dt, L0_xattn_A_re, L0_xattn_A_im, L0_xattn_C_re, L0_xattn_C_im, L0_xattn_D_skip, L0_xattn_mod_gate, L0_ffn_w_red, L0_ffn_wg, L0_ffn_w1, L0_ffn_b1, L0_ffn_w2, L0_ffn_b2, L1_attn_time_decay, L1_attn_time_first, L1_attn_time_mix_k, L1_attn_time_mix_v, L1_attn_time_mix_r, L1_attn_Wk, L1_attn_Wv, L1_attn_Wr, L1_attn_Wo, L1_xattn_Wq, L1_xattn_bq, L1_xattn_Wk, L1_xattn_bk, L1_xattn_Wv, L1_xattn_bv, L1_xattn_Wo, L1_xattn_bo, L1_xattn_ln_gamma, L1_xattn_ln_beta, L1_ffn_Wr, L1_ffn_br, L1_ffn_ln_g, L1_ffn_ln_b, L1_ffn_W1, L1_ffn_b1, L1_ffn_W2, L1_ffn_b2, L2_attn_in_proj_weight, L2_attn_in_proj_bias, L2_attn_gamma, L2_attn_linear_alpha, L2_attn_linear_gamma, L2_attn_out_proj_weight, L2_attn_out_proj_bias, L2_xattn_wq, L2_xattn_bq, L2_xattn_wk, L2_xattn_bk, L2_xattn_wv, L2_xattn_bv, L2_xattn_wo, L2_xattn_bo, L2_ffn_norm_gamma, L2_ffn_slot_norm_gamma, L2_ffn_slot_embeds, L2_ffn_w1, L2_ffn_b1, L2_ffn_w2, L2_ffn_b2, L3_attn_Wq, L3_attn_bq, L3_attn_Wk, L3_attn_bk, L3_attn_Wv, L3_attn_bv, L3_attn_Wo, L3_attn_bo, L3_xattn_Wq, L3_xattn_Wk, L3_xattn_Wv, L3_xattn_Wo, L3_xattn_bo, L3_ffn_ln1_w, L3_ffn_ln1_b, L3_ffn_ln2_w, L3_ffn_ln2_b, L3_ffn_Wqkv, L3_ffn_bqkv, L3_ffn_Wo, L3_ffn_bo, L3_ffn_gate_W, L3_ffn_fc1_w, L3_ffn_fc1_b, L3_ffn_fc2_w, L3_ffn_fc2_b):
    import jax
    import jax.numpy as jnp

    def _L0_attn_ref(x, Wq, bq, Wk, bk, Wv, bv, Wg, bg, gamma, beta):
        import jax, jax.numpy as jnp
        import numpy as np
        HIDDEN = 128
        HEADS = 16
        HEAD_DIM = HIDDEN // HEADS
        EPS = 1e-05
        B, S, H = x.shape

        def heads(t):
            return t.reshape(B, S, HEADS, HEAD_DIM).transpose(0, 2, 1, 3)
        Q = heads(x @ Wq + bq)
        K = heads(x @ Wk + bk)
        V = heads(x @ Wv + bv)
        scores = jnp.einsum('bhqd,bhkd->bhqk', Q, K) / jnp.sqrt(jnp.float32(HEAD_DIM))
        flow = scores - scores.transpose(0, 1, 3, 2)
        w = jax.nn.softmax(flow, axis=-1)
        flowed = jnp.einsum('bhqk,bhkd->bhqd', w, V)
        flowed = flowed.transpose(0, 2, 1, 3).reshape(B, S, H)
        gate = jax.nn.sigmoid(jnp.concatenate([x, flowed], axis=-1) @ Wg + bg)
        y = x + gate * flowed
        mu = jnp.mean(y, axis=-1, keepdims=True)
        var = jnp.mean(jnp.square(y - mu), axis=-1, keepdims=True)
        return (y - mu) * jax.lax.rsqrt(var + EPS) * gamma + beta

    def _L0_xattn_ref(x_text, x_vision, text_mask, vision_mask, Wq, Wk, Wv, W_film_in, b_film_in, W_film_out, b_film_out, g_norm_in, b_norm_in, g_norm_out, b_norm_out, g_ffn, b_ffn, W1, b1, W2, b2, log_dt, A_re, A_im, C_re, C_im, D_skip, mod_gate):
        import jax, jax.numpy as jnp
        import numpy as np
        B, T, DT, G, DV = (16, 64, 128, 72, 96)
        H, DH = (4, 32)
        INNER = H * DH
        HID = 4 * DT
        N_STATE = 64
        K_TOP = 32

        def layernorm(x, g, b, eps=1e-05):
            m = x.mean(-1, keepdims=True)
            v = x.var(-1, keepdims=True)
            return (x - m) * jax.lax.rsqrt(v + eps) * g + b

        def s4d(x, log_dt, A_re, A_im, C_re, C_im, D_skip):
            Bb, L, D = x.shape
            dt = jnp.exp(log_dt)
            A = A_re + 1j * A_im
            C = C_re + 1j * C_im
            dtA = dt[:, None] * A
            dC = C * (jnp.exp(dtA) - 1.0) / A
            powers = jnp.exp(dtA[:, :, None] * jnp.arange(L))
            K = 2.0 * jnp.einsum('dn,dnl->dl', dC, powers).real
            n = 2 * L
            Kf = jnp.fft.rfft(K, n=n, axis=-1)
            xf = jnp.fft.rfft(x, n=n, axis=1)
            y = jnp.fft.irfft(xf * Kf.T[None], n=n, axis=1)[:, :L]
            return y + x * D_skip
        Bb, Tt, D = x_text.shape
        Gg = x_vision.shape[1]
        Q = (x_text @ Wq).reshape(Bb, Tt, H, DH)
        K = (x_vision @ Wk).reshape(Bb, Gg, H, DH)
        scores = jnp.einsum('bthd,bghd->bhtg', Q, K) / np.sqrt(DH).astype(np.float32)
        scores = jnp.where(vision_mask[:, None, None, :], scores, -jnp.inf)
        topv, topi = jax.lax.top_k(scores, K_TOP)
        probs = jax.nn.softmax(topv, axis=-1)
        bi = jnp.arange(Bb)[:, None, None, None]
        hi = jnp.arange(H)[None, :, None, None]
        ti = jnp.arange(Tt)[None, None, :, None]
        attn = jnp.zeros_like(scores).at[bi, hi, ti, topi].set(probs)
        attn_mean = attn.mean(axis=1)
        V = x_vision @ Wv
        c_t = jnp.einsum('btg,bgd->btd', attn_mean, V)
        c_t = c_t * text_mask[..., None]
        x = layernorm(x_text, g_norm_in, b_norm_in)
        scale_in, shift_in = jnp.split(c_t @ W_film_in + b_film_in, 2, axis=-1)
        x = x * (1.0 + mod_gate * scale_in) + mod_gate * shift_in
        y = s4d(x, log_dt, A_re, A_im, C_re, C_im, D_skip)
        scale_out, shift_out = jnp.split(c_t @ W_film_out + b_film_out, 2, axis=-1)
        y = y * (1.0 + mod_gate * scale_out) + mod_gate * shift_out
        xt = x_text + y
        h = layernorm(xt, g_ffn, b_ffn)
        h = jax.nn.gelu(h @ W1 + b1, approximate=False) @ W2 + b2
        xt = xt + h
        return layernorm(xt, g_norm_out, b_norm_out)

    def _L0_ffn_ref(hidden_states, w_red, wg, w1, b1, w2, b2):
        import jax, jax.numpy as jnp
        import numpy as np
        E, D, F, GATE_DIM = (8, 128, 512, 16)
        B, T = (2, 256)
        b, t, c = hidden_states.shape
        x = hidden_states.reshape(-1, c)
        red = x @ w_red
        wg_n = wg / jnp.maximum(jnp.linalg.norm(wg, axis=1, keepdims=True), 0.0001)
        logits = red @ wg_n.T
        gates = jax.nn.softmax(logits, axis=1)
        idx = jnp.argmax(gates, axis=1)
        scores = jnp.take_along_axis(gates, idx[:, None], axis=1)
        h = jax.nn.gelu(jnp.einsum('td,edf->etf', x, w1) + b1[:, None, :], approximate=False)
        y = jnp.einsum('etf,efd->etd', h, w2) + b2[:, None, :]
        out = jnp.take_along_axis(y, idx[None, :, None], axis=0)[0]
        out = out * scores
        return out.reshape(b, t, c)

    def _L1_attn_ref(x, time_decay, time_first, time_mix_k, time_mix_v, time_mix_r, Wk, Wv, Wr, Wo):
        import jax, jax.numpy as jnp
        import numpy as np
        B, T, C = (8, 128, 128)

        def wkv(w_param, u, k, v):
            w = -jnp.exp(w_param.astype(jnp.float32))
            kf = k.astype(jnp.float32)
            vf = v.astype(jnp.float32)
            Bn, Tn, Cn = kf.shape
            aa0 = jnp.zeros((Bn, Cn), jnp.float32)
            bb0 = jnp.zeros((Bn, Cn), jnp.float32)
            pp0 = jnp.full((Bn, Cn), -1e+38, jnp.float32)

            def step(carry, kv_t):
                aa, bb, pp = carry
                kt, vt = kv_t
                ww = u + kt
                p = jnp.maximum(pp, ww)
                e1 = jnp.exp(pp - p)
                e2 = jnp.exp(ww - p)
                y = (e1 * aa + e2 * vt) / (e1 * bb + e2)
                ww2 = pp + w
                p2 = jnp.maximum(ww2, kt)
                e1b = jnp.exp(ww2 - p2)
                e2b = jnp.exp(kt - p2)
                return ((e1b * aa + e2b * vt, e1b * bb + e2b, p2), y)
            kT = jnp.swapaxes(kf, 0, 1)
            vT = jnp.swapaxes(vf, 0, 1)
            _, ys = jax.lax.scan(step, (aa0, bb0, pp0), (kT, vT))
            return jnp.swapaxes(ys, 0, 1).astype(k.dtype)
        xx = jnp.pad(x, ((0, 0), (1, 0), (0, 0)))[:, :-1, :]
        xk = x * time_mix_k + xx * (1 - time_mix_k)
        xv = x * time_mix_v + xx * (1 - time_mix_v)
        xr = x * time_mix_r + xx * (1 - time_mix_r)
        k = jnp.einsum('btc,dc->btd', xk, Wk)
        v = jnp.einsum('btc,dc->btd', xv, Wv)
        sr = jax.nn.sigmoid(jnp.einsum('btc,dc->btd', xr, Wr))
        rwkv = sr * wkv(time_decay, time_first, k, v)
        return jnp.einsum('btd,cd->btc', rwkv, Wo)

    def _L1_xattn_ref(query, key, value, Wq, bq, Wk, bk, Wv, bv, Wo, bo, ln_gamma, ln_beta):
        import jax, jax.numpy as jnp
        import numpy as np
        QUERY_DIM, KV_DIM, EMBED_DIM, NUM_HEADS = (128, 96, 128, 16)
        HEAD_DIM = EMBED_DIM // NUM_HEADS
        SCALE = HEAD_DIM ** (-0.5)
        LN_EPS = 1e-05

        def _l2norm(x, eps=1e-12):
            n = jnp.sqrt(jnp.sum(x * x, axis=-1, keepdims=True))
            return x / jnp.maximum(n, eps)
        B, Nq, _ = query.shape
        Nk = key.shape[1]
        Qp = query @ Wq + bq
        K = _l2norm(key @ Wk + bk)
        V = value @ Wv + bv
        Q = _l2norm(Qp)
        Q = Q.reshape(B, Nq, NUM_HEADS, HEAD_DIM).transpose(0, 2, 1, 3)
        K = K.reshape(B, Nk, NUM_HEADS, HEAD_DIM).transpose(0, 2, 1, 3)
        V = V.reshape(B, Nk, NUM_HEADS, HEAD_DIM).transpose(0, 2, 1, 3)
        scores = jnp.einsum('bhqd,bhkd->bhqk', Q, K) * SCALE
        attn = jax.nn.softmax(scores, axis=-1)
        out = jnp.einsum('bhqk,bhkd->bhqd', attn, V)
        out = out.transpose(0, 2, 1, 3).reshape(B, Nq, EMBED_DIM)
        out = out @ Wo + bo
        x = out + Qp
        mu = jnp.mean(x, axis=-1, keepdims=True)
        var = jnp.mean((x - mu) ** 2, axis=-1, keepdims=True)
        return (x - mu) / jnp.sqrt(var + LN_EPS) * ln_gamma + ln_beta

    def _L1_ffn_ref(x, Wr, br, ln_g, ln_b, W1, b1, W2, b2):
        import jax, jax.numpy as jnp
        import numpy as np
        B, S, D, F, E = (4, 256, 128, 512, 8)
        LN_EPS = 1e-05
        tokens_shape = x.shape[:-1]
        xt = x.reshape(-1, x.shape[-1])
        router_logits = xt @ Wr + br
        router_probs = jax.nn.softmax(router_logits, axis=-1)
        gates = jnp.max(router_probs, axis=-1, keepdims=True)
        idx = jnp.argmax(router_probs, axis=-1)
        onehot = jax.nn.one_hot(idx, E, dtype=xt.dtype)
        mu = jnp.mean(xt, axis=-1, keepdims=True)
        var = jnp.mean(jnp.square(xt - mu), axis=-1, keepdims=True)
        xn = (xt - mu) * jax.lax.rsqrt(var + LN_EPS) * ln_g + ln_b
        h = jnp.einsum('te,td,edf->tf', onehot, xn, W1) + b1[idx]
        h = jax.nn.relu(h)
        y = jnp.einsum('te,tf,efd->td', onehot, h, W2) + b2[idx]
        y = y * gates
        return y.reshape(tokens_shape + (y.shape[-1],))

    def _L2_attn_ref(x, in_proj_weight, in_proj_bias, gamma, linear_alpha, linear_gamma, out_proj_weight, out_proj_bias):
        import jax, jax.numpy as jnp
        import numpy as np
        S, B, E, H = (256, 2, 128, 16)
        D = E // H
        s, b, e = x.shape
        qkv = jnp.einsum('sbe,fe->sbf', x, in_proj_weight) + in_proj_bias
        qkv = qkv * gamma
        q, k, v = jnp.split(qkv, 3, axis=-1)

        def to_heads(t):
            return t.reshape(s, b * H, D).transpose(1, 0, 2)
        q, k, v = (to_heads(q), to_heads(k), to_heads(v))
        q = q / jnp.sqrt(jnp.asarray(D, dtype=q.dtype))
        scores = jnp.einsum('bsd,btd->bst', q, k)
        causal = jnp.tril(jnp.ones((s, s), dtype=bool))
        scores = jnp.where(causal[None], scores, jnp.asarray(-jnp.inf, scores.dtype))
        attn = jax.nn.softmax(scores, axis=-1)
        out = jnp.einsum('bst,btd->bsd', attn, v)
        out = out.transpose(1, 0, 2).reshape(s, b, e)
        out = out * linear_alpha
        out = jnp.einsum('sbe,fe->sbf', out, out_proj_weight) + out_proj_bias
        out = out * linear_gamma
        return out

    def _L2_xattn_ref(x, y, wq, bq, wk, bk, wv, bv, wo, bo):
        import jax, jax.numpy as jnp
        import numpy as np
        N_HEADS = 16
        D_EMBED = 128
        D_CROSS = 96
        D_HEAD = D_EMBED // N_HEADS
        B, SQ, _ = x.shape
        SKV = y.shape[1]
        q = (x @ wq + bq).reshape(B, SQ, N_HEADS, D_HEAD)
        k = (y @ wk + bk).reshape(B, SKV, N_HEADS, D_HEAD)
        v = (y @ wv + bv).reshape(B, SKV, N_HEADS, D_HEAD)
        scores = jnp.einsum('bqhd,bkhd->bhqk', q, k) / jnp.sqrt(jnp.asarray(D_HEAD, x.dtype))
        attn = jax.nn.softmax(scores, axis=-1)
        out = jnp.einsum('bhqk,bkhd->bqhd', attn, v).reshape(B, SQ, D_EMBED)
        return out @ wo + bo

    def _L2_ffn_ref(x, norm_gamma, slot_norm_gamma, slot_embeds, w1, b1, w2, b2):
        import jax, jax.numpy as jnp
        import numpy as np
        B, SEQ, DIM = (2, 512, 128)
        E, S = (8, 64)
        HID = 4 * DIM
        SCALE = DIM ** 0.5

        def rmsnorm(x, gamma):
            n = jnp.linalg.norm(x, axis=-1, keepdims=True)
            return x / jnp.maximum(n, 1e-12) * SCALE * gamma
        xn = rmsnorm(x, norm_gamma)
        sn = rmsnorm(slot_embeds, slot_norm_gamma)
        logits = jnp.einsum('bnd,esd->bnes', xn, sn)
        dispatch = jax.nn.softmax(logits, axis=1)
        b, n, e, s = logits.shape
        combine = jax.nn.softmax(logits.reshape(b, n, e * s), axis=-1)
        slots = jnp.einsum('bnd,bnes->besd', xn, dispatch)
        h = jnp.einsum('besd,edh->besh', slots, w1) + b1[None, :, None, :]
        h = jax.nn.gelu(h, approximate=False)
        eo = jnp.einsum('besh,ehd->besd', h, w2) + b2[None, :, None, :]
        eo = eo.reshape(b, e * s, DIM)
        out = jnp.einsum('bmd,bnm->bnd', eo, combine)
        return out

    def _L3_attn_ref(x, Wq, bq, Wk, bk, Wv, bv, Wo, bo):
        import jax, jax.numpy as jnp
        import numpy as np
        NUM_HEADS = 16

        def _feature(x):
            return jax.nn.elu(x) + 1.0
        B, N, E = x.shape
        H = NUM_HEADS
        d = E // H

        def proj(t, W, b):
            return t @ W.T + b

        def split_heads(t):
            return t.reshape(B, N, H, d).transpose(0, 2, 1, 3)
        q = _feature(split_heads(proj(x, Wq, bq)))
        k = _feature(split_heads(proj(x, Wk, bk)))
        v = split_heads(proj(x, Wv, bv))
        kv = jnp.cumsum(k[..., :, None] * v[..., None, :], axis=2)
        o = jnp.einsum('bhnd,bhnde->bhne', q, kv)
        o = o.transpose(0, 2, 1, 3).reshape(B, N, E)
        return o @ Wo.T + bo

    def _L3_xattn_ref(x, context, Wq, Wk, Wv, Wo, bo):
        import jax, jax.numpy as jnp
        import numpy as np
        H = 8
        D = 64
        SCALE = D ** (-0.5)
        B, Nq, _ = x.shape
        Nkv = context.shape[1]
        q = (x @ Wq).reshape(B, Nq, H, D)
        k = (context @ Wk).reshape(B, Nkv, H, D)
        v = (context @ Wv).reshape(B, Nkv, H, D)
        sim = jnp.einsum('bihd,bjhd->bhij', q, k) * SCALE
        attn = jax.nn.softmax(sim, axis=-1)
        out = jnp.einsum('bhij,bjhd->bihd', attn, v).reshape(B, Nq, H * D)
        return out @ Wo + bo

    def _L3_ffn_ref(x, ln1_w, ln1_b, ln2_w, ln2_b, Wqkv, bqkv, Wo, bo, gate_W, fc1_w, fc1_b, fc2_w, fc2_b):
        import jax, jax.numpy as jnp
        import numpy as np
        D_MODEL = 128
        N_HEADS = 16
        HEAD_DIM = D_MODEL // N_HEADS
        FFN_DIM = 512
        N_EXPERTS = 8
        TOP_K = 2
        BATCH = 4
        SEQ = 128

        def _layernorm(x, w, b, eps=1e-05):
            mu = jnp.mean(x, axis=-1, keepdims=True)
            var = jnp.mean(jnp.square(x - mu), axis=-1, keepdims=True)
            return (x - mu) * jax.lax.rsqrt(var + eps) * w + b

        def _causal_attention(nx, Wqkv, bqkv, Wo, bo):
            B, S, D = nx.shape
            qkv = nx @ Wqkv + bqkv
            q, k, v = jnp.split(qkv, 3, axis=-1)
            q = q.reshape(B, S, N_HEADS, HEAD_DIM)
            k = k.reshape(B, S, N_HEADS, HEAD_DIM)
            v = v.reshape(B, S, N_HEADS, HEAD_DIM)
            scores = jnp.einsum('bqhd,bkhd->bhqk', q, k) / jnp.sqrt(jnp.float32(HEAD_DIM))
            causal = jnp.tril(jnp.ones((S, S), bool))
            scores = jnp.where(causal, scores, jnp.finfo(scores.dtype).min)
            attn = jax.nn.softmax(scores, axis=-1)
            out = jnp.einsum('bhqk,bkhd->bqhd', attn, v).reshape(B, S, D)
            return out @ Wo + bo

        def _moe_ffn(nx, gate_W, fc1_w, fc1_b, fc2_w, fc2_b):
            gate_logits = nx @ gate_W
            topk_vals, topk_idx = jax.lax.top_k(gate_logits, TOP_K)
            gate_w = jax.nn.softmax(topk_vals, axis=-1)
            dense_gates = jnp.sum(jax.nn.one_hot(topk_idx, N_EXPERTS, dtype=nx.dtype) * gate_w[..., None], axis=-2)
            moe_out = jnp.zeros_like(nx)
            for e in range(N_EXPERTS):
                h = jax.nn.gelu(jnp.einsum('bsd,fd->bsf', nx, fc1_w[e]) + fc1_b[e], approximate=False)
                y = jnp.einsum('bsf,df->bsd', h, fc2_w[e]) + fc2_b[e]
                moe_out = moe_out + y * dense_gates[..., e:e + 1]
            return moe_out
        nx = _layernorm(x, ln1_w, ln1_b)
        attn_out = _causal_attention(nx, Wqkv, bqkv, Wo, bo)
        x = x + attn_out
        nx2 = _layernorm(x, ln2_w, ln2_b)
        moe_out = _moe_ffn(nx2, gate_W, fc1_w, fc1_b, fc2_w, fc2_b)
        return x + moe_out
    x = _layernorm(x + _L0_attn_ref(x, L0_attn_Wq, L0_attn_bq, L0_attn_Wk, L0_attn_bk, L0_attn_Wv, L0_attn_bv, L0_attn_Wg, L0_attn_bg, L0_attn_gamma, L0_attn_beta), axis=-1)
    x = _layernorm(x + _L0_xattn_ref(x, ctx_768, mask_BxS_bf1, mask_BxS2_bf1, L0_xattn_Wq, L0_xattn_Wk, L0_xattn_Wv, L0_xattn_W_film_in, L0_xattn_b_film_in, L0_xattn_W_film_out, L0_xattn_b_film_out, L0_xattn_g_norm_in, L0_xattn_b_norm_in, L0_xattn_g_norm_out, L0_xattn_b_norm_out, L0_xattn_g_ffn, L0_xattn_b_ffn, L0_xattn_W1, L0_xattn_b1, L0_xattn_W2, L0_xattn_b2, L0_xattn_log_dt, L0_xattn_A_re, L0_xattn_A_im, L0_xattn_C_re, L0_xattn_C_im, L0_xattn_D_skip, L0_xattn_mod_gate), axis=-1)
    x = _layernorm(x + _L0_ffn_ref(x, L0_ffn_w_red, L0_ffn_wg, L0_ffn_w1, L0_ffn_b1, L0_ffn_w2, L0_ffn_b2), axis=-1)
    x = _layernorm(x + _L1_attn_ref(x, L1_attn_time_decay, L1_attn_time_first, L1_attn_time_mix_k, L1_attn_time_mix_v, L1_attn_time_mix_r, L1_attn_Wk, L1_attn_Wv, L1_attn_Wr, L1_attn_Wo), axis=-1)
    x = _layernorm(x + _L1_xattn_ref(x, ctx_768, ctx_768, L1_xattn_Wq, L1_xattn_bq, L1_xattn_Wk, L1_xattn_bk, L1_xattn_Wv, L1_xattn_bv, L1_xattn_Wo, L1_xattn_bo, L1_xattn_ln_gamma, L1_xattn_ln_beta), axis=-1)
    x = _layernorm(x + _L1_ffn_ref(x, L1_ffn_Wr, L1_ffn_br, L1_ffn_ln_g, L1_ffn_ln_b, L1_ffn_W1, L1_ffn_b1, L1_ffn_W2, L1_ffn_b2), axis=-1)
    x = _layernorm(x + _L2_attn_ref(x, L2_attn_in_proj_weight, L2_attn_in_proj_bias, L2_attn_gamma, L2_attn_linear_alpha, L2_attn_linear_gamma, L2_attn_out_proj_weight, L2_attn_out_proj_bias), axis=-1)
    x = _layernorm(x + _L2_xattn_ref(x, ctx_768, L2_xattn_wq, L2_xattn_bq, L2_xattn_wk, L2_xattn_bk, L2_xattn_wv, L2_xattn_bv, L2_xattn_wo, L2_xattn_bo), axis=-1)
    x = _layernorm(x + _L2_ffn_ref(x, L2_ffn_norm_gamma, L2_ffn_slot_norm_gamma, L2_ffn_slot_embeds, L2_ffn_w1, L2_ffn_b1, L2_ffn_w2, L2_ffn_b2), axis=-1)
    x = _layernorm(x + _L3_attn_ref(x, L3_attn_Wq, L3_attn_bq, L3_attn_Wk, L3_attn_bk, L3_attn_Wv, L3_attn_bv, L3_attn_Wo, L3_attn_bo), axis=-1)
    x = _layernorm(x + _L3_xattn_ref(x, ctx_768, L3_xattn_Wq, L3_xattn_Wk, L3_xattn_Wv, L3_xattn_Wo, L3_xattn_bo), axis=-1)
    x = _layernorm(x + _L3_ffn_ref(x, L3_ffn_ln1_w, L3_ffn_ln1_b, L3_ffn_ln2_w, L3_ffn_ln2_b, L3_ffn_Wqkv, L3_ffn_bqkv, L3_ffn_Wo, L3_ffn_bo, L3_ffn_gate_W, L3_ffn_fc1_w, L3_ffn_fc1_b, L3_ffn_fc2_w, L3_ffn_fc2_b), axis=-1)
    return x

_drawn_inputs = setup_inputs


def setup_inputs(seed=0):
    import zlib

    import numpy as np

    out = dict(_drawn_inputs(seed))
    spreads = {'L0_attn_bq': (0.0, 0.375),
     'L0_attn_bk': (0.0, 0.315),
     'L0_attn_bv': (0.0, 0.1),
     'L0_attn_bg': (0.0, 0.465),
     'L0_attn_gamma': (1.0, 0.2),
     'L0_attn_beta': (0.0, 0.1),
     'L0_xattn_b_film_in': (0.0, 0.1),
     'L0_xattn_b_film_out': (0.0, 0.1),
     'L0_xattn_g_norm_in': (1.0, 0.2),
     'L0_xattn_b_norm_in': (0.0, 0.1),
     'L0_xattn_g_norm_out': (1.0, 0.2),
     'L0_xattn_b_norm_out': (0.0, 0.1),
     'L0_xattn_g_ffn': (1.0, 0.6),
     'L0_xattn_b_ffn': (0.0, 0.525),
     'L0_xattn_b1': (0.0, 0.286),
     'L0_xattn_b2': (0.0, 0.1),
     'L0_xattn_A_re': (-0.5, 0.549),
     'L1_xattn_bq': (0.0, 0.1),
     'L1_xattn_bk': (0.0, 2.0),
     'L1_xattn_bv': (0.0, 0.1),
     'L1_xattn_bo': (0.0, 0.1),
     'L1_xattn_ln_gamma': (1.0, 0.2),
     'L1_xattn_ln_beta': (0.0, 0.1),
     'L1_ffn_br': (0.0, 0.305),
     'L1_ffn_ln_g': (1.0, 0.6),
     'L1_ffn_ln_b': (0.0, 0.8),
     'L1_ffn_b1': (0.0, 0.358),
     'L1_ffn_b2': (0.0, 0.267),
     'L2_xattn_bq': (0.0, 0.1),
     'L2_xattn_bk': (0.0, 2.0),
     'L2_xattn_bv': (0.0, 0.1),
     'L2_xattn_bo': (0.0, 0.1),
     'L2_ffn_norm_gamma': (1.0, 0.2),
     'L2_ffn_slot_norm_gamma': (1.0, 0.2),
     'L2_ffn_b1': (0.0, 0.1),
     'L2_ffn_b2': (0.0, 0.1),
     'L3_xattn_bo': (0.0, 0.1),
     'L3_ffn_ln1_w': (1.0, 0.2),
     'L3_ffn_ln1_b': (0.0, 0.297),
     'L3_ffn_ln2_w': (1.0, 0.2),
     'L3_ffn_ln2_b': (0.0, 0.1),
     'L3_ffn_bqkv': (0.0, 0.1),
     'L3_ffn_bo': (0.0, 0.1),
     'L3_ffn_fc1_b': (0.0, 0.344),
     'L3_ffn_fc2_b': (0.0, 0.1)}
    factors = {'L0_xattn_Wq': 5.465,
     'L0_xattn_Wk': 4.956,
     'L0_xattn_W_film_out': 2.696,
     'L0_ffn_w_red': 3.805,
     'L0_ffn_wg': 3.098,
     'L0_ffn_w1': 3.188,
     'L0_ffn_b1': 8.0,
     'L0_ffn_w2': 3.57,
     'L0_ffn_b2': 4.681,
     'L1_xattn_Wk': 200.0,
     'L1_ffn_W1': 2.759,
     'L2_attn_gamma': 4.706,
     'L2_attn_linear_alpha': 4.55,
     'L2_attn_linear_gamma': 2.722,
     'L3_attn_bq': 4.711,
     'L3_attn_bk': 3.641,
     'L3_attn_bo': 200.0}
    for name, (base, spread) in spreads.items():
        noise = np.random.default_rng([zlib.crc32(name.encode()), seed]).standard_normal(out[name].shape)
        drawn = base * np.exp(spread * noise) if base else spread * noise
        out[name] = jnp.asarray(drawn.astype(out[name].dtype))
    for name, factor in factors.items():
        out[name] = (out[name] * factor).astype(out[name].dtype)
    return out
```

```python
from contextlib import ExitStack

import numpy as np
import concourse.bass as bass
from concourse import mybir

F32 = mybir.dt.float32
BF16 = mybir.dt.bfloat16
U32 = mybir.dt.uint32
U8 = mybir.dt.uint8
ALU = mybir.AluOpType
ACT = mybir.ActivationFunctionType
AX = mybir.AxisListType.X

B, T, D = 32, 128, 128
TC, DC = 120, 96
LANES = 2
STEPS = B // LANES
E, F = 8, 512
FC = F // 128
LN_EPS = 1e-5
NEG = -1e30


def at(eng, sem, n, each=1):
    eng.wait_ge(sem, (n + 1) * each)


def at_alone(eng, sem, n, passed):
    at(eng, sem, n)
    eng.sem_inc(passed, 1)


class Scope:

    def __init__(self, nc, name):
        self.nc, self.name, self.stack, self.sems = nc, name, ExitStack(), []
        self.passed = self.sem("passed")

    def sb(self, name, shape, dtype=F32):
        return self.stack.enter_context(self.nc.sbuf_tensor(f"{self.name}_{name}", shape, dtype))

    def lanes(self, name, shape, dtype=F32):
        return [self.sb(f"{name}{lane}", shape, dtype) for lane in range(LANES)]

    def psum(self, name, shape, dtype=F32):
        return self.stack.enter_context(self.nc.psum_tensor(f"{self.name}_{name}", shape, dtype))

    def sem(self, name):
        s = self.nc.alloc_semaphore(f"{self.name}_{name}")
        self.sems.append(s)
        return s

    def close(self):
        self.stack.close()
        self.nc.clear_and_free_semaphores(self.sems)
        self.nc.all_engine_barrier()


def row_bc(vec, n=128):
    return vec.rearrange("(a d) -> a d", a=1).to_broadcast([n, vec.shape[0]])


def col(vec):
    return vec.rearrange("(d a) -> d a", a=1)


class Core:

    def __init__(self, nc, stack, I):
        self.nc, self.I = nc, I

        def sb(name, shape, dtype=F32):
            return stack.enter_context(nc.sbuf_tensor(name, shape, dtype))

        self.X = sb("X", [T, B, D])
        self.ident = sb("ident", [128, 128])
        self.anti = sb("anti", [128, 128])
        self.identb = sb("identb", [128, 128], BF16)
        self.ones = sb("ones", [128, 128])
        self.neghalf = sb("neghalf", [128, 128])


def load_block(core):
    nc, I = core.nc, core.I
    s = Scope(nc, "load")
    x_in, zeroed, made = s.sem("x_in"), s.sem("zeroed"), s.sem("made")
    with nc.Block() as block:
        @block.sync
        def _(sp):
            sp.dma_start(core.X[:], I["x"].rearrange("b t d -> t b d")).then_inc(x_in, 16)
            sp.wait_ge(x_in, 16)

        @block.gpsimd
        def _(pool):
            pool.memset(core.ident[:], 0.0).then_inc(zeroed, 1)
            pool.memset(core.ones[:], 1.0).then_inc(made, 1)
            pool.memset(core.neghalf[:], -0.5).then_inc(made, 1)
            pool.memset(core.anti[:], 0.0).then_inc(zeroed, 1)
            pool.wait_ge(zeroed, 2)
            pool.affine_select(out=core.anti[:], in_=core.anti[:], compare_op=ALU.not_equal, fill=1.0,
                               base=-127, pattern=[[1, 128]], channel_multiplier=1).then_inc(made, 1)
            pool.affine_select(out=core.ident[:], in_=core.ident[:], compare_op=ALU.not_equal, fill=1.0,
                               base=0, pattern=[[-1, 128]], channel_multiplier=1).then_inc(made, 1)
            pool.wait_ge(made, 4)
            pool.tensor_copy(core.identb[:], core.ident[:]).then_inc(made, 1)
            pool.wait_ge(made, 5)
    s.close()


def store_block(core, out):
    nc = core.nc
    s = Scope(nc, "store")
    x_out = s.sem("x_out")
    with nc.Block() as block:
        @block.sync
        def _(sp):
            sp.dma_start(out.rearrange("b t d -> t b d"), core.X[:]).then_inc(x_out, 16)
            sp.wait_ge(x_out, 16)
    s.close()


def attention(core, name, *, H, Dh, Wq, Wk, Wv, Wo, bq=None, bk=None, bv=None, bo=None,
              context=False, flow=False, mask=None, form="softmax", post="plain", extra=None):
    nc, I, X = core.nc, core.I, core.X
    extra = extra or {}
    s = Scope(nc, name)
    K = TC if context else T
    KD = DC if context else D
    J = 4 if Dh == 8 else 2
    R = 128 // J
    C = H // J
    HD = H * Dh
    NB = HD // 128
    G = min(H, 512 // (Dh + 1)) if Dh == 8 else 4
    scale = float(Dh) ** -0.5
    shifted = form == "softmax"
    strided = post == "l2self"

    pads = []
    wq = s.sb("wq", [D, C, J, R])
    wk = s.sb("wk", [KD, C, J, R])
    pads += [wq, wk]
    wv = s.sb("wv", [KD, HD])
    wo = s.sb("wo", [128, NB, D])
    loads = [(wq[:, :, :, 0:Dh], I[Wq].rearrange("e (c j d) -> e c j d", c=C, j=J)),
             (wk[:, :, :, 0:Dh], I[Wk].rearrange("e (c j d) -> e c j d", c=C, j=J)),
             (wv[:], I[Wv]), (wo[:], I[Wo].rearrange("(n p) d -> p n d", p=128))]

    def padded_column(key, tag):
        t = s.sb(tag, [128, C])
        pads.append(t)
        for j in range(J):
            loads.append((t[j * R:j * R + Dh, :], I[key].rearrange("(c j d) -> d c j", c=C, j=J)[:, :, j]))
        return t

    def row(key, tag, n=128):
        t = s.sb(tag, [n, I[key].shape[0]])
        loads.append((t[:], row_bc(I[key], n)))
        return t

    bqp = padded_column(bq, "bq") if bq else None
    bkp = padded_column(bk, "bk") if bk else None
    bvr = row(bv, "bv", K) if bv else None
    bor = row(bo, "bo") if bo else None
    if post == "gate":
        wg = s.sb("wg", [128, 2, D])
        loads.append((wg[:], I["L0_attn_Wg"].rearrange("(n p) d -> p n d", p=128)))
        bgr, gam, bet = row("L0_attn_bg", "bg"), row("L0_attn_gamma", "gam"), row("L0_attn_beta", "bet")
    if post == "l1x":
        wqf = s.sb("wqf", [D, HD])
        loads.append((wqf[:], I[Wq]))
        bqr, gam, bet = row(bq, "bqr"), row("L1_xattn_ln_gamma", "gam"), row("L1_xattn_ln_beta", "bet")
    if post == "l2self":
        gq, gk = padded_column("L2_attn_gamma_q", "gq"), padded_column("L2_attn_gamma_k", "gk")
        gv, alpha, lgam = row("L2_attn_gamma_v", "gv"), row("L2_attn_alpha", "alpha"), row("L2_attn_lgamma", "lgam")
    if post == "l3ffn":
        l1w, l1b = row("L3_ffn_ln1_w", "l1w"), row("L3_ffn_ln1_b", "l1b")
    if mask:
        mask_in = s.sb("mask_in", [T, T])
        loads.append((mask_in[:], I[mask]))
        mask_ready = s.sem("mask_ready")
        msk = s.sb("msk", [T, C, T], BF16) if shifted else mask_in

    xs = s.lanes("xs", [T, D])
    xT = s.lanes("xT", [D, T])
    cs = s.lanes("cs", [KD, K]) if context else None
    q4 = s.lanes("q4", [128, C, T])
    k4 = s.lanes("k4", [128, C, K])
    nk4 = s.lanes("nk4", [128, C, K]) if flow else None
    V = s.lanes("V", [K, H, Dh + 1])
    S = s.lanes("S", [T, J, C, K]) if shifted else None
    PT = s.lanes("PT", [K, J * C, T])
    mx = s.lanes("mx", [T, J, C])
    rz = s.lanes("rz", [T, H])
    oS = s.lanes("oS", [T, H, Dh])
    oT = s.lanes("oT", [128, NB, T])
    r = s.lanes("r", [T, D])
    r2 = s.lanes("r2", [T, D])
    st = s.lanes("st", [T, 6])
    mv = s.lanes("mv", [T, 2])
    ve = s.lanes("ve", [T, 1])
    rs = s.lanes("rs", [T, 1])
    sq4 = s.lanes("sq4", [128, C, T]) if form in ("bounded", "linear") else None
    nrm = s.lanes("nrm", [128, 2, T]) if form == "bounded" else None
    k4sq = s.lanes("k4sq", [128, C, K]) if form == "bounded" else None
    y_bias_added = s.sem("y_bias_added")
    ps = [s.psum(f"ps{lane}", [128, 4, 512]) for lane in range(LANES)]

    names = ("pads_zeroed weights_in ones_set slot_free x_copied xT_psum xT_ready qkv_psum q_ready k_ready "
             "v_ready scores_psum max_ready shifted_ready p_ready pT_psum pT_low pT_high o_psum z_ready o_ready "
             "oT_psum oT_ready y_psum r_ready stats mean_var var_eps rstd_ready")
    sem = {n: s.sem(n) for n in names.split()}
    S_ = type("Ready", (), sem)
    post_sems = {}

    def extra_sem(n):
        post_sems[n] = s.sem(n)
        return post_sems[n]

    two_norms = post in ("gate", "l1x")
    ctx_in = [s.sem(f"ctx_in{lane}") for lane in range(LANES)] if context else None
    if two_norms:
        r1_ready, stats1, mv1, ve1, rstd1, n1_ready, g1_ready, b1_ready = [
            extra_sem(n) for n in ("r1_ready", "stats1", "mean_var1", "var_eps1", "rstd1_ready",
                                   "normed1", "scaled1", "offset1")]
    if post == "gate":
        gate_psum, gate_in, gate_exp, gate_1p, gate_ready, gated = [
            extra_sem(n) for n in ("gate_psum", "gate_in", "gate_exp", "gate_plus1", "gate_ready", "gated")]
    if post == "l1x":
        qf_psum, qf_ready = extra_sem("qf_psum"), extra_sem("qf_ready")
        out_biased = extra_sem("out_biased")
        qf = s.lanes("qf", [T, D])
    if form == "bounded":
        sq_ready, norm_psum, norm_safe, norm_ready = [extra_sem(n) for n in
                                                      ("squares", "norm_psum", "norm_safe", "norm_ready")]
        q_raw, k_raw = extra_sem("q_raw"), extra_sem("k_raw")
    if form == "linear":
        q_raw, q_low, q_exp, k_raw, k_low, k_exp = [extra_sem(n) for n in
                                                    ("q_raw", "q_low", "q_exp", "k_raw", "k_low", "k_exp")]
    if post == "l2self":
        q_raw, k_raw, v_raw, o_norm = [extra_sem(n) for n in ("q_raw", "k_raw", "v_raw", "o_normed")]
        y_scaled = extra_sem("y_scaled")
        x_in, x_stored = ([s.sem(f"{n}{lane}") for lane in range(LANES)] for n in ("x_in", "x_stored"))
    if flow:
        nk_ready = extra_sem("nk_ready")
    if post == "l3ffn":
        i_stats, i_mv, i_ve, i_rstd, i_n, i_g, x_loaded = [extra_sem(n) for n in
            ("in_stats", "in_mean_var", "in_var_eps", "in_rstd", "in_normed", "in_scaled", "in_loaded")]
        xn = s.lanes("xn", [T, D])
    def xpart(lane):
        return xn[lane] if post == "l3ffn" else xs[lane]

    with nc.Block() as block:
        @block.sync
        def _(sp):
            sp.wait_ge(S_.pads_zeroed, len(pads))
            with nc.allow_non_contiguous_dma(reason="weights are rearranged once"):
                for dst, src in loads:
                    sp.dma_start(dst, src).then_inc(S_.weights_in, 16)
            if context:
                with sp.Fori(0, STEPS) as i:
                    for lane in range(LANES):
                        n = i * LANES + lane
                        at(sp, S_.slot_free, n)
                        sp.dma_start(cs[lane][:], I["ctxT"][:, bass.ds(n * K, K)]).then_inc(ctx_in[lane], 16)
            if strided:
                for lane in range(LANES):
                    sp.sem_inc(x_stored[lane], 16)
                xd, od = I["x_mid"], I["x_mid_out"]
                with sp.Fori(0, STEPS) as i:
                    for lane in range(LANES):
                        n = i * LANES + lane
                        at(sp, x_stored[lane], i, 16)
                        sp.dma_start(xs[lane][:], xd[bass.ds(n * 4, 4), :, :].rearrange("p s d -> (p s) d")).then_inc(x_in[lane], 16)
                    for lane in range(LANES):
                        n = i * LANES + lane
                        at(sp, S_.slot_free, n + LANES)
                        sp.dma_start(od[bass.ds(n * 4, 4), :, :].rearrange("p s d -> (p s) d"), r2[lane][:]).then_inc(x_stored[lane], 16)
                for lane in range(LANES):
                    sp.wait_ge(x_stored[lane], (STEPS + 1) * 16)

        @block.gpsimd
        def _(pool):
            for t in pads:
                pool.memset(t[:], 0.0).then_inc(S_.pads_zeroed, 1)
            for lane in range(LANES):
                pool.memset(V[lane][:], 1.0).then_inc(S_.ones_set, 1)
            pool.sem_inc(S_.slot_free, LANES)
            with pool.Fori(0, STEPS) as i:
                for lane in range(LANES):
                    n = i * LANES + lane
                    at(pool, S_.slot_free, n)
                    if not strided:
                        pool.tensor_copy(xs[lane][:], X[:, bass.ds(n, 1), :].rearrange("t a d -> t (a d)")).then_inc(S_.x_copied, 1)
                if post == "l3ffn":
                    for lane in range(LANES):
                        at(pool, i_ve, i * LANES + lane)
                        pool.tensor_tensor(rs[lane][:], ve[lane][:], core.neghalf[:, 0:1], ALU.pow).then_inc(i_rstd, 1)
                if form == "bounded":
                    for lane in range(LANES):
                        at(pool, norm_safe, i * LANES + lane)
                        pool.tensor_tensor(nrm[lane][:, 0, :], nrm[lane][:, 0, :], core.neghalf[:, 0:T], ALU.pow).then_inc(norm_ready, 1)
                        pool.tensor_tensor(nrm[lane][:, 1, 0:K], nrm[lane][:, 1, 0:K], core.neghalf[:, 0:K], ALU.pow).then_inc(norm_ready, 1)
                if two_norms:
                    for lane in range(LANES):
                        at(pool, ve1, i * LANES + lane)
                        pool.tensor_tensor(rs[lane][:], ve[lane][:], core.neghalf[:, 0:1], ALU.pow).then_inc(rstd1, 1)
                for lane in range(LANES if post != "l3ffn" else 0):
                    at(pool, S_.var_eps, i * LANES + lane)
                    pool.tensor_tensor(rs[lane][:], ve[lane][:], core.neghalf[:, 0:1], ALU.pow).then_inc(S_.rstd_ready, 1)

        @block.tensor
        def _(pe):
            pe.wait_ge(S_.weights_in, 16 * len(loads))
            if mask and shifted:
                pe.wait_ge(mask_ready, 1)
            with pe.Fori(0, STEPS) as i:
                for lane in range(LANES):
                    n = i * LANES + lane
                    if post == "l3ffn":
                        at(pe, i_g, n)
                    elif strided:
                        at(pe, x_in[lane], i, 16)
                    else:
                        at(pe, S_.x_copied, n)
                    pe.transpose(ps[lane][:, 0, 0:T], xpart(lane)[:], core.ident[:]).then_inc(S_.xT_psum, 1)
                for lane in range(LANES):
                    n = i * LANES + lane
                    src = cs[lane] if context else xT[lane]
                    if context:
                        at(pe, ctx_in[lane], i, 16)
                    at(pe, S_.xT_ready, n)
                    if post == "l1x":
                        pe.matmul(ps[lane][:, 0, 0:D], xT[lane][:], wqf[:], start=True, stop=True).then_inc(qf_psum, 1)
                    pe.matmul(ps[lane][0:K, 3, 0:HD], src[:], wv[:], start=True, stop=True)
                    for c in range(C):
                        pe.matmul(ps[lane][:, 1, c * T:(c + 1) * T], wq[:, c].rearrange("e j r -> e (j r)"),
                                  xT[lane][:], start=True, stop=True)
                    for c in range(C):
                        last = pe.matmul(ps[lane][:, 2, c * K:(c + 1) * K], wk[:, c].rearrange("e j r -> e (j r)"),
                                         src[:], start=True, stop=True)
                    last.then_inc(S_.qkv_psum, 1)
                if form == "bounded":
                    for lane in range(LANES):
                        n = i * LANES + lane
                        at(pe, sq_ready, n, 2)
                        at(pe, qf_ready, n)
                        for c in range(C):
                            pe.matmul(ps[lane][:, 0, 0:T], core.ones[:], sq4[lane][:, c, :], start=c == 0, stop=c == C - 1)
                        for c in range(C):
                            last = pe.matmul(ps[lane][:, 0, T:T + K], core.ones[:], k4sq[lane][:, c, :], start=c == 0, stop=c == C - 1)
                        last.then_inc(norm_psum, 1)
                for lane in range(LANES):
                    n = i * LANES + lane
                    at(pe, S_.q_ready, n)
                    at(pe, S_.k_ready, n)
                    at(pe, S_.v_ready, n)
                    if flow:
                        at(pe, nk_ready, n)
                    if shifted:
                        if mask:
                            for j in range(J):
                                pe.matmul(ps[lane][:, j, 0:C * K], core.identb[:], msk[:].rearrange("t c k -> t (c k)"), start=True, stop=False, skip_group_check=True)
                        for c in range(C):
                            for j in range(J):
                                rows = slice(j * R, j * R + Dh)
                                o = ps[lane][:, j, c * K:(c + 1) * K]
                                last = pe.matmul(o, q4[lane][rows, c, :], k4[lane][rows, c, :], start=not mask,
                                                 stop=not flow, skip_group_check=True)
                                if flow:
                                    last = pe.matmul(o, nk4[lane][rows, c, :], q4[lane][rows, c, :], start=False, stop=True,
                                                     skip_group_check=True)
                    else:
                        for c in range(C):
                            for j in range(J):
                                rows = slice(j * R, j * R + Dh)
                                last = pe.matmul(ps[lane][0:K, j, c * T:(c + 1) * T], k4[lane][rows, c, :], q4[lane][rows, c, :],
                                                 start=True, stop=True)
                    last.then_inc(S_.scores_psum, 1)
                if shifted:
                    for lane in range(LANES):
                        n = i * LANES + lane
                        at(pe, S_.p_ready, n)
                        for j in range(J):
                            for c in range(C):
                                last = pe.transpose(ps[lane][0:K, j, c * T:(c + 1) * T], S[lane][:, j, c, :], core.ident[:])
                        last.then_inc(S_.pT_psum, 1)
                for lane in range(LANES):
                    n = i * LANES + lane
                    at(pe, S_.pT_low, n)
                    if form != "bounded":
                        at(pe, S_.pT_high, n)
                    for h in range(H):
                        o = ps[lane][:, h // G, (h % G) * (Dh + 1):(h % G + 1) * (Dh + 1)]
                        last = pe.matmul(o, PT[lane][:, (h % J) * C + h // J, :], V[lane][:, h, :], start=True, stop=True)
                    last.then_inc(S_.o_psum, 1)
                for lane in range(LANES):
                    n = i * LANES + lane
                    at(pe, S_.o_ready, n)
                    ov = oS[lane][:].rearrange("t h d -> t (h d)")
                    for b in range(NB):
                        last = pe.transpose(ps[lane][:, 2, b * T:(b + 1) * T], ov[:, b * 128:(b + 1) * 128], core.ident[:])
                    last.then_inc(S_.oT_psum, 1)
                for lane in range(LANES):
                    n = i * LANES + lane
                    at(pe, S_.oT_ready, n)
                    if post == "gate":
                        pe.matmul(ps[lane][:, 3, 0:D], xT[lane][:], wg[:, 0, :], start=True, stop=False)
                        pe.matmul(ps[lane][:, 3, 0:D], oT[lane][:, 0, :], wg[:, 1, :], start=False, stop=True).then_inc(gate_psum, 1)
                    else:
                        for b in range(NB):
                            last = pe.matmul(ps[lane][:, 3, 0:D], oT[lane][:, b, :], wo[:, b, :], start=b == 0, stop=b == NB - 1)
                        last.then_inc(S_.y_psum, 1)

        @block.scalar
        def _(act):
            act.wait_ge(S_.ones_set, LANES)
            with act.Fori(0, STEPS) as i:
                for lane in range(LANES):
                    at(act, S_.xT_psum, i * LANES + lane)
                    act.activation(xT[lane][:], ps[lane][:, 0, 0:T], ACT.Copy).then_inc(S_.xT_ready, 1)
                if form == "linear":
                    for lane in range(LANES):
                        n = i * LANES + lane
                        at(act, q_low, n)
                        act.activation(sq4[lane][:], sq4[lane][:], ACT.Exp).then_inc(q_exp, 1)
                    for lane in range(LANES):
                        n = i * LANES + lane
                        at(act, k_low, n)
                        act.activation(sq4[lane][:], sq4[lane][:], ACT.Exp).then_inc(k_exp, 1)
                if not bv:
                    for lane in range(LANES):
                        at(act, S_.qkv_psum, i * LANES + lane)
                        act.activation(V[lane][:, :, 0:Dh], ps[lane][0:K, 3, 0:HD].rearrange("k (h d) -> k h d", h=H),
                                       ACT.Copy).then_inc(S_.v_ready, 1)
                if shifted:
                    for lane in range(LANES):
                        at(act, S_.shifted_ready, i * LANES + lane)
                        act.activation(S[lane][:], S[lane][:], ACT.Exp, scale=scale).then_inc(S_.p_ready, 1)
                    for lane in range(LANES):
                        at(act, S_.pT_psum, i * LANES + lane)
                        half = J // 2
                        act.activation(PT[lane][:, 0:half * C, :], ps[lane][0:K, 0:half, :].rearrange("k j (c t) -> k (j c) t", t=T)[:, 0:half * C, :],
                                       ACT.Copy).then_inc(S_.pT_low, 1)
                if form == "bounded":
                    for lane in range(LANES):
                        at(act, S_.scores_psum, i * LANES + lane)
                        act.activation(PT[lane][:], ps[lane][0:K, 0:J, :].rearrange("k j (c t) -> k (j c) t", t=T),
                                       ACT.Exp, scale=scale).then_inc(S_.pT_low, 1)
                for lane in range(LANES):
                    at(act, S_.oT_psum, i * LANES + lane)
                    act.activation(oT[lane][:], ps[lane][:, 2, 0:NB * T].rearrange("p (b t) -> p b t", b=NB), ACT.Copy).then_inc(S_.oT_ready, 1)
                if post == "gate":
                    for lane in range(LANES):
                        at(act, gate_in, i * LANES + lane)
                        act.activation(r2[lane][:], r2[lane][:], ACT.Exp, scale=-1.0).then_inc(gate_exp, 1)

        @block.vector
        def _(dve):
            dve.wait_ge(S_.ones_set, LANES)
            dve.wait_ge(S_.weights_in, 16 * len(loads))
            if mask and shifted:
                dve.tensor_copy(msk[:], mask_in[:].unsqueeze(1).to_broadcast([T, C, T])).then_inc(mask_ready, 1)

            def norm(src, n, lane, sems):
                dve.bn_stats(st[lane][:], src).then_inc(sems[0], 1)
                at_alone(dve, sems[0], n, s.passed)
                dve.bn_aggr(mv[lane][:], st[lane][:]).then_inc(sems[1], 1)
                at(dve, sems[1], n)
                dve.tensor_scalar(ve[lane][:], mv[lane][:, 1:2], LN_EPS, None, ALU.add).then_inc(sems[2], 1)

            def normed(src, n, lane, rstd, dst, done):
                at(dve, rstd, n)
                dve.tensor_scalar(dst, src, mv[lane][:, 0:1], rs[lane][:, 0:1], ALU.subtract, ALU.mult).then_inc(done, 1)

            with dve.Fori(0, STEPS) as i:
                if post == "l3ffn":
                    for lane in range(LANES):
                        n = i * LANES + lane
                        at(dve, S_.x_copied, n)
                        norm(xs[lane][:], n, lane, (i_stats, i_mv, i_ve))
                    for lane in range(LANES):
                        n = i * LANES + lane
                        normed(xs[lane][:], n, lane, i_rstd, xn[lane][:], i_n)
                        at(dve, i_n, n)
                        dve.tensor_tensor(xn[lane][:], xn[lane][:], l1w[:], ALU.mult).then_inc(x_loaded, 1)
                        at(dve, x_loaded, n)
                        dve.tensor_tensor(xn[lane][:], xn[lane][:], l1b[:], ALU.add).then_inc(i_g, 1)
                for lane in range(LANES):
                    n = i * LANES + lane
                    at(dve, S_.qkv_psum, n)
                    pq = ps[lane][:, 1, 0:C * T].rearrange("p (c t) -> p c t", c=C)
                    pk = ps[lane][:, 2, 0:C * K].rearrange("p (c t) -> p c t", c=C)
                    for which, dst, src, b, W in (("q", q4[lane], pq, bqp, T), ("k", k4[lane], pk, bkp, K)):
                        raw = form in ("bounded", "linear") or post == "l2self"
                        done = {"q": q_raw, "k": k_raw}[which] if raw else {"q": S_.q_ready, "k": S_.k_ready}[which]
                        if b is None:
                            dve.tensor_copy(dst[:], src).then_inc(done, 1)
                        else:
                            dve.tensor_tensor(dst[:], src, b[:].unsqueeze(2).to_broadcast([128, C, W]), ALU.add).then_inc(done, 1)
                    if flow:
                        at(dve, S_.k_ready, n)
                        dve.tensor_scalar(nk4[lane][:], k4[lane][:], -1.0, None, ALU.mult).then_inc(nk_ready, 1)
                    if post == "l2self":
                        at(dve, q_raw, n)
                        dve.tensor_tensor(q4[lane][:], q4[lane][:], gq[:].unsqueeze(2).to_broadcast([128, C, T]), ALU.mult).then_inc(S_.q_ready, 1)
                        at(dve, k_raw, n)
                        dve.tensor_tensor(k4[lane][:], k4[lane][:], gk[:].unsqueeze(2).to_broadcast([128, C, K]), ALU.mult).then_inc(S_.k_ready, 1)
                    if bv:
                        vv = V[lane][:, :, 0:Dh]
                        dve.tensor_tensor(vv, ps[lane][0:K, 3, 0:HD].rearrange("k (h d) -> k h d", h=H),
                                          bvr[:].rearrange("k (h d) -> k h d", h=H), ALU.add).then_inc(v_raw if post == "l2self" else S_.v_ready, 1)
                        if post == "l2self":
                            at(dve, v_raw, n)
                            dve.tensor_tensor(vv, vv, gv[:].rearrange("k (h d) -> k h d", h=H), ALU.mult).then_inc(S_.v_ready, 1)
                    if post == "l1x":
                        at(dve, qf_psum, n)
                        dve.tensor_tensor(qf[lane][:], ps[lane][:, 0, 0:D], bqr[:], ALU.add).then_inc(qf_ready, 1)
                if form == "linear":
                    for t4, raw, low, ex, ready, W in ((q4, q_raw, q_low, q_exp, S_.q_ready, T), (k4, k_raw, k_low, k_exp, S_.k_ready, K)):
                        for lane in range(LANES):
                            n = i * LANES + lane
                            at(dve, raw, n)
                            if ready is S_.k_ready:
                                at(dve, S_.q_ready, n)
                            dve.tensor_scalar(sq4[lane][:], t4[lane][:], 0.0, None, ALU.min).then_inc(low, 1)
                        for lane in range(LANES):
                            n = i * LANES + lane
                            at(dve, ex, n)
                            dve.scalar_tensor_tensor(out=t4[lane][:], in0=t4[lane][:], scalar=0.0, in1=sq4[lane][:],
                                                     op0=ALU.max, op1=ALU.add).then_inc(ready, 1)
                if form == "bounded":
                    for lane in range(LANES):
                        n = i * LANES + lane
                        at(dve, q_raw, n)
                        at(dve, k_raw, n)
                        dve.tensor_tensor(sq4[lane][:], q4[lane][:], q4[lane][:], ALU.mult).then_inc(sq_ready, 1)
                        dve.tensor_tensor(k4sq[lane][:], k4[lane][:], k4[lane][:], ALU.mult).then_inc(sq_ready, 1)
                    for lane in range(LANES):
                        n = i * LANES + lane
                        at(dve, norm_psum, n)
                        dve.tensor_scalar(nrm[lane][:, :, :].rearrange("p a t -> p (a t)")[:, 0:T + K], ps[lane][:, 0, 0:T + K],
                                          1e-24, None, ALU.max).then_inc(norm_safe, 1)
                    for lane in range(LANES):
                        n = i * LANES + lane
                        at(dve, norm_ready, n, 2)
                        dve.tensor_tensor(q4[lane][:], q4[lane][:], nrm[lane][:, 0:1, :].to_broadcast([128, C, T]), ALU.mult).then_inc(S_.q_ready, 1)
                        dve.tensor_tensor(k4[lane][:], k4[lane][:], nrm[lane][:, 1:2, 0:K].to_broadcast([128, C, K]), ALU.mult).then_inc(S_.k_ready, 1)
                if shifted:
                    for lane in range(LANES):
                        n = i * LANES + lane
                        at(dve, S_.scores_psum, n)
                        sc = ps[lane][:, 0:J, 0:C * K].rearrange("t j (c k) -> t j c k", c=C)
                        dve.tensor_reduce(mx[lane][:], sc, AX.X, ALU.max).then_inc(S_.max_ready, 1)
                        at(dve, S_.max_ready, n)
                        dve.tensor_tensor(S[lane][:], sc, mx[lane][:].unsqueeze(3).to_broadcast([T, J, C, K]),
                                          ALU.subtract).then_inc(S_.shifted_ready, 1)
                    for lane in range(LANES):
                        at(dve, S_.pT_psum, i * LANES + lane)
                        half = J // 2
                        dve.tensor_copy(PT[lane][:, half * C:, :], ps[lane][0:K, half:J, :].rearrange("k j (c t) -> k (j c) t", t=T)).then_inc(S_.pT_high, 1)
                elif form == "linear":
                    for lane in range(LANES):
                        at(dve, S_.scores_psum, i * LANES + lane)
                        for half, done in ((0, S_.pT_low), (1, S_.pT_high)):
                            a, b = half * J // 2, (half + 1) * J // 2
                            dve.tensor_tensor(PT[lane][:, a * C:b * C, :], ps[lane][0:K, a:b, :].rearrange("k j (c t) -> k (j c) t", t=T),
                                              msk[:].unsqueeze(1).to_broadcast([K, (b - a) * C, T]), ALU.mult).then_inc(done, 1)
                for lane in range(LANES):
                    n = i * LANES + lane
                    at(dve, S_.o_psum, n)
                    NG = H // G
                    po = ps[lane][:, 0:NG, 0:G * (Dh + 1)].rearrange("t n (g d) -> t n g d", g=G)
                    ov = oS[lane][:].rearrange("t (n g) d -> t n g d", n=NG)
                    if form == "linear":
                        dve.tensor_copy(ov, po[:, :, :, 0:Dh]).then_inc(S_.o_ready, 1)
                        continue
                    rv = rz[lane][:].rearrange("t (n g) -> t n g", n=NG)
                    dve.reciprocal(rv.unsqueeze(3), po[:, :, :, Dh:Dh + 1]).then_inc(S_.z_ready, 1)
                    at(dve, S_.z_ready, n)
                    dve.tensor_tensor(ov, po[:, :, :, 0:Dh], rv.unsqueeze(3).to_broadcast([T, NG, G, Dh]),
                                      ALU.mult).then_inc(o_norm if post == "l2self" else S_.o_ready, 1)
                    if post == "l2self":
                        at(dve, o_norm, n)
                        of = oS[lane][:].rearrange("t h d -> t (h d)")
                        dve.tensor_tensor(of, of, alpha[:], ALU.mult).then_inc(S_.o_ready, 1)
                if post == "gate":
                    for lane in range(LANES):
                        n = i * LANES + lane
                        at(dve, gate_psum, n)
                        dve.tensor_tensor(r2[lane][:], ps[lane][:, 3, 0:D], bgr[:], ALU.add).then_inc(gate_in, 1)
                    for lane in range(LANES):
                        n = i * LANES + lane
                        at(dve, gate_exp, n)
                        dve.tensor_scalar(r2[lane][:], r2[lane][:], 1.0, None, ALU.add).then_inc(gate_1p, 1)
                        at(dve, gate_1p, n)
                        dve.reciprocal(r2[lane][:], r2[lane][:]).then_inc(gate_ready, 1)
                        at(dve, gate_ready, n)
                        dve.tensor_tensor(r[lane][:], r2[lane][:], oS[lane][:].rearrange("t h d -> t (h d)"), ALU.mult).then_inc(gated, 1)
                        at(dve, gated, n)
                        dve.tensor_tensor(r[lane][:], r[lane][:], xs[lane][:], ALU.add).then_inc(r1_ready, 1)
                elif post == "l1x":
                    for lane in range(LANES):
                        n = i * LANES + lane
                        at(dve, S_.y_psum, n)
                        dve.tensor_tensor(r[lane][:], ps[lane][:, 3, 0:D], bor[:], ALU.add).then_inc(out_biased, 1)
                        at(dve, out_biased, n)
                        dve.tensor_tensor(r[lane][:], r[lane][:], qf[lane][:], ALU.add).then_inc(r1_ready, 1)
                if two_norms:
                    for lane in range(LANES):
                        n = i * LANES + lane
                        at(dve, r1_ready, n)
                        norm(r[lane][:], n, lane, (stats1, mv1, ve1))
                    for lane in range(LANES):
                        n = i * LANES + lane
                        normed(r[lane][:], n, lane, rstd1, r2[lane][:], n1_ready)
                        at(dve, n1_ready, n)
                        dve.tensor_tensor(r2[lane][:], r2[lane][:], gam[:], ALU.mult).then_inc(g1_ready, 1)
                        at(dve, g1_ready, n)
                        dve.tensor_tensor(r2[lane][:], r2[lane][:], bet[:], ALU.add).then_inc(b1_ready, 1)
                        at(dve, b1_ready, n)
                        dve.tensor_tensor(r[lane][:], r2[lane][:], xs[lane][:], ALU.add).then_inc(S_.r_ready, 1)
                else:
                    for lane in range(LANES):
                        n = i * LANES + lane
                        at(dve, S_.y_psum, n)
                        if bor is None:
                            dve.tensor_tensor(r[lane][:], ps[lane][:, 3, 0:D], xs[lane][:], ALU.add).then_inc(S_.r_ready, 1)
                        else:
                            dve.tensor_tensor(r[lane][:], ps[lane][:, 3, 0:D], bor[:], ALU.add).then_inc(y_bias_added, 1)
                            at(dve, y_bias_added, n)
                            if strided:
                                dve.tensor_tensor(r[lane][:], r[lane][:], lgam[:], ALU.mult).then_inc(y_scaled, 1)
                                at(dve, y_scaled, n)
                            dve.tensor_tensor(r[lane][:], r[lane][:], xs[lane][:], ALU.add).then_inc(S_.r_ready, 1)
                if post == "l3ffn":
                    for lane in range(LANES):
                        n = i * LANES + lane
                        at(dve, S_.r_ready, n)
                        dve.tensor_copy(extra["X1"][:, bass.ds(n, 1), :].rearrange("t a d -> t (a d)"), r[lane][:]).then_inc(S_.slot_free, 1)
                else:
                    for lane in range(LANES):
                        n = i * LANES + lane
                        at(dve, S_.r_ready, n)
                        norm(r[lane][:], n, lane, (S_.stats, S_.mean_var, S_.var_eps))
                    for lane in range(LANES):
                        n = i * LANES + lane
                        dst = r2[lane][:] if strided else X[:, bass.ds(n, 1), :].rearrange("t a d -> t (a d)")
                        normed(r[lane][:], n, lane, S_.rstd_ready, dst, S_.slot_free)
    s.close()


def batch_axis_attention(core):
    nc, I, X = core.nc, core.I, core.X
    before = nc.dram_tensor("x_by_position", (T, B, D), F32, kind="Internal").ap()
    after = nc.dram_tensor("x_by_position_out", (T, B, D), F32, kind="Internal").ap()
    I["x_mid"], I["x_mid_out"] = before, after
    s = Scope(nc, "L2out")
    moved = s.sem("moved")
    with nc.Block() as block:
        @block.sync
        def _(sp):
            sp.dma_start(before, X[:]).then_inc(moved, 16)
            sp.wait_ge(moved, 16)
    s.close()
    attention(core, "L2self", H=16, Dh=8, Wq="L2_attn_Wq", Wk="L2_attn_Wk", Wv="L2_attn_Wv", Wo="L2_attn_WoT",
              bq="L2_attn_bq", bk="L2_attn_bk", bv="L2_attn_bv", bo="L2_attn_out_proj_bias",
              mask="mask_within", post="l2self")
    s = Scope(nc, "L2back")
    back = s.sem("back")
    with nc.Block() as block:
        @block.sync
        def _(sp):
            sp.dma_start(X[:], after).then_inc(back, 16)
            sp.wait_ge(back, 16)
    s.close()


def expert_pass(core, name, *, w1, b1, w2, act, xT, gates):
    nc, I, X = core.nc, core.I, core.X
    s = Scope(nc, name)
    CH = 4
    N = B // CH
    w1s, w2s, b1s = s.lanes("w1", [D, F]), s.lanes("w2", [128, FC, D]), s.lanes("b1", [128, FC])
    hT = s.lanes("hT", [128, FC, CH * T])
    gy = s.lanes("gy", [T, CH, D])
    ph = s.psum("ph", [128, FC, 512])
    py = s.psum("py", [128, 2, 512])
    w_in = [s.sem(f"weights_in{k}") for k in range(LANES)]
    h_psum, h_ready, y_psum, y_gated, added = [s.sem(n) for n in ("h_psum", "h_ready", "y_psum", "y_gated", "added")]
    H0, Y0, G0, A0 = FC, 2 * N, 2, 1
    Xf, xTf = X[:].rearrange("t b d -> t (b d)"), xT[:]

    with nc.Block() as block:
        @block.sync
        def _(sp):
            with sp.Fori(0, E // LANES) as i:
                for lane in range(LANES):
                    e = i * LANES + lane
                    sp.wait_ge(y_psum, (e + 1) * N)
                    with nc.allow_non_contiguous_dma(reason="a bias column"):
                        sp.dma_start(w1s[lane][:], I[w1][bass.ds(e, 1)].rearrange("a d f -> d (a f)")).then_inc(w_in[lane], 16)
                        sp.dma_start(w2s[lane][:], I[w2][bass.ds(e, 1)].rearrange("a (c p) d -> p (a c) d", p=128)).then_inc(w_in[lane], 16)
                        sp.dma_start(b1s[lane][:], I[b1][bass.ds(e, 1)].rearrange("a (c p) -> p (a c)", p=128)).then_inc(w_in[lane], 16)

        @block.tensor
        def _(pe):
            pe.sem_inc(y_psum, Y0)
            pe.sem_inc(h_ready, H0)
            with pe.Fori(0, E // LANES) as i:
                for lane in range(LANES):
                    e = i * LANES + lane
                    with pe.Fori(0, N // 2) as c2:
                        at(pe, w_in[lane], i, 48)
                        for par in range(2):
                            m = e * N + c2 * 2 + par
                            for f in range(FC):
                                pe.wait_ge(h_ready, m * FC + f + 1)
                                pe.matmul(ph[:, f, :], w1s[lane][:, f * 128:(f + 1) * 128],
                                          xTf[:, bass.ds((c2 * 2 + par) * (CH * T), CH * T)], start=True, stop=True).then_inc(h_psum, 1)
                        for par in range(2):
                            m = e * N + c2 * 2 + par
                            pe.wait_ge(h_ready, m * FC + FC + H0)
                            pe.wait_ge(y_gated, m + 1)
                            for b in range(CH):
                                for f in range(FC):
                                    last = pe.matmul(py[:, par, b * D:(b + 1) * D], hT[par][:, f, b * T:(b + 1) * T],
                                                     w2s[lane][:, f, :], start=f == 0, stop=f == FC - 1)
                            last.then_inc(y_psum, 1)

        @block.scalar
        def _(act_eng):
            with act_eng.Fori(0, E // LANES) as i:
                for lane in range(LANES):
                    e = i * LANES + lane
                    with act_eng.Fori(0, N // 2) as c2:
                        at(act_eng, w_in[lane], i, 48)
                        for par in range(2):
                            m = e * N + c2 * 2 + par
                            act_eng.wait_ge(y_psum, m - 1 + Y0)
                            for f in range(FC):
                                act_eng.wait_ge(h_psum, m * FC + f + 1)
                                act_eng.activation(hT[par][:, f, :], ph[:, f, :], act, bias=b1s[lane][:, f:f + 1]).then_inc(h_ready, 1)

        @block.vector
        def _(dve):
            dve.sem_inc(y_gated, G0)
            dve.sem_inc(added, A0)
            with dve.Fori(0, E * N // 8) as i:
                for k in range(8):
                    m = i * 8 + k
                    par = k % 2
                    dve.wait_ge(y_psum, m + 1 + Y0)
                    dve.wait_ge(added, m + A0)
                    dve.tensor_tensor(gy[par][:], py[:, par, :].rearrange("t (b d) -> t b d", b=CH),
                                      gates[:].rearrange("t e b -> t (e b)")[:, bass.ds(m * CH, CH)].unsqueeze(2).to_broadcast([T, CH, D]),
                                      ALU.mult).then_inc(y_gated, 1)
                    dve.wait_ge(y_gated, m + 1 + G0)
                    xc = Xf[:, k * CH * D:(k + 1) * CH * D]
                    dve.tensor_tensor(xc, xc, gy[par][:].rearrange("t b d -> t (b d)"), ALU.add).then_inc(added, 1)
    s.close()


def norm_all(core, name):
    nc, X = core.nc, core.X
    s = Scope(nc, name)
    sq = s.sb("sq", [T, B, D])
    mean, ve, rstd = s.sb("mean", [T, B]), s.sb("ve", [T, B]), s.sb("rstd", [T, B])
    step, var_eps, rstd_ready = s.sem("step"), s.sem("var_eps"), s.sem("rstd_ready")
    with nc.Block() as block:
        @block.gpsimd
        def _(pool):
            pool.wait_ge(var_eps, 1)
            pool.tensor_tensor(rstd[:], ve[:], core.neghalf[:, 0:B], ALU.pow).then_inc(rstd_ready, 1)

        @block.vector
        def _(dve):
            dve.tensor_reduce(mean[:], X[:], AX.X, ALU.add).then_inc(step, 1)
            dve.wait_ge(step, 1)
            dve.tensor_scalar(mean[:], mean[:], 1.0 / D, None, ALU.mult).then_inc(step, 1)
            dve.wait_ge(step, 2)
            dve.tensor_tensor(X[:], X[:], mean[:].unsqueeze(2).to_broadcast([T, B, D]), ALU.subtract).then_inc(step, 1)
            dve.wait_ge(step, 3)
            dve.tensor_tensor(sq[:], X[:], X[:], ALU.mult).then_inc(step, 1)
            dve.wait_ge(step, 4)
            dve.tensor_reduce(ve[:], sq[:], AX.X, ALU.add).then_inc(step, 1)
            dve.wait_ge(step, 5)
            dve.tensor_scalar(ve[:], ve[:], 1.0 / D, LN_EPS, ALU.mult, ALU.add).then_inc(var_eps, 1)
            dve.wait_ge(rstd_ready, 1)
            dve.tensor_tensor(X[:], X[:], rstd[:].unsqueeze(2).to_broadcast([T, B, D]), ALU.mult).then_inc(step, 1)
            dve.wait_ge(step, 6)
    s.close()


def route(core, name, xT, gates, *, kind, top, X1=None):
    nc, I, X = core.nc, core.I, core.X
    s = Scope(nc, name)
    NK = E if top == 1 else 2
    loads = []

    def tile(tag, shape, src):
        t = s.sb(tag, shape)
        loads.append((t[:], src))
        return t

    b2 = tile("b2", [E, D], I[{"L0": "L0_ffn_b2", "L1": "L1_ffn_b2", "L3": "L3_ffn_fc2_b"}[kind]])
    iota = tile("iota", [T, E], row_bc(I["iota8"]))
    normed_input = kind != "L0"
    if kind == "L0":
        w_red = tile("w_red", [D, 16], I["L0_ffn_w_red"])
        wgT = tile("wgT", [16, E], I["L0_ffn_wg"].rearrange("e g -> g e"))
        wsq, wnorm, wgn = s.sb("wsq", [16, E]), s.sb("wnorm", [16, E]), s.sb("wgn", [16, E])
        redT = s.lanes("redT", [16, T])
    elif kind == "L1":
        wr = tile("wr", [D, E], I["L1_ffn_Wr"])
        br = tile("br", [T, E], row_bc(I["L1_ffn_br"]))
        gam, bet = tile("gam", [T, D], row_bc(I["L1_ffn_ln_g"])), tile("bet", [T, D], row_bc(I["L1_ffn_ln_b"]))
    else:
        wr = tile("wr", [D, E], I["L3_ffn_gate_W"])
        gam, bet = tile("gam", [T, D], row_bc(I["L3_ffn_ln2_w"])), tile("bet", [T, D], row_bc(I["L3_ffn_ln2_b"]))
    xs, xn, xTs, gT = s.lanes("xs", [T, D]), s.lanes("xn", [T, D]), s.lanes("xTs", [D, T]), s.lanes("gT", [E, T])
    lg, m8, nmx = s.lanes("lg", [T, E]), s.lanes("m8", [T, 8]), s.lanes("nmx", [T, 1])
    idx, idf, ex = s.lanes("idx", [T, 8], U32), s.lanes("idf", [T, 8]), s.lanes("ex", [T, 8])
    sm, pr, g8, g8b = s.lanes("sm", [T, 1]), s.lanes("pr", [T, 8]), s.lanes("g8", [T, E]), s.lanes("g8b", [T, E])
    st, mv, ve, rs, xb = s.lanes("st", [T, 6]), s.lanes("mv", [T, 2]), s.lanes("ve", [T, 1]), s.lanes("rs", [T, 1]), s.lanes("xb", [T, D])
    ps = [s.psum(f"ps{lane}", [128, 4, 512]) for lane in range(LANES)]
    names = ("weights_in lane_free x_copied x_psum xT_ready xnT_ready red_psum red_ready logits_psum logits_ready sorted negmax "
             "index_ready index_float exp_ready recip_ready prob_ready gate1 gate2 gate_ready gT_psum gT_ready bias_psum "
             "biased stats mean_var var_eps rstd normed scaled offset wsq_ready wnorm_psum wnorm_safe wnorm_pow wg_ready gate_stored")
    S_ = type("Ready", (), {n: s.sem(n) for n in names.split()})
    with nc.Block() as block:
        @block.sync
        def _(sp):
            with nc.allow_non_contiguous_dma(reason="small weights, once"):
                for dst, src in loads:
                    sp.dma_start(dst, src).then_inc(S_.weights_in, 16)

        @block.gpsimd
        def _(pool):
            if kind == "L0":
                pool.wait_ge(S_.wnorm_safe, 1)
                pool.tensor_tensor(wnorm[:], wnorm[:], core.neghalf[0:16, 0:E], ALU.pow).then_inc(S_.wnorm_pow, 1)
            pool.sem_inc(S_.lane_free, LANES)
            with pool.Fori(0, STEPS) as i:
                for lane in range(LANES):
                    n = i * LANES + lane
                    at(pool, S_.lane_free, n)
                    pool.tensor_copy(xs[lane][:], (X1 or X)[:, bass.ds(n, 1), :].rearrange("t a d -> t (a d)")).then_inc(S_.x_copied, 1)
                if normed_input:
                    for lane in range(LANES):
                        at(pool, S_.var_eps, i * LANES + lane)
                        pool.tensor_tensor(rs[lane][:], ve[lane][:], core.neghalf[:, 0:1], ALU.pow).then_inc(S_.rstd, 1)

        @block.tensor
        def _(pe):
            pe.wait_ge(S_.weights_in, 16 * len(loads))
            if kind == "L0":
                pe.wait_ge(S_.wsq_ready, 1)
                pe.matmul(ps[0][0:16, 0, 0:E], core.ones[0:16, 0:16], wsq[:], start=True, stop=True).then_inc(S_.wnorm_psum, 1)
                pe.wait_ge(S_.wg_ready, 1)
            with pe.Fori(0, STEPS) as i:
                for lane in range(LANES):
                    n = i * LANES + lane
                    if normed_input:
                        at(pe, S_.offset, n)
                        pe.transpose(ps[lane][:, 0, 128:256], xn[lane][:], core.ident[:])
                    at(pe, S_.x_copied, n)
                    pe.transpose(ps[lane][:, 0, 0:T], xs[lane][:], core.ident[:]).then_inc(S_.x_psum, 1)
                if kind == "L0":
                    for lane in range(LANES):
                        at(pe, S_.xT_ready, i * LANES + lane)
                        pe.matmul(ps[lane][0:16, 1, 0:T], w_red[:], xTs[lane][:], start=True, stop=True).then_inc(S_.red_psum, 1)
                for lane in range(LANES):
                    n = i * LANES + lane
                    if kind == "L0":
                        at(pe, S_.red_ready, n)
                        pe.matmul(ps[lane][:, 2, 0:E], redT[lane][:], wgn[:], start=True, stop=True).then_inc(S_.logits_psum, 1)
                    else:
                        at(pe, S_.xT_ready, n)
                        pe.matmul(ps[lane][:, 2, 0:E], xTs[lane][:], wr[:], start=True, stop=True).then_inc(S_.logits_psum, 1)
                for lane in range(LANES):
                    at(pe, S_.gate_ready, i * LANES + lane)
                    pe.transpose(ps[lane][0:E, 1, 128:256], g8[lane][:], core.ident[:]).then_inc(S_.gT_psum, 1)
                for lane in range(LANES):
                    at(pe, S_.gT_ready, i * LANES + lane)
                    pe.matmul(ps[lane][:, 3, 0:D], gT[lane][:], b2[:], start=True, stop=True).then_inc(S_.bias_psum, 1)

        @block.scalar
        def _(act):
            with act.Fori(0, STEPS) as i:
                for lane in range(LANES):
                    n = i * LANES + lane
                    at(act, S_.x_psum, n)
                    logits_of = ps[lane][:, 0, 128:256] if kind == "L3" else ps[lane][:, 0, 0:T]
                    experts_of = ps[lane][:, 0, 128:256] if normed_input else ps[lane][:, 0, 0:T]
                    act.activation(xTs[lane][:], logits_of, ACT.Copy).then_inc(S_.xT_ready, 1)
                    act.activation(xT[:, bass.ds(n * T, T)], experts_of, ACT.Copy).then_inc(S_.xnT_ready, 1)
                if kind == "L0":
                    for lane in range(LANES):
                        at(act, S_.red_psum, i * LANES + lane)
                        act.activation(redT[lane][:], ps[lane][0:16, 1, 0:T], ACT.Copy).then_inc(S_.red_ready, 1)
                for lane in range(LANES):
                    at(act, S_.negmax, i * LANES + lane)
                    act.activation(ex[lane][:, 0:NK], m8[lane][:, 0:NK], ACT.Exp, bias=nmx[lane][:, 0:1],
                                   accum_out=sm[lane][:]).then_inc(S_.exp_ready, 1)
                for lane in range(LANES):
                    at(act, S_.gT_psum, i * LANES + lane)
                    act.activation(gT[lane][:], ps[lane][0:E, 1, 128:256], ACT.Copy).then_inc(S_.gT_ready, 1)

        @block.vector
        def _(dve):
            dve.wait_ge(S_.weights_in, 16 * len(loads))
            if kind == "L0":
                dve.tensor_tensor(wsq[:], wgT[:], wgT[:], ALU.mult).then_inc(S_.wsq_ready, 1)
                dve.wait_ge(S_.wnorm_psum, 1)
                dve.tensor_scalar(wnorm[:], ps[0][0:16, 0, 0:E], 1e-8, None, ALU.max).then_inc(S_.wnorm_safe, 1)
                dve.wait_ge(S_.wnorm_pow, 1)
                dve.tensor_tensor(wgn[:], wgT[:], wnorm[:], ALU.mult).then_inc(S_.wg_ready, 1)
            with dve.Fori(0, STEPS) as i:
                if normed_input:
                    for lane in range(LANES):
                        n = i * LANES + lane
                        at(dve, S_.x_copied, n)
                        dve.bn_stats(st[lane][:], xs[lane][:]).then_inc(S_.stats, 1)
                        at_alone(dve, S_.stats, n, s.passed)
                        dve.bn_aggr(mv[lane][:], st[lane][:]).then_inc(S_.mean_var, 1)
                        at(dve, S_.mean_var, n)
                        dve.tensor_scalar(ve[lane][:], mv[lane][:, 1:2], LN_EPS, None, ALU.add).then_inc(S_.var_eps, 1)
                    for lane in range(LANES):
                        n = i * LANES + lane
                        at(dve, S_.rstd, n)
                        dve.tensor_scalar(xn[lane][:], xs[lane][:], mv[lane][:, 0:1], rs[lane][:, 0:1], ALU.subtract, ALU.mult).then_inc(S_.normed, 1)
                        at(dve, S_.normed, n)
                        dve.tensor_tensor(xn[lane][:], xn[lane][:], gam[:], ALU.mult).then_inc(S_.scaled, 1)
                        at(dve, S_.scaled, n)
                        dve.tensor_tensor(xn[lane][:], xn[lane][:], bet[:], ALU.add).then_inc(S_.offset, 1)
                for lane in range(LANES):
                    n = i * LANES + lane
                    at(dve, S_.logits_psum, n)
                    if kind == "L1":
                        dve.tensor_tensor(lg[lane][:], ps[lane][:, 2, 0:E], br[:], ALU.add).then_inc(S_.logits_ready, 1)
                    else:
                        dve.tensor_copy(lg[lane][:], ps[lane][:, 2, 0:E]).then_inc(S_.logits_ready, 1)
                    at_alone(dve, S_.logits_ready, n, s.passed)
                    dve.max(m8[lane][:], lg[lane][:]).then_inc(S_.sorted, 1)
                    at(dve, S_.sorted, n)
                    dve.tensor_scalar(nmx[lane][:], m8[lane][:, 0:1], -1.0, None, ALU.mult).then_inc(S_.negmax, 1)
                    dve.max_index(idx[lane][:], m8[lane][:], lg[lane][:]).then_inc(S_.index_ready, 1)
                    at(dve, S_.index_ready, n)
                    dve.tensor_copy(idf[lane][:], idx[lane][:]).then_inc(S_.index_float, 1)
                for lane in range(LANES):
                    n = i * LANES + lane
                    at(dve, S_.exp_ready, n)
                    dve.reciprocal(sm[lane][:], sm[lane][:]).then_inc(S_.recip_ready, 1)
                    at(dve, S_.recip_ready, n)
                    dve.tensor_scalar(pr[lane][:, 0:top], ex[lane][:, 0:top], sm[lane][:, 0:1], None, ALU.mult).then_inc(S_.prob_ready, 1)
                    at(dve, S_.prob_ready, n)
                    dve.tensor_scalar(g8[lane][:], iota[:], idf[lane][:, 0:1], pr[lane][:, 0:1], ALU.is_equal, ALU.mult).then_inc(S_.gate_ready if top == 1 else S_.gate1, 1)
                    if top == 2:
                        dve.tensor_scalar(g8b[lane][:], iota[:], idf[lane][:, 1:2], pr[lane][:, 1:2], ALU.is_equal, ALU.mult).then_inc(S_.gate2, 1)
                        at(dve, S_.gate2, n)
                        dve.tensor_tensor(g8[lane][:], g8[lane][:], g8b[lane][:], ALU.add).then_inc(S_.gate_ready, 1)
                    at(dve, S_.gate_ready, n)
                    dve.tensor_copy(gates[:, :, bass.ds(n, 1)], g8[lane][:].unsqueeze(2)).then_inc(S_.gate_stored, 1)
                for lane in range(LANES):
                    n = i * LANES + lane
                    at(dve, S_.bias_psum, n)
                    dve.tensor_tensor(xb[lane][:], ps[lane][:, 3, 0:D], xs[lane][:], ALU.add).then_inc(S_.biased, 1)
                    at(dve, S_.biased, n)
                    row = X[:, bass.ds(n, 1), :].rearrange("t a d -> t (a d)")
                    if X1 is None:
                        dve.tensor_copy(row, xb[lane][:]).then_inc(S_.lane_free, 1)
                    else:
                        dve.tensor_tensor(row, row, xb[lane][:], ALU.add).then_inc(S_.lane_free, 1)
    s.close()


def experts_top1(core, name):
    nc = core.nc
    kind = name[:2]
    with ExitStack() as stack:
        xT = stack.enter_context(nc.sbuf_tensor(f"{name}_xT", [D, B * T], F32))
        gates = stack.enter_context(nc.sbuf_tensor(f"{name}_gates", [T, E, B], F32))
        route(core, f"{name}_route", xT, gates, kind=kind, top=1)
        w = ("w1", "b1", "w2") if kind == "L0" else ("W1", "b1", "W2")
        expert_pass(core, f"{name}_pass", w1=f"{kind}_ffn_{w[0]}", b1=f"{kind}_ffn_{w[1]}", w2=f"{kind}_ffn_{w[2]}",
                    act=ACT.Gelu if kind == "L0" else ACT.Relu, xT=xT, gates=gates)
    norm_all(core, f"{name}_norm")


def block_experts(core):
    nc = core.nc
    with ExitStack() as stack:
        X1 = stack.enter_context(nc.sbuf_tensor("X1", [T, B, D], F32))
        attention(core, "L3self", H=16, Dh=8, Wq="L3_ffn_Wq", Wk="L3_ffn_Wk", Wv="L3_ffn_Wv", Wo="L3_ffn_Wo",
                  bq="L3_ffn_bq", bk="L3_ffn_bk", bv="L3_ffn_bv", bo="L3_ffn_bo", mask="mask_causal",
                  post="l3ffn", extra={"X1": X1})
        xT = stack.enter_context(nc.sbuf_tensor("L3ffn_xT", [D, B * T], F32))
        gates = stack.enter_context(nc.sbuf_tensor("L3ffn_gates", [T, E, B], F32))
        route(core, "L3ffn_route", xT, gates, kind="L3", top=2, X1=X1)
        expert_pass(core, "L3ffn_pass", w1="L3_ffn_fc1T", b1="L3_ffn_fc1_b", w2="L3_ffn_fc2T", act=ACT.Gelu,
                    xT=xT, gates=gates)
    norm_all(core, "L3ffn_norm")


def wkv_mix(core):
    nc, I, X = core.nc, core.I, core.X
    s = Scope(nc, "wkv")
    loads = []

    def tile(tag, shape, src):
        t = s.sb(tag, shape)
        loads.append((t[:], src))
        return t

    mix = {c: tile(f"mix_{c}", [D, 1], col(I[f"L1_attn_time_mix_{c}"])) for c in "kvr"}
    W = {c: tile(f"W{c}", [D, D], I[f"L1_attn_W{c}T"]) for c in "kvr"}
    Wo = tile("Wo", [D, D], I["L1_attn_WoT"])
    decay_in = tile("decay_in", [D, 1], col(I["L1_attn_time_decay"]))
    first = tile("first", [D, 1], col(I["L1_attn_time_first"]))
    decay, decays = s.sb("decay", [D, 1]), s.sb("decays", [D, T])
    rest = {c: s.sb(f"rest_{c}", [D, 1]) for c in "kvr"}
    START = -1e38

    xs, r = s.lanes("xs", [T, D]), s.lanes("r", [T, D])
    xT = s.lanes("xT", [D, T + 1])
    mixed = {c: s.lanes(f"mixed_{c}", [D, T]) for c in "kvr"}
    shifted = {c: s.lanes(f"shifted_{c}", [D, T]) for c in "kvr"}
    k, v, sr = s.lanes("k", [D, T]), s.lanes("v", [D, T]), s.lanes("sr", [D, T])
    pp, aa, bb = s.lanes("pp", [D, T + 1]), s.lanes("aa", [D, T + 1]), s.lanes("bb", [D, T + 1])
    ex = s.lanes("ex", [D, 4, T])
    ww, p = s.lanes("ww", [D, T]), s.lanes("p", [D, T])
    ev, num, den, y = s.lanes("ev", [D, 2, T]), s.lanes("num", [D, T]), s.lanes("den", [D, T]), s.lanes("y", [D, T])
    st, mv, ve, rs = s.lanes("st", [T, 6]), s.lanes("mv", [T, 2]), s.lanes("ve", [T, 1]), s.lanes("rs", [T, 1])
    ps = [s.psum(f"ps{lane}", [128, 4, 512]) for lane in range(LANES)]
    names = ("weights_in lane_free starts_set decay_exp decay_neg decays_ready rests_ready x_copied x_psum xT_ready mixed_ready "
             "rest_mixed kvr_psum kv_ready r_exp r_plus1 r_ready max_scanned exps_in exps_ready ev_ready sums_scanned ww_ready "
             "p_ready num1 num2 den1 den2 den_inv y_scaled y_ready out_psum sum_ready stats mean_var var_eps rstd")
    S_ = type("Ready", (), {n: s.sem(n) for n in names.split()})
    with nc.Block() as block:
        @block.sync
        def _(sp):
            with nc.allow_non_contiguous_dma(reason="small weights, once"):
                for dst, src in loads:
                    sp.dma_start(dst, src).then_inc(S_.weights_in, 16)

        @block.gpsimd
        def _(pool):
            for lane in range(LANES):
                pool.memset(xT[lane][:, 0:1], 0.0).then_inc(S_.starts_set, 1)
                pool.memset(pp[lane][:, 0:1], START).then_inc(S_.starts_set, 1)
                pool.memset(aa[lane][:, 0:1], 0.0).then_inc(S_.starts_set, 1)
                pool.memset(bb[lane][:, 0:1], 0.0).then_inc(S_.starts_set, 1)
            pool.sem_inc(S_.lane_free, LANES)
            with pool.Fori(0, STEPS) as i:
                for lane in range(LANES):
                    n = i * LANES + lane
                    at(pool, S_.lane_free, n)
                    pool.tensor_copy(xs[lane][:], X[:, bass.ds(n, 1), :].rearrange("t a d -> t (a d)")).then_inc(S_.x_copied, 1)
                for lane in range(LANES):
                    at(pool, S_.var_eps, i * LANES + lane)
                    pool.tensor_tensor(rs[lane][:], ve[lane][:], core.neghalf[:, 0:1], ALU.pow).then_inc(S_.rstd, 1)

        @block.tensor
        def _(pe):
            pe.wait_ge(S_.weights_in, 16 * len(loads))
            with pe.Fori(0, STEPS) as i:
                for lane in range(LANES):
                    at(pe, S_.x_copied, i * LANES + lane)
                    pe.transpose(ps[lane][:, 0, 0:T], xs[lane][:], core.ident[:]).then_inc(S_.x_psum, 1)
                for lane in range(LANES):
                    at(pe, S_.mixed_ready, i * LANES + lane, 3)
                    for j, c in enumerate("kvr"):
                        last = pe.matmul(ps[lane][:, 1, j * T:(j + 1) * T], W[c][:], mixed[c][lane][:], start=True, stop=True)
                    last.then_inc(S_.kvr_psum, 1)
                for lane in range(LANES):
                    at(pe, S_.y_ready, i * LANES + lane)
                    pe.matmul(ps[lane][:, 2, 0:D], y[lane][:], Wo[:], start=True, stop=True).then_inc(S_.out_psum, 1)

        @block.scalar
        def _(act):
            act.wait_ge(S_.weights_in, 16 * len(loads))
            act.activation(decay[:], decay_in[:], ACT.Exp).then_inc(S_.decay_exp, 1)
            act.wait_ge(S_.starts_set, 4 * LANES)
            with act.Fori(0, STEPS) as i:
                for lane in range(LANES):
                    at(act, S_.x_psum, i * LANES + lane)
                    act.activation(xT[lane][:, 1:T + 1], ps[lane][:, 0, 0:T], ACT.Copy).then_inc(S_.xT_ready, 1)
                for lane in range(LANES):
                    at(act, S_.kvr_psum, i * LANES + lane)
                    act.activation(k[lane][:], ps[lane][:, 1, 0:T], ACT.Copy).then_inc(S_.kv_ready, 1)
                    act.activation(v[lane][:], ps[lane][:, 1, T:2 * T], ACT.Copy).then_inc(S_.kv_ready, 1)
                    act.activation(sr[lane][:], ps[lane][:, 1, 2 * T:3 * T], ACT.Exp, scale=-1.0).then_inc(S_.r_exp, 1)
                for lane in range(LANES):
                    at(act, S_.exps_in, i * LANES + lane, 4)
                    act.activation(ex[lane][:], ex[lane][:], ACT.Exp).then_inc(S_.exps_ready, 1)

        @block.vector
        def _(dve):
            dve.wait_ge(S_.starts_set, 4 * LANES)
            dve.wait_ge(S_.decay_exp, 1)
            dve.tensor_scalar(decay[:], decay[:], -1.0, None, ALU.mult).then_inc(S_.decay_neg, 1)
            dve.wait_ge(S_.decay_neg, 1)
            dve.tensor_scalar(decays[:], core.ones[:], decay[:, 0:1], None, ALU.mult).then_inc(S_.decays_ready, 1)
            for c in "kvr":
                dve.tensor_scalar(rest[c][:], mix[c][:], -1.0, 1.0, ALU.mult, ALU.add).then_inc(S_.rests_ready, 1)
            dve.wait_ge(S_.decays_ready, 1)
            dve.wait_ge(S_.rests_ready, 3)
            with dve.Fori(0, STEPS) as i:
                for lane in range(LANES):
                    n = i * LANES + lane
                    at(dve, S_.xT_ready, n)
                    for c in "kvr":
                        dve.tensor_scalar(shifted[c][lane][:], xT[lane][:, 0:T], rest[c][:, 0:1], None, ALU.mult).then_inc(S_.rest_mixed, 1)
                    at(dve, S_.rest_mixed, n, 3)
                    for c in "kvr":
                        dve.scalar_tensor_tensor(out=mixed[c][lane][:], in0=xT[lane][:, 1:T + 1], scalar=mix[c][:, 0:1],
                                                 in1=shifted[c][lane][:], op0=ALU.mult, op1=ALU.add).then_inc(S_.mixed_ready, 1)
                for lane in range(LANES):
                    n = i * LANES + lane
                    at(dve, S_.kv_ready, n, 2)
                    dve.tensor_tensor_scan(pp[lane][:, 1:T + 1], decays[:], k[lane][:], START, ALU.add, ALU.max).then_inc(S_.max_scanned, 1)
                    dve.tensor_scalar(ww[lane][:], k[lane][:], first[:, 0:1], None, ALU.add).then_inc(S_.ww_ready, 1)
                    at(dve, S_.ww_ready, n)
                    at(dve, S_.max_scanned, n)
                    dve.tensor_tensor(p[lane][:], pp[lane][:, 0:T], ww[lane][:], ALU.max).then_inc(S_.p_ready, 1)
                    dve.scalar_tensor_tensor(out=ex[lane][:, 0, :], in0=pp[lane][:, 0:T], scalar=decay[:, 0:1],
                                             in1=pp[lane][:, 1:T + 1], op0=ALU.add, op1=ALU.subtract).then_inc(S_.exps_in, 1)
                    dve.tensor_tensor(ex[lane][:, 1, :], k[lane][:], pp[lane][:, 1:T + 1], ALU.subtract).then_inc(S_.exps_in, 1)
                    at(dve, S_.p_ready, n)
                    dve.tensor_tensor(ex[lane][:, 2, :], pp[lane][:, 0:T], p[lane][:], ALU.subtract).then_inc(S_.exps_in, 1)
                    dve.tensor_tensor(ex[lane][:, 3, :], ww[lane][:], p[lane][:], ALU.subtract).then_inc(S_.exps_in, 1)
                for lane in range(LANES):
                    n = i * LANES + lane
                    at(dve, S_.exps_ready, n)
                    dve.tensor_tensor(ev[lane][:, 0, :], ex[lane][:, 1, :], v[lane][:], ALU.mult).then_inc(S_.ev_ready, 1)
                    dve.tensor_tensor(ev[lane][:, 1, :], ex[lane][:, 3, :], v[lane][:], ALU.mult).then_inc(S_.ev_ready, 1)
                    dve.tensor_tensor_scan(bb[lane][:, 1:T + 1], ex[lane][:, 0, :], ex[lane][:, 1, :], 0.0, ALU.mult, ALU.add).then_inc(S_.sums_scanned, 1)
                    at(dve, S_.ev_ready, n, 2)
                    dve.tensor_tensor_scan(aa[lane][:, 1:T + 1], ex[lane][:, 0, :], ev[lane][:, 0, :], 0.0, ALU.mult, ALU.add).then_inc(S_.sums_scanned, 1)
                    at(dve, S_.sums_scanned, n, 2)
                    dve.tensor_tensor(den[lane][:], ex[lane][:, 2, :], bb[lane][:, 0:T], ALU.mult).then_inc(S_.den1, 1)
                    dve.tensor_tensor(num[lane][:], ex[lane][:, 2, :], aa[lane][:, 0:T], ALU.mult).then_inc(S_.num1, 1)
                    at(dve, S_.den1, n)
                    dve.tensor_tensor(den[lane][:], den[lane][:], ex[lane][:, 3, :], ALU.add).then_inc(S_.den2, 1)
                    at(dve, S_.num1, n)
                    dve.tensor_tensor(num[lane][:], num[lane][:], ev[lane][:, 1, :], ALU.add).then_inc(S_.num2, 1)
                    at(dve, S_.r_exp, n)
                    dve.tensor_scalar(sr[lane][:], sr[lane][:], 1.0, None, ALU.add).then_inc(S_.r_plus1, 1)
                    at(dve, S_.r_plus1, n)
                    dve.reciprocal(sr[lane][:], sr[lane][:]).then_inc(S_.r_ready, 1)
                    at(dve, S_.den2, n)
                    dve.reciprocal(den[lane][:], den[lane][:]).then_inc(S_.den_inv, 1)
                    at(dve, S_.den_inv, n)
                    at(dve, S_.num2, n)
                    dve.tensor_tensor(num[lane][:], num[lane][:], den[lane][:], ALU.mult).then_inc(S_.y_scaled, 1)
                    at(dve, S_.r_ready, n)
                    at(dve, S_.y_scaled, n)
                    dve.tensor_tensor(y[lane][:], num[lane][:], sr[lane][:], ALU.mult).then_inc(S_.y_ready, 1)
                for lane in range(LANES):
                    n = i * LANES + lane
                    at(dve, S_.out_psum, n)
                    dve.tensor_tensor(r[lane][:], ps[lane][:, 2, 0:D], xs[lane][:], ALU.add).then_inc(S_.sum_ready, 1)
                    at(dve, S_.sum_ready, n)
                    dve.bn_stats(st[lane][:], r[lane][:]).then_inc(S_.stats, 1)
                    at_alone(dve, S_.stats, n, s.passed)
                    dve.bn_aggr(mv[lane][:], st[lane][:]).then_inc(S_.mean_var, 1)
                    at(dve, S_.mean_var, n)
                    dve.tensor_scalar(ve[lane][:], mv[lane][:, 1:2], LN_EPS, None, ALU.add).then_inc(S_.var_eps, 1)
                for lane in range(LANES):
                    n = i * LANES + lane
                    at(dve, S_.rstd, n)
                    dve.tensor_scalar(X[:, bass.ds(n, 1), :].rearrange("t a d -> t (a d)"), r[lane][:], mv[lane][:, 0:1],
                                      rs[lane][:, 0:1], ALU.subtract, ALU.mult).then_inc(S_.lane_free, 1)
    s.close()


def soft_experts(core):
    nc, I, X = core.nc, core.I, core.X
    NS = I["L2_ffn_slot_embeds"].shape[1]
    SC = E * NS // 128
    with ExitStack() as stack:
        snT = stack.enter_context(nc.sbuf_tensor("snT", [D, E * NS], F32))
        slots = stack.enter_context(nc.sbuf_tensor("slotsT", [D, E, B, NS], F32))
        slot_keys(core, snT, SC)
        dispatch_or_combine(core, "dispatch", snT, slots, SC, NS, combine=False)
        slot_pass(core, slots, NS)
        dispatch_or_combine(core, "combine", snT, slots, SC, NS, combine=True)


def slot_keys(core, snT, SC):
    nc, I = core.nc, core.I
    s = Scope(nc, "slotkeys")
    emb, sq = s.sb("emb", [128, SC, D]), s.sb("sq", [128, SC, D])
    gam = s.sb("gam", [128, D])
    ss = s.sb("ss", [128, SC])
    ps = s.psum("ps", [128, SC, 128])
    loaded, step, safe, inv, scaled, turned, done = [s.sem(n) for n in ("loaded", "step", "safe", "inverse", "scaled", "turned", "done")]
    with nc.Block() as block:
        @block.sync
        def _(sp):
            sp.dma_start(emb[:], I["L2_ffn_slot_embeds"].rearrange("e s d -> (e s) d").rearrange("(c p) d -> p c d", p=128)).then_inc(loaded, 16)
            sp.dma_start(gam[:], row_bc(I["L2_ffn_slot_norm_gamma"])).then_inc(loaded, 16)

        @block.gpsimd
        def _(pool):
            pool.wait_ge(safe, 1)
            pool.tensor_tensor(ss[:], ss[:], core.neghalf[:, 0:SC], ALU.pow).then_inc(inv, 1)

        @block.tensor
        def _(pe):
            pe.wait_ge(scaled, 1)
            for c in range(SC):
                last = pe.transpose(ps[:, c, :], emb[:, c, :], core.ident[:])
            last.then_inc(turned, 1)

        @block.vector
        def _(dve):
            dve.wait_ge(loaded, 32)
            dve.tensor_tensor(sq[:], emb[:], emb[:], ALU.mult).then_inc(step, 1)
            dve.wait_ge(step, 1)
            dve.tensor_reduce(ss[:], sq[:], AX.X, ALU.add).then_inc(step, 1)
            dve.wait_ge(step, 2)
            dve.tensor_scalar(ss[:], ss[:], 1e-24, None, ALU.max).then_inc(safe, 1)
            dve.wait_ge(inv, 1)
            dve.tensor_tensor(emb[:], emb[:], ss[:].unsqueeze(2).to_broadcast([128, SC, D]), ALU.mult).then_inc(step, 1)
            dve.wait_ge(step, 3)
            dve.tensor_scalar(emb[:], emb[:], float(D) ** 0.5, None, ALU.mult).then_inc(step, 1)
            dve.wait_ge(step, 4)
            dve.tensor_tensor(emb[:], emb[:], gam[:].unsqueeze(1).to_broadcast([128, SC, D]), ALU.mult).then_inc(scaled, 1)

        @block.scalar
        def _(act):
            act.wait_ge(turned, 1)
            act.activation(snT[:], ps[:].rearrange("p c s -> p (c s)"), ACT.Copy).then_inc(done, 1)
            act.wait_ge(done, 1)
    s.close()


def dispatch_or_combine(core, name, snT, slots, SC, NS, *, combine):
    nc, I, X = core.nc, core.I, core.X
    s = Scope(nc, name)
    gam = s.sb("gam", [T, D])
    xs, sq, xn, xnT = s.lanes("xs", [T, D]), s.lanes("sq", [T, D]), s.lanes("xn", [T, D]), s.lanes("xnT", [D, T])
    ss = s.lanes("ss", [T, 1])
    rs = s.lanes("rs", [T, 1])
    mx, zz = s.lanes("mx", [128, SC]), s.lanes("zz", [128, SC])
    P = s.lanes("P", [128, SC, 128])
    PT = s.lanes("PT", [128, SC, 128])
    ps = [s.psum(f"ps{lane}", [128, 4, 512]) for lane in range(LANES)]
    r, st, mv, ve = s.lanes("r", [T, D]), s.lanes("st", [T, 6]), s.lanes("mv", [T, 2]), s.lanes("ve", [T, 1])
    eT, eo = (s.lanes("eT", [D, E, NS]), s.lanes("eo", [128, SC, D])) if combine else (None, None)
    names = ("gamma_in lane_free x_copied squared square_sum sum_safe inv_norm unit scaled x_normed x_psum xT_ready logits_psum "
             "max_ready shifted exp_ready sum_ready recip_ready weights_ready turned_psum turned_ready out_psum slots_copied "
             "eo_psum eo_ready out_scaled r_ready stats mean_var var_eps rstd")
    S_ = type("Ready", (), {n: s.sem(n) for n in names.split()})
    with nc.Block() as block:
        @block.sync
        def _(sp):
            sp.dma_start(gam[:], row_bc(I["L2_ffn_norm_gamma"])).then_inc(S_.gamma_in, 16)

        @block.gpsimd
        def _(pool):
            pool.sem_inc(S_.lane_free, LANES)
            with pool.Fori(0, STEPS) as i:
                for lane in range(LANES):
                    n = i * LANES + lane
                    at(pool, S_.lane_free, n)
                    pool.tensor_copy(xs[lane][:], X[:, bass.ds(n, 1), :].rearrange("t a d -> t (a d)")).then_inc(S_.x_copied, 1)
                    if combine:
                        pool.tensor_copy(eT[lane][:], slots[:, :, bass.ds(n, 1), :].rearrange("d e a s -> d e (a s)")).then_inc(S_.slots_copied, 1)
                for lane in range(LANES):
                    at(pool, S_.sum_safe, i * LANES + lane)
                    pool.tensor_tensor(rs[lane][:], ss[lane][:], core.neghalf[:, 0:1], ALU.pow).then_inc(S_.inv_norm, 1)
                if combine:
                    for lane in range(LANES):
                        at(pool, S_.var_eps, i * LANES + lane)
                        pool.tensor_tensor(rs[lane][:], ve[lane][:], core.neghalf[:, 0:1], ALU.pow).then_inc(S_.rstd, 1)

        @block.tensor
        def _(pe):
            with pe.Fori(0, STEPS) as i:
                for lane in range(LANES):
                    at(pe, S_.x_normed, i * LANES + lane)
                    pe.transpose(ps[lane][:, 0, 0:T], xn[lane][:], core.ident[:]).then_inc(S_.x_psum, 1)
                for lane in range(LANES):
                    at(pe, S_.xT_ready, i * LANES + lane)
                    if combine:
                        pe.matmul(ps[lane][:, 1, :], xnT[lane][:], snT[:], start=True, stop=True).then_inc(S_.logits_psum, 1)
                    else:
                        for c in range(SC):
                            last = pe.matmul(ps[lane][:, 1, c * T:(c + 1) * T], snT[:, c * 128:(c + 1) * 128], xnT[lane][:], start=True, stop=True)
                        last.then_inc(S_.logits_psum, 1)
                if combine:
                    for lane in range(LANES):
                        at(pe, S_.slots_copied, i * LANES + lane)
                        ef = eT[lane][:].rearrange("d e s -> d (e s)")
                        for c in range(SC):
                            last = pe.transpose(ps[lane][:, 3, c * D:(c + 1) * D], ef[:, c * 128:(c + 1) * 128], core.ident[:])
                        last.then_inc(S_.eo_psum, 1)
                for lane in range(LANES):
                    at(pe, S_.weights_ready, i * LANES + lane)
                    for c in range(SC):
                        last = pe.transpose(ps[lane][:, 2, c * 128:(c + 1) * 128], P[lane][:, c, :], core.ident[:])
                    last.then_inc(S_.turned_psum, 1)
                for lane in range(LANES):
                    n = i * LANES + lane
                    at(pe, S_.turned_ready, n)
                    if combine:
                        at(pe, S_.eo_ready, n)
                        for c in range(SC):
                            last = pe.matmul(ps[lane][:, 0, 0:D], PT[lane][:, c, :], eo[lane][:, c, :], start=c == 0, stop=c == SC - 1)
                        last.then_inc(S_.out_psum, 1)
                    else:
                        pe.matmul(ps[lane][:, 0, :], xn[lane][:], PT[lane][:].rearrange("t c s -> t (c s)"), start=True, stop=True).then_inc(S_.out_psum, 1)

        @block.scalar
        def _(act):
            with act.Fori(0, STEPS) as i:
                for lane in range(LANES):
                    at(act, S_.x_copied, i * LANES + lane)
                    act.activation(sq[lane][:], xs[lane][:], ACT.Square, accum_out=ss[lane][:]).then_inc(S_.square_sum, 1)
                for lane in range(LANES):
                    at(act, S_.x_psum, i * LANES + lane)
                    act.activation(xnT[lane][:], ps[lane][:, 0, 0:T], ACT.Copy).then_inc(S_.xT_ready, 1)
                if combine:
                    for lane in range(LANES):
                        at(act, S_.eo_psum, i * LANES + lane)
                        act.activation(eo[lane][:].rearrange("m c d -> m (c d)"), ps[lane][:, 3, :], ACT.Copy).then_inc(S_.eo_ready, 1)
                for lane in range(LANES):
                    at(act, S_.shifted, i * LANES + lane)
                    if combine:
                        act.activation(P[lane][:].rearrange("t c s -> t (c s)"), ps[lane][:, 1, :], ACT.Exp, bias=mx[lane][:, 0:1],
                                       accum_out=zz[lane][:, 0:1]).then_inc(S_.exp_ready, 1)
                    else:
                        act.activation(P[lane][:], P[lane][:], ACT.Exp).then_inc(S_.exp_ready, 1)
                for lane in range(LANES):
                    at(act, S_.turned_psum, i * LANES + lane)
                    act.activation(PT[lane][:].rearrange("t c s -> t (c s)"), ps[lane][:, 2, :], ACT.Copy).then_inc(S_.turned_ready, 1)

        @block.vector
        def _(dve):
            dve.wait_ge(S_.gamma_in, 16)
            with dve.Fori(0, STEPS) as i:
                for lane in range(LANES):
                    n = i * LANES + lane
                    at(dve, S_.square_sum, n)
                    dve.tensor_scalar(ss[lane][:], ss[lane][:], 1e-24, None, ALU.max).then_inc(S_.sum_safe, 1)
                for lane in range(LANES):
                    n = i * LANES + lane
                    at(dve, S_.inv_norm, n)
                    dve.tensor_scalar(xn[lane][:], xs[lane][:], rs[lane][:, 0:1], float(D) ** 0.5, ALU.mult, ALU.mult).then_inc(S_.unit, 1)
                    at(dve, S_.unit, n)
                    dve.tensor_tensor(xn[lane][:], xn[lane][:], gam[:], ALU.mult).then_inc(S_.x_normed, 1)
                for lane in range(LANES):
                    n = i * LANES + lane
                    at(dve, S_.logits_psum, n)
                    if combine:
                        dve.tensor_reduce(mx[lane][:, 1:2], ps[lane][:, 1, :], AX.X, ALU.max).then_inc(S_.max_ready, 1)
                        at(dve, S_.max_ready, n)
                        dve.tensor_scalar(mx[lane][:, 0:1], mx[lane][:, 1:2], -1.0, None, ALU.mult).then_inc(S_.shifted, 1)
                    else:
                        lt = ps[lane][:, 1, :].rearrange("m (c t) -> m c t", c=SC)
                        dve.tensor_reduce(mx[lane][:], lt, AX.X, ALU.max).then_inc(S_.max_ready, 1)
                        at(dve, S_.max_ready, n)
                        dve.tensor_tensor(P[lane][:], lt, mx[lane][:].unsqueeze(2).to_broadcast([128, SC, T]), ALU.subtract).then_inc(S_.shifted, 1)
                for lane in range(LANES):
                    n = i * LANES + lane
                    at(dve, S_.exp_ready, n)
                    if combine:
                        dve.reciprocal(zz[lane][:, 1:2], zz[lane][:, 0:1]).then_inc(S_.recip_ready, 1)
                        at(dve, S_.recip_ready, n)
                        dve.tensor_scalar(P[lane][:], P[lane][:], zz[lane][:, 1:2], None, ALU.mult).then_inc(S_.weights_ready, 1)
                    else:
                        dve.tensor_reduce(zz[lane][:], P[lane][:], AX.X, ALU.add).then_inc(S_.sum_ready, 1)
                        at(dve, S_.sum_ready, n)
                        dve.reciprocal(mx[lane][:], zz[lane][:]).then_inc(S_.recip_ready, 1)
                        at(dve, S_.recip_ready, n)
                        dve.tensor_tensor(P[lane][:], P[lane][:], mx[lane][:].unsqueeze(2).to_broadcast([128, SC, T]), ALU.mult).then_inc(S_.weights_ready, 1)
                for lane in range(LANES):
                    n = i * LANES + lane
                    at(dve, S_.out_psum, n)
                    if not combine:
                        dve.tensor_copy(slots[:, :, bass.ds(n, 1), :], ps[lane][:, 0, :].rearrange("d (e a s) -> d e a s", e=E, a=1)).then_inc(S_.lane_free, 1)
                        continue
                    dve.tensor_tensor(r[lane][:], ps[lane][:, 0, 0:D], xs[lane][:], ALU.add).then_inc(S_.r_ready, 1)
                    at(dve, S_.r_ready, n)
                    dve.bn_stats(st[lane][:], r[lane][:]).then_inc(S_.stats, 1)
                    at_alone(dve, S_.stats, n, s.passed)
                    dve.bn_aggr(mv[lane][:], st[lane][:]).then_inc(S_.mean_var, 1)
                    at(dve, S_.mean_var, n)
                    dve.tensor_scalar(ve[lane][:], mv[lane][:, 1:2], LN_EPS, None, ALU.add).then_inc(S_.var_eps, 1)
                if combine:
                    for lane in range(LANES):
                        n = i * LANES + lane
                        at(dve, S_.rstd, n)
                        dve.tensor_scalar(X[:, bass.ds(n, 1), :].rearrange("t a d -> t (a d)"), r[lane][:], mv[lane][:, 0:1],
                                          rs[lane][:, 0:1], ALU.subtract, ALU.mult).then_inc(S_.lane_free, 1)
    s.close()


def slot_pass(core, slots, NS):
    nc, I = core.nc, core.I
    s = Scope(nc, "slotpass")
    CW = 512
    N = B * NS // CW
    w1s, w2s, b1s, b2s = (s.lanes("w1", [D, F]), s.lanes("w2", [128, FC, D]), s.lanes("b1", [128, FC]), s.lanes("b2", [D, 1]))
    hT = s.lanes("hT", [128, FC, CW])
    ph = s.psum("ph", [128, FC, 512])
    py = s.psum("py", [128, 2, 512])
    w_in = [s.sem(f"weights_in{k}") for k in range(LANES)]
    h_psum, h_ready, y_psum, y_stored = [s.sem(n) for n in ("h_psum", "h_ready", "y_psum", "y_stored")]
    H0, Y0 = FC, 2
    S0 = 2 * N
    sf = slots[:].rearrange("d e b s -> d (e b s)")
    with nc.Block() as block:
        @block.sync
        def _(sp):
            with sp.Fori(0, E // LANES) as i:
                for lane in range(LANES):
                    e = i * LANES + lane
                    sp.wait_ge(y_stored, (e + 1) * N)
                    with nc.allow_non_contiguous_dma(reason="bias columns"):
                        sp.dma_start(w1s[lane][:], I["L2_ffn_w1"][bass.ds(e, 1)].rearrange("a d f -> d (a f)")).then_inc(w_in[lane], 16)
                        sp.dma_start(w2s[lane][:], I["L2_ffn_w2"][bass.ds(e, 1)].rearrange("a (c p) d -> p (a c) d", p=128)).then_inc(w_in[lane], 16)
                        sp.dma_start(b1s[lane][:], I["L2_ffn_b1"][bass.ds(e, 1)].rearrange("a (c p) -> p (a c)", p=128)).then_inc(w_in[lane], 16)
                        sp.dma_start(b2s[lane][:], I["L2_ffn_b2"][bass.ds(e, 1)].rearrange("a d -> d a")).then_inc(w_in[lane], 16)

        @block.tensor
        def _(pe):
            pe.sem_inc(y_psum, Y0)
            pe.sem_inc(h_ready, H0)
            with pe.Fori(0, E // LANES) as i:
                for lane in range(LANES):
                    e = i * LANES + lane
                    with pe.Fori(0, N // 2) as c2:
                        at(pe, w_in[lane], i, 64)
                        for par in range(2):
                            m = e * N + c2 * 2 + par
                            for f in range(FC):
                                pe.wait_ge(h_ready, m * FC + f + 1)
                                pe.matmul(ph[:, f, :], w1s[lane][:, f * 128:(f + 1) * 128], sf[:, bass.ds(m * CW, CW)],
                                          start=True, stop=True).then_inc(h_psum, 1)
                        for par in range(2):
                            m = e * N + c2 * 2 + par
                            pe.wait_ge(h_ready, m * FC + FC + H0)
                            pe.wait_ge(y_stored, m - 1 + S0)
                            for f in range(FC):
                                last = pe.matmul(py[:, par, :], w2s[lane][:, f, :], hT[par][:, f, :], start=f == 0, stop=f == FC - 1)
                            last.then_inc(y_psum, 1)

        @block.scalar
        def _(act):
            with act.Fori(0, E // LANES) as i:
                for lane in range(LANES):
                    e = i * LANES + lane
                    with act.Fori(0, N // 2) as c2:
                        at(act, w_in[lane], i, 64)
                        for par in range(2):
                            m = e * N + c2 * 2 + par
                            act.wait_ge(y_psum, m - 1 + Y0)
                            for f in range(FC):
                                act.wait_ge(h_psum, m * FC + f + 1)
                                act.activation(hT[par][:, f, :], ph[:, f, :], ACT.Gelu, bias=b1s[lane][:, f:f + 1]).then_inc(h_ready, 1)

        @block.vector
        def _(dve):
            dve.sem_inc(y_stored, S0)
            with dve.Fori(0, E // LANES) as i:
                for lane in range(LANES):
                    e = i * LANES + lane
                    with dve.Fori(0, N // 2) as c2:
                        at(dve, w_in[lane], i, 64)
                        for par in range(2):
                            m = e * N + c2 * 2 + par
                            dve.wait_ge(y_psum, m + 1 + Y0)
                            dve.tensor_scalar(sf[:, bass.ds(m * CW, CW)], py[:, par, :], b2s[lane][:, 0:1], None, ALU.add).then_inc(y_stored, 1)
    s.close()


def text_vision(core):
    nc = core.nc
    with ExitStack() as stack:
        Y = stack.enter_context(nc.sbuf_tensor("Y", [T, B, D], F32))
        FO = stack.enter_context(nc.sbuf_tensor("FO", [T, B, 2 * D], F32))
        kernel_dram = nc.dram_tensor("s4d_kernel", (D, 2 * T), F32, kind="Internal").ap()
        topk_film(core, Y, FO)
        s4d_kernel(core, kernel_dram)
        s4d_convolve(core, Y, kernel_dram)
        film_ffn(core, Y, FO)


def topk_film(core, Y, FO):
    nc, I, X = core.nc, core.I, core.X
    s = Scope(nc, "topk")
    H, Dh, TOP = 4, 32, 32
    ROUNDS = TOP // 8
    scale = 1.0 / float(np.sqrt(Dh).astype(np.float32))
    TAKEN = -3e38
    loads = []

    def tile(tag, shape, src, dtype=F32):
        t = s.sb(tag, shape, dtype)
        loads.append((t[:], src))
        return t

    wq = tile("wq", [D, D], I["L0_xattn_Wq"])
    wk, wv = tile("wk", [DC, D], I["L0_xattn_Wk"]), tile("wv", [DC, D], I["L0_xattn_Wv"])
    gam, bet = tile("gam", [T, D], row_bc(I["L0_xattn_g_norm_in"])), tile("bet", [T, D], row_bc(I["L0_xattn_b_norm_in"]))
    mg = tile("mg", [T, 1], row_bc(I["L0_xattn_mod_gate"]))
    wf, bf = s.sb("wf", [D, 4 * D]), s.sb("bf", [T, 4 * D])
    for j, side in enumerate(("in", "out")):
        loads.append((wf[:, 2 * D * j:2 * D * (j + 1)], I[f"L0_xattn_W_film_{side}"]))
        loads.append((bf[:, 2 * D * j:2 * D * (j + 1)], row_bc(I[f"L0_xattn_b_film_{side}"])))
    tm8 = tile("tm8", [T, B], I["text_mask_T"], U8)
    tmask = s.sb("tmask", [T, B])
    xs, xn, xT, cs = s.lanes("xs", [T, D]), s.lanes("xn", [T, D]), s.lanes("xT", [D, T]), s.lanes("cs", [DC, TC])
    vm8, vbias, tm = s.lanes("vm8", [T, TC], U8), s.lanes("vbias", [T, TC]), s.lanes("tm", [T, 1])
    qT, kT, V = s.lanes("qT", [D, T]), s.lanes("kT", [D, TC]), s.lanes("V", [TC, D])
    S, W, P = s.lanes("S", [T, H, TC]), s.lanes("W", [T, H, TC]), s.lanes("P", [T, H, TC])
    m8 = s.lanes("m8", [T, ROUNDS, H, 8])
    sm, rz = s.lanes("sm", [T, H]), s.lanes("rz", [T, H])
    am, aT, cT = s.lanes("am", [T, TC]), s.lanes("aT", [TC, T]), s.lanes("cT", [D, T])
    film, yo = s.lanes("film", [T, 4 * D]), s.lanes("yo", [T, D])
    st, mv, ve, rs = s.lanes("st", [T, 6]), s.lanes("mv", [T, 2]), s.lanes("ve", [T, 1]), s.lanes("rs", [T, 1])
    ps = [s.psum(f"ps{lane}", [128, 4, 512]) for lane in range(LANES)]
    names = ("weights_in lane_free x_copied tm_copied x_psum xT_ready qkv_psum qk_ready v_ready bias_ready scores_psum scores_ready "
             "round_sorted round_taken shifted exp_ready kept sum_ready recip_ready recip_scaled weighted attn_ready attnT_psum attnT_ready "
             "c_psum c_ready film_psum film_biased film_gated scale_ready stats mean_var var_eps rstd normed scaled offset "
             "modulated tmask_ready work_ready out_stored")
    S_ = type("Ready", (), {n: s.sem(n) for n in names.split()})
    ctx_in = [s.sem(f"ctx_in{k}") for k in range(LANES)]
    with nc.Block() as block:
        @block.sync
        def _(sp):
            with nc.allow_non_contiguous_dma(reason="small weights, once"):
                for dst, src in loads:
                    sp.dma_start(dst, src).then_inc(S_.weights_in, 16)
            with sp.Fori(0, STEPS) as i:
                for lane in range(LANES):
                    n = i * LANES + lane
                    at(sp, S_.lane_free, n)
                    sp.dma_start(cs[lane][:], I["ctxT"][:, bass.ds(n * TC, TC)]).then_inc(ctx_in[lane], 16)
                    sp.dma_start(vm8[lane][:], I["mask_BxS2_bf1"][bass.ds(n, 1), :].to_broadcast([T, TC])).then_inc(ctx_in[lane], 16)

        @block.gpsimd
        def _(pool):
            pool.wait_ge(S_.weights_in, 16 * len(loads))
            pool.tensor_copy(tmask[:], tm8[:]).then_inc(S_.tmask_ready, 1)
            pool.wait_ge(S_.tmask_ready, 1)
            pool.sem_inc(S_.lane_free, LANES)
            with pool.Fori(0, STEPS) as i:
                for lane in range(LANES):
                    n = i * LANES + lane
                    at(pool, S_.lane_free, n)
                    pool.tensor_copy(xs[lane][:], X[:, bass.ds(n, 1), :].rearrange("t a d -> t (a d)")).then_inc(S_.x_copied, 1)
                    pool.tensor_copy(tm[lane][:], tmask[:, bass.ds(n, 1)]).then_inc(S_.tm_copied, 1)
                for lane in range(LANES):
                    at(pool, S_.var_eps, i * LANES + lane)
                    pool.tensor_tensor(rs[lane][:], ve[lane][:], core.neghalf[:, 0:1], ALU.pow).then_inc(S_.rstd, 1)

        @block.tensor
        def _(pe):
            pe.wait_ge(S_.weights_in, 16 * len(loads))
            with pe.Fori(0, STEPS) as i:
                for lane in range(LANES):
                    at(pe, S_.x_copied, i * LANES + lane)
                    pe.transpose(ps[lane][:, 0, 0:T], xs[lane][:], core.ident[:]).then_inc(S_.x_psum, 1)
                for lane in range(LANES):
                    at(pe, ctx_in[lane], i, 32)
                    at(pe, S_.xT_ready, i * LANES + lane)
                    pe.matmul(ps[lane][:, 1, 0:T], wq[:], xT[lane][:], start=True, stop=True)
                    pe.matmul(ps[lane][:, 1, T:T + TC], wk[:], cs[lane][:], start=True, stop=True)
                    pe.matmul(ps[lane][0:TC, 2, 0:D], cs[lane][:], wv[:], start=True, stop=True).then_inc(S_.qkv_psum, 1)
                for lane in range(LANES):
                    n = i * LANES + lane
                    at(pe, S_.v_ready, n)
                    at(pe, S_.qk_ready, n, 2)
                    for h in range(H):
                        rows = slice(h * Dh, (h + 1) * Dh)
                        last = pe.matmul(ps[lane][:, h, 0:TC], qT[lane][rows, :], kT[lane][rows, :], start=True, stop=True)
                    last.then_inc(S_.scores_psum, 1)
                for lane in range(LANES):
                    at(pe, S_.attn_ready, i * LANES + lane)
                    pe.transpose(ps[lane][0:TC, 0, 0:T], am[lane][:], core.ident[:]).then_inc(S_.attnT_psum, 1)
                for lane in range(LANES):
                    at(pe, S_.attnT_ready, i * LANES + lane)
                    pe.matmul(ps[lane][:, 1, 0:T], V[lane][:], aT[lane][:], start=True, stop=True).then_inc(S_.c_psum, 1)
                for lane in range(LANES):
                    at(pe, S_.c_ready, i * LANES + lane)
                    pe.matmul(ps[lane][:, 2, :], cT[lane][:], wf[:], start=True, stop=True).then_inc(S_.film_psum, 1)

        @block.scalar
        def _(act):
            with act.Fori(0, STEPS) as i:
                for lane in range(LANES):
                    at(act, S_.x_psum, i * LANES + lane)
                    act.activation(xT[lane][:], ps[lane][:, 0, 0:T], ACT.Copy).then_inc(S_.xT_ready, 1)
                for lane in range(LANES):
                    at(act, S_.qkv_psum, i * LANES + lane)
                    act.activation(qT[lane][:], ps[lane][:, 1, 0:T], ACT.Copy).then_inc(S_.qk_ready, 1)
                    act.activation(kT[lane][:], ps[lane][:, 1, T:T + TC], ACT.Copy).then_inc(S_.qk_ready, 1)
                    act.activation(V[lane][:], ps[lane][0:TC, 2, 0:D], ACT.Copy).then_inc(S_.v_ready, 1)
                for lane in range(LANES):
                    at(act, S_.shifted, i * LANES + lane)
                    act.activation(P[lane][:], P[lane][:], ACT.Exp, scale=scale).then_inc(S_.exp_ready, 1)
                for lane in range(LANES):
                    at(act, S_.attnT_psum, i * LANES + lane)
                    act.activation(aT[lane][:], ps[lane][0:TC, 0, 0:T], ACT.Copy).then_inc(S_.attnT_ready, 1)
                for lane in range(LANES):
                    at(act, S_.c_psum, i * LANES + lane)
                    act.activation(cT[lane][:], ps[lane][:, 1, 0:T], ACT.Copy).then_inc(S_.c_ready, 1)

        @block.vector
        def _(dve):
            dve.wait_ge(S_.weights_in, 16 * len(loads))
            with dve.Fori(0, STEPS) as i:
                for lane in range(LANES):
                    n = i * LANES + lane
                    at(dve, ctx_in[lane], i, 32)
                    dve.tensor_scalar(vbias[lane][:], vm8[lane][:], -NEG, NEG, ALU.mult, ALU.add).then_inc(S_.bias_ready, 1)
                    at(dve, S_.x_copied, n)
                    dve.bn_stats(st[lane][:], xs[lane][:]).then_inc(S_.stats, 1)
                    at_alone(dve, S_.stats, n, s.passed)
                    dve.bn_aggr(mv[lane][:], st[lane][:]).then_inc(S_.mean_var, 1)
                    at(dve, S_.mean_var, n)
                    dve.tensor_scalar(ve[lane][:], mv[lane][:, 1:2], LN_EPS, None, ALU.add).then_inc(S_.var_eps, 1)
                for lane in range(LANES):
                    n = i * LANES + lane
                    at(dve, S_.rstd, n)
                    dve.tensor_scalar(xn[lane][:], xs[lane][:], mv[lane][:, 0:1], rs[lane][:, 0:1], ALU.subtract, ALU.mult).then_inc(S_.normed, 1)
                    at(dve, S_.normed, n)
                    dve.tensor_tensor(xn[lane][:], xn[lane][:], gam[:], ALU.mult).then_inc(S_.scaled, 1)
                    at(dve, S_.scaled, n)
                    dve.tensor_tensor(xn[lane][:], xn[lane][:], bet[:], ALU.add).then_inc(S_.offset, 1)
                for lane in range(LANES):
                    n = i * LANES + lane
                    at(dve, S_.scores_psum, n)
                    at(dve, S_.bias_ready, n)
                    dve.tensor_tensor(S[lane][:], ps[lane][:, :, 0:TC], vbias[lane][:].unsqueeze(1).to_broadcast([T, H, TC]), ALU.add).then_inc(S_.scores_ready, 1)
                    at(dve, S_.scores_ready, n)
                    dve.tensor_copy(W[lane][:], S[lane][:]).then_inc(S_.work_ready, 1)
                    at_alone(dve, S_.work_ready, n, s.passed)
                    for q in range(ROUNDS):
                        if q:
                            at_alone(dve, S_.round_taken, n * (ROUNDS * H) + q * H - 1, s.passed)
                        for h in range(H):
                            dve.max(m8[lane][:, q, h, :], W[lane][:, h, :]).then_inc(S_.round_sorted, 1)
                        at_alone(dve, S_.round_sorted, n * (ROUNDS * H) + (q + 1) * H - 1, s.passed)
                        for h in range(H):
                            dve.match_replace(W[lane][:, h, :], m8[lane][:, q, h, :], W[lane][:, h, :], TAKEN).then_inc(S_.round_taken, 1)
                    dve.tensor_tensor(P[lane][:], S[lane][:], m8[lane][:, 0, :, 0:1].to_broadcast([T, H, TC]), ALU.subtract).then_inc(S_.shifted, 1)
                for lane in range(LANES):
                    n = i * LANES + lane
                    at(dve, S_.exp_ready, n)
                    at(dve, S_.round_taken, (n + 1) * (ROUNDS * H) - 1)
                    dve.scalar_tensor_tensor(out=P[lane][:], in0=W[lane][:], scalar=-2e38, in1=P[lane][:], op0=ALU.is_lt, op1=ALU.mult).then_inc(S_.kept, 1)
                    at(dve, S_.kept, n)
                    dve.tensor_reduce(sm[lane][:], P[lane][:], AX.X, ALU.add).then_inc(S_.sum_ready, 1)
                    at(dve, S_.sum_ready, n)
                    dve.reciprocal(rz[lane][:], sm[lane][:]).then_inc(S_.recip_ready, 1)
                    at(dve, S_.recip_ready, n)
                    dve.tensor_scalar(rz[lane][:], rz[lane][:], 1.0 / H, None, ALU.mult).then_inc(S_.recip_scaled, 1)
                    at(dve, S_.recip_scaled, n)
                    dve.tensor_tensor(P[lane][:], P[lane][:], rz[lane][:].unsqueeze(2).to_broadcast([T, H, TC]), ALU.mult).then_inc(S_.weighted, 1)
                    at(dve, S_.weighted, n)
                    dve.tensor_reduce(am[lane][:], P[lane][:].rearrange("t h k -> t k h"), AX.X, ALU.add).then_inc(S_.attn_ready, 1)
                for lane in range(LANES):
                    n = i * LANES + lane
                    at(dve, S_.film_psum, n)
                    at(dve, S_.tm_copied, n)
                    dve.scalar_tensor_tensor(out=film[lane][:], in0=ps[lane][:, 2, :], scalar=tm[lane][:, 0:1], in1=bf[:], op0=ALU.mult, op1=ALU.add).then_inc(S_.film_biased, 1)
                    at(dve, S_.film_biased, n)
                    dve.tensor_scalar(film[lane][:], film[lane][:], mg[:, 0:1], None, ALU.mult).then_inc(S_.film_gated, 1)
                    at(dve, S_.film_gated, n)
                    f4 = film[lane][:].rearrange("t (a b d) -> t a b d", a=2, b=2)
                    dve.tensor_scalar(f4[:, :, 0, :], f4[:, :, 0, :], 1.0, None, ALU.add).then_inc(S_.scale_ready, 1)
                    at(dve, S_.scale_ready, n)
                    at(dve, S_.offset, n)
                    dve.tensor_tensor(yo[lane][:], xn[lane][:], film[lane][:, 0:D], ALU.mult).then_inc(S_.modulated, 1)
                    dve.tensor_copy(FO[:, bass.ds(n, 1), :].rearrange("t a d -> t (a d)"), film[lane][:, 2 * D:4 * D]).then_inc(S_.out_stored, 1)
                    at(dve, S_.modulated, n)
                    dve.tensor_tensor(Y[:, bass.ds(n, 1), :].rearrange("t a d -> t (a d)"), yo[lane][:], film[lane][:, D:2 * D], ALU.add).then_inc(S_.lane_free, 1)
    s.close()


def s4d_kernel(core, kernel_dram):
    nc, I = core.nc, core.I
    s = Scope(nc, "s4d")
    NSt = I["L0_xattn_A_re"].shape[1]
    NA_, NB_ = 8, 16
    TWO_PI = (6.28125, 1.9350051879882812e-3, 3.0199159795e-7)
    ROUND = 1.5 * 2.0 ** 23
    PI = 3.1415925
    Are, Aim, Cre, Cim = (s.sb(n, [D, NSt]) for n in ("Are", "Aim", "Cre", "Cim"))
    ldt, dt, skip = s.sb("ldt", [D, 1]), s.sb("dt", [D, 1]), s.sb("skip", [D, 1])
    mag, ang, turn, snh, sn_, cs_ = (s.sb(n, [D, NSt]) for n in ("mag", "ang", "turn", "snh", "sin", "cos"))
    U = s.sb("U", [D, 2, NSt, NA_])
    V = s.sb("V", [D, 2, NSt, NB_])
    w = s.sb("w", [D, 7, 2, NSt])
    dC, den = s.sb("dC", [D, 2, NSt]), s.sb("den", [D, NSt])
    ta, tb = s.sb("ta", [D, NSt, 8]), s.sb("tb", [D, NSt, 8])
    zm, cz = s.sb("zm", [D, 2, NSt]), s.sb("cz", [D, 2, NSt])
    prod = s.sb("prod", [D, 2, NSt, NB_])
    K, Kp = s.sb("K", [D, T]), s.sb("Kp", [D, 2 * T])
    loaded, step, dt_ready, angle_ready, sines_ready, padded, kernel_ready, stored = [
        s.sem(n) for n in ("loaded", "step", "dt_ready", "angle_ready", "sines_ready", "padded", "kernel_ready", "stored")]
    with nc.Block() as block:
        @block.sync
        def _(sp):
            loads = [(Are, "A_re"), (Aim, "A_im"), (Cre, "C_re"), (Cim, "C_im")]
            for t, key in loads:
                sp.dma_start(t[:], I[f"L0_xattn_{key}"]).then_inc(loaded, 16)
            with nc.allow_non_contiguous_dma(reason="two columns"):
                sp.dma_start(ldt[:], col(I["L0_xattn_log_dt"])).then_inc(loaded, 16)
                sp.dma_start(skip[:], col(I["L0_xattn_D_skip"])).then_inc(loaded, 16)
            sp.wait_ge(kernel_ready, 1)
            sp.wait_ge(padded, 1)
            sp.dma_start(kernel_dram, Kp[:]).then_inc(stored, 16)
            sp.wait_ge(stored, 16)

        @block.gpsimd
        def _(pool):
            pool.memset(Kp[:], 0.0).then_inc(padded, 1)

        @block.scalar
        def _(act):
            act.wait_ge(loaded, 96)
            act.activation(dt[:], ldt[:], ACT.Exp).then_inc(dt_ready, 1)
            act.wait_ge(dt_ready, 1)
            act.activation(mag[:], Are[:], ACT.Exp, scale=dt[:, 0:1]).then_inc(dt_ready, 1)
            act.wait_ge(angle_ready, 1)
            act.activation(sn_[:], ang[:], ACT.Sin).then_inc(sines_ready, 1)
            act.activation(snh[:], ang[:], ACT.Sin, scale=0.5).then_inc(sines_ready, 1)

        @block.vector
        def _(dve):
            links = [0]

            def link(ins):
                links[0] += 1
                ins.then_inc(step, 1)
                dve.wait_ge(step, links[0])

            def product(out, a, b, shape):
                n, m = shape
                x, y = ta[:, :, 0:m], tb[:, :, 0:m]
                for k, (p, q, op) in enumerate((((0, 0), (1, 1), ALU.subtract), ((0, 1), (1, 0), ALU.add))):
                    link(dve.tensor_tensor(x, a[p[0]], b[p[1]], ALU.mult))
                    link(dve.tensor_tensor(y, a[q[0]], b[q[1]], ALU.mult))
                    link(dve.tensor_tensor(out[k], x, y, op))

            def pair(t):
                return t[:, 0, :].unsqueeze(2), t[:, 1, :].unsqueeze(2)

            def wide(t, m):
                return tuple(v.to_broadcast([D, NSt, m]) for v in pair(t))

            dve.wait_ge(loaded, 96)
            dve.wait_ge(dt_ready, 2)
            link(dve.tensor_scalar(ang[:], Aim[:], dt[:, 0:1], None, ALU.mult))
            link(dve.tensor_scalar(turn[:], ang[:], float(1.0 / (2.0 * np.pi)), None, ALU.mult))
            link(dve.tensor_scalar(turn[:], turn[:], ROUND, None, ALU.add))
            link(dve.tensor_scalar(turn[:], turn[:], -ROUND, None, ALU.add))
            for part in TWO_PI:
                link(dve.scalar_tensor_tensor(out=ang[:], in0=turn[:], scalar=-part, in1=ang[:], op0=ALU.mult, op1=ALU.add))
            link(dve.tensor_scalar(ang[:], ang[:], PI, None, ALU.min))
            dve.tensor_scalar(ang[:], ang[:], -PI, None, ALU.max).then_inc(angle_ready, 1)
            dve.wait_ge(sines_ready, 2)
            link(dve.tensor_tensor(cs_[:], snh[:], snh[:], ALU.mult))
            link(dve.tensor_scalar(cs_[:], cs_[:], -2.0, 1.0, ALU.mult, ALU.add))
            link(dve.tensor_tensor(w[:, 0, 0, :], mag[:], cs_[:], ALU.mult))
            link(dve.tensor_tensor(w[:, 0, 1, :], mag[:], sn_[:], ALU.mult))
            for k in range(6):
                product(pair(w[:, k + 1]), pair(w[:, k]), pair(w[:, k]), (NSt, 1))
            link(dve.tensor_scalar(zm[:, 0, :], w[:, 0, 0, :], -1.0, None, ALU.add))
            link(dve.tensor_copy(zm[:, 1, :], w[:, 0, 1, :]))
            product(pair(cz), (Cre[:].unsqueeze(2), Cim[:].unsqueeze(2)), pair(zm), (NSt, 1))
            link(dve.tensor_tensor(den[:], Are[:], Are[:], ALU.mult))
            link(dve.tensor_tensor(snh[:], Aim[:], Aim[:], ALU.mult))
            link(dve.tensor_tensor(den[:], den[:], snh[:], ALU.add))
            link(dve.reciprocal(den[:], den[:]))
            link(dve.tensor_scalar(turn[:], Aim[:], -1.0, None, ALU.mult))
            product(pair(dC), pair(cz), (Are[:].unsqueeze(2), turn[:].unsqueeze(2)), (NSt, 1))
            for k in range(2):
                link(dve.scalar_tensor_tensor(out=U[:, k, :, 0], in0=dC[:, k, :], scalar=2.0, in1=den[:], op0=ALU.mult, op1=ALU.mult))
            for j in range(3):
                m = 1 << j
                product((U[:, 0, :, m:2 * m], U[:, 1, :, m:2 * m]), (U[:, 0, :, 0:m], U[:, 1, :, 0:m]), wide(w[:, 4 + j], m), (NSt, m))
            link(dve.memset(V[:, 0, :, 0:1], 1.0))
            link(dve.memset(V[:, 1, :, 0:1], 0.0))
            for j in range(4):
                m = 1 << j
                product((V[:, 0, :, m:2 * m], V[:, 1, :, m:2 * m]), (V[:, 0, :, 0:m], V[:, 1, :, 0:m]), wide(w[:, j], m), (NSt, m))
            link(dve.tensor_scalar(V[:, 1], V[:, 1], -1.0, None, ALU.mult))
            for a in range(NA_):
                link(dve.tensor_tensor(prod[:], V[:], U[:, :, :, a:a + 1].to_broadcast([D, 2, NSt, NB_]), ALU.mult))
                link(dve.tensor_reduce(K[:, a * NB_:(a + 1) * NB_], prod[:].rearrange("d c n b -> d b (c n)"), AX.X, ALU.add))
            link(dve.tensor_tensor(K[:, 0:1], K[:, 0:1], skip[:], ALU.add))
            dve.wait_ge(padded, 1)
            dve.tensor_copy(Kp[:, 0:T], K[:, ::-1]).then_inc(kernel_ready, 1)
    s.close()


def s4d_convolve(core, Y, kernel_dram):
    nc = core.nc
    s = Scope(nc, "conv")
    CH = 16
    N = D // CH
    tz = s.lanes("toeplitz", [T, CH, T])
    ps = [s.psum(f"ps{k}", [T, CH, B]) for k in range(LANES)]
    toeplitz_in = [s.sem(f"toeplitz_in{k}") for k in range(LANES)]
    y_psum, y_stored = s.sem("y_psum"), s.sem("y_stored")
    Yd = Y[:].rearrange("t b d -> t d b")
    with nc.Block() as block:
        @block.sync
        def _(sp):
            for c in range(N):
                lane = c % LANES
                if c >= LANES:
                    sp.wait_ge(y_psum, c - LANES + 1)
                base = kernel_dram[c * CH:(c + 1) * CH, :]
                src = bass.AP(base.tensor, c * CH * 2 * T, [[1, T], [2 * T, CH], [1, T]])
                sp.dma_start(tz[lane][:], src).then_inc(toeplitz_in[lane], 16)

        @block.tensor
        def _(pe):
            for c in range(N):
                lane = c % LANES
                pe.wait_ge(toeplitz_in[lane], 16 * (c // LANES + 1))
                if c >= LANES:
                    pe.wait_ge(y_stored, c - LANES + 1)
                for k in range(CH):
                    last = pe.matmul(ps[lane][:, k, :], tz[lane][:, k, :], Yd[:, c * CH + k, :], start=True, stop=True)
                last.then_inc(y_psum, 1)

        @block.vector
        def _(dve):
            for c in range(N):
                dve.wait_ge(y_psum, c + 1)
                dve.tensor_copy(Yd[:, c * CH:(c + 1) * CH, :], ps[c % LANES][:]).then_inc(y_stored, 1)
    s.close()


def film_ffn(core, Y, FO):
    nc, I, X = core.nc, core.I, core.X
    s = Scope(nc, "filmffn")
    loads = []

    def tile(tag, shape, src):
        t = s.sb(tag, shape)
        loads.append((t[:], src))
        return t

    p = "L0_xattn_"
    w1, w2 = tile("w1", [D, F], I[p + "W1"]), tile("w2", [128, FC, D], I[p + "W2"].rearrange("(c p) d -> p c d", p=128))
    b1, b2 = tile("b1", [128, FC], I[p + "b1"].rearrange("(c p) -> p c", p=128)), tile("b2", [T, D], row_bc(I[p + "b2"]))
    gf, bf = tile("gf", [T, D], row_bc(I[p + "g_ffn"])), tile("bf", [T, D], row_bc(I[p + "b_ffn"]))
    go, bo = tile("go", [T, D], row_bc(I[p + "g_norm_out"])), tile("bo", [T, D], row_bc(I[p + "b_norm_out"]))
    xs, ys, fo = s.lanes("xs", [T, D]), s.lanes("ys", [T, D]), s.lanes("fo", [T, 2 * D])
    xt, xn, xT, hT = s.lanes("xt", [T, D]), s.lanes("xn", [T, D]), s.lanes("xT", [D, T]), s.lanes("hT", [128, FC, T])
    st, mv, ve, rs = s.lanes("st", [T, 6]), s.lanes("mv", [T, 2]), s.lanes("ve", [T, 1]), s.lanes("rs", [T, 1])
    ps = [s.psum(f"ps{lane}", [128, 4, 512]) for lane in range(LANES)]
    names = ("weights_in lane_free copied turned modulated shifted xt_ready n_psum nT_ready h_psum h_ready y_psum y_biased xt2_ready sum_ready"
             + "".join(f" stats{k} mean_var{k} var_eps{k} rstd{k} normed{k} scaled{k} offset{k}" for k in range(3)))
    sems = {n: s.sem(n) for n in names.split()}
    S_ = type("Ready", (), sems)
    stats, mean_var, var_eps, rstd, normed, scaled, offset = (
        [sems[f"{n}{k}"] for k in range(3)] for n in ("stats", "mean_var", "var_eps", "rstd", "normed", "scaled", "offset"))
    with nc.Block() as block:
        @block.sync
        def _(sp):
            with nc.allow_non_contiguous_dma(reason="small weights, once"):
                for dst, src in loads:
                    sp.dma_start(dst, src).then_inc(S_.weights_in, 16)

        @block.gpsimd
        def _(pool):
            pool.sem_inc(S_.lane_free, LANES)
            with pool.Fori(0, STEPS) as i:
                for lane in range(LANES):
                    n = i * LANES + lane
                    at(pool, S_.lane_free, n)
                    for dst, src in ((xs, X), (fo, FO)):
                        pool.tensor_copy(dst[lane][:], src[:, bass.ds(n, 1), :].rearrange("t a d -> t (a d)")).then_inc(S_.copied, 1)
                for k in range(3):
                    for lane in range(LANES):
                        at(pool, var_eps[k], i * LANES + lane)
                        pool.tensor_tensor(rs[lane][:], ve[lane][:], core.neghalf[:, 0:1], ALU.pow).then_inc(rstd[k], 1)

        @block.tensor
        def _(pe):
            pe.wait_ge(S_.weights_in, 16 * len(loads))
            with pe.Fori(0, STEPS) as i:
                for lane in range(LANES):
                    n = i * LANES + lane
                    at(pe, S_.copied, n, 2)
                    pe.matmul(ps[lane][:, 3, 0:D], core.anti[:], Y[:, bass.ds(n, 1), :].rearrange("t a d -> t (a d)"), start=True, stop=True).then_inc(S_.turned, 1)
                for lane in range(LANES):
                    at(pe, offset[0], i * LANES + lane)
                    pe.transpose(ps[lane][:, 0, 0:T], xn[lane][:], core.ident[:]).then_inc(S_.n_psum, 1)
                for lane in range(LANES):
                    at(pe, S_.nT_ready, i * LANES + lane)
                    for f in range(FC):
                        last = pe.matmul(ps[lane][:, 1, f * T:(f + 1) * T], w1[:, f * 128:(f + 1) * 128], xT[lane][:], start=True, stop=True)
                    last.then_inc(S_.h_psum, 1)
                for lane in range(LANES):
                    at(pe, S_.h_ready, i * LANES + lane, FC)
                    for f in range(FC):
                        last = pe.matmul(ps[lane][:, 2, 0:D], hT[lane][:, f, :], w2[:, f, :], start=f == 0, stop=f == FC - 1)
                    last.then_inc(S_.y_psum, 1)

        @block.scalar
        def _(act):
            act.wait_ge(S_.weights_in, 16 * len(loads))
            with act.Fori(0, STEPS) as i:
                for lane in range(LANES):
                    at(act, S_.n_psum, i * LANES + lane)
                    act.activation(xT[lane][:], ps[lane][:, 0, 0:T], ACT.Copy).then_inc(S_.nT_ready, 1)
                for lane in range(LANES):
                    at(act, S_.h_psum, i * LANES + lane)
                    for f in range(FC):
                        act.activation(hT[lane][:, f, :], ps[lane][:, 1, f * T:(f + 1) * T], ACT.Gelu, bias=b1[:, f:f + 1]).then_inc(S_.h_ready, 1)

        @block.vector
        def _(dve):
            dve.wait_ge(S_.weights_in, 16 * len(loads))

            def norm_stats(src, n, lane, k):
                dve.bn_stats(st[lane][:], src).then_inc(stats[k], 1)
                at_alone(dve, stats[k], n, s.passed)
                dve.bn_aggr(mv[lane][:], st[lane][:]).then_inc(mean_var[k], 1)
                at(dve, mean_var[k], n)
                dve.tensor_scalar(ve[lane][:], mv[lane][:, 1:2], LN_EPS, None, ALU.add).then_inc(var_eps[k], 1)

            def norm_apply(dst, src, n, lane, k):
                at(dve, rstd[k], n)
                return dve.tensor_scalar(dst, src, mv[lane][:, 0:1], rs[lane][:, 0:1], ALU.subtract, ALU.mult)

            def affine(n, lane, k, g, b):
                at(dve, normed[k], n)
                dve.tensor_tensor(xn[lane][:], xn[lane][:], g[:], ALU.mult).then_inc(scaled[k], 1)
                at(dve, scaled[k], n)
                dve.tensor_tensor(xn[lane][:], xn[lane][:], b[:], ALU.add).then_inc(offset[k], 1)

            with dve.Fori(0, STEPS) as i:
                for lane in range(LANES):
                    n = i * LANES + lane
                    at(dve, S_.copied, n, 2)
                    at(dve, S_.turned, n)
                    dve.tensor_tensor(xt[lane][:], ps[lane][:, 3, 0:D], fo[lane][:, 0:D], ALU.mult).then_inc(S_.modulated, 1)
                    at(dve, S_.modulated, n)
                    dve.tensor_tensor(xt[lane][:], xt[lane][:], fo[lane][:, D:2 * D], ALU.add).then_inc(S_.shifted, 1)
                    at(dve, S_.shifted, n)
                    dve.tensor_tensor(xt[lane][:], xt[lane][:], xs[lane][:], ALU.add).then_inc(S_.xt_ready, 1)
                    at(dve, S_.xt_ready, n)
                    norm_stats(xt[lane][:], n, lane, 0)
                for lane in range(LANES):
                    n = i * LANES + lane
                    norm_apply(xn[lane][:], xt[lane][:], n, lane, 0).then_inc(normed[0], 1)
                    affine(n, lane, 0, gf, bf)
                for lane in range(LANES):
                    n = i * LANES + lane
                    at(dve, S_.y_psum, n)
                    dve.tensor_tensor(ys[lane][:], ps[lane][:, 2, 0:D], b2[:], ALU.add).then_inc(S_.y_biased, 1)
                    at(dve, S_.y_biased, n)
                    dve.tensor_tensor(xt[lane][:], xt[lane][:], ys[lane][:], ALU.add).then_inc(S_.xt2_ready, 1)
                    at(dve, S_.xt2_ready, n)
                    norm_stats(xt[lane][:], n, lane, 1)
                for lane in range(LANES):
                    n = i * LANES + lane
                    norm_apply(xn[lane][:], xt[lane][:], n, lane, 1).then_inc(normed[1], 1)
                    affine(n, lane, 1, go, bo)
                    at(dve, offset[1], n)
                    dve.tensor_tensor(xt[lane][:], xn[lane][:], xs[lane][:], ALU.add).then_inc(S_.sum_ready, 1)
                    at(dve, S_.sum_ready, n)
                    norm_stats(xt[lane][:], n, lane, 2)
                for lane in range(LANES):
                    n = i * LANES + lane
                    norm_apply(X[:, bass.ds(n, 1), :].rearrange("t a d -> t (a d)"), xt[lane][:], n, lane, 2).then_inc(S_.lane_free, 1)
    s.close()


def lay_out(inputs):
    a = {k: np.ascontiguousarray(v) for k, v in inputs.items()}
    for key in ("mask_BxS_bf1", "mask_BxS2_bf1"):
        a[key] = a[key].view(np.uint8)
    a["text_mask_T"] = a.pop("mask_BxS_bf1").T
    a["L0_xattn_mod_gate"] = a["L0_xattn_mod_gate"].reshape(1)
    a["ctxT"] = a.pop("ctx_768").transpose(2, 0, 1).reshape(DC, B * TC)
    w, b, g = a.pop("L2_attn_in_proj_weight"), a.pop("L2_attn_in_proj_bias"), a.pop("L2_attn_gamma").reshape(-1)
    w3, b3 = a.pop("L3_ffn_Wqkv"), a.pop("L3_ffn_bqkv")
    for n, c in enumerate("qkv"):
        part = slice(n * D, (n + 1) * D)
        a[f"L2_attn_W{c}"], a[f"L2_attn_b{c}"], a[f"L2_attn_gamma_{c}"] = w[part].T, b[part], g[part]
        a[f"L3_ffn_W{c}"], a[f"L3_ffn_b{c}"] = w3[:, part], b3[part]
        a[f"L3_attn_W{c}T"] = a.pop(f"L3_attn_W{c}").T
    a["L3_attn_WoT"] = a.pop("L3_attn_Wo").T
    a["L2_attn_WoT"] = a.pop("L2_attn_out_proj_weight").T
    a["L2_attn_alpha"] = a.pop("L2_attn_linear_alpha").reshape(-1)
    a["L2_attn_lgamma"] = a.pop("L2_attn_linear_gamma").reshape(-1)
    for c in "kvr":
        a[f"L1_attn_time_mix_{c}"] = a[f"L1_attn_time_mix_{c}"].reshape(-1)
        a[f"L1_attn_W{c}T"] = a.pop(f"L1_attn_W{c}").T
    a["L1_attn_WoT"] = a.pop("L1_attn_Wo").T
    a["L3_ffn_fc1T"] = a.pop("L3_ffn_fc1_w").transpose(0, 2, 1)
    a["L3_ffn_fc2T"] = a.pop("L3_ffn_fc2_w").transpose(0, 2, 1)
    i, j = np.arange(T)[:, None], np.arange(T)[None, :]
    causal, within = j <= i, (j <= i) & (i // B == j // B)
    for name, sees in (("mask_causal", causal), ("mask_within", within)):
        a[name] = np.where(sees, 0.0, NEG).astype(np.float32)
    a["iota8"] = np.arange(E, dtype=np.float32)
    a["mask_causal_T"] = causal.T.astype(np.float32)
    return {k: np.ascontiguousarray(v) for k, v in a.items()}


def build(nc, I, out, stages=tuple(range(12))):
    I = dict(I)
    with ExitStack() as stack:
        core = Core(nc, stack, I)
        load_block(core)
        if 0 in stages:
            attention(core, "L0self", H=16, Dh=8, Wq="L0_attn_Wq", Wk="L0_attn_Wk", Wv="L0_attn_Wv", Wo="L0_attn_Wq",
                      bq="L0_attn_bq", bk="L0_attn_bk", bv="L0_attn_bv", flow=True, post="gate")
        if 1 in stages:
            text_vision(core)
        if 2 in stages:
            experts_top1(core, "L0ffn")
        if 3 in stages:
            wkv_mix(core)
        if 4 in stages:
            attention(core, "L1x", H=16, Dh=8, Wq="L1_xattn_Wq", Wk="L1_xattn_Wk", Wv="L1_xattn_Wv", Wo="L1_xattn_Wo",
                      bq="L1_xattn_bq", bk="L1_xattn_bk", bv="L1_xattn_bv", bo="L1_xattn_bo", context=True,
                      form="bounded", post="l1x")
        if 5 in stages:
            experts_top1(core, "L1ffn")
        if 6 in stages:
            batch_axis_attention(core)
        if 7 in stages:
            attention(core, "L2x", H=16, Dh=8, Wq="L2_xattn_wq", Wk="L2_xattn_wk", Wv="L2_xattn_wv", Wo="L2_xattn_wo",
                      bq="L2_xattn_bq", bk="L2_xattn_bk", bv="L2_xattn_bv", bo="L2_xattn_bo", context=True)
        if 8 in stages:
            soft_experts(core)
        if 9 in stages:
            attention(core, "L3lin", H=16, Dh=8, Wq="L3_attn_WqT", Wk="L3_attn_WkT", Wv="L3_attn_WvT", Wo="L3_attn_WoT",
                      bq="L3_attn_bq", bk="L3_attn_bk", bv="L3_attn_bv", bo="L3_attn_bo", form="linear",
                      mask="mask_causal_T")
        if 10 in stages:
            attention(core, "L3x", H=8, Dh=64, Wq="L3_xattn_Wq", Wk="L3_xattn_Wk", Wv="L3_xattn_Wv", Wo="L3_xattn_Wo",
                      bo="L3_xattn_bo", context=True)
        if 11 in stages:
            block_experts(core)
        store_block(core, out)


STAGES = tuple(range(12))


def kernel(**inputs):
    from concourse import bacc
    from concourse.bass_utils import run_bass_kernel_spmd

    nc = bacc.Bacc("TRN2", target_bir_lowering=False, num_devices=1)
    arrays = lay_out(inputs)
    I = {k: nc.dram_tensor(f"in_{k}", v.shape, mybir.dt.from_np(v.dtype), kind="ExternalInput").ap()
         for k, v in arrays.items()}
    out = nc.dram_tensor("out_x", (B, T, D), F32, kind="ExternalOutput").ap()
    build(nc, I, out, STAGES)
    r = run_bass_kernel_spmd(nc, [{f"in_{k}": v for k, v in arrays.items()}], core_ids=[0])
    return r.results[0]["out_x"]
```

```python
from contextlib import ExitStack

import numpy as np
import concourse.bass as bass
from concourse import mybir

F32 = mybir.dt.float32
BF16 = mybir.dt.bfloat16
U32 = mybir.dt.uint32
U8 = mybir.dt.uint8
ALU = mybir.AluOpType
ACT = mybir.ActivationFunctionType
AX = mybir.AxisListType.X

B, T, D = 32, 128, 128
TC, DC = 120, 96
LANES = 2
STEPS = B // LANES
E, F = 8, 512
FC = F // 128
LN_EPS = 1e-5
NEG = -1e30


def at(eng, sem, n, each=1):
    eng.wait_ge(sem, (n + 1) * each)


def at_alone(eng, sem, n, passed):
    at(eng, sem, n)
    eng.sem_inc(passed, 1)


class Scope:

    def __init__(self, nc, name):
        self.nc, self.name, self.stack, self.sems = nc, name, ExitStack(), []
        self.passed = self.sem("passed")

    def sb(self, name, shape, dtype=F32):
        return self.stack.enter_context(self.nc.sbuf_tensor(f"{self.name}_{name}", shape, dtype))

    def lanes(self, name, shape, dtype=F32):
        return [self.sb(f"{name}{lane}", shape, dtype) for lane in range(LANES)]

    def psum(self, name, shape, dtype=F32):
        return self.stack.enter_context(self.nc.psum_tensor(f"{self.name}_{name}", shape, dtype))

    def sem(self, name):
        s = self.nc.alloc_semaphore(f"{self.name}_{name}")
        self.sems.append(s)
        return s

    def close(self):
        self.stack.close()
        self.nc.clear_and_free_semaphores(self.sems)
        self.nc.all_engine_barrier()


def row_bc(vec, n=128):
    return vec.rearrange("(a d) -> a d", a=1).to_broadcast([n, vec.shape[0]])


def col(vec):
    return vec.rearrange("(d a) -> d a", a=1)


class Core:

    def __init__(self, nc, stack, I):
        self.nc, self.I = nc, I

        def sb(name, shape, dtype=F32):
            return stack.enter_context(nc.sbuf_tensor(name, shape, dtype))

        self.X = sb("X", [T, B, D])
        self.ident = sb("ident", [128, 128])
        self.anti = sb("anti", [128, 128])
        self.identb = sb("identb", [128, 128], BF16)
        self.ones = sb("ones", [128, 128])
        self.neghalf = sb("neghalf", [128, 128])


def load_block(core):
    nc, I = core.nc, core.I
    s = Scope(nc, "load")
    x_in, zeroed, made = s.sem("x_in"), s.sem("zeroed"), s.sem("made")
    with nc.Block() as block:
        @block.sync
        def _(sp):
            sp.dma_start(core.X[:], I["x"].rearrange("b t d -> t b d")).then_inc(x_in, 16)
            sp.wait_ge(x_in, 16)

        @block.gpsimd
        def _(pool):
            pool.memset(core.ident[:], 0.0).then_inc(zeroed, 1)
            pool.memset(core.ones[:], 1.0).then_inc(made, 1)
            pool.memset(core.neghalf[:], -0.5).then_inc(made, 1)
            pool.memset(core.anti[:], 0.0).then_inc(zeroed, 1)
            pool.wait_ge(zeroed, 2)
            pool.affine_select(out=core.anti[:], in_=core.anti[:], compare_op=ALU.not_equal, fill=1.0,
                               base=-127, pattern=[[1, 128]], channel_multiplier=1).then_inc(made, 1)
            pool.affine_select(out=core.ident[:], in_=core.ident[:], compare_op=ALU.not_equal, fill=1.0,
                               base=0, pattern=[[-1, 128]], channel_multiplier=1).then_inc(made, 1)
            pool.wait_ge(made, 4)
            pool.tensor_copy(core.identb[:], core.ident[:]).then_inc(made, 1)
            pool.wait_ge(made, 5)
    s.close()


def store_block(core, out):
    nc = core.nc
    s = Scope(nc, "store")
    x_out = s.sem("x_out")
    with nc.Block() as block:
        @block.sync
        def _(sp):
            sp.dma_start(out.rearrange("b t d -> t b d"), core.X[:]).then_inc(x_out, 16)
            sp.wait_ge(x_out, 16)
    s.close()


def attention(core, name, *, H, Dh, Wq, Wk, Wv, Wo=None, bq=None, bk=None, bv=None, bo=None,
              context=False, flow=False, mask=None, form="softmax", post="plain", x_after=None):
    nc, I, X = core.nc, core.I, core.X
    s = Scope(nc, name)
    small = Dh == 8
    K = TC if context else T
    KD = DC if context else D
    J = 4 if small else 2
    R = 128 // J
    C = H // J
    HD = H * Dh
    NB = HD // 128
    G = H if small else 4
    Q = 2 * Dh if flow else Dh
    scale = float(Dh) ** -0.5
    shifted = form == "softmax"
    two_norms = post in ("gate", "l1x")
    scaled = post == "l2self"
    HJ = J // 2

    loads, zeroed = [], []
    WC = 4 if post == "gate" else 3
    if small:
        wx = s.sb("wx", [D, WC, HD])
        loads.append((wx[:, 0, :], I[Wq]))
        if context:
            wc = s.sb("wc", [DC, 2, HD])
            loads += [(wc[:, 0, :], I[Wk]), (wc[:, 1, :], I[Wv])]
        else:
            loads += [(wx[:, 1, :], I[Wk]), (wx[:, 2, :], I[Wv])]
        brow = s.sb("brow", [128, 4, HD])
        for a, key in enumerate((bq, bk, bv)):
            loads.append((brow[:, a, :], row_bc(I[key])))
        if post == "gate":
            loads += [(wx[:, 3, :], I["L0_attn_Wg"][0:D, :]), (brow[:, 3, :], row_bc(I["L0_attn_bg"]))]
        if post == "l1x":
            loads.append((brow[:, 3, :], row_bc(I[bo])))
    else:
        wx = s.sb("wx", [D, HD])
        wk = s.sb("wk", [DC, HD])
        wv = s.sb("wv", [DC, HD])
        loads += [(wx[:], I[Wq]), (wk[:], I[Wk]), (wv[:], I[Wv])]
    wo = s.sb("wo", [128, NB, D])
    loads.append((wo[:], I["L0_attn_Wg"][D:2 * D, :].rearrange("(n p) d -> p n d", n=1) if post == "gate"
                  else I[Wo].rearrange("(n p) d -> p n d", p=128)))

    def row(key, tag):
        t = s.sb(tag, [128, D])
        loads.append((t[:], row_bc(I[key])))
        return t

    bor = row(bo, "bo") if post in ("plain", "l2self", "l3ffn") else None
    if two_norms:
        pre = "L0_attn_" if post == "gate" else "L1_xattn_ln_"
        gam, bet = row(pre + "gamma", "gam"), row(pre + "beta", "bet")
    if post == "l3ffn":
        l1w, l1b = row("L3_ffn_ln1_w", "l1w"), row("L3_ffn_ln1_b", "l1b")
    if scaled:
        grow = s.sb("grow", [128, 3, HD])
        for a, c in enumerate("qkv"):
            loads.append((grow[:, a, :], row_bc(I[f"L2_attn_gamma_{c}"])))
        alpha, lgam = s.sb("alpha", [128, 1]), row("L2_attn_lgamma", "lgam")
        loads.append((alpha[:], col(I["L2_attn_alpha"])))
    if mask:
        mask_in = s.sb("mask_in", [T, T])
        loads.append((mask_in[:], I[mask]))
        msk = s.sb("msk", [T, C, T], BF16) if shifted else mask_in

    def pair(tag, shape):
        return [s.sb(f"{tag}{p}", shape) for p in (0, 1)]

    xs = pair("xs", [T, D])
    xT = s.sb("xT", [D, T])
    cs = pair("cs", [DC, K]) if context else None
    U = pair("U", [128, 3, H, 32]) if small else None
    V = [u[:, 2, :, 0:Dh + 1] for u in U] if small else [v[:] for v in pair("V", [128, H, Dh + 1])]
    q4 = s.sb("q4", [128, C, T])
    k4 = s.sb("k4", [128, C, K])
    S = s.sb("S", [T, J, C, K]) if shifted else None
    PTs = pair("PT", [K, J, C, T])
    mx = s.sb("mx", [T, J, C])
    rz = s.sb("rz", [T, H])
    oS = s.sb("oS", [T, H, Dh])
    outT = s.sb("outT", [128, C, T]) if small else None
    oT = s.sb("oT", [128, NB, T])
    kept = s.sb("kept", [T, B, D])
    r = s.sb("r", [T, D])
    rm = s.sb("rm", [T, D])
    xo = s.sb("xo", [T, D])
    gt = s.sb("gt", [T, D])
    st, mv, ve, rs = s.sb("st", [T, 6]), s.sb("mv", [T, 2]), s.sb("ve", [T, 1]), s.sb("rs", [T, 1])
    st1, mv1, ve1, rs1 = s.sb("st1", [T, 6]), s.sb("mv1", [T, 2]), s.sb("ve1", [T, 1]), s.sb("rs1", [T, 1])
    sq = s.sb("sq", [T, 2, H, Dh])
    ss = s.sb("ss", [T, 2])
    ef, rl = s.sb("ef", [T, 2, H, Dh]), s.sb("rl", [T, 2, H, Dh])

    bank = s.psum("bank", [128, 8, 512])
    scores = bank[:, 0:J, :]
    if small:
        q_ps, k_ps, proj_ps = bank[:, 4, :], bank[:, 5, :], bank[:, 6, :]
        outT_ps, o_ps = bank[:, 7, :], bank[:, 7:8, :]
        y_ps, oT_ps = bank[:, 7, 0:D], bank[:, 7, 128:128 + T]
    else:
        o_ps = bank[:, 2:4, 0:G * (Dh + 1)]
        y_ps = bank[:, 2, 384:512]
        q_ps, k_ps, proj_ps, oT_ps = bank[:, 4, :], bank[:, 5, :], bank[:, 6, :], bank[:, 7, :]

    xT_ps = bank[:, 4, 0:T]

    def sems(names):
        return [s.sem(n) for n in names.split()]

    weights_in, zeroed, setup = sems("weights_in zeroed setup")
    x_ready, xT_psum, xT_ready, proj_psum, u_ready, qkT_psum, q_ready, k_ready, v_ready = sems(
        "x_ready xT_psum xT_ready proj_psum u_ready qkT_psum q_ready k_ready v_ready")
    s_psum, max_ready, shifted_ready, p_ready, pT_psum, pT_ready = [
        sems(f"{n}_low {n}_high") for n in ("scores_psum", "max", "shifted", "p", "pT_psum", "pT")]
    o_psum, z_ready, o_ready, oT_psum, oT_ready, y_psum, y_read, stats, mean_var, var_eps, rstd, finished = sems(
        "o_psum z_ready o_ready oT_psum oT_ready y_psum y_read stats mean_var var_eps rstd finished")
    kept_ready, normed, q_biased, outT_psum, outT_ready = sems("kept_ready normed q_biased outT_psum outT_ready")
    ctx_in = sems("ctx_in_even ctx_in_odd") if context else None
    if two_norms:
        r1_ready, stats1, mean_var1, var_eps1, rstd1, normed1, scaled1, offset1, r_ready = sems(
            "r1_ready stats1 mean_var1 var_eps1 rstd1 normed1 scaled1 offset1 r_ready")
    if post == "gate":
        gate_in, gate_exp, gate_plus1, gate_ready, gated = sems("gate_in gate_exp gate_plus1 gate_ready gated")
    if form == "bounded":
        squares, square_sum, norm_safe, norm_ready, raw = sems("squares square_sum norm_safe norm_ready raw")
    if form == "linear":
        raw, low, expd = sems("raw low expd")
    if flow:
        raw = s.sem("raw")
    if post == "l3ffn":
        i_copied, i_stats, i_mv, i_ve, i_rstd, i_normed, i_scaled = sems(
            "in_copied in_stats in_mean_var in_var_eps in_rstd in_normed in_scaled")
    setups = 0
    if scaled:
        setups += 5
    if post == "l1x":
        setups += 1
    if mask and shifted:
        setups += 1

    def tile(buffer, n):
        return buffer[:, n, :] if isinstance(n, int) else buffer[:, bass.ds(n, 1), :].rearrange("t a d -> t (a d)")

    def steps(eng, step):
        step(-2, 0, fetch=True)
        step(-1, 1, fetch=True, front=True)
        step(0, 0, fetch=True, front=True, main=True)
        step(1, 1, fetch=True, front=True, main=True, tail=True)
        with eng.Fori(0, (B - 4) // 2) as i:
            step(i * 2 + 2, 0, fetch=True, front=True, main=True, tail=True, output=True)
            step(i * 2 + 3, 1, fetch=True, front=True, main=True, tail=True, output=True)
        step(B - 2, 0, front=True, main=True, tail=True, output=True)
        step(B - 1, 1, main=True, tail=True, output=True)
        step(B, 0, tail=True, output=True)
        step(B + 1, 1, output=True)

    halves = ((0, range(0, HJ)), (1, range(HJ, J)))

    with nc.Block() as block:
        @block.sync
        def _(sp):
            with nc.allow_non_contiguous_dma(reason="weights are rearranged once"):
                for dst, src in loads:
                    sp.dma_start(dst, src).then_inc(weights_in, 16)
            if context:
                for p in (0, 1):
                    sp.dma_start(cs[p][:], I["ctxT"][:, p * K:(p + 1) * K]).then_inc(ctx_in[p], 16)
                with sp.Fori(0, (B - 2) // 2) as i:
                    for p in (0, 1):
                        n = i * 2 + p
                        at(sp, proj_psum, n)
                        sp.dma_start(cs[p][:], I["ctxT"][:, bass.ds(n * K + 2 * K, K)]).then_inc(ctx_in[p], 16)

        @block.gpsimd
        def _(pool):
            for p in (0, 1):
                if small:
                    pool.memset(U[p][:], 0.0).then_inc(zeroed, 1)
                    pool.wait_ge(zeroed, 1 + 2 * p)
                    pool.memset(U[p][:, 2, :, Dh:Dh + 1], 1.0).then_inc(zeroed, 1)
                else:
                    pool.memset(V[p], 1.0).then_inc(zeroed, 2)
            pool.wait_ge(weights_in, 16 * len(loads))
            if setups:
                pool.wait_ge(setup, setups)

            def step(n, p, fetch=False, front=False, main=False, tail=False, output=False):
                f, t = n + 2, n - 2
                if fetch:
                    x_new = xs[p]
                    if not (isinstance(f, int) and f < 2):
                        at_alone(pool, xT_psum, f - 2, s.passed)
                    if post == "l3ffn":
                        pool.tensor_copy(x_new[:], tile(X, f)).then_inc(i_copied, 1)
                        at(pool, i_ve, f)
                        pool.tensor_tensor(rs1[:], ve1[:], core.neghalf[:, 0:1], ALU.pow).then_inc(i_rstd, 1)
                        at_alone(pool, i_rstd, f, s.passed)
                        at_alone(pool, i_copied, f, s.passed)
                        pool.tensor_scalar(x_new[:], x_new[:], mv1[:, 0:1], rs1[:, 0:1], ALU.subtract, ALU.mult).then_inc(i_normed, 1)
                        at(pool, i_normed, f)
                        pool.tensor_tensor(x_new[:], x_new[:], l1w[:], ALU.mult).then_inc(i_scaled, 1)
                        at(pool, i_scaled, f)
                        pool.tensor_tensor(x_new[:], x_new[:], l1b[:], ALU.add).then_inc(x_ready, 1)
                    else:
                        pool.tensor_copy(x_new[:], tile(X, f)).then_inc(x_ready, 1)
                    if bor is not None:
                        pool.tensor_tensor(tile(kept, f), tile(X, f), bor[:], ALU.add).then_inc(kept_ready, 1)
                if front and form == "bounded":
                    at(pool, norm_safe, n + 1)
                    pool.tensor_tensor(ss[:], ss[:], core.neghalf[:, 0:2], ALU.pow).then_inc(norm_ready, 1)
                if output:
                    if two_norms:
                        at(pool, var_eps1, t)
                        pool.tensor_tensor(rs1[:], ve1[:], core.neghalf[:, 0:1], ALU.pow).then_inc(rstd1, 1)
                        at_alone(pool, rstd1, t, s.passed)
                        pool.tensor_scalar(rm[:], r[:], mv1[:, 0:1], rs1[:, 0:1], ALU.subtract, ALU.mult).then_inc(normed1, 1)
                        at(pool, normed1, t)
                        pool.tensor_tensor(rm[:], rm[:], gam[:], ALU.mult).then_inc(scaled1, 1)
                        at(pool, scaled1, t)
                        pool.tensor_tensor(rm[:], rm[:], bet[:], ALU.add).then_inc(offset1, 1)
                        at(pool, offset1, t)
                        pool.tensor_tensor(rm[:], rm[:], tile(X, t), ALU.add).then_inc(r_ready, 1)
                    if post != "l3ffn":
                        at(pool, var_eps, t)
                        pool.tensor_tensor(rs[:], ve[:], core.neghalf[:, 0:1], ALU.pow).then_inc(rstd, 1)
                        at_alone(pool, rstd, t, s.passed)
                        pool.tensor_scalar(xo[:], (rm if two_norms else r)[:], mv[:, 0:1], rs[:, 0:1],
                                           ALU.subtract, ALU.mult).then_inc(normed, 1)
                        at_alone(pool, normed, t, s.passed)
                        pool.tensor_copy(tile(X, t), xo[:]).then_inc(finished, 1)
            steps(pool, step)
            if post != "l3ffn":
                pool.wait_ge(finished, B + 1)

        @block.tensor
        def _(pe):
            pe.wait_ge(weights_in, 16 * len(loads))
            if setups:
                pe.wait_ge(setup, setups)

            def step(n, p, fetch=False, front=False, main=False, tail=False, output=False):
                f, t, d = n + 1, n - 1, n - 2

                def score_products(half, tiles):
                    if not (isinstance(n, int) and n == 0):
                        pe.wait_ge(pT_ready[half], n)
                    if mask and shifted:
                        for j in tiles:
                            pe.matmul(scores[:, j, 0:C * K], core.identb[:],
                                      msk[:].rearrange("t c k -> t (c k)"), start=True, stop=False, skip_group_check=True)
                    for c in range(C):
                        for j in tiles:
                            rows = slice(j * R, j * R + Q)
                            if shifted:
                                last = pe.matmul(scores[:, j, c * K:(c + 1) * K], q4[rows, c, :], k4[rows, c, :],
                                                 start=not mask, stop=True, skip_group_check=True)
                            else:
                                last = pe.matmul(scores[0:K, j, c * T:(c + 1) * T], k4[rows, c, :], q4[rows, c, :],
                                                 start=True, stop=True)
                    last.then_inc(s_psum[half], 1)

                def transposed(half, tiles):
                    at(pe, p_ready[half], n)
                    for c in range(C):
                        for j in tiles:
                            last = pe.transpose(scores[0:K, j, c * T:(c + 1) * T], S[:, j, c, :], core.ident[:])
                    last.then_inc(pT_psum[half], 1)

                if main:
                    at(pe, q_ready, n)
                    at(pe, k_ready, n)
                if front:
                    if not (isinstance(f, int) and f < 1):
                        pe.wait_ge(xT_ready, f)
                    at(pe, x_ready, f)
                    pe.transpose(xT_ps, xs[1 - p][:], core.ident[:]).then_inc(xT_psum, 1)
                if output and small:
                    at(pe, outT_ready, d)
                    for c in range(C):
                        last = pe.transpose(o_ps[:, 0, c * T:(c + 1) * T], outT[:, c, :], core.ident[:])
                    last.then_inc(o_psum, 1)
                if main:
                    score_products(*halves[0])
                if output:
                    at(pe, o_ready, d)
                    ov = oS[:].rearrange("t h d -> t (h d)")
                    for b in range(NB):
                        last = pe.transpose(oT_ps[:, b * T:(b + 1) * T], ov[:, b * 128:(b + 1) * 128], core.ident[:])
                    last.then_inc(oT_psum, 1)
                if front:
                    at(pe, xT_ready, f)
                    if context:
                        pe.wait_ge(ctx_in[1 - p], (f // 2 + 1) * 16 if isinstance(f, int) else f * 8 + 16 - 8 * (1 - p))
                    if not (isinstance(f, int) and f < 1):
                        pe.wait_ge(v_ready, f)
                    if small and context:
                        pe.matmul(proj_ps[:, 0:HD], xT[:], wx[:, 0, :], start=True, stop=True)
                        pe.matmul(proj_ps[0:K, HD:3 * HD], cs[1 - p][:], wc[:].rearrange("e a d -> e (a d)"),
                                  start=True, stop=True).then_inc(proj_psum, 1)
                    elif small:
                        pe.matmul(proj_ps[:, 0:WC * HD], xT[:], wx[:].rearrange("e a d -> e (a d)"),
                                  start=True, stop=True).then_inc(proj_psum, 1)
                    else:
                        for c in range(C):
                            pe.matmul(q_ps[:, c * T:(c + 1) * T], wx[:, c * 128:(c + 1) * 128], xT[:], start=True, stop=True)
                        for c in range(C):
                            pe.matmul(k_ps[:, c * K:(c + 1) * K], wk[:, c * 128:(c + 1) * 128], cs[1 - p][:], start=True, stop=True)
                        pe.matmul(proj_ps[0:K, :], cs[1 - p][:], wv[:], start=True, stop=True).then_inc(proj_psum, 1)
                if main:
                    score_products(*halves[1])
                if output:
                    at(pe, oT_ready, d)
                    for b in range(NB):
                        last = pe.matmul(y_ps, oT[:, b, :], wo[:, b, :], start=b == 0, stop=b == NB - 1)
                    last.then_inc(y_psum, 1)
                if front and small:
                    at(pe, u_ready, f)
                    for c in range(C):
                        pe.transpose(q_ps[:, c * T:(c + 1) * T], U[1 - p][:, 0, c * J:(c + 1) * J, :].rearrange("t h r -> t (h r)"), core.ident[:])
                    for c in range(C):
                        last = pe.transpose(k_ps[:, c * K:(c + 1) * K], U[1 - p][0:K, 1, c * J:(c + 1) * J, :].rearrange("t h r -> t (h r)"),
                                            core.ident[0:K, 0:K])
                    last.then_inc(qkT_psum, 1)
                if main and shifted:
                    transposed(*halves[0])
                if tail:
                    at(pe, pT_ready[0], t)
                    at(pe, pT_ready[1], t)
                    at(pe, v_ready, t)
                    at(pe, y_read, t)
                    if small:
                        for c in range(C):
                            for j in range(J):
                                last = pe.matmul(outT_ps[j * R:(j + 1) * R, c * T:(c + 1) * T], U[1 - p][0:K, 2, c * J + j, :],
                                                 PTs[1 - p][:, j, c, :], start=True, stop=True)
                        last.then_inc(outT_psum, 1)
                    else:
                        for h in range(H):
                            o = o_ps[:, h // G, (h % G) * (Dh + 1):(h % G + 1) * (Dh + 1)]
                            last = pe.matmul(o, PTs[1 - p][:, h % J, h // J, :], V[1 - p][0:K, h, :], start=True, stop=True)
                        last.then_inc(o_psum, 1)
                if main and shifted:
                    transposed(*halves[1])
            steps(pe, step)

        @block.scalar
        def _(act):
            act.wait_ge(zeroed, 4)

            def step(n, p, fetch=False, front=False, main=False, tail=False, output=False):
                f, t, d = n + 1, n - 1, n - 2

                def exponentials(half):
                    own = slice(half * HJ, (half + 1) * HJ)
                    if shifted:
                        at(act, shifted_ready[half], n)
                        act.activation(S[:, own], S[:, own], ACT.Exp, scale=scale).then_inc(p_ready[half], 1)
                    elif form == "bounded":
                        at(act, s_psum[half], n)
                        act.activation(PTs[p][:, own], scores[0:K, own].rearrange("k j (c t) -> k j c t", t=T),
                                       ACT.Exp, scale=scale).then_inc(pT_ready[half], 1)

                if front:
                    at(act, xT_psum, f)
                    act.activation(xT[:], xT_ps, ACT.Copy).then_inc(xT_ready, 1)
                if main:
                    exponentials(0)
                if output:
                    at(act, oT_psum, d)
                    act.activation(oT[:], oT_ps[:, 0:NB * T].rearrange("p (b t) -> p b t", b=NB), ACT.Copy).then_inc(oT_ready, 1)
                if front and form == "linear":
                    at(act, raw, f)
                    act.activation(ef[:], sq[:], ACT.Exp).then_inc(expd, 1)
                if main:
                    exponentials(1)
                if output and post == "gate":
                    at(act, gate_in, d)
                    act.activation(gt[:], gt[:], ACT.Exp, scale=-1.0).then_inc(gate_exp, 1)
                if front:
                    at(act, qkT_psum if small else proj_psum, f)
                    if main and not small:
                        at(act, s_psum[1], n)
                    act.activation(q4[:], q_ps.rearrange("p (c t) -> p c t", c=C), ACT.Copy).then_inc(q_ready, 1)
                    if small:
                        act.activation(k4[:], k_ps[:, 0:C * K].rearrange("p (c t) -> p c t", c=C), ACT.Copy).then_inc(k_ready, 1)
                if main and shifted:
                    at(act, pT_psum[0], n)
                    act.activation(PTs[p][:, 0:HJ], scores[0:K, 0:HJ].rearrange("k j (c t) -> k j c t", t=T),
                                   ACT.Copy).then_inc(pT_ready[0], 1)
                if tail and small:
                    at(act, outT_psum, t)
                    act.activation(outT[:], outT_ps.rearrange("p (c t) -> p c t", c=C), ACT.Copy).then_inc(outT_ready, 1)
                if front and not small:
                    if tail:
                        at(act, o_psum, t)
                    act.activation(V[1 - p][0:K, :, 0:Dh], proj_ps[0:K].rearrange("k (h d) -> k h d", h=H),
                                   ACT.Copy).then_inc(v_ready, 1)
            steps(act, step)

        @block.vector
        def _(dve):
            dve.wait_ge(zeroed, 4)
            dve.wait_ge(weights_in, 16 * len(loads))
            if scaled:
                dve.tensor_tensor(wx[:], wx[:], grow[:], ALU.mult).then_inc(setup, 1)
                dve.tensor_tensor(brow[:, 0:3, :], brow[:, 0:3, :], grow[:], ALU.mult).then_inc(setup, 1)
                dve.tensor_tensor(bor[:], bor[:], lgam[:], ALU.mult).then_inc(setup, 1)
                dve.tensor_tensor(wo[:, 0, :], wo[:, 0, :], lgam[:], ALU.mult).then_inc(setup, 1)
                dve.wait_ge(setup, 4)
                dve.tensor_scalar(wo[:, 0, :], wo[:, 0, :], alpha[:, 0:1], None, ALU.mult).then_inc(setup, 1)
            if post == "l1x":
                dve.tensor_tensor(brow[:, 3, :], brow[:, 3, :], brow[:, 0, :], ALU.add).then_inc(setup, 1)
            if mask and shifted:
                dve.tensor_copy(msk[:], mask_in[:].unsqueeze(1).to_broadcast([T, C, T])).then_inc(setup, 1)
            if setups:
                dve.wait_ge(setup, setups)
            dve.sem_inc(y_read, 1)
            dve.sem_inc(finished, 1)

            def norm(src, n, bufs, done):
                st_, mv_, ve_ = bufs
                dve.bn_stats(st_[:], src).then_inc(done[0], 1)
                at_alone(dve, done[0], n, s.passed)
                dve.bn_aggr(mv_[:], st_[:]).then_inc(done[1], 1)
                at(dve, done[1], n)
                dve.tensor_scalar(ve_[:], mv_[:, 1:2], LN_EPS, None, ALU.add).then_inc(done[2], 1)

            def step(n, p, fetch=False, front=False, main=False, tail=False, output=False):
                f, t, d = n + 1, n - 1, n - 2

                def shift(half):
                    own = slice(half * HJ, (half + 1) * HJ)
                    at(dve, s_psum[half], n)
                    if shifted:
                        sc = scores[:, own, 0:C * K].rearrange("t j (c k) -> t j c k", c=C)
                        dve.tensor_reduce(mx[:, own], sc, AX.X, ALU.max).then_inc(max_ready[half], 1)
                        at(dve, max_ready[half], n)
                        dve.tensor_tensor(S[:, own], sc, mx[:, own].unsqueeze(3).to_broadcast([T, HJ, C, K]),
                                          ALU.subtract).then_inc(shifted_ready[half], 1)
                    else:
                        dve.tensor_tensor(PTs[p][:, own].rearrange("k j c t -> k (j c) t"), scores[0:K, own].rearrange("k j (c t) -> k (j c) t", t=T),
                                          msk[:].unsqueeze(1).to_broadcast([K, HJ * C, T]), ALU.mult).then_inc(pT_ready[half], 1)

                if fetch and post == "l3ffn":
                    a = n + 2
                    if not (isinstance(a, int) and a < 1):
                        dve.wait_ge(x_ready, a)
                    norm(tile(X, a), a, (st1, mv1, ve1), (i_stats, i_mv, i_ve))
                if output:
                    at(dve, o_psum, d)
                    po = o_ps.rearrange("t n (g d) -> t n g d", g=G)
                    ov = oS[:].rearrange("t (n g) d -> t n g d", g=G)
                    if form == "linear":
                        dve.tensor_copy(ov, po[:, :, :, 0:Dh]).then_inc(o_ready, 1)
                    else:
                        rv = rz[:].rearrange("t (n g) -> t n g", g=G)
                        dve.reciprocal(rv.unsqueeze(3), po[:, :, :, Dh:Dh + 1]).then_inc(z_ready, 1)
                        at(dve, z_ready, d)
                        dve.tensor_tensor(ov, po[:, :, :, 0:Dh], rv.unsqueeze(3).to_broadcast([T, H // G, G, Dh]),
                                          ALU.mult).then_inc(o_ready, 1)
                if main and form != "bounded":
                    shift(0)
                if front and small:
                    at(dve, proj_psum, f)
                    u = U[1 - p]
                    pp = proj_ps.rearrange("t (a h d) -> t a h d", a=4, h=H)
                    bb = brow[:].rearrange("t a (h d) -> t a h d", h=H)
                    if post in ("gate", "l1x"):
                        a = 3 if post == "gate" else 0
                        dve.tensor_tensor(tile(kept, f), proj_ps[:, a * HD:(a + 1) * HD], brow[:, 3, :], ALU.add).then_inc(kept_ready, 1)
                    if form == "linear":
                        dve.tensor_tensor(sq[:], pp[:, 0:2], bb[:, 0:2], ALU.add).then_inc(raw, 1)
                        at(dve, raw, f)
                        dve.tensor_scalar(rl[:], sq[:], 0.0, None, ALU.max).then_inc(low, 1)
                    elif form == "bounded":
                        dve.tensor_tensor(u[:, 0, :, 0:Dh], pp[:, 0], bb[:, 0], ALU.add).then_inc(raw, 1)
                        dve.tensor_tensor(u[0:K, 1, :, 0:Dh], pp[0:K, 1], bb[0:K, 1], ALU.add).then_inc(raw, 1)
                        at(dve, raw, f, 2)
                        dve.tensor_tensor(sq[:], u[:, 0:2, :, 0:Dh], u[:, 0:2, :, 0:Dh], ALU.mult).then_inc(squares, 1)
                        at(dve, squares, f)
                        dve.tensor_reduce(ss[:], sq[:].rearrange("t a h d -> t a (h d)"), AX.X, ALU.add).then_inc(square_sum, 1)
                        at(dve, square_sum, f)
                        dve.tensor_scalar(ss[:], ss[:], 1e-24, None, ALU.max).then_inc(norm_safe, 1)
                    elif flow:
                        dve.tensor_tensor(u[:, 0:2, :, 0:Dh], pp[:, 0:2], bb[:, 0:2], ALU.add).then_inc(raw, 1)
                        at(dve, raw, f)
                        dve.tensor_scalar(u[:, 0, :, Dh:Q], u[:, 1, :, 0:Dh], -1.0, None, ALU.mult).then_inc(q_biased, 1)
                        dve.tensor_copy(u[:, 1, :, Dh:Q], u[:, 0, :, 0:Dh]).then_inc(u_ready, 1)
                    elif context:
                        dve.tensor_tensor(u[:, 0, :, 0:Dh], pp[:, 0], bb[:, 0], ALU.add).then_inc(q_biased, 1)
                        dve.tensor_tensor(u[0:K, 1, :, 0:Dh], pp[0:K, 1], bb[0:K, 1], ALU.add).then_inc(u_ready, 1)
                    else:
                        dve.tensor_tensor(u[:, 0:2, :, 0:Dh], pp[:, 0:2], bb[:, 0:2], ALU.add).then_inc(u_ready, 1)
                if front and form == "bounded":
                    u = U[1 - p]
                    at(dve, norm_ready, f)
                    dve.tensor_tensor(u[:, 0:2, :, 0:Dh], u[:, 0:2, :, 0:Dh],
                                      ss[:].unsqueeze(2).unsqueeze(3).to_broadcast([T, 2, H, Dh]), ALU.mult).then_inc(u_ready, 1)
                if front and form == "linear":
                    u = U[1 - p]
                    at(dve, expd, f)
                    at(dve, low, f)
                    dve.scalar_tensor_tensor(out=u[:, 0:2, :, 0:Dh], in0=ef[:], scalar=1.0, in1=rl[:],
                                             op0=ALU.min, op1=ALU.add).then_inc(u_ready, 1)
                if main and form != "bounded":
                    shift(1)
                if front and not small:
                    at(dve, proj_psum, f)
                    if main:
                        at(dve, s_psum[1], n)
                    dve.tensor_copy(k4[:], k_ps[:, 0:C * K].rearrange("p (c t) -> p c t", c=C)).then_inc(k_ready, 1)
                if output:
                    at(dve, y_psum, d)
                    if post == "gate":
                        dve.tensor_tensor(gt[:], y_ps, tile(kept, d), ALU.add).then_inc(gate_in, 1)
                        at(dve, gate_in, d)
                        dve.sem_inc(y_read, 1)
                        at(dve, gate_exp, d)
                        dve.tensor_scalar(gt[:], gt[:], 1.0, None, ALU.add).then_inc(gate_plus1, 1)
                        at(dve, gate_plus1, d)
                        dve.reciprocal(gt[:], gt[:]).then_inc(gate_ready, 1)
                        at(dve, gate_ready, d)
                        dve.tensor_tensor(gt[:], gt[:], oS[:].rearrange("t h d -> t (h d)"), ALU.mult).then_inc(gated, 1)
                        at(dve, gated, d)
                        at(dve, finished, d)
                        dve.tensor_tensor(r[:], gt[:], tile(X, d), ALU.add).then_inc(r1_ready, 1)
                        at(dve, r1_ready, d)
                        norm(r[:], d, (st1, mv1, ve1), (stats1, mean_var1, var_eps1))
                    elif post == "l3ffn":
                        at(dve, kept_ready, d)
                        dve.tensor_tensor(tile(x_after, d), y_ps, tile(kept, d), ALU.add).then_inc(y_read, 1)
                    else:
                        at(dve, kept_ready, d)
                        at(dve, finished, d)
                        dve.tensor_tensor(r[:], y_ps, tile(kept, d), ALU.add).then_inc(y_read, 1)
                        at(dve, y_read, d + 1)
                        if post == "l1x":
                            norm(r[:], d, (st1, mv1, ve1), (stats1, mean_var1, var_eps1))
                        else:
                            norm(r[:], d, (st, mv, ve), (stats, mean_var, var_eps))
                if front and small:
                    if tail:
                        at(dve, outT_psum, t)
                    else:
                        at(dve, proj_psum, f)
                    dve.tensor_tensor(U[1 - p][0:K, 2, :, 0:Dh], proj_ps[0:K, 2 * HD:3 * HD].rearrange("t (h d) -> t h d", h=H),
                                      brow[0:K, 2, :].rearrange("t (h d) -> t h d", h=H), ALU.add).then_inc(v_ready, 1)
                if main and shifted:
                    at(dve, pT_psum[1], n)
                    dve.tensor_copy(PTs[p][:, HJ:J], scores[0:K, HJ:J].rearrange("k j (c t) -> k j c t", t=T)).then_inc(pT_ready[1], 1)
                if output and two_norms:
                    at(dve, r_ready, d)
                    norm(rm[:], d, (st, mv, ve), (stats, mean_var, var_eps))
            steps(dve, step)
    s.close()


def batch_axis_attention(core):
    nc, X = core.nc, core.X
    before = nc.dram_tensor("x_by_position", (T, B, D), F32, kind="Internal").ap()
    after = nc.dram_tensor("x_by_batch", (T, B, D), F32, kind="Internal").ap()

    def reorder(name, order_out, order_in):
        s = Scope(nc, name)
        moved = s.sem("moved")
        with nc.Block() as block:
            @block.sync
            def _(sp):
                sp.dma_start(order_out, X[:]).then_inc(moved, 16)
                sp.wait_ge(moved, 16)
                sp.dma_start(X[:], order_in).then_inc(moved, 16)
                sp.wait_ge(moved, 32)
        s.close()

    def by_tile(a):
        return a.rearrange("(n g) b d -> (g b) n d", g=T // B)
    reorder("L2out", before, by_tile(before))
    attention(core, "L2self", H=16, Dh=8, Wq="L2_attn_Wq", Wk="L2_attn_Wk", Wv="L2_attn_Wv", Wo="L2_attn_WoT",
              bq="L2_attn_bq", bk="L2_attn_bk", bv="L2_attn_bv", bo="L2_attn_out_proj_bias",
              mask="mask_within", post="l2self")
    reorder("L2back", by_tile(after), after)


def expert_pass(core, name, *, w1, b1, w2, act, xT, gates):
    nc, I, X = core.nc, core.I, core.X
    s = Scope(nc, name)
    CH = 4
    N = B // CH
    w1s, w2s, b1s = s.lanes("w1", [D, F]), s.lanes("w2", [128, FC, D]), s.lanes("b1", [128, FC])
    hT = s.lanes("hT", [128, FC, CH * T])
    gy = s.lanes("gy", [T, CH, D])
    ph = s.psum("ph", [128, FC, 512])
    py = s.psum("py", [128, 2, 512])
    w_in = [s.sem(f"weights_in{k}") for k in range(LANES)]
    h_psum, h_ready, y_psum, y_gated, added = [s.sem(n) for n in ("h_psum", "h_ready", "y_psum", "y_gated", "added")]
    H0, Y0, G0, A0 = FC, 2 * N, 2, 1
    Xf, xTf = X[:].rearrange("t b d -> t (b d)"), xT[:]

    with nc.Block() as block:
        @block.sync
        def _(sp):
            with sp.Fori(0, E // LANES) as i:
                for lane in range(LANES):
                    e = i * LANES + lane
                    sp.wait_ge(y_psum, (e + 1) * N)
                    with nc.allow_non_contiguous_dma(reason="a bias column"):
                        sp.dma_start(w1s[lane][:], I[w1][bass.ds(e, 1)].rearrange("a d f -> d (a f)")).then_inc(w_in[lane], 16)
                        sp.dma_start(w2s[lane][:], I[w2][bass.ds(e, 1)].rearrange("a (c p) d -> p (a c) d", p=128)).then_inc(w_in[lane], 16)
                        sp.dma_start(b1s[lane][:], I[b1][bass.ds(e, 1)].rearrange("a (c p) -> p (a c)", p=128)).then_inc(w_in[lane], 16)

        @block.tensor
        def _(pe):
            pe.sem_inc(y_psum, Y0)
            pe.sem_inc(h_ready, H0)
            with pe.Fori(0, E // LANES) as i:
                for lane in range(LANES):
                    e = i * LANES + lane
                    with pe.Fori(0, N // 2) as c2:
                        at(pe, w_in[lane], i, 48)
                        for par in range(2):
                            m = e * N + c2 * 2 + par
                            for f in range(FC):
                                pe.wait_ge(h_ready, m * FC + f + 1)
                                pe.matmul(ph[:, f, :], w1s[lane][:, f * 128:(f + 1) * 128],
                                          xTf[:, bass.ds((c2 * 2 + par) * (CH * T), CH * T)], start=True, stop=True).then_inc(h_psum, 1)
                        for par in range(2):
                            m = e * N + c2 * 2 + par
                            pe.wait_ge(h_ready, m * FC + FC + H0)
                            pe.wait_ge(y_gated, m + 1)
                            for b in range(CH):
                                for f in range(FC):
                                    last = pe.matmul(py[:, par, b * D:(b + 1) * D], hT[par][:, f, b * T:(b + 1) * T],
                                                     w2s[lane][:, f, :], start=f == 0, stop=f == FC - 1)
                            last.then_inc(y_psum, 1)

        @block.scalar
        def _(act_eng):
            with act_eng.Fori(0, E // LANES) as i:
                for lane in range(LANES):
                    e = i * LANES + lane
                    with act_eng.Fori(0, N // 2) as c2:
                        at(act_eng, w_in[lane], i, 48)
                        for par in range(2):
                            m = e * N + c2 * 2 + par
                            act_eng.wait_ge(y_psum, m - 1 + Y0)
                            for f in range(FC):
                                act_eng.wait_ge(h_psum, m * FC + f + 1)
                                act_eng.activation(hT[par][:, f, :], ph[:, f, :], act, bias=b1s[lane][:, f:f + 1]).then_inc(h_ready, 1)

        @block.vector
        def _(dve):
            dve.sem_inc(y_gated, G0)
            dve.sem_inc(added, A0)
            with dve.Fori(0, E * N // 8) as i:
                for k in range(8):
                    m = i * 8 + k
                    par = k % 2
                    dve.wait_ge(y_psum, m + 1 + Y0)
                    dve.wait_ge(added, m + A0)
                    dve.tensor_tensor(gy[par][:], py[:, par, :].rearrange("t (b d) -> t b d", b=CH),
                                      gates[:].rearrange("t e b -> t (e b)")[:, bass.ds(m * CH, CH)].unsqueeze(2).to_broadcast([T, CH, D]),
                                      ALU.mult).then_inc(y_gated, 1)
                    dve.wait_ge(y_gated, m + 1 + G0)
                    xc = Xf[:, k * CH * D:(k + 1) * CH * D]
                    dve.tensor_tensor(xc, xc, gy[par][:].rearrange("t b d -> t (b d)"), ALU.add).then_inc(added, 1)
    s.close()


def norm_all(core, name):
    nc, X = core.nc, core.X
    s = Scope(nc, name)
    sq = s.sb("sq", [T, B, D])
    mean, ve, rstd = s.sb("mean", [T, B]), s.sb("ve", [T, B]), s.sb("rstd", [T, B])
    step, var_eps, rstd_ready = s.sem("step"), s.sem("var_eps"), s.sem("rstd_ready")
    with nc.Block() as block:
        @block.gpsimd
        def _(pool):
            pool.wait_ge(var_eps, 1)
            pool.tensor_tensor(rstd[:], ve[:], core.neghalf[:, 0:B], ALU.pow).then_inc(rstd_ready, 1)

        @block.vector
        def _(dve):
            dve.tensor_reduce(mean[:], X[:], AX.X, ALU.add).then_inc(step, 1)
            dve.wait_ge(step, 1)
            dve.tensor_scalar(mean[:], mean[:], 1.0 / D, None, ALU.mult).then_inc(step, 1)
            dve.wait_ge(step, 2)
            dve.tensor_tensor(X[:], X[:], mean[:].unsqueeze(2).to_broadcast([T, B, D]), ALU.subtract).then_inc(step, 1)
            dve.wait_ge(step, 3)
            dve.tensor_tensor(sq[:], X[:], X[:], ALU.mult).then_inc(step, 1)
            dve.wait_ge(step, 4)
            dve.tensor_reduce(ve[:], sq[:], AX.X, ALU.add).then_inc(step, 1)
            dve.wait_ge(step, 5)
            dve.tensor_scalar(ve[:], ve[:], 1.0 / D, LN_EPS, ALU.mult, ALU.add).then_inc(var_eps, 1)
            dve.wait_ge(rstd_ready, 1)
            dve.tensor_tensor(X[:], X[:], rstd[:].unsqueeze(2).to_broadcast([T, B, D]), ALU.mult).then_inc(step, 1)
            dve.wait_ge(step, 6)
    s.close()


def route(core, name, xT, gates, *, kind, top, X1=None):
    nc, I, X = core.nc, core.I, core.X
    s = Scope(nc, name)
    NK = E if top == 1 else 2
    loads = []

    def tile(tag, shape, src):
        t = s.sb(tag, shape)
        loads.append((t[:], src))
        return t

    b2 = tile("b2", [E, D], I[{"L0": "L0_ffn_b2", "L1": "L1_ffn_b2", "L3": "L3_ffn_fc2_b"}[kind]])
    iota = tile("iota", [T, E], row_bc(I["iota8"]))
    normed_input = kind != "L0"
    if kind == "L0":
        w_red = tile("w_red", [D, 16], I["L0_ffn_w_red"])
        wgT = tile("wgT", [16, E], I["L0_ffn_wg"].rearrange("e g -> g e"))
        wsq, wnorm, wgn = s.sb("wsq", [16, E]), s.sb("wnorm", [16, E]), s.sb("wgn", [16, E])
        redT = s.lanes("redT", [16, T])
    elif kind == "L1":
        wr = tile("wr", [D, E], I["L1_ffn_Wr"])
        br = tile("br", [T, E], row_bc(I["L1_ffn_br"]))
        gam, bet = tile("gam", [T, D], row_bc(I["L1_ffn_ln_g"])), tile("bet", [T, D], row_bc(I["L1_ffn_ln_b"]))
    else:
        wr = tile("wr", [D, E], I["L3_ffn_gate_W"])
        gam, bet = tile("gam", [T, D], row_bc(I["L3_ffn_ln2_w"])), tile("bet", [T, D], row_bc(I["L3_ffn_ln2_b"]))
    xs, xn, xTs, gT = s.lanes("xs", [T, D]), s.lanes("xn", [T, D]), s.lanes("xTs", [D, T]), s.lanes("gT", [E, T])
    lg, m8, nmx = s.lanes("lg", [T, E]), s.lanes("m8", [T, 8]), s.lanes("nmx", [T, 1])
    idx, idf, ex = s.lanes("idx", [T, 8], U32), s.lanes("idf", [T, 8]), s.lanes("ex", [T, 8])
    sm, pr, g8, g8b = s.lanes("sm", [T, 1]), s.lanes("pr", [T, 8]), s.lanes("g8", [T, E]), s.lanes("g8b", [T, E])
    st, mv, ve, rs, xb = s.lanes("st", [T, 6]), s.lanes("mv", [T, 2]), s.lanes("ve", [T, 1]), s.lanes("rs", [T, 1]), s.lanes("xb", [T, D])
    ps = [s.psum(f"ps{lane}", [128, 4, 512]) for lane in range(LANES)]
    names = ("weights_in lane_free x_copied x_psum xT_ready xnT_ready red_psum red_ready logits_psum logits_ready sorted negmax "
             "index_ready index_float exp_ready recip_ready prob_ready gate1 gate2 gate_ready gT_psum gT_ready bias_psum "
             "biased stats mean_var var_eps rstd normed scaled offset wsq_ready wnorm_psum wnorm_safe wnorm_pow wg_ready gate_stored")
    S_ = type("Ready", (), {n: s.sem(n) for n in names.split()})
    with nc.Block() as block:
        @block.sync
        def _(sp):
            with nc.allow_non_contiguous_dma(reason="small weights, once"):
                for dst, src in loads:
                    sp.dma_start(dst, src).then_inc(S_.weights_in, 16)

        @block.gpsimd
        def _(pool):
            if kind == "L0":
                pool.wait_ge(S_.wnorm_safe, 1)
                pool.tensor_tensor(wnorm[:], wnorm[:], core.neghalf[0:16, 0:E], ALU.pow).then_inc(S_.wnorm_pow, 1)
            pool.sem_inc(S_.lane_free, LANES)
            with pool.Fori(0, STEPS) as i:
                for lane in range(LANES):
                    n = i * LANES + lane
                    at(pool, S_.lane_free, n)
                    pool.tensor_copy(xs[lane][:], (X1 or X)[:, bass.ds(n, 1), :].rearrange("t a d -> t (a d)")).then_inc(S_.x_copied, 1)
                if normed_input:
                    for lane in range(LANES):
                        at(pool, S_.var_eps, i * LANES + lane)
                        pool.tensor_tensor(rs[lane][:], ve[lane][:], core.neghalf[:, 0:1], ALU.pow).then_inc(S_.rstd, 1)

        @block.tensor
        def _(pe):
            pe.wait_ge(S_.weights_in, 16 * len(loads))
            if kind == "L0":
                pe.wait_ge(S_.wsq_ready, 1)
                pe.matmul(ps[0][0:16, 0, 0:E], core.ones[0:16, 0:16], wsq[:], start=True, stop=True).then_inc(S_.wnorm_psum, 1)
                pe.wait_ge(S_.wg_ready, 1)
            with pe.Fori(0, STEPS) as i:
                for lane in range(LANES):
                    n = i * LANES + lane
                    if normed_input:
                        at(pe, S_.offset, n)
                        pe.transpose(ps[lane][:, 0, 128:256], xn[lane][:], core.ident[:])
                    at(pe, S_.x_copied, n)
                    pe.transpose(ps[lane][:, 0, 0:T], xs[lane][:], core.ident[:]).then_inc(S_.x_psum, 1)
                if kind == "L0":
                    for lane in range(LANES):
                        at(pe, S_.xT_ready, i * LANES + lane)
                        pe.matmul(ps[lane][0:16, 1, 0:T], w_red[:], xTs[lane][:], start=True, stop=True).then_inc(S_.red_psum, 1)
                for lane in range(LANES):
                    n = i * LANES + lane
                    if kind == "L0":
                        at(pe, S_.red_ready, n)
                        pe.matmul(ps[lane][:, 2, 0:E], redT[lane][:], wgn[:], start=True, stop=True).then_inc(S_.logits_psum, 1)
                    else:
                        at(pe, S_.xT_ready, n)
                        pe.matmul(ps[lane][:, 2, 0:E], xTs[lane][:], wr[:], start=True, stop=True).then_inc(S_.logits_psum, 1)
                for lane in range(LANES):
                    at(pe, S_.gate_ready, i * LANES + lane)
                    pe.transpose(ps[lane][0:E, 1, 128:256], g8[lane][:], core.ident[:]).then_inc(S_.gT_psum, 1)
                for lane in range(LANES):
                    at(pe, S_.gT_ready, i * LANES + lane)
                    pe.matmul(ps[lane][:, 3, 0:D], gT[lane][:], b2[:], start=True, stop=True).then_inc(S_.bias_psum, 1)

        @block.scalar
        def _(act):
            with act.Fori(0, STEPS) as i:
                for lane in range(LANES):
                    n = i * LANES + lane
                    at(act, S_.x_psum, n)
                    logits_of = ps[lane][:, 0, 128:256] if kind == "L3" else ps[lane][:, 0, 0:T]
                    experts_of = ps[lane][:, 0, 128:256] if normed_input else ps[lane][:, 0, 0:T]
                    act.activation(xTs[lane][:], logits_of, ACT.Copy).then_inc(S_.xT_ready, 1)
                    act.activation(xT[:, bass.ds(n * T, T)], experts_of, ACT.Copy).then_inc(S_.xnT_ready, 1)
                if kind == "L0":
                    for lane in range(LANES):
                        at(act, S_.red_psum, i * LANES + lane)
                        act.activation(redT[lane][:], ps[lane][0:16, 1, 0:T], ACT.Copy).then_inc(S_.red_ready, 1)
                for lane in range(LANES):
                    at(act, S_.negmax, i * LANES + lane)
                    act.activation(ex[lane][:, 0:NK], m8[lane][:, 0:NK], ACT.Exp, bias=nmx[lane][:, 0:1],
                                   accum_out=sm[lane][:]).then_inc(S_.exp_ready, 1)
                for lane in range(LANES):
                    at(act, S_.gT_psum, i * LANES + lane)
                    act.activation(gT[lane][:], ps[lane][0:E, 1, 128:256], ACT.Copy).then_inc(S_.gT_ready, 1)

        @block.vector
        def _(dve):
            dve.wait_ge(S_.weights_in, 16 * len(loads))
            if kind == "L0":
                dve.tensor_tensor(wsq[:], wgT[:], wgT[:], ALU.mult).then_inc(S_.wsq_ready, 1)
                dve.wait_ge(S_.wnorm_psum, 1)
                dve.tensor_scalar(wnorm[:], ps[0][0:16, 0, 0:E], 1e-8, None, ALU.max).then_inc(S_.wnorm_safe, 1)
                dve.wait_ge(S_.wnorm_pow, 1)
                dve.tensor_tensor(wgn[:], wgT[:], wnorm[:], ALU.mult).then_inc(S_.wg_ready, 1)
            with dve.Fori(0, STEPS) as i:
                if normed_input:
                    for lane in range(LANES):
                        n = i * LANES + lane
                        at(dve, S_.x_copied, n)
                        dve.bn_stats(st[lane][:], xs[lane][:]).then_inc(S_.stats, 1)
                        at_alone(dve, S_.stats, n, s.passed)
                        dve.bn_aggr(mv[lane][:], st[lane][:]).then_inc(S_.mean_var, 1)
                        at(dve, S_.mean_var, n)
                        dve.tensor_scalar(ve[lane][:], mv[lane][:, 1:2], LN_EPS, None, ALU.add).then_inc(S_.var_eps, 1)
                    for lane in range(LANES):
                        n = i * LANES + lane
                        at(dve, S_.rstd, n)
                        dve.tensor_scalar(xn[lane][:], xs[lane][:], mv[lane][:, 0:1], rs[lane][:, 0:1], ALU.subtract, ALU.mult).then_inc(S_.normed, 1)
                        at(dve, S_.normed, n)
                        dve.tensor_tensor(xn[lane][:], xn[lane][:], gam[:], ALU.mult).then_inc(S_.scaled, 1)
                        at(dve, S_.scaled, n)
                        dve.tensor_tensor(xn[lane][:], xn[lane][:], bet[:], ALU.add).then_inc(S_.offset, 1)
                for lane in range(LANES):
                    n = i * LANES + lane
                    at(dve, S_.logits_psum, n)
                    if kind == "L1":
                        dve.tensor_tensor(lg[lane][:], ps[lane][:, 2, 0:E], br[:], ALU.add).then_inc(S_.logits_ready, 1)
                    else:
                        dve.tensor_copy(lg[lane][:], ps[lane][:, 2, 0:E]).then_inc(S_.logits_ready, 1)
                    at_alone(dve, S_.logits_ready, n, s.passed)
                    dve.max(m8[lane][:], lg[lane][:]).then_inc(S_.sorted, 1)
                    at(dve, S_.sorted, n)
                    dve.tensor_scalar(nmx[lane][:], m8[lane][:, 0:1], -1.0, None, ALU.mult).then_inc(S_.negmax, 1)
                    dve.max_index(idx[lane][:], m8[lane][:], lg[lane][:]).then_inc(S_.index_ready, 1)
                    at(dve, S_.index_ready, n)
                    dve.tensor_copy(idf[lane][:], idx[lane][:]).then_inc(S_.index_float, 1)
                for lane in range(LANES):
                    n = i * LANES + lane
                    at(dve, S_.exp_ready, n)
                    dve.reciprocal(sm[lane][:], sm[lane][:]).then_inc(S_.recip_ready, 1)
                    at(dve, S_.recip_ready, n)
                    dve.tensor_scalar(pr[lane][:, 0:top], ex[lane][:, 0:top], sm[lane][:, 0:1], None, ALU.mult).then_inc(S_.prob_ready, 1)
                    at(dve, S_.prob_ready, n)
                    dve.tensor_scalar(g8[lane][:], iota[:], idf[lane][:, 0:1], pr[lane][:, 0:1], ALU.is_equal, ALU.mult).then_inc(S_.gate_ready if top == 1 else S_.gate1, 1)
                    if top == 2:
                        dve.tensor_scalar(g8b[lane][:], iota[:], idf[lane][:, 1:2], pr[lane][:, 1:2], ALU.is_equal, ALU.mult).then_inc(S_.gate2, 1)
                        at(dve, S_.gate2, n)
                        dve.tensor_tensor(g8[lane][:], g8[lane][:], g8b[lane][:], ALU.add).then_inc(S_.gate_ready, 1)
                    at(dve, S_.gate_ready, n)
                    dve.tensor_copy(gates[:, :, bass.ds(n, 1)], g8[lane][:].unsqueeze(2)).then_inc(S_.gate_stored, 1)
                for lane in range(LANES):
                    n = i * LANES + lane
                    at(dve, S_.bias_psum, n)
                    dve.tensor_tensor(xb[lane][:], ps[lane][:, 3, 0:D], xs[lane][:], ALU.add).then_inc(S_.biased, 1)
                    at(dve, S_.biased, n)
                    row = X[:, bass.ds(n, 1), :].rearrange("t a d -> t (a d)")
                    if X1 is None:
                        dve.tensor_copy(row, xb[lane][:]).then_inc(S_.lane_free, 1)
                    else:
                        dve.tensor_tensor(row, row, xb[lane][:], ALU.add).then_inc(S_.lane_free, 1)
    s.close()


def experts_top1(core, name):
    nc = core.nc
    kind = name[:2]
    with ExitStack() as stack:
        xT = stack.enter_context(nc.sbuf_tensor(f"{name}_xT", [D, B * T], F32))
        gates = stack.enter_context(nc.sbuf_tensor(f"{name}_gates", [T, E, B], F32))
        route(core, f"{name}_route", xT, gates, kind=kind, top=1)
        w = ("w1", "b1", "w2") if kind == "L0" else ("W1", "b1", "W2")
        expert_pass(core, f"{name}_pass", w1=f"{kind}_ffn_{w[0]}", b1=f"{kind}_ffn_{w[1]}", w2=f"{kind}_ffn_{w[2]}",
                    act=ACT.Gelu if kind == "L0" else ACT.Relu, xT=xT, gates=gates)
    norm_all(core, f"{name}_norm")


def block_experts(core):
    nc = core.nc
    with ExitStack() as stack:
        X1 = stack.enter_context(nc.sbuf_tensor("X1", [T, B, D], F32))
        attention(core, "L3self", H=16, Dh=8, Wq="L3_ffn_Wq", Wk="L3_ffn_Wk", Wv="L3_ffn_Wv", Wo="L3_ffn_Wo",
                  bq="L3_ffn_bq", bk="L3_ffn_bk", bv="L3_ffn_bv", bo="L3_ffn_bo", mask="mask_causal",
                  post="l3ffn", x_after=X1)
        xT = stack.enter_context(nc.sbuf_tensor("L3ffn_xT", [D, B * T], F32))
        gates = stack.enter_context(nc.sbuf_tensor("L3ffn_gates", [T, E, B], F32))
        route(core, "L3ffn_route", xT, gates, kind="L3", top=2, X1=X1)
        expert_pass(core, "L3ffn_pass", w1="L3_ffn_fc1T", b1="L3_ffn_fc1_b", w2="L3_ffn_fc2T", act=ACT.Gelu,
                    xT=xT, gates=gates)
    norm_all(core, "L3ffn_norm")


def wkv_mix(core):
    nc, I, X = core.nc, core.I, core.X
    s = Scope(nc, "wkv")
    loads = []

    def tile(tag, shape, src):
        t = s.sb(tag, shape)
        loads.append((t[:], src))
        return t

    mix = {c: tile(f"mix_{c}", [D, 1], col(I[f"L1_attn_time_mix_{c}"])) for c in "kvr"}
    W = {c: tile(f"W{c}", [D, D], I[f"L1_attn_W{c}T"]) for c in "kvr"}
    Wo = tile("Wo", [D, D], I["L1_attn_WoT"])
    decay_in = tile("decay_in", [D, 1], col(I["L1_attn_time_decay"]))
    first = tile("first", [D, 1], col(I["L1_attn_time_first"]))
    decay, decays = s.sb("decay", [D, 1]), s.sb("decays", [D, T])
    rest = {c: s.sb(f"rest_{c}", [D, 1]) for c in "kvr"}
    START = -1e38

    xs, r = s.lanes("xs", [T, D]), s.lanes("r", [T, D])
    xT = s.lanes("xT", [D, T + 1])
    mixed = {c: s.lanes(f"mixed_{c}", [D, T]) for c in "kvr"}
    shifted = {c: s.lanes(f"shifted_{c}", [D, T]) for c in "kvr"}
    k, v, sr = s.lanes("k", [D, T]), s.lanes("v", [D, T]), s.lanes("sr", [D, T])
    pp, aa, bb = s.lanes("pp", [D, T + 1]), s.lanes("aa", [D, T + 1]), s.lanes("bb", [D, T + 1])
    ex = s.lanes("ex", [D, 4, T])
    ww, p = s.lanes("ww", [D, T]), s.lanes("p", [D, T])
    ev, num, den, y = s.lanes("ev", [D, 2, T]), s.lanes("num", [D, T]), s.lanes("den", [D, T]), s.lanes("y", [D, T])
    st, mv, ve, rs = s.lanes("st", [T, 6]), s.lanes("mv", [T, 2]), s.lanes("ve", [T, 1]), s.lanes("rs", [T, 1])
    ps = [s.psum(f"ps{lane}", [128, 4, 512]) for lane in range(LANES)]
    names = ("weights_in lane_free starts_set decay_exp decay_neg decays_ready rests_ready x_copied x_psum xT_ready mixed_ready "
             "rest_mixed kvr_psum kv_ready r_exp r_plus1 r_ready max_scanned exps_in exps_ready ev_ready sums_scanned ww_ready "
             "p_ready num1 num2 den1 den2 den_inv y_scaled y_ready out_psum sum_ready stats mean_var var_eps rstd")
    S_ = type("Ready", (), {n: s.sem(n) for n in names.split()})
    with nc.Block() as block:
        @block.sync
        def _(sp):
            with nc.allow_non_contiguous_dma(reason="small weights, once"):
                for dst, src in loads:
                    sp.dma_start(dst, src).then_inc(S_.weights_in, 16)

        @block.gpsimd
        def _(pool):
            for lane in range(LANES):
                pool.memset(xT[lane][:, 0:1], 0.0).then_inc(S_.starts_set, 1)
                pool.memset(pp[lane][:, 0:1], START).then_inc(S_.starts_set, 1)
                pool.memset(aa[lane][:, 0:1], 0.0).then_inc(S_.starts_set, 1)
                pool.memset(bb[lane][:, 0:1], 0.0).then_inc(S_.starts_set, 1)
            pool.sem_inc(S_.lane_free, LANES)
            with pool.Fori(0, STEPS) as i:
                for lane in range(LANES):
                    n = i * LANES + lane
                    at(pool, S_.lane_free, n)
                    pool.tensor_copy(xs[lane][:], X[:, bass.ds(n, 1), :].rearrange("t a d -> t (a d)")).then_inc(S_.x_copied, 1)
                for lane in range(LANES):
                    at(pool, S_.var_eps, i * LANES + lane)
                    pool.tensor_tensor(rs[lane][:], ve[lane][:], core.neghalf[:, 0:1], ALU.pow).then_inc(S_.rstd, 1)

        @block.tensor
        def _(pe):
            pe.wait_ge(S_.weights_in, 16 * len(loads))
            with pe.Fori(0, STEPS) as i:
                for lane in range(LANES):
                    at(pe, S_.x_copied, i * LANES + lane)
                    pe.transpose(ps[lane][:, 0, 0:T], xs[lane][:], core.ident[:]).then_inc(S_.x_psum, 1)
                for lane in range(LANES):
                    at(pe, S_.mixed_ready, i * LANES + lane, 3)
                    for j, c in enumerate("kvr"):
                        last = pe.matmul(ps[lane][:, 1, j * T:(j + 1) * T], W[c][:], mixed[c][lane][:], start=True, stop=True)
                    last.then_inc(S_.kvr_psum, 1)
                for lane in range(LANES):
                    at(pe, S_.y_ready, i * LANES + lane)
                    pe.matmul(ps[lane][:, 2, 0:D], y[lane][:], Wo[:], start=True, stop=True).then_inc(S_.out_psum, 1)

        @block.scalar
        def _(act):
            act.wait_ge(S_.weights_in, 16 * len(loads))
            act.activation(decay[:], decay_in[:], ACT.Exp).then_inc(S_.decay_exp, 1)
            act.wait_ge(S_.starts_set, 4 * LANES)
            with act.Fori(0, STEPS) as i:
                for lane in range(LANES):
                    at(act, S_.x_psum, i * LANES + lane)
                    act.activation(xT[lane][:, 1:T + 1], ps[lane][:, 0, 0:T], ACT.Copy).then_inc(S_.xT_ready, 1)
                for lane in range(LANES):
                    at(act, S_.kvr_psum, i * LANES + lane)
                    act.activation(k[lane][:], ps[lane][:, 1, 0:T], ACT.Copy).then_inc(S_.kv_ready, 1)
                    act.activation(v[lane][:], ps[lane][:, 1, T:2 * T], ACT.Copy).then_inc(S_.kv_ready, 1)
                    act.activation(sr[lane][:], ps[lane][:, 1, 2 * T:3 * T], ACT.Exp, scale=-1.0).then_inc(S_.r_exp, 1)
                for lane in range(LANES):
                    at(act, S_.exps_in, i * LANES + lane, 4)
                    act.activation(ex[lane][:], ex[lane][:], ACT.Exp).then_inc(S_.exps_ready, 1)

        @block.vector
        def _(dve):
            dve.wait_ge(S_.starts_set, 4 * LANES)
            dve.wait_ge(S_.decay_exp, 1)
            dve.tensor_scalar(decay[:], decay[:], -1.0, None, ALU.mult).then_inc(S_.decay_neg, 1)
            dve.wait_ge(S_.decay_neg, 1)
            dve.tensor_scalar(decays[:], core.ones[:], decay[:, 0:1], None, ALU.mult).then_inc(S_.decays_ready, 1)
            for c in "kvr":
                dve.tensor_scalar(rest[c][:], mix[c][:], -1.0, 1.0, ALU.mult, ALU.add).then_inc(S_.rests_ready, 1)
            dve.wait_ge(S_.decays_ready, 1)
            dve.wait_ge(S_.rests_ready, 3)
            with dve.Fori(0, STEPS) as i:
                for lane in range(LANES):
                    n = i * LANES + lane
                    at(dve, S_.xT_ready, n)
                    for c in "kvr":
                        dve.tensor_scalar(shifted[c][lane][:], xT[lane][:, 0:T], rest[c][:, 0:1], None, ALU.mult).then_inc(S_.rest_mixed, 1)
                    at(dve, S_.rest_mixed, n, 3)
                    for c in "kvr":
                        dve.scalar_tensor_tensor(out=mixed[c][lane][:], in0=xT[lane][:, 1:T + 1], scalar=mix[c][:, 0:1],
                                                 in1=shifted[c][lane][:], op0=ALU.mult, op1=ALU.add).then_inc(S_.mixed_ready, 1)
                for lane in range(LANES):
                    n = i * LANES + lane
                    at(dve, S_.kv_ready, n, 2)
                    dve.tensor_tensor_scan(pp[lane][:, 1:T + 1], decays[:], k[lane][:], START, ALU.add, ALU.max).then_inc(S_.max_scanned, 1)
                    dve.tensor_scalar(ww[lane][:], k[lane][:], first[:, 0:1], None, ALU.add).then_inc(S_.ww_ready, 1)
                    at(dve, S_.ww_ready, n)
                    at(dve, S_.max_scanned, n)
                    dve.tensor_tensor(p[lane][:], pp[lane][:, 0:T], ww[lane][:], ALU.max).then_inc(S_.p_ready, 1)
                    dve.scalar_tensor_tensor(out=ex[lane][:, 0, :], in0=pp[lane][:, 0:T], scalar=decay[:, 0:1],
                                             in1=pp[lane][:, 1:T + 1], op0=ALU.add, op1=ALU.subtract).then_inc(S_.exps_in, 1)
                    dve.tensor_tensor(ex[lane][:, 1, :], k[lane][:], pp[lane][:, 1:T + 1], ALU.subtract).then_inc(S_.exps_in, 1)
                    at(dve, S_.p_ready, n)
                    dve.tensor_tensor(ex[lane][:, 2, :], pp[lane][:, 0:T], p[lane][:], ALU.subtract).then_inc(S_.exps_in, 1)
                    dve.tensor_tensor(ex[lane][:, 3, :], ww[lane][:], p[lane][:], ALU.subtract).then_inc(S_.exps_in, 1)
                for lane in range(LANES):
                    n = i * LANES + lane
                    at(dve, S_.exps_ready, n)
                    dve.tensor_tensor(ev[lane][:, 0, :], ex[lane][:, 1, :], v[lane][:], ALU.mult).then_inc(S_.ev_ready, 1)
                    dve.tensor_tensor(ev[lane][:, 1, :], ex[lane][:, 3, :], v[lane][:], ALU.mult).then_inc(S_.ev_ready, 1)
                    dve.tensor_tensor_scan(bb[lane][:, 1:T + 1], ex[lane][:, 0, :], ex[lane][:, 1, :], 0.0, ALU.mult, ALU.add).then_inc(S_.sums_scanned, 1)
                    at(dve, S_.ev_ready, n, 2)
                    dve.tensor_tensor_scan(aa[lane][:, 1:T + 1], ex[lane][:, 0, :], ev[lane][:, 0, :], 0.0, ALU.mult, ALU.add).then_inc(S_.sums_scanned, 1)
                    at(dve, S_.sums_scanned, n, 2)
                    dve.tensor_tensor(den[lane][:], ex[lane][:, 2, :], bb[lane][:, 0:T], ALU.mult).then_inc(S_.den1, 1)
                    dve.tensor_tensor(num[lane][:], ex[lane][:, 2, :], aa[lane][:, 0:T], ALU.mult).then_inc(S_.num1, 1)
                    at(dve, S_.den1, n)
                    dve.tensor_tensor(den[lane][:], den[lane][:], ex[lane][:, 3, :], ALU.add).then_inc(S_.den2, 1)
                    at(dve, S_.num1, n)
                    dve.tensor_tensor(num[lane][:], num[lane][:], ev[lane][:, 1, :], ALU.add).then_inc(S_.num2, 1)
                    at(dve, S_.r_exp, n)
                    dve.tensor_scalar(sr[lane][:], sr[lane][:], 1.0, None, ALU.add).then_inc(S_.r_plus1, 1)
                    at(dve, S_.r_plus1, n)
                    dve.reciprocal(sr[lane][:], sr[lane][:]).then_inc(S_.r_ready, 1)
                    at(dve, S_.den2, n)
                    dve.reciprocal(den[lane][:], den[lane][:]).then_inc(S_.den_inv, 1)
                    at(dve, S_.den_inv, n)
                    at(dve, S_.num2, n)
                    dve.tensor_tensor(num[lane][:], num[lane][:], den[lane][:], ALU.mult).then_inc(S_.y_scaled, 1)
                    at(dve, S_.r_ready, n)
                    at(dve, S_.y_scaled, n)
                    dve.tensor_tensor(y[lane][:], num[lane][:], sr[lane][:], ALU.mult).then_inc(S_.y_ready, 1)
                for lane in range(LANES):
                    n = i * LANES + lane
                    at(dve, S_.out_psum, n)
                    dve.tensor_tensor(r[lane][:], ps[lane][:, 2, 0:D], xs[lane][:], ALU.add).then_inc(S_.sum_ready, 1)
                    at(dve, S_.sum_ready, n)
                    dve.bn_stats(st[lane][:], r[lane][:]).then_inc(S_.stats, 1)
                    at_alone(dve, S_.stats, n, s.passed)
                    dve.bn_aggr(mv[lane][:], st[lane][:]).then_inc(S_.mean_var, 1)
                    at(dve, S_.mean_var, n)
                    dve.tensor_scalar(ve[lane][:], mv[lane][:, 1:2], LN_EPS, None, ALU.add).then_inc(S_.var_eps, 1)
                for lane in range(LANES):
                    n = i * LANES + lane
                    at(dve, S_.rstd, n)
                    dve.tensor_scalar(X[:, bass.ds(n, 1), :].rearrange("t a d -> t (a d)"), r[lane][:], mv[lane][:, 0:1],
                                      rs[lane][:, 0:1], ALU.subtract, ALU.mult).then_inc(S_.lane_free, 1)
    s.close()


def soft_experts(core):
    nc, I, X = core.nc, core.I, core.X
    NS = I["L2_ffn_slot_embeds"].shape[1]
    SC = E * NS // 128
    with ExitStack() as stack:
        snT = stack.enter_context(nc.sbuf_tensor("snT", [D, E * NS], F32))
        slots = stack.enter_context(nc.sbuf_tensor("slotsT", [D, E, B, NS], F32))
        slot_keys(core, snT, SC)
        dispatch_or_combine(core, "dispatch", snT, slots, SC, NS, combine=False)
        slot_pass(core, slots, NS)
        dispatch_or_combine(core, "combine", snT, slots, SC, NS, combine=True)


def slot_keys(core, snT, SC):
    nc, I = core.nc, core.I
    s = Scope(nc, "slotkeys")
    emb, sq = s.sb("emb", [128, SC, D]), s.sb("sq", [128, SC, D])
    gam = s.sb("gam", [128, D])
    ss = s.sb("ss", [128, SC])
    ps = s.psum("ps", [128, SC, 128])
    loaded, step, safe, inv, scaled, turned, done = [s.sem(n) for n in ("loaded", "step", "safe", "inverse", "scaled", "turned", "done")]
    with nc.Block() as block:
        @block.sync
        def _(sp):
            sp.dma_start(emb[:], I["L2_ffn_slot_embeds"].rearrange("e s d -> (e s) d").rearrange("(c p) d -> p c d", p=128)).then_inc(loaded, 16)
            sp.dma_start(gam[:], row_bc(I["L2_ffn_slot_norm_gamma"])).then_inc(loaded, 16)

        @block.gpsimd
        def _(pool):
            pool.wait_ge(safe, 1)
            pool.tensor_tensor(ss[:], ss[:], core.neghalf[:, 0:SC], ALU.pow).then_inc(inv, 1)

        @block.tensor
        def _(pe):
            pe.wait_ge(scaled, 1)
            for c in range(SC):
                last = pe.transpose(ps[:, c, :], emb[:, c, :], core.ident[:])
            last.then_inc(turned, 1)

        @block.vector
        def _(dve):
            dve.wait_ge(loaded, 32)
            dve.tensor_tensor(sq[:], emb[:], emb[:], ALU.mult).then_inc(step, 1)
            dve.wait_ge(step, 1)
            dve.tensor_reduce(ss[:], sq[:], AX.X, ALU.add).then_inc(step, 1)
            dve.wait_ge(step, 2)
            dve.tensor_scalar(ss[:], ss[:], 1e-24, None, ALU.max).then_inc(safe, 1)
            dve.wait_ge(inv, 1)
            dve.tensor_tensor(emb[:], emb[:], ss[:].unsqueeze(2).to_broadcast([128, SC, D]), ALU.mult).then_inc(step, 1)
            dve.wait_ge(step, 3)
            dve.tensor_scalar(emb[:], emb[:], float(D) ** 0.5, None, ALU.mult).then_inc(step, 1)
            dve.wait_ge(step, 4)
            dve.tensor_tensor(emb[:], emb[:], gam[:].unsqueeze(1).to_broadcast([128, SC, D]), ALU.mult).then_inc(scaled, 1)

        @block.scalar
        def _(act):
            act.wait_ge(turned, 1)
            act.activation(snT[:], ps[:].rearrange("p c s -> p (c s)"), ACT.Copy).then_inc(done, 1)
            act.wait_ge(done, 1)
    s.close()


def dispatch_or_combine(core, name, snT, slots, SC, NS, *, combine):
    nc, I, X = core.nc, core.I, core.X
    s = Scope(nc, name)
    gam = s.sb("gam", [T, D])
    xs, sq, xn, xnT = s.lanes("xs", [T, D]), s.lanes("sq", [T, D]), s.lanes("xn", [T, D]), s.lanes("xnT", [D, T])
    ss = s.lanes("ss", [T, 1])
    rs = s.lanes("rs", [T, 1])
    mx, zz = s.lanes("mx", [128, SC]), s.lanes("zz", [128, SC])
    P = s.lanes("P", [128, SC, 128])
    PT = s.lanes("PT", [128, SC, 128])
    ps = [s.psum(f"ps{lane}", [128, 4, 512]) for lane in range(LANES)]
    r, st, mv, ve = s.lanes("r", [T, D]), s.lanes("st", [T, 6]), s.lanes("mv", [T, 2]), s.lanes("ve", [T, 1])
    eT, eo = (s.lanes("eT", [D, E, NS]), s.lanes("eo", [128, SC, D])) if combine else (None, None)
    names = ("gamma_in lane_free x_copied squared square_sum sum_safe inv_norm unit scaled x_normed x_psum xT_ready logits_psum "
             "max_ready shifted exp_ready sum_ready recip_ready weights_ready turned_psum turned_ready out_psum slots_copied "
             "eo_psum eo_ready out_scaled r_ready stats mean_var var_eps rstd")
    S_ = type("Ready", (), {n: s.sem(n) for n in names.split()})
    with nc.Block() as block:
        @block.sync
        def _(sp):
            sp.dma_start(gam[:], row_bc(I["L2_ffn_norm_gamma"])).then_inc(S_.gamma_in, 16)

        @block.gpsimd
        def _(pool):
            pool.sem_inc(S_.lane_free, LANES)
            with pool.Fori(0, STEPS) as i:
                for lane in range(LANES):
                    n = i * LANES + lane
                    at(pool, S_.lane_free, n)
                    pool.tensor_copy(xs[lane][:], X[:, bass.ds(n, 1), :].rearrange("t a d -> t (a d)")).then_inc(S_.x_copied, 1)
                    if combine:
                        pool.tensor_copy(eT[lane][:], slots[:, :, bass.ds(n, 1), :].rearrange("d e a s -> d e (a s)")).then_inc(S_.slots_copied, 1)
                for lane in range(LANES):
                    at(pool, S_.sum_safe, i * LANES + lane)
                    pool.tensor_tensor(rs[lane][:], ss[lane][:], core.neghalf[:, 0:1], ALU.pow).then_inc(S_.inv_norm, 1)
                if combine:
                    for lane in range(LANES):
                        at(pool, S_.var_eps, i * LANES + lane)
                        pool.tensor_tensor(rs[lane][:], ve[lane][:], core.neghalf[:, 0:1], ALU.pow).then_inc(S_.rstd, 1)

        @block.tensor
        def _(pe):
            with pe.Fori(0, STEPS) as i:
                for lane in range(LANES):
                    at(pe, S_.x_normed, i * LANES + lane)
                    pe.transpose(ps[lane][:, 0, 0:T], xn[lane][:], core.ident[:]).then_inc(S_.x_psum, 1)
                for lane in range(LANES):
                    at(pe, S_.xT_ready, i * LANES + lane)
                    if combine:
                        pe.matmul(ps[lane][:, 1, :], xnT[lane][:], snT[:], start=True, stop=True).then_inc(S_.logits_psum, 1)
                    else:
                        for c in range(SC):
                            last = pe.matmul(ps[lane][:, 1, c * T:(c + 1) * T], snT[:, c * 128:(c + 1) * 128], xnT[lane][:], start=True, stop=True)
                        last.then_inc(S_.logits_psum, 1)
                if combine:
                    for lane in range(LANES):
                        at(pe, S_.slots_copied, i * LANES + lane)
                        ef = eT[lane][:].rearrange("d e s -> d (e s)")
                        for c in range(SC):
                            last = pe.transpose(ps[lane][:, 3, c * D:(c + 1) * D], ef[:, c * 128:(c + 1) * 128], core.ident[:])
                        last.then_inc(S_.eo_psum, 1)
                for lane in range(LANES):
                    at(pe, S_.weights_ready, i * LANES + lane)
                    for c in range(SC):
                        last = pe.transpose(ps[lane][:, 2, c * 128:(c + 1) * 128], P[lane][:, c, :], core.ident[:])
                    last.then_inc(S_.turned_psum, 1)
                for lane in range(LANES):
                    n = i * LANES + lane
                    at(pe, S_.turned_ready, n)
                    if combine:
                        at(pe, S_.eo_ready, n)
                        for c in range(SC):
                            last = pe.matmul(ps[lane][:, 0, 0:D], PT[lane][:, c, :], eo[lane][:, c, :], start=c == 0, stop=c == SC - 1)
                        last.then_inc(S_.out_psum, 1)
                    else:
                        pe.matmul(ps[lane][:, 0, :], xn[lane][:], PT[lane][:].rearrange("t c s -> t (c s)"), start=True, stop=True).then_inc(S_.out_psum, 1)

        @block.scalar
        def _(act):
            with act.Fori(0, STEPS) as i:
                for lane in range(LANES):
                    at(act, S_.x_copied, i * LANES + lane)
                    act.activation(sq[lane][:], xs[lane][:], ACT.Square, accum_out=ss[lane][:]).then_inc(S_.square_sum, 1)
                for lane in range(LANES):
                    at(act, S_.x_psum, i * LANES + lane)
                    act.activation(xnT[lane][:], ps[lane][:, 0, 0:T], ACT.Copy).then_inc(S_.xT_ready, 1)
                if combine:
                    for lane in range(LANES):
                        at(act, S_.eo_psum, i * LANES + lane)
                        act.activation(eo[lane][:].rearrange("m c d -> m (c d)"), ps[lane][:, 3, :], ACT.Copy).then_inc(S_.eo_ready, 1)
                for lane in range(LANES):
                    at(act, S_.shifted, i * LANES + lane)
                    if combine:
                        act.activation(P[lane][:].rearrange("t c s -> t (c s)"), ps[lane][:, 1, :], ACT.Exp, bias=mx[lane][:, 0:1],
                                       accum_out=zz[lane][:, 0:1]).then_inc(S_.exp_ready, 1)
                    else:
                        act.activation(P[lane][:], P[lane][:], ACT.Exp).then_inc(S_.exp_ready, 1)
                for lane in range(LANES):
                    at(act, S_.turned_psum, i * LANES + lane)
                    act.activation(PT[lane][:].rearrange("t c s -> t (c s)"), ps[lane][:, 2, :], ACT.Copy).then_inc(S_.turned_ready, 1)

        @block.vector
        def _(dve):
            dve.wait_ge(S_.gamma_in, 16)
            with dve.Fori(0, STEPS) as i:
                for lane in range(LANES):
                    n = i * LANES + lane
                    at(dve, S_.square_sum, n)
                    dve.tensor_scalar(ss[lane][:], ss[lane][:], 1e-24, None, ALU.max).then_inc(S_.sum_safe, 1)
                for lane in range(LANES):
                    n = i * LANES + lane
                    at(dve, S_.inv_norm, n)
                    dve.tensor_scalar(xn[lane][:], xs[lane][:], rs[lane][:, 0:1], float(D) ** 0.5, ALU.mult, ALU.mult).then_inc(S_.unit, 1)
                    at(dve, S_.unit, n)
                    dve.tensor_tensor(xn[lane][:], xn[lane][:], gam[:], ALU.mult).then_inc(S_.x_normed, 1)
                for lane in range(LANES):
                    n = i * LANES + lane
                    at(dve, S_.logits_psum, n)
                    if combine:
                        dve.tensor_reduce(mx[lane][:, 1:2], ps[lane][:, 1, :], AX.X, ALU.max).then_inc(S_.max_ready, 1)
                        at(dve, S_.max_ready, n)
                        dve.tensor_scalar(mx[lane][:, 0:1], mx[lane][:, 1:2], -1.0, None, ALU.mult).then_inc(S_.shifted, 1)
                    else:
                        lt = ps[lane][:, 1, :].rearrange("m (c t) -> m c t", c=SC)
                        dve.tensor_reduce(mx[lane][:], lt, AX.X, ALU.max).then_inc(S_.max_ready, 1)
                        at(dve, S_.max_ready, n)
                        dve.tensor_tensor(P[lane][:], lt, mx[lane][:].unsqueeze(2).to_broadcast([128, SC, T]), ALU.subtract).then_inc(S_.shifted, 1)
                for lane in range(LANES):
                    n = i * LANES + lane
                    at(dve, S_.exp_ready, n)
                    if combine:
                        dve.reciprocal(zz[lane][:, 1:2], zz[lane][:, 0:1]).then_inc(S_.recip_ready, 1)
                        at(dve, S_.recip_ready, n)
                        dve.tensor_scalar(P[lane][:], P[lane][:], zz[lane][:, 1:2], None, ALU.mult).then_inc(S_.weights_ready, 1)
                    else:
                        dve.tensor_reduce(zz[lane][:], P[lane][:], AX.X, ALU.add).then_inc(S_.sum_ready, 1)
                        at(dve, S_.sum_ready, n)
                        dve.reciprocal(mx[lane][:], zz[lane][:]).then_inc(S_.recip_ready, 1)
                        at(dve, S_.recip_ready, n)
                        dve.tensor_tensor(P[lane][:], P[lane][:], mx[lane][:].unsqueeze(2).to_broadcast([128, SC, T]), ALU.mult).then_inc(S_.weights_ready, 1)
                for lane in range(LANES):
                    n = i * LANES + lane
                    at(dve, S_.out_psum, n)
                    if not combine:
                        dve.tensor_copy(slots[:, :, bass.ds(n, 1), :], ps[lane][:, 0, :].rearrange("d (e a s) -> d e a s", e=E, a=1)).then_inc(S_.lane_free, 1)
                        continue
                    dve.tensor_tensor(r[lane][:], ps[lane][:, 0, 0:D], xs[lane][:], ALU.add).then_inc(S_.r_ready, 1)
                    at(dve, S_.r_ready, n)
                    dve.bn_stats(st[lane][:], r[lane][:]).then_inc(S_.stats, 1)
                    at_alone(dve, S_.stats, n, s.passed)
                    dve.bn_aggr(mv[lane][:], st[lane][:]).then_inc(S_.mean_var, 1)
                    at(dve, S_.mean_var, n)
                    dve.tensor_scalar(ve[lane][:], mv[lane][:, 1:2], LN_EPS, None, ALU.add).then_inc(S_.var_eps, 1)
                if combine:
                    for lane in range(LANES):
                        n = i * LANES + lane
                        at(dve, S_.rstd, n)
                        dve.tensor_scalar(X[:, bass.ds(n, 1), :].rearrange("t a d -> t (a d)"), r[lane][:], mv[lane][:, 0:1],
                                          rs[lane][:, 0:1], ALU.subtract, ALU.mult).then_inc(S_.lane_free, 1)
    s.close()


def slot_pass(core, slots, NS):
    nc, I = core.nc, core.I
    s = Scope(nc, "slotpass")
    CW = 512
    N = B * NS // CW
    w1s, w2s, b1s, b2s = (s.lanes("w1", [D, F]), s.lanes("w2", [128, FC, D]), s.lanes("b1", [128, FC]), s.lanes("b2", [D, 1]))
    hT = s.lanes("hT", [128, FC, CW])
    ph = s.psum("ph", [128, FC, 512])
    py = s.psum("py", [128, 2, 512])
    w_in = [s.sem(f"weights_in{k}") for k in range(LANES)]
    h_psum, h_ready, y_psum, y_stored = [s.sem(n) for n in ("h_psum", "h_ready", "y_psum", "y_stored")]
    H0, Y0 = FC, 2
    S0 = 2 * N
    sf = slots[:].rearrange("d e b s -> d (e b s)")
    with nc.Block() as block:
        @block.sync
        def _(sp):
            with sp.Fori(0, E // LANES) as i:
                for lane in range(LANES):
                    e = i * LANES + lane
                    sp.wait_ge(y_stored, (e + 1) * N)
                    with nc.allow_non_contiguous_dma(reason="bias columns"):
                        sp.dma_start(w1s[lane][:], I["L2_ffn_w1"][bass.ds(e, 1)].rearrange("a d f -> d (a f)")).then_inc(w_in[lane], 16)
                        sp.dma_start(w2s[lane][:], I["L2_ffn_w2"][bass.ds(e, 1)].rearrange("a (c p) d -> p (a c) d", p=128)).then_inc(w_in[lane], 16)
                        sp.dma_start(b1s[lane][:], I["L2_ffn_b1"][bass.ds(e, 1)].rearrange("a (c p) -> p (a c)", p=128)).then_inc(w_in[lane], 16)
                        sp.dma_start(b2s[lane][:], I["L2_ffn_b2"][bass.ds(e, 1)].rearrange("a d -> d a")).then_inc(w_in[lane], 16)

        @block.tensor
        def _(pe):
            pe.sem_inc(y_psum, Y0)
            pe.sem_inc(h_ready, H0)
            with pe.Fori(0, E // LANES) as i:
                for lane in range(LANES):
                    e = i * LANES + lane
                    with pe.Fori(0, N // 2) as c2:
                        at(pe, w_in[lane], i, 64)
                        for par in range(2):
                            m = e * N + c2 * 2 + par
                            for f in range(FC):
                                pe.wait_ge(h_ready, m * FC + f + 1)
                                pe.matmul(ph[:, f, :], w1s[lane][:, f * 128:(f + 1) * 128], sf[:, bass.ds(m * CW, CW)],
                                          start=True, stop=True).then_inc(h_psum, 1)
                        for par in range(2):
                            m = e * N + c2 * 2 + par
                            pe.wait_ge(h_ready, m * FC + FC + H0)
                            pe.wait_ge(y_stored, m - 1 + S0)
                            for f in range(FC):
                                last = pe.matmul(py[:, par, :], w2s[lane][:, f, :], hT[par][:, f, :], start=f == 0, stop=f == FC - 1)
                            last.then_inc(y_psum, 1)

        @block.scalar
        def _(act):
            with act.Fori(0, E // LANES) as i:
                for lane in range(LANES):
                    e = i * LANES + lane
                    with act.Fori(0, N // 2) as c2:
                        at(act, w_in[lane], i, 64)
                        for par in range(2):
                            m = e * N + c2 * 2 + par
                            act.wait_ge(y_psum, m - 1 + Y0)
                            for f in range(FC):
                                act.wait_ge(h_psum, m * FC + f + 1)
                                act.activation(hT[par][:, f, :], ph[:, f, :], ACT.Gelu, bias=b1s[lane][:, f:f + 1]).then_inc(h_ready, 1)

        @block.vector
        def _(dve):
            dve.sem_inc(y_stored, S0)
            with dve.Fori(0, E // LANES) as i:
                for lane in range(LANES):
                    e = i * LANES + lane
                    with dve.Fori(0, N // 2) as c2:
                        at(dve, w_in[lane], i, 64)
                        for par in range(2):
                            m = e * N + c2 * 2 + par
                            dve.wait_ge(y_psum, m + 1 + Y0)
                            dve.tensor_scalar(sf[:, bass.ds(m * CW, CW)], py[:, par, :], b2s[lane][:, 0:1], None, ALU.add).then_inc(y_stored, 1)
    s.close()


def text_vision(core):
    nc = core.nc
    with ExitStack() as stack:
        Y = stack.enter_context(nc.sbuf_tensor("Y", [T, B, D], F32))
        FO = stack.enter_context(nc.sbuf_tensor("FO", [T, B, 2 * D], F32))
        kernel_dram = nc.dram_tensor("s4d_kernel", (D, 2 * T), F32, kind="Internal").ap()
        topk_film(core, Y, FO)
        s4d_kernel(core, kernel_dram)
        s4d_convolve(core, Y, kernel_dram)
        film_ffn(core, Y, FO)


def topk_film(core, Y, FO):
    nc, I, X = core.nc, core.I, core.X
    s = Scope(nc, "topk")
    H, Dh, TOP = 4, 32, 32
    ROUNDS = TOP // 8
    scale = 1.0 / float(np.sqrt(Dh).astype(np.float32))
    TAKEN = -3e38
    loads = []

    def tile(tag, shape, src, dtype=F32):
        t = s.sb(tag, shape, dtype)
        loads.append((t[:], src))
        return t

    wq = tile("wq", [D, D], I["L0_xattn_Wq"])
    wk, wv = tile("wk", [DC, D], I["L0_xattn_Wk"]), tile("wv", [DC, D], I["L0_xattn_Wv"])
    gam, bet = tile("gam", [T, D], row_bc(I["L0_xattn_g_norm_in"])), tile("bet", [T, D], row_bc(I["L0_xattn_b_norm_in"]))
    mg = tile("mg", [T, 1], row_bc(I["L0_xattn_mod_gate"]))
    wf, bf = s.sb("wf", [D, 4 * D]), s.sb("bf", [T, 4 * D])
    for j, side in enumerate(("in", "out")):
        loads.append((wf[:, 2 * D * j:2 * D * (j + 1)], I[f"L0_xattn_W_film_{side}"]))
        loads.append((bf[:, 2 * D * j:2 * D * (j + 1)], row_bc(I[f"L0_xattn_b_film_{side}"])))
    tm8 = tile("tm8", [T, B], I["text_mask_T"], U8)
    tmask = s.sb("tmask", [T, B])
    xs, xn, xT, cs = s.lanes("xs", [T, D]), s.lanes("xn", [T, D]), s.lanes("xT", [D, T]), s.lanes("cs", [DC, TC])
    vm8, vbias, tm = s.lanes("vm8", [T, TC], U8), s.lanes("vbias", [T, TC]), s.lanes("tm", [T, 1])
    qT, kT, V = s.lanes("qT", [D, T]), s.lanes("kT", [D, TC]), s.lanes("V", [TC, D])
    S, W, P = s.lanes("S", [T, H, TC]), s.lanes("W", [T, H, TC]), s.lanes("P", [T, H, TC])
    m8 = s.lanes("m8", [T, ROUNDS, H, 8])
    sm, rz = s.lanes("sm", [T, H]), s.lanes("rz", [T, H])
    am, aT, cT = s.lanes("am", [T, TC]), s.lanes("aT", [TC, T]), s.lanes("cT", [D, T])
    film, yo = s.lanes("film", [T, 4 * D]), s.lanes("yo", [T, D])
    st, mv, ve, rs = s.lanes("st", [T, 6]), s.lanes("mv", [T, 2]), s.lanes("ve", [T, 1]), s.lanes("rs", [T, 1])
    ps = [s.psum(f"ps{lane}", [128, 4, 512]) for lane in range(LANES)]
    names = ("weights_in lane_free x_copied tm_copied x_psum xT_ready qkv_psum qk_ready v_ready bias_ready scores_psum scores_ready "
             "round_sorted round_taken shifted exp_ready kept sum_ready recip_ready recip_scaled weighted attn_ready attnT_psum attnT_ready "
             "c_psum c_ready film_psum film_biased film_gated scale_ready stats mean_var var_eps rstd normed scaled offset "
             "modulated tmask_ready work_ready out_stored")
    S_ = type("Ready", (), {n: s.sem(n) for n in names.split()})
    ctx_in = [s.sem(f"ctx_in{k}") for k in range(LANES)]
    with nc.Block() as block:
        @block.sync
        def _(sp):
            with nc.allow_non_contiguous_dma(reason="small weights, once"):
                for dst, src in loads:
                    sp.dma_start(dst, src).then_inc(S_.weights_in, 16)
            with sp.Fori(0, STEPS) as i:
                for lane in range(LANES):
                    n = i * LANES + lane
                    at(sp, S_.lane_free, n)
                    sp.dma_start(cs[lane][:], I["ctxT"][:, bass.ds(n * TC, TC)]).then_inc(ctx_in[lane], 16)
                    sp.dma_start(vm8[lane][:], I["mask_BxS2_bf1"][bass.ds(n, 1), :].to_broadcast([T, TC])).then_inc(ctx_in[lane], 16)

        @block.gpsimd
        def _(pool):
            pool.wait_ge(S_.weights_in, 16 * len(loads))
            pool.tensor_copy(tmask[:], tm8[:]).then_inc(S_.tmask_ready, 1)
            pool.wait_ge(S_.tmask_ready, 1)
            pool.sem_inc(S_.lane_free, LANES)
            with pool.Fori(0, STEPS) as i:
                for lane in range(LANES):
                    n = i * LANES + lane
                    at(pool, S_.lane_free, n)
                    pool.tensor_copy(xs[lane][:], X[:, bass.ds(n, 1), :].rearrange("t a d -> t (a d)")).then_inc(S_.x_copied, 1)
                    pool.tensor_copy(tm[lane][:], tmask[:, bass.ds(n, 1)]).then_inc(S_.tm_copied, 1)
                for lane in range(LANES):
                    at(pool, S_.var_eps, i * LANES + lane)
                    pool.tensor_tensor(rs[lane][:], ve[lane][:], core.neghalf[:, 0:1], ALU.pow).then_inc(S_.rstd, 1)

        @block.tensor
        def _(pe):
            pe.wait_ge(S_.weights_in, 16 * len(loads))
            with pe.Fori(0, STEPS) as i:
                for lane in range(LANES):
                    at(pe, S_.x_copied, i * LANES + lane)
                    pe.transpose(ps[lane][:, 0, 0:T], xs[lane][:], core.ident[:]).then_inc(S_.x_psum, 1)
                for lane in range(LANES):
                    at(pe, ctx_in[lane], i, 32)
                    at(pe, S_.xT_ready, i * LANES + lane)
                    pe.matmul(ps[lane][:, 1, 0:T], wq[:], xT[lane][:], start=True, stop=True)
                    pe.matmul(ps[lane][:, 1, T:T + TC], wk[:], cs[lane][:], start=True, stop=True)
                    pe.matmul(ps[lane][0:TC, 2, 0:D], cs[lane][:], wv[:], start=True, stop=True).then_inc(S_.qkv_psum, 1)
                for lane in range(LANES):
                    n = i * LANES + lane
                    at(pe, S_.v_ready, n)
                    at(pe, S_.qk_ready, n, 2)
                    for h in range(H):
                        rows = slice(h * Dh, (h + 1) * Dh)
                        last = pe.matmul(ps[lane][:, h, 0:TC], qT[lane][rows, :], kT[lane][rows, :], start=True, stop=True)
                    last.then_inc(S_.scores_psum, 1)
                for lane in range(LANES):
                    at(pe, S_.attn_ready, i * LANES + lane)
                    pe.transpose(ps[lane][0:TC, 0, 0:T], am[lane][:], core.ident[:]).then_inc(S_.attnT_psum, 1)
                for lane in range(LANES):
                    at(pe, S_.attnT_ready, i * LANES + lane)
                    pe.matmul(ps[lane][:, 1, 0:T], V[lane][:], aT[lane][:], start=True, stop=True).then_inc(S_.c_psum, 1)
                for lane in range(LANES):
                    at(pe, S_.c_ready, i * LANES + lane)
                    pe.matmul(ps[lane][:, 2, :], cT[lane][:], wf[:], start=True, stop=True).then_inc(S_.film_psum, 1)

        @block.scalar
        def _(act):
            with act.Fori(0, STEPS) as i:
                for lane in range(LANES):
                    at(act, S_.x_psum, i * LANES + lane)
                    act.activation(xT[lane][:], ps[lane][:, 0, 0:T], ACT.Copy).then_inc(S_.xT_ready, 1)
                for lane in range(LANES):
                    at(act, S_.qkv_psum, i * LANES + lane)
                    act.activation(qT[lane][:], ps[lane][:, 1, 0:T], ACT.Copy).then_inc(S_.qk_ready, 1)
                    act.activation(kT[lane][:], ps[lane][:, 1, T:T + TC], ACT.Copy).then_inc(S_.qk_ready, 1)
                    act.activation(V[lane][:], ps[lane][0:TC, 2, 0:D], ACT.Copy).then_inc(S_.v_ready, 1)
                for lane in range(LANES):
                    at(act, S_.shifted, i * LANES + lane)
                    act.activation(P[lane][:], P[lane][:], ACT.Exp, scale=scale).then_inc(S_.exp_ready, 1)
                for lane in range(LANES):
                    at(act, S_.attnT_psum, i * LANES + lane)
                    act.activation(aT[lane][:], ps[lane][0:TC, 0, 0:T], ACT.Copy).then_inc(S_.attnT_ready, 1)
                for lane in range(LANES):
                    at(act, S_.c_psum, i * LANES + lane)
                    act.activation(cT[lane][:], ps[lane][:, 1, 0:T], ACT.Copy).then_inc(S_.c_ready, 1)

        @block.vector
        def _(dve):
            dve.wait_ge(S_.weights_in, 16 * len(loads))
            with dve.Fori(0, STEPS) as i:
                for lane in range(LANES):
                    n = i * LANES + lane
                    at(dve, ctx_in[lane], i, 32)
                    dve.tensor_scalar(vbias[lane][:], vm8[lane][:], -NEG, NEG, ALU.mult, ALU.add).then_inc(S_.bias_ready, 1)
                    at(dve, S_.x_copied, n)
                    dve.bn_stats(st[lane][:], xs[lane][:]).then_inc(S_.stats, 1)
                    at_alone(dve, S_.stats, n, s.passed)
                    dve.bn_aggr(mv[lane][:], st[lane][:]).then_inc(S_.mean_var, 1)
                    at(dve, S_.mean_var, n)
                    dve.tensor_scalar(ve[lane][:], mv[lane][:, 1:2], LN_EPS, None, ALU.add).then_inc(S_.var_eps, 1)
                for lane in range(LANES):
                    n = i * LANES + lane
                    at(dve, S_.rstd, n)
                    dve.tensor_scalar(xn[lane][:], xs[lane][:], mv[lane][:, 0:1], rs[lane][:, 0:1], ALU.subtract, ALU.mult).then_inc(S_.normed, 1)
                    at(dve, S_.normed, n)
                    dve.tensor_tensor(xn[lane][:], xn[lane][:], gam[:], ALU.mult).then_inc(S_.scaled, 1)
                    at(dve, S_.scaled, n)
                    dve.tensor_tensor(xn[lane][:], xn[lane][:], bet[:], ALU.add).then_inc(S_.offset, 1)
                for lane in range(LANES):
                    n = i * LANES + lane
                    at(dve, S_.scores_psum, n)
                    at(dve, S_.bias_ready, n)
                    dve.tensor_tensor(S[lane][:], ps[lane][:, :, 0:TC], vbias[lane][:].unsqueeze(1).to_broadcast([T, H, TC]), ALU.add).then_inc(S_.scores_ready, 1)
                    at(dve, S_.scores_ready, n)
                    dve.tensor_copy(W[lane][:], S[lane][:]).then_inc(S_.work_ready, 1)
                    at_alone(dve, S_.work_ready, n, s.passed)
                    for q in range(ROUNDS):
                        if q:
                            at_alone(dve, S_.round_taken, n * (ROUNDS * H) + q * H - 1, s.passed)
                        for h in range(H):
                            dve.max(m8[lane][:, q, h, :], W[lane][:, h, :]).then_inc(S_.round_sorted, 1)
                        at_alone(dve, S_.round_sorted, n * (ROUNDS * H) + (q + 1) * H - 1, s.passed)
                        for h in range(H):
                            dve.match_replace(W[lane][:, h, :], m8[lane][:, q, h, :], W[lane][:, h, :], TAKEN).then_inc(S_.round_taken, 1)
                    dve.tensor_tensor(P[lane][:], S[lane][:], m8[lane][:, 0, :, 0:1].to_broadcast([T, H, TC]), ALU.subtract).then_inc(S_.shifted, 1)
                for lane in range(LANES):
                    n = i * LANES + lane
                    at(dve, S_.exp_ready, n)
                    at(dve, S_.round_taken, (n + 1) * (ROUNDS * H) - 1)
                    dve.scalar_tensor_tensor(out=P[lane][:], in0=W[lane][:], scalar=-2e38, in1=P[lane][:], op0=ALU.is_lt, op1=ALU.mult).then_inc(S_.kept, 1)
                    at(dve, S_.kept, n)
                    dve.tensor_reduce(sm[lane][:], P[lane][:], AX.X, ALU.add).then_inc(S_.sum_ready, 1)
                    at(dve, S_.sum_ready, n)
                    dve.reciprocal(rz[lane][:], sm[lane][:]).then_inc(S_.recip_ready, 1)
                    at(dve, S_.recip_ready, n)
                    dve.tensor_scalar(rz[lane][:], rz[lane][:], 1.0 / H, None, ALU.mult).then_inc(S_.recip_scaled, 1)
                    at(dve, S_.recip_scaled, n)
                    dve.tensor_tensor(P[lane][:], P[lane][:], rz[lane][:].unsqueeze(2).to_broadcast([T, H, TC]), ALU.mult).then_inc(S_.weighted, 1)
                    at(dve, S_.weighted, n)
                    dve.tensor_reduce(am[lane][:], P[lane][:].rearrange("t h k -> t k h"), AX.X, ALU.add).then_inc(S_.attn_ready, 1)
                for lane in range(LANES):
                    n = i * LANES + lane
                    at(dve, S_.film_psum, n)
                    at(dve, S_.tm_copied, n)
                    dve.scalar_tensor_tensor(out=film[lane][:], in0=ps[lane][:, 2, :], scalar=tm[lane][:, 0:1], in1=bf[:], op0=ALU.mult, op1=ALU.add).then_inc(S_.film_biased, 1)
                    at(dve, S_.film_biased, n)
                    dve.tensor_scalar(film[lane][:], film[lane][:], mg[:, 0:1], None, ALU.mult).then_inc(S_.film_gated, 1)
                    at(dve, S_.film_gated, n)
                    f4 = film[lane][:].rearrange("t (a b d) -> t a b d", a=2, b=2)
                    dve.tensor_scalar(f4[:, :, 0, :], f4[:, :, 0, :], 1.0, None, ALU.add).then_inc(S_.scale_ready, 1)
                    at(dve, S_.scale_ready, n)
                    at(dve, S_.offset, n)
                    dve.tensor_tensor(yo[lane][:], xn[lane][:], film[lane][:, 0:D], ALU.mult).then_inc(S_.modulated, 1)
                    dve.tensor_copy(FO[:, bass.ds(n, 1), :].rearrange("t a d -> t (a d)"), film[lane][:, 2 * D:4 * D]).then_inc(S_.out_stored, 1)
                    at(dve, S_.modulated, n)
                    dve.tensor_tensor(Y[:, bass.ds(n, 1), :].rearrange("t a d -> t (a d)"), yo[lane][:], film[lane][:, D:2 * D], ALU.add).then_inc(S_.lane_free, 1)
    s.close()


def s4d_kernel(core, kernel_dram):
    nc, I = core.nc, core.I
    s = Scope(nc, "s4d")
    NSt = I["L0_xattn_A_re"].shape[1]
    NA_, NB_ = 8, 16
    TWO_PI = (6.28125, 1.9350051879882812e-3, 3.0199159795e-7)
    ROUND = 1.5 * 2.0 ** 23
    PI = 3.1415925
    Are, Aim, Cre, Cim = (s.sb(n, [D, NSt]) for n in ("Are", "Aim", "Cre", "Cim"))
    ldt, dt, skip = s.sb("ldt", [D, 1]), s.sb("dt", [D, 1]), s.sb("skip", [D, 1])
    mag, ang, turn, snh, sn_, cs_ = (s.sb(n, [D, NSt]) for n in ("mag", "ang", "turn", "snh", "sin", "cos"))
    U = s.sb("U", [D, 2, NSt, NA_])
    V = s.sb("V", [D, 2, NSt, NB_])
    w = s.sb("w", [D, 7, 2, NSt])
    dC, den = s.sb("dC", [D, 2, NSt]), s.sb("den", [D, NSt])
    ta, tb = s.sb("ta", [D, NSt, 8]), s.sb("tb", [D, NSt, 8])
    zm, cz = s.sb("zm", [D, 2, NSt]), s.sb("cz", [D, 2, NSt])
    prod = s.sb("prod", [D, 2, NSt, NB_])
    K, Kp = s.sb("K", [D, T]), s.sb("Kp", [D, 2 * T])
    loaded, step, dt_ready, angle_ready, sines_ready, padded, kernel_ready, stored = [
        s.sem(n) for n in ("loaded", "step", "dt_ready", "angle_ready", "sines_ready", "padded", "kernel_ready", "stored")]
    with nc.Block() as block:
        @block.sync
        def _(sp):
            loads = [(Are, "A_re"), (Aim, "A_im"), (Cre, "C_re"), (Cim, "C_im")]
            for t, key in loads:
                sp.dma_start(t[:], I[f"L0_xattn_{key}"]).then_inc(loaded, 16)
            with nc.allow_non_contiguous_dma(reason="two columns"):
                sp.dma_start(ldt[:], col(I["L0_xattn_log_dt"])).then_inc(loaded, 16)
                sp.dma_start(skip[:], col(I["L0_xattn_D_skip"])).then_inc(loaded, 16)
            sp.wait_ge(kernel_ready, 1)
            sp.wait_ge(padded, 1)
            sp.dma_start(kernel_dram, Kp[:]).then_inc(stored, 16)
            sp.wait_ge(stored, 16)

        @block.gpsimd
        def _(pool):
            pool.memset(Kp[:], 0.0).then_inc(padded, 1)

        @block.scalar
        def _(act):
            act.wait_ge(loaded, 96)
            act.activation(dt[:], ldt[:], ACT.Exp).then_inc(dt_ready, 1)
            act.wait_ge(dt_ready, 1)
            act.activation(mag[:], Are[:], ACT.Exp, scale=dt[:, 0:1]).then_inc(dt_ready, 1)
            act.wait_ge(angle_ready, 1)
            act.activation(sn_[:], ang[:], ACT.Sin).then_inc(sines_ready, 1)
            act.activation(snh[:], ang[:], ACT.Sin, scale=0.5).then_inc(sines_ready, 1)

        @block.vector
        def _(dve):
            links = [0]

            def link(ins):
                links[0] += 1
                ins.then_inc(step, 1)
                dve.wait_ge(step, links[0])

            def product(out, a, b, shape):
                n, m = shape
                x, y = ta[:, :, 0:m], tb[:, :, 0:m]
                for k, (p, q, op) in enumerate((((0, 0), (1, 1), ALU.subtract), ((0, 1), (1, 0), ALU.add))):
                    link(dve.tensor_tensor(x, a[p[0]], b[p[1]], ALU.mult))
                    link(dve.tensor_tensor(y, a[q[0]], b[q[1]], ALU.mult))
                    link(dve.tensor_tensor(out[k], x, y, op))

            def pair(t):
                return t[:, 0, :].unsqueeze(2), t[:, 1, :].unsqueeze(2)

            def wide(t, m):
                return tuple(v.to_broadcast([D, NSt, m]) for v in pair(t))

            dve.wait_ge(loaded, 96)
            dve.wait_ge(dt_ready, 2)
            link(dve.tensor_scalar(ang[:], Aim[:], dt[:, 0:1], None, ALU.mult))
            link(dve.tensor_scalar(turn[:], ang[:], float(1.0 / (2.0 * np.pi)), None, ALU.mult))
            link(dve.tensor_scalar(turn[:], turn[:], ROUND, None, ALU.add))
            link(dve.tensor_scalar(turn[:], turn[:], -ROUND, None, ALU.add))
            for part in TWO_PI:
                link(dve.scalar_tensor_tensor(out=ang[:], in0=turn[:], scalar=-part, in1=ang[:], op0=ALU.mult, op1=ALU.add))
            link(dve.tensor_scalar(ang[:], ang[:], PI, None, ALU.min))
            dve.tensor_scalar(ang[:], ang[:], -PI, None, ALU.max).then_inc(angle_ready, 1)
            dve.wait_ge(sines_ready, 2)
            link(dve.tensor_tensor(cs_[:], snh[:], snh[:], ALU.mult))
            link(dve.tensor_scalar(cs_[:], cs_[:], -2.0, 1.0, ALU.mult, ALU.add))
            link(dve.tensor_tensor(w[:, 0, 0, :], mag[:], cs_[:], ALU.mult))
            link(dve.tensor_tensor(w[:, 0, 1, :], mag[:], sn_[:], ALU.mult))
            for k in range(6):
                product(pair(w[:, k + 1]), pair(w[:, k]), pair(w[:, k]), (NSt, 1))
            link(dve.tensor_scalar(zm[:, 0, :], w[:, 0, 0, :], -1.0, None, ALU.add))
            link(dve.tensor_copy(zm[:, 1, :], w[:, 0, 1, :]))
            product(pair(cz), (Cre[:].unsqueeze(2), Cim[:].unsqueeze(2)), pair(zm), (NSt, 1))
            link(dve.tensor_tensor(den[:], Are[:], Are[:], ALU.mult))
            link(dve.tensor_tensor(snh[:], Aim[:], Aim[:], ALU.mult))
            link(dve.tensor_tensor(den[:], den[:], snh[:], ALU.add))
            link(dve.reciprocal(den[:], den[:]))
            link(dve.tensor_scalar(turn[:], Aim[:], -1.0, None, ALU.mult))
            product(pair(dC), pair(cz), (Are[:].unsqueeze(2), turn[:].unsqueeze(2)), (NSt, 1))
            for k in range(2):
                link(dve.scalar_tensor_tensor(out=U[:, k, :, 0], in0=dC[:, k, :], scalar=2.0, in1=den[:], op0=ALU.mult, op1=ALU.mult))
            for j in range(3):
                m = 1 << j
                product((U[:, 0, :, m:2 * m], U[:, 1, :, m:2 * m]), (U[:, 0, :, 0:m], U[:, 1, :, 0:m]), wide(w[:, 4 + j], m), (NSt, m))
            link(dve.memset(V[:, 0, :, 0:1], 1.0))
            link(dve.memset(V[:, 1, :, 0:1], 0.0))
            for j in range(4):
                m = 1 << j
                product((V[:, 0, :, m:2 * m], V[:, 1, :, m:2 * m]), (V[:, 0, :, 0:m], V[:, 1, :, 0:m]), wide(w[:, j], m), (NSt, m))
            link(dve.tensor_scalar(V[:, 1], V[:, 1], -1.0, None, ALU.mult))
            for a in range(NA_):
                link(dve.tensor_tensor(prod[:], V[:], U[:, :, :, a:a + 1].to_broadcast([D, 2, NSt, NB_]), ALU.mult))
                link(dve.tensor_reduce(K[:, a * NB_:(a + 1) * NB_], prod[:].rearrange("d c n b -> d b (c n)"), AX.X, ALU.add))
            link(dve.tensor_tensor(K[:, 0:1], K[:, 0:1], skip[:], ALU.add))
            dve.wait_ge(padded, 1)
            dve.tensor_copy(Kp[:, 0:T], K[:, ::-1]).then_inc(kernel_ready, 1)
    s.close()


def s4d_convolve(core, Y, kernel_dram):
    nc = core.nc
    s = Scope(nc, "conv")
    CH = 16
    N = D // CH
    tz = s.lanes("toeplitz", [T, CH, T])
    ps = [s.psum(f"ps{k}", [T, CH, B]) for k in range(LANES)]
    toeplitz_in = [s.sem(f"toeplitz_in{k}") for k in range(LANES)]
    y_psum, y_stored = s.sem("y_psum"), s.sem("y_stored")
    Yd = Y[:].rearrange("t b d -> t d b")
    with nc.Block() as block:
        @block.sync
        def _(sp):
            for c in range(N):
                lane = c % LANES
                if c >= LANES:
                    sp.wait_ge(y_psum, c - LANES + 1)
                base = kernel_dram[c * CH:(c + 1) * CH, :]
                src = bass.AP(base.tensor, c * CH * 2 * T, [[1, T], [2 * T, CH], [1, T]])
                sp.dma_start(tz[lane][:], src).then_inc(toeplitz_in[lane], 16)

        @block.tensor
        def _(pe):
            for c in range(N):
                lane = c % LANES
                pe.wait_ge(toeplitz_in[lane], 16 * (c // LANES + 1))
                if c >= LANES:
                    pe.wait_ge(y_stored, c - LANES + 1)
                for k in range(CH):
                    last = pe.matmul(ps[lane][:, k, :], tz[lane][:, k, :], Yd[:, c * CH + k, :], start=True, stop=True)
                last.then_inc(y_psum, 1)

        @block.vector
        def _(dve):
            for c in range(N):
                dve.wait_ge(y_psum, c + 1)
                dve.tensor_copy(Yd[:, c * CH:(c + 1) * CH, :], ps[c % LANES][:]).then_inc(y_stored, 1)
    s.close()


def film_ffn(core, Y, FO):
    nc, I, X = core.nc, core.I, core.X
    s = Scope(nc, "filmffn")
    loads = []

    def tile(tag, shape, src):
        t = s.sb(tag, shape)
        loads.append((t[:], src))
        return t

    p = "L0_xattn_"
    w1, w2 = tile("w1", [D, F], I[p + "W1"]), tile("w2", [128, FC, D], I[p + "W2"].rearrange("(c p) d -> p c d", p=128))
    b1, b2 = tile("b1", [128, FC], I[p + "b1"].rearrange("(c p) -> p c", p=128)), tile("b2", [T, D], row_bc(I[p + "b2"]))
    gf, bf = tile("gf", [T, D], row_bc(I[p + "g_ffn"])), tile("bf", [T, D], row_bc(I[p + "b_ffn"]))
    go, bo = tile("go", [T, D], row_bc(I[p + "g_norm_out"])), tile("bo", [T, D], row_bc(I[p + "b_norm_out"]))
    xs, ys, fo = s.lanes("xs", [T, D]), s.lanes("ys", [T, D]), s.lanes("fo", [T, 2 * D])
    xt, xn, xT, hT = s.lanes("xt", [T, D]), s.lanes("xn", [T, D]), s.lanes("xT", [D, T]), s.lanes("hT", [128, FC, T])
    st, mv, ve, rs = s.lanes("st", [T, 6]), s.lanes("mv", [T, 2]), s.lanes("ve", [T, 1]), s.lanes("rs", [T, 1])
    ps = [s.psum(f"ps{lane}", [128, 4, 512]) for lane in range(LANES)]
    names = ("weights_in lane_free copied turned modulated shifted xt_ready n_psum nT_ready h_psum h_ready y_psum y_biased xt2_ready sum_ready"
             + "".join(f" stats{k} mean_var{k} var_eps{k} rstd{k} normed{k} scaled{k} offset{k}" for k in range(3)))
    sems = {n: s.sem(n) for n in names.split()}
    S_ = type("Ready", (), sems)
    stats, mean_var, var_eps, rstd, normed, scaled, offset = (
        [sems[f"{n}{k}"] for k in range(3)] for n in ("stats", "mean_var", "var_eps", "rstd", "normed", "scaled", "offset"))
    with nc.Block() as block:
        @block.sync
        def _(sp):
            with nc.allow_non_contiguous_dma(reason="small weights, once"):
                for dst, src in loads:
                    sp.dma_start(dst, src).then_inc(S_.weights_in, 16)

        @block.gpsimd
        def _(pool):
            pool.sem_inc(S_.lane_free, LANES)
            with pool.Fori(0, STEPS) as i:
                for lane in range(LANES):
                    n = i * LANES + lane
                    at(pool, S_.lane_free, n)
                    for dst, src in ((xs, X), (fo, FO)):
                        pool.tensor_copy(dst[lane][:], src[:, bass.ds(n, 1), :].rearrange("t a d -> t (a d)")).then_inc(S_.copied, 1)
                for k in range(3):
                    for lane in range(LANES):
                        at(pool, var_eps[k], i * LANES + lane)
                        pool.tensor_tensor(rs[lane][:], ve[lane][:], core.neghalf[:, 0:1], ALU.pow).then_inc(rstd[k], 1)

        @block.tensor
        def _(pe):
            pe.wait_ge(S_.weights_in, 16 * len(loads))
            with pe.Fori(0, STEPS) as i:
                for lane in range(LANES):
                    n = i * LANES + lane
                    at(pe, S_.copied, n, 2)
                    pe.matmul(ps[lane][:, 3, 0:D], core.anti[:], Y[:, bass.ds(n, 1), :].rearrange("t a d -> t (a d)"), start=True, stop=True).then_inc(S_.turned, 1)
                for lane in range(LANES):
                    at(pe, offset[0], i * LANES + lane)
                    pe.transpose(ps[lane][:, 0, 0:T], xn[lane][:], core.ident[:]).then_inc(S_.n_psum, 1)
                for lane in range(LANES):
                    at(pe, S_.nT_ready, i * LANES + lane)
                    for f in range(FC):
                        last = pe.matmul(ps[lane][:, 1, f * T:(f + 1) * T], w1[:, f * 128:(f + 1) * 128], xT[lane][:], start=True, stop=True)
                    last.then_inc(S_.h_psum, 1)
                for lane in range(LANES):
                    at(pe, S_.h_ready, i * LANES + lane, FC)
                    for f in range(FC):
                        last = pe.matmul(ps[lane][:, 2, 0:D], hT[lane][:, f, :], w2[:, f, :], start=f == 0, stop=f == FC - 1)
                    last.then_inc(S_.y_psum, 1)

        @block.scalar
        def _(act):
            act.wait_ge(S_.weights_in, 16 * len(loads))
            with act.Fori(0, STEPS) as i:
                for lane in range(LANES):
                    at(act, S_.n_psum, i * LANES + lane)
                    act.activation(xT[lane][:], ps[lane][:, 0, 0:T], ACT.Copy).then_inc(S_.nT_ready, 1)
                for lane in range(LANES):
                    at(act, S_.h_psum, i * LANES + lane)
                    for f in range(FC):
                        act.activation(hT[lane][:, f, :], ps[lane][:, 1, f * T:(f + 1) * T], ACT.Gelu, bias=b1[:, f:f + 1]).then_inc(S_.h_ready, 1)

        @block.vector
        def _(dve):
            dve.wait_ge(S_.weights_in, 16 * len(loads))

            def norm_stats(src, n, lane, k):
                dve.bn_stats(st[lane][:], src).then_inc(stats[k], 1)
                at_alone(dve, stats[k], n, s.passed)
                dve.bn_aggr(mv[lane][:], st[lane][:]).then_inc(mean_var[k], 1)
                at(dve, mean_var[k], n)
                dve.tensor_scalar(ve[lane][:], mv[lane][:, 1:2], LN_EPS, None, ALU.add).then_inc(var_eps[k], 1)

            def norm_apply(dst, src, n, lane, k):
                at(dve, rstd[k], n)
                return dve.tensor_scalar(dst, src, mv[lane][:, 0:1], rs[lane][:, 0:1], ALU.subtract, ALU.mult)

            def affine(n, lane, k, g, b):
                at(dve, normed[k], n)
                dve.tensor_tensor(xn[lane][:], xn[lane][:], g[:], ALU.mult).then_inc(scaled[k], 1)
                at(dve, scaled[k], n)
                dve.tensor_tensor(xn[lane][:], xn[lane][:], b[:], ALU.add).then_inc(offset[k], 1)

            with dve.Fori(0, STEPS) as i:
                for lane in range(LANES):
                    n = i * LANES + lane
                    at(dve, S_.copied, n, 2)
                    at(dve, S_.turned, n)
                    dve.tensor_tensor(xt[lane][:], ps[lane][:, 3, 0:D], fo[lane][:, 0:D], ALU.mult).then_inc(S_.modulated, 1)
                    at(dve, S_.modulated, n)
                    dve.tensor_tensor(xt[lane][:], xt[lane][:], fo[lane][:, D:2 * D], ALU.add).then_inc(S_.shifted, 1)
                    at(dve, S_.shifted, n)
                    dve.tensor_tensor(xt[lane][:], xt[lane][:], xs[lane][:], ALU.add).then_inc(S_.xt_ready, 1)
                    at(dve, S_.xt_ready, n)
                    norm_stats(xt[lane][:], n, lane, 0)
                for lane in range(LANES):
                    n = i * LANES + lane
                    norm_apply(xn[lane][:], xt[lane][:], n, lane, 0).then_inc(normed[0], 1)
                    affine(n, lane, 0, gf, bf)
                for lane in range(LANES):
                    n = i * LANES + lane
                    at(dve, S_.y_psum, n)
                    dve.tensor_tensor(ys[lane][:], ps[lane][:, 2, 0:D], b2[:], ALU.add).then_inc(S_.y_biased, 1)
                    at(dve, S_.y_biased, n)
                    dve.tensor_tensor(xt[lane][:], xt[lane][:], ys[lane][:], ALU.add).then_inc(S_.xt2_ready, 1)
                    at(dve, S_.xt2_ready, n)
                    norm_stats(xt[lane][:], n, lane, 1)
                for lane in range(LANES):
                    n = i * LANES + lane
                    norm_apply(xn[lane][:], xt[lane][:], n, lane, 1).then_inc(normed[1], 1)
                    affine(n, lane, 1, go, bo)
                    at(dve, offset[1], n)
                    dve.tensor_tensor(xt[lane][:], xn[lane][:], xs[lane][:], ALU.add).then_inc(S_.sum_ready, 1)
                    at(dve, S_.sum_ready, n)
                    norm_stats(xt[lane][:], n, lane, 2)
                for lane in range(LANES):
                    n = i * LANES + lane
                    norm_apply(X[:, bass.ds(n, 1), :].rearrange("t a d -> t (a d)"), xt[lane][:], n, lane, 2).then_inc(S_.lane_free, 1)
    s.close()


def lay_out(inputs):
    a = {k: np.ascontiguousarray(v) for k, v in inputs.items()}
    for key in ("mask_BxS_bf1", "mask_BxS2_bf1"):
        a[key] = a[key].view(np.uint8)
    a["text_mask_T"] = a.pop("mask_BxS_bf1").T
    a["L0_xattn_mod_gate"] = a["L0_xattn_mod_gate"].reshape(1)
    a["ctxT"] = a.pop("ctx_768").transpose(2, 0, 1).reshape(DC, B * TC)
    w, b, g = a.pop("L2_attn_in_proj_weight"), a.pop("L2_attn_in_proj_bias"), a.pop("L2_attn_gamma").reshape(-1)
    w3, b3 = a.pop("L3_ffn_Wqkv"), a.pop("L3_ffn_bqkv")
    for n, c in enumerate("qkv"):
        part = slice(n * D, (n + 1) * D)
        a[f"L2_attn_W{c}"], a[f"L2_attn_b{c}"], a[f"L2_attn_gamma_{c}"] = w[part].T, b[part], g[part]
        a[f"L3_ffn_W{c}"], a[f"L3_ffn_b{c}"] = w3[:, part], b3[part]
        a[f"L3_attn_W{c}T"] = a.pop(f"L3_attn_W{c}").T
    a["L3_attn_WoT"] = a.pop("L3_attn_Wo").T
    a["L2_attn_WoT"] = a.pop("L2_attn_out_proj_weight").T
    a["L2_attn_alpha"] = a.pop("L2_attn_linear_alpha").reshape(-1)
    a["L2_attn_lgamma"] = a.pop("L2_attn_linear_gamma").reshape(-1)
    for c in "kvr":
        a[f"L1_attn_time_mix_{c}"] = a[f"L1_attn_time_mix_{c}"].reshape(-1)
        a[f"L1_attn_W{c}T"] = a.pop(f"L1_attn_W{c}").T
    a["L1_attn_WoT"] = a.pop("L1_attn_Wo").T
    a["L3_ffn_fc1T"] = a.pop("L3_ffn_fc1_w").transpose(0, 2, 1)
    a["L3_ffn_fc2T"] = a.pop("L3_ffn_fc2_w").transpose(0, 2, 1)
    i, j = np.arange(T)[:, None], np.arange(T)[None, :]
    causal, within = j <= i, (j <= i) & (i // B == j // B)
    for name, sees in (("mask_causal", causal), ("mask_within", within)):
        a[name] = np.where(sees, 0.0, NEG).astype(np.float32)
    a["iota8"] = np.arange(E, dtype=np.float32)
    a["mask_causal_T"] = causal.T.astype(np.float32)
    return {k: np.ascontiguousarray(v) for k, v in a.items()}


def build(nc, I, out, stages=tuple(range(12))):
    I = dict(I)
    with ExitStack() as stack:
        core = Core(nc, stack, I)
        load_block(core)
        if 0 in stages:
            attention(core, "L0self", H=16, Dh=8, Wq="L0_attn_Wq", Wk="L0_attn_Wk", Wv="L0_attn_Wv", Wo="L0_attn_Wq",
                      bq="L0_attn_bq", bk="L0_attn_bk", bv="L0_attn_bv", flow=True, post="gate")
        if 1 in stages:
            text_vision(core)
        if 2 in stages:
            experts_top1(core, "L0ffn")
        if 3 in stages:
            wkv_mix(core)
        if 4 in stages:
            attention(core, "L1x", H=16, Dh=8, Wq="L1_xattn_Wq", Wk="L1_xattn_Wk", Wv="L1_xattn_Wv", Wo="L1_xattn_Wo",
                      bq="L1_xattn_bq", bk="L1_xattn_bk", bv="L1_xattn_bv", bo="L1_xattn_bo", context=True,
                      form="bounded", post="l1x")
        if 5 in stages:
            experts_top1(core, "L1ffn")
        if 6 in stages:
            batch_axis_attention(core)
        if 7 in stages:
            attention(core, "L2x", H=16, Dh=8, Wq="L2_xattn_wq", Wk="L2_xattn_wk", Wv="L2_xattn_wv", Wo="L2_xattn_wo",
                      bq="L2_xattn_bq", bk="L2_xattn_bk", bv="L2_xattn_bv", bo="L2_xattn_bo", context=True)
        if 8 in stages:
            soft_experts(core)
        if 9 in stages:
            attention(core, "L3lin", H=16, Dh=8, Wq="L3_attn_WqT", Wk="L3_attn_WkT", Wv="L3_attn_WvT", Wo="L3_attn_WoT",
                      bq="L3_attn_bq", bk="L3_attn_bk", bv="L3_attn_bv", bo="L3_attn_bo", form="linear",
                      mask="mask_causal_T")
        if 10 in stages:
            attention(core, "L3x", H=8, Dh=64, Wq="L3_xattn_Wq", Wk="L3_xattn_Wk", Wv="L3_xattn_Wv", Wo="L3_xattn_Wo",
                      bo="L3_xattn_bo", context=True)
        if 11 in stages:
            block_experts(core)
        store_block(core, out)


STAGES = tuple(range(12))


def kernel(**inputs):
    from concourse import bacc
    from concourse.bass_utils import run_bass_kernel_spmd

    nc = bacc.Bacc("TRN2", target_bir_lowering=False, num_devices=1)
    arrays = lay_out(inputs)
    I = {k: nc.dram_tensor(f"in_{k}", v.shape, mybir.dt.from_np(v.dtype), kind="ExternalInput").ap()
         for k, v in arrays.items()}
    out = nc.dram_tensor("out_x", (B, T, D), F32, kind="ExternalOutput").ap()
    build(nc, I, out, STAGES)
    r = run_bass_kernel_spmd(nc, [{f"in_{k}": v for k, v in arrays.items()}], core_ids=[0])
    return r.results[0]["out_x"]
```

```python
from contextlib import ExitStack

import numpy as np
import concourse.bass as bass
from concourse import mybir

F32 = mybir.dt.float32
BF16 = mybir.dt.bfloat16
U32 = mybir.dt.uint32
U8 = mybir.dt.uint8
ALU = mybir.AluOpType
ACT = mybir.ActivationFunctionType
AX = mybir.AxisListType.X

B, T, D = 32, 128, 128
TC, DC = 120, 96
LANES = 2
STEPS = B // LANES
MANY = 4
E, F = 8, 512
FC = F // 128
LN_EPS = 1e-5
NEG = -1e30


def at(eng, sem, n, each=1):
    eng.wait_ge(sem, (n + 1) * each)


def at_alone(eng, sem, n, passed):
    at(eng, sem, n)
    eng.sem_inc(passed, 1)


class Scope:

    def __init__(self, nc, name):
        self.nc, self.name, self.stack, self.sems = nc, name, ExitStack(), []
        self.passed = self.sem("passed")

    def sb(self, name, shape, dtype=F32):
        return self.stack.enter_context(self.nc.sbuf_tensor(f"{self.name}_{name}", shape, dtype))

    def lanes(self, name, shape, dtype=F32, n=LANES):
        return [self.sb(f"{name}{lane}", shape, dtype) for lane in range(n)]

    def psum(self, name, shape, dtype=F32):
        return self.stack.enter_context(self.nc.psum_tensor(f"{self.name}_{name}", shape, dtype))

    def sem(self, name):
        s = self.nc.alloc_semaphore(f"{self.name}_{name}")
        self.sems.append(s)
        return s

    def close(self):
        self.stack.close()
        self.nc.clear_and_free_semaphores(self.sems)
        self.nc.all_engine_barrier()


def row_bc(vec, n=128):
    return vec.rearrange("(a d) -> a d", a=1).to_broadcast([n, vec.shape[0]])


def col(vec):
    return vec.rearrange("(d a) -> d a", a=1)


class Core:

    def __init__(self, nc, stack, I):
        self.nc, self.I = nc, I

        def sb(name, shape, dtype=F32):
            return stack.enter_context(nc.sbuf_tensor(name, shape, dtype))

        self.X = sb("X", [T, B, D])
        self.ident = sb("ident", [128, 128])
        self.anti = sb("anti", [128, 128])
        self.identb = sb("identb", [128, 128], BF16)
        self.ones = sb("ones", [128, 128])
        self.neghalf = sb("neghalf", [128, 128])


def load_block(core):
    nc, I = core.nc, core.I
    s = Scope(nc, "load")
    x_in, zeroed, made = s.sem("x_in"), s.sem("zeroed"), s.sem("made")
    with nc.Block() as block:
        @block.sync
        def _(sp):
            sp.dma_start(core.X[:], I["x"].rearrange("b t d -> t b d")).then_inc(x_in, 16)
            sp.wait_ge(x_in, 16)

        @block.gpsimd
        def _(pool):
            pool.memset(core.ident[:], 0.0).then_inc(zeroed, 1)
            pool.memset(core.ones[:], 1.0).then_inc(made, 1)
            pool.memset(core.neghalf[:], -0.5).then_inc(made, 1)
            pool.memset(core.anti[:], 0.0).then_inc(zeroed, 1)
            pool.wait_ge(zeroed, 2)
            pool.affine_select(out=core.anti[:], in_=core.anti[:], compare_op=ALU.not_equal, fill=1.0,
                               base=-127, pattern=[[1, 128]], channel_multiplier=1).then_inc(made, 1)
            pool.affine_select(out=core.ident[:], in_=core.ident[:], compare_op=ALU.not_equal, fill=1.0,
                               base=0, pattern=[[-1, 128]], channel_multiplier=1).then_inc(made, 1)
            pool.wait_ge(made, 4)
            pool.tensor_copy(core.identb[:], core.ident[:]).then_inc(made, 1)
            pool.wait_ge(made, 5)
    s.close()


def store_block(core, out):
    nc = core.nc
    s = Scope(nc, "store")
    x_out = s.sem("x_out")
    with nc.Block() as block:
        @block.sync
        def _(sp):
            sp.dma_start(out.rearrange("b t d -> t b d"), core.X[:]).then_inc(x_out, 16)
            sp.wait_ge(x_out, 16)
    s.close()


def attention(core, name, *, H, Dh, Wq, Wk, Wv, Wo=None, bq=None, bk=None, bv=None, bo=None,
              context=False, flow=False, mask=None, form="softmax", post="plain", x_after=None):
    nc, I, X = core.nc, core.I, core.X
    s = Scope(nc, name)
    small = Dh == 8
    K = TC if context else T
    KD = DC if context else D
    J = 4 if small else 2
    R = 128 // J
    C = H // J
    HD = H * Dh
    NB = HD // 128
    G = H if small else 4
    Q = 2 * Dh if flow else Dh
    scale = float(Dh) ** -0.5
    shifted = form == "softmax"
    two_norms = post in ("gate", "l1x")
    scaled = post == "l2self"
    HJ = J // 2

    loads, zeroed = [], []
    WC = 4 if post == "gate" else 3
    if small:
        wx = s.sb("wx", [D, WC, HD])
        loads.append((wx[:, 0, :], I[Wq]))
        if context:
            wc = s.sb("wc", [DC, 2, HD])
            loads += [(wc[:, 0, :], I[Wk]), (wc[:, 1, :], I[Wv])]
        else:
            loads += [(wx[:, 1, :], I[Wk]), (wx[:, 2, :], I[Wv])]
        brow = s.sb("brow", [128, 4, HD])
        for a, key in enumerate((bq, bk, bv)):
            loads.append((brow[:, a, :], row_bc(I[key])))
        if post == "gate":
            loads += [(wx[:, 3, :], I["L0_attn_Wg"][0:D, :]), (brow[:, 3, :], row_bc(I["L0_attn_bg"]))]
        if post == "l1x":
            loads.append((brow[:, 3, :], row_bc(I[bo])))
    else:
        wx = s.sb("wx", [D, HD])
        wk = s.sb("wk", [DC, HD])
        wv = s.sb("wv", [DC, HD])
        loads += [(wx[:], I[Wq]), (wk[:], I[Wk]), (wv[:], I[Wv])]
    wo = s.sb("wo", [128, NB, D])
    loads.append((wo[:], I["L0_attn_Wg"][D:2 * D, :].rearrange("(n p) d -> p n d", n=1) if post == "gate"
                  else I[Wo].rearrange("(n p) d -> p n d", p=128)))

    def row(key, tag):
        t = s.sb(tag, [128, D])
        loads.append((t[:], row_bc(I[key])))
        return t

    bor = row(bo, "bo") if post in ("plain", "l2self", "l3ffn") else None
    if two_norms:
        pre = "L0_attn_" if post == "gate" else "L1_xattn_ln_"
        gam, bet = row(pre + "gamma", "gam"), row(pre + "beta", "bet")
    if post == "l3ffn":
        l1w, l1b = row("L3_ffn_ln1_w", "l1w"), row("L3_ffn_ln1_b", "l1b")
    if scaled:
        grow = s.sb("grow", [128, 3, HD])
        for a, c in enumerate("qkv"):
            loads.append((grow[:, a, :], row_bc(I[f"L2_attn_gamma_{c}"])))
        alpha, lgam = s.sb("alpha", [128, 1]), row("L2_attn_lgamma", "lgam")
        loads.append((alpha[:], col(I["L2_attn_alpha"])))
    if mask:
        mask_in = s.sb("mask_in", [T, T])
        loads.append((mask_in[:], I[mask]))
        msk = s.sb("msk", [T, C, T], BF16) if shifted else mask_in

    def pair(tag, shape):
        return [s.sb(f"{tag}{p}", shape) for p in (0, 1)]

    xs = pair("xs", [T, D])
    xT = s.sb("xT", [D, T])
    cs = pair("cs", [DC, K]) if context else None
    U = pair("U", [128, 3, H, 32]) if small else None
    V = [u[:, 2, :, 0:Dh + 1] for u in U] if small else [v[:] for v in pair("V", [128, H, Dh + 1])]
    q4 = s.sb("q4", [128, C, T])
    k4 = s.sb("k4", [128, C, K])
    S = s.sb("S", [T, J, C, K]) if shifted else None
    PTs = pair("PT", [K, J, C, T])
    mx = s.sb("mx", [T, J, C])
    rz = s.sb("rz", [T, H])
    oS = s.sb("oS", [T, H, Dh])
    outT = s.sb("outT", [128, C, T]) if small else None
    oT = s.sb("oT", [128, NB, T])
    kept = s.sb("kept", [T, B, D])
    r = s.sb("r", [T, D])
    rm = s.sb("rm", [T, D])
    xo = s.sb("xo", [T, D])
    gt = s.sb("gt", [T, D])
    xb = s.sb("xb", [T, D])
    st, mv, ve, rs = s.sb("st", [T, 6]), s.sb("mv", [T, 2]), s.sb("ve", [T, 1]), s.sb("rs", [T, 1])
    st1, mv1, ve1, rs1 = s.sb("st1", [T, 6]), s.sb("mv1", [T, 2]), s.sb("ve1", [T, 1]), s.sb("rs1", [T, 1])
    sq = s.sb("sq", [T, 2, H, Dh])
    ss = s.sb("ss", [T, 2])
    ef, rl = s.sb("ef", [T, 2, H, Dh]), s.sb("rl", [T, 2, H, Dh])

    bank = s.psum("bank", [128, 8, 512])
    scores = bank[:, 0:J, :]
    if small:
        q_ps, k_ps, proj_ps = bank[:, 4, :], bank[:, 5, :], bank[:, 6, :]
        outT_ps, o_ps = bank[:, 7, :], bank[:, 7:8, :]
        y_ps, oT_ps = bank[:, 7, 0:D], bank[:, 7, 128:128 + T]
    else:
        o_ps = bank[:, 2:4, 0:G * (Dh + 1)]
        y_ps = bank[:, 2, 384:512]
        q_ps, k_ps, proj_ps, oT_ps = bank[:, 4, :], bank[:, 5, :], bank[:, 6, :], bank[:, 7, :]

    xT_ps = bank[:, 4, 0:T]

    def sems(names):
        return [s.sem(n) for n in names.split()]

    weights_in, zeroed, setup = sems("weights_in zeroed setup")
    x_ready, xT_psum, xT_ready, proj_psum, u_ready, qkT_psum, q_ready, k_ready, v_ready = sems(
        "x_ready xT_psum xT_ready proj_psum u_ready qkT_psum q_ready k_ready v_ready")
    s_psum, max_ready, shifted_ready, p_ready, pT_psum, pT_ready = [
        sems(f"{n}_low {n}_high") for n in ("scores_psum", "max", "shifted", "p", "pT_psum", "pT")]
    o_psum, z_ready, o_ready, oT_psum, oT_ready, y_psum, y_read, stats, mean_var, var_eps, rstd, finished = sems(
        "o_psum z_ready o_ready oT_psum oT_ready y_psum y_read stats mean_var var_eps rstd finished")
    kept_ready, normed, q_biased, outT_psum, outT_ready = sems("kept_ready normed q_biased outT_psum outT_ready")
    ctx_in = sems("ctx_in_even ctx_in_odd") if context else None
    if two_norms:
        r1_ready, stats1, mean_var1, var_eps1, rstd1, scaled1, xb_ready, r_ready = sems(
            "r1_ready stats1 mean_var1 var_eps1 rstd1 scaled1 xb_ready r_ready")
    if post == "gate":
        gate_in, gate_exp, gate_plus1, gate_ready, gated = sems("gate_in gate_exp gate_plus1 gate_ready gated")
    if form == "bounded":
        squares, square_sum, norm_safe, norm_ready, raw = sems("squares square_sum norm_safe norm_ready raw")
    if form == "linear":
        raw, low, expd = sems("raw low expd")
    if flow:
        raw = s.sem("raw")
    if post == "l3ffn":
        i_copied, i_stats, i_mv, i_ve, i_rstd, i_normed, i_scaled = sems(
            "in_copied in_stats in_mean_var in_var_eps in_rstd in_normed in_scaled")
    setups = 0
    if scaled:
        setups += 5
    if post == "l1x":
        setups += 1
    if mask and shifted:
        setups += 1

    def tile(buffer, n):
        return buffer[:, n, :] if isinstance(n, int) else buffer[:, bass.ds(n, 1), :].rearrange("t a d -> t (a d)")

    def steps(eng, step):
        step(-2, 0, fetch=True)
        step(-1, 1, fetch=True, front=True)
        step(0, 0, fetch=True, front=True, main=True)
        step(1, 1, fetch=True, front=True, main=True, tail=True)
        with eng.Fori(0, (B - 4) // 2) as i:
            step(i * 2 + 2, 0, fetch=True, front=True, main=True, tail=True, output=True)
            step(i * 2 + 3, 1, fetch=True, front=True, main=True, tail=True, output=True)
        step(B - 2, 0, front=True, main=True, tail=True, output=True)
        step(B - 1, 1, main=True, tail=True, output=True)
        step(B, 0, tail=True, output=True)
        step(B + 1, 1, output=True)

    halves = ((0, range(0, HJ)), (1, range(HJ, J)))

    with nc.Block() as block:
        @block.sync
        def _(sp):
            with nc.allow_non_contiguous_dma(reason="weights are rearranged once"):
                for dst, src in loads:
                    sp.dma_start(dst, src).then_inc(weights_in, 16)
            if context:
                for p in (0, 1):
                    sp.dma_start(cs[p][:], I["ctxT"][:, p * K:(p + 1) * K]).then_inc(ctx_in[p], 16)
                with sp.Fori(0, (B - 2) // 2) as i:
                    for p in (0, 1):
                        n = i * 2 + p
                        at(sp, proj_psum, n)
                        sp.dma_start(cs[p][:], I["ctxT"][:, bass.ds(n * K + 2 * K, K)]).then_inc(ctx_in[p], 16)

        @block.gpsimd
        def _(pool):
            for p in (0, 1):
                if small:
                    pool.memset(U[p][:], 0.0).then_inc(zeroed, 1)
                    pool.wait_ge(zeroed, 1 + 2 * p)
                    pool.memset(U[p][:, 2, :, Dh:Dh + 1], 1.0).then_inc(zeroed, 1)
                else:
                    pool.memset(V[p], 1.0).then_inc(zeroed, 2)
            pool.wait_ge(weights_in, 16 * len(loads))
            if setups:
                pool.wait_ge(setup, setups)

            def step(n, p, fetch=False, front=False, main=False, tail=False, output=False):
                f, t = n + 2, n - 2
                if fetch:
                    x_new = xs[p]
                    if not (isinstance(f, int) and f < 2):
                        at_alone(pool, xT_psum, f - 2, s.passed)
                    if post == "l3ffn":
                        pool.tensor_copy(x_new[:], tile(X, f)).then_inc(i_copied, 1)
                        at(pool, i_ve, f)
                        pool.tensor_tensor(rs1[:], ve1[:], core.neghalf[:, 0:1], ALU.pow).then_inc(i_rstd, 1)
                        at_alone(pool, i_rstd, f, s.passed)
                        at_alone(pool, i_copied, f, s.passed)
                        pool.tensor_scalar(x_new[:], x_new[:], mv1[:, 0:1], rs1[:, 0:1], ALU.subtract, ALU.mult).then_inc(i_normed, 1)
                        at(pool, i_normed, f)
                        pool.tensor_tensor(x_new[:], x_new[:], l1w[:], ALU.mult).then_inc(i_scaled, 1)
                        at(pool, i_scaled, f)
                        pool.tensor_tensor(x_new[:], x_new[:], l1b[:], ALU.add).then_inc(x_ready, 1)
                    else:
                        pool.tensor_copy(x_new[:], tile(X, f)).then_inc(x_ready, 1)
                    if bor is not None:
                        pool.tensor_tensor(tile(kept, f), tile(X, f), bor[:], ALU.add).then_inc(kept_ready, 1)
                if front and form == "bounded":
                    at(pool, norm_safe, n + 1)
                    pool.tensor_tensor(ss[:], ss[:], core.neghalf[:, 0:2], ALU.pow).then_inc(norm_ready, 1)
                if output:
                    if two_norms:
                        if not (isinstance(t, int) and t < 1):
                            at_alone(pool, r_ready, t - 1, s.passed)
                        pool.tensor_tensor(xb[:], tile(X, t), bet[:], ALU.add).then_inc(xb_ready, 1)
                        at(pool, var_eps1, t)
                        pool.tensor_tensor(rs1[:], ve1[:], core.neghalf[:, 0:1], ALU.pow).then_inc(rstd1, 1)
                    if post != "l3ffn":
                        at(pool, var_eps, t)
                        pool.tensor_tensor(rs[:], ve[:], core.neghalf[:, 0:1], ALU.pow).then_inc(rstd, 1)
                        at_alone(pool, rstd, t, s.passed)
                        pool.tensor_scalar(xo[:], (rm if two_norms else r)[:], mv[:, 0:1], rs[:, 0:1],
                                           ALU.subtract, ALU.mult).then_inc(normed, 1)
                        at_alone(pool, normed, t, s.passed)
                        pool.tensor_copy(tile(X, t), xo[:]).then_inc(finished, 1)
            steps(pool, step)
            if post != "l3ffn":
                pool.wait_ge(finished, B + 1)

        @block.tensor
        def _(pe):
            pe.wait_ge(weights_in, 16 * len(loads))
            if setups:
                pe.wait_ge(setup, setups)

            def step(n, p, fetch=False, front=False, main=False, tail=False, output=False):
                f, t, d = n + 1, n - 1, n - 2

                def score_products(half, tiles):
                    if not (isinstance(n, int) and n == 0):
                        pe.wait_ge(pT_ready[half], n)
                    if mask and shifted:
                        for j in tiles:
                            pe.matmul(scores[:, j, 0:C * K], core.identb[:],
                                      msk[:].rearrange("t c k -> t (c k)"), start=True, stop=False, skip_group_check=True)
                    for c in range(C):
                        for j in tiles:
                            rows = slice(j * R, j * R + Q)
                            if shifted:
                                last = pe.matmul(scores[:, j, c * K:(c + 1) * K], q4[rows, c, :], k4[rows, c, :],
                                                 start=not mask, stop=True, skip_group_check=True)
                            else:
                                last = pe.matmul(scores[0:K, j, c * T:(c + 1) * T], k4[rows, c, :], q4[rows, c, :],
                                                 start=True, stop=True)
                    last.then_inc(s_psum[half], 1)

                def transposed(half, tiles):
                    at(pe, p_ready[half], n)
                    for c in range(C):
                        for j in tiles:
                            last = pe.transpose(scores[0:K, j, c * T:(c + 1) * T], S[:, j, c, :], core.ident[:])
                    last.then_inc(pT_psum[half], 1)

                def heads_back():
                    if not small:
                        return
                    at(pe, outT_ready, d)
                    for c in range(C):
                        last = pe.transpose(o_ps[:, 0, c * T:(c + 1) * T], outT[:, c, :], core.ident[:])
                    last.then_inc(o_psum, 1)

                def turned():
                    at(pe, o_ready, d)
                    ov = oS[:].rearrange("t h d -> t (h d)")
                    for b in range(NB):
                        last = pe.transpose(oT_ps[:, b * T:(b + 1) * T], ov[:, b * 128:(b + 1) * 128], core.ident[:])
                    last.then_inc(oT_psum, 1)

                def projected():
                    at(pe, oT_ready, d)
                    for b in range(NB):
                        last = pe.matmul(y_ps, oT[:, b, :], wo[:, b, :], start=b == 0, stop=b == NB - 1)
                    last.then_inc(y_psum, 1)

                if main:
                    at(pe, q_ready, n)
                    at(pe, k_ready, n)
                if front:
                    if not (isinstance(f, int) and f < 1):
                        pe.wait_ge(xT_ready, f)
                    at(pe, x_ready, f)
                    pe.transpose(xT_ps, xs[1 - p][:], core.ident[:]).then_inc(xT_psum, 1)
                if main:
                    score_products(*halves[0])
                if output:
                    heads_back()
                if front:
                    at(pe, xT_ready, f)
                    if context:
                        pe.wait_ge(ctx_in[1 - p], (f // 2 + 1) * 16 if isinstance(f, int) else f * 8 + 16 - 8 * (1 - p))
                    if not (isinstance(f, int) and f < 1):
                        pe.wait_ge(v_ready, f)
                    if small and context:
                        pe.matmul(proj_ps[:, 0:HD], xT[:], wx[:, 0, :], start=True, stop=True)
                        pe.matmul(proj_ps[0:K, HD:3 * HD], cs[1 - p][:], wc[:].rearrange("e a d -> e (a d)"),
                                  start=True, stop=True).then_inc(proj_psum, 1)
                    elif small:
                        pe.matmul(proj_ps[:, 0:WC * HD], xT[:], wx[:].rearrange("e a d -> e (a d)"),
                                  start=True, stop=True).then_inc(proj_psum, 1)
                    else:
                        for c in range(C):
                            pe.matmul(q_ps[:, c * T:(c + 1) * T], wx[:, c * 128:(c + 1) * 128], xT[:], start=True, stop=True)
                        for c in range(C):
                            pe.matmul(k_ps[:, c * K:(c + 1) * K], wk[:, c * 128:(c + 1) * 128], cs[1 - p][:], start=True, stop=True)
                        pe.matmul(proj_ps[0:K, :], cs[1 - p][:], wv[:], start=True, stop=True).then_inc(proj_psum, 1)
                if output:
                    turned()
                if main:
                    score_products(*halves[1])
                if output:
                    projected()
                if front and small:
                    at(pe, u_ready, f)
                    for c in range(C):
                        pe.transpose(q_ps[:, c * T:(c + 1) * T], U[1 - p][:, 0, c * J:(c + 1) * J, :].rearrange("t h r -> t (h r)"), core.ident[:])
                    for c in range(C):
                        last = pe.transpose(k_ps[:, c * K:(c + 1) * K], U[1 - p][0:K, 1, c * J:(c + 1) * J, :].rearrange("t h r -> t (h r)"),
                                            core.ident[0:K, 0:K])
                    last.then_inc(qkT_psum, 1)
                if main and shifted:
                    transposed(*halves[0])
                if tail:
                    at(pe, pT_ready[0], t)
                    at(pe, pT_ready[1], t)
                    at(pe, v_ready, t)
                    at(pe, y_read, t)
                    if small:
                        for c in range(C):
                            for j in range(J):
                                last = pe.matmul(outT_ps[j * R:(j + 1) * R, c * T:(c + 1) * T], U[1 - p][0:K, 2, c * J + j, :],
                                                 PTs[1 - p][:, j, c, :], start=True, stop=True)
                        last.then_inc(outT_psum, 1)
                    else:
                        for h in range(H):
                            o = o_ps[:, h // G, (h % G) * (Dh + 1):(h % G + 1) * (Dh + 1)]
                            last = pe.matmul(o, PTs[1 - p][:, h % J, h // J, :], V[1 - p][0:K, h, :], start=True, stop=True)
                        last.then_inc(o_psum, 1)
                if main and shifted:
                    transposed(*halves[1])
            steps(pe, step)

        @block.scalar
        def _(act):
            act.wait_ge(zeroed, 4)

            def step(n, p, fetch=False, front=False, main=False, tail=False, output=False):
                f, t, d = n + 1, n - 1, n - 2

                def exponentials(half):
                    own = slice(half * HJ, (half + 1) * HJ)
                    if shifted:
                        at(act, shifted_ready[half], n)
                        act.activation(S[:, own], S[:, own], ACT.Exp, scale=scale).then_inc(p_ready[half], 1)
                    elif form == "bounded":
                        at(act, s_psum[half], n)
                        act.activation(PTs[p][:, own], scores[0:K, own].rearrange("k j (c t) -> k j c t", t=T),
                                       ACT.Exp, scale=scale).then_inc(pT_ready[half], 1)

                if front:
                    at(act, xT_psum, f)
                    act.activation(xT[:], xT_ps, ACT.Copy).then_inc(xT_ready, 1)
                if output:
                    at(act, oT_psum, d)
                    act.activation(oT[:], oT_ps[:, 0:NB * T].rearrange("p (b t) -> p b t", b=NB), ACT.Copy).then_inc(oT_ready, 1)
                if main:
                    exponentials(0)
                if front and form == "linear":
                    at(act, raw, f)
                    act.activation(ef[:], sq[:], ACT.Exp).then_inc(expd, 1)
                if output and post == "gate":
                    at(act, gate_in, d)
                    act.activation(gt[:], gt[:], ACT.Exp, scale=-1.0).then_inc(gate_exp, 1)
                if main:
                    exponentials(1)
                if front:
                    at(act, qkT_psum if small else proj_psum, f)
                    if main and not small:
                        at(act, s_psum[1], n)
                    act.activation(q4[:], q_ps.rearrange("p (c t) -> p c t", c=C), ACT.Copy).then_inc(q_ready, 1)
                    if small:
                        act.activation(k4[:], k_ps[:, 0:C * K].rearrange("p (c t) -> p c t", c=C), ACT.Copy).then_inc(k_ready, 1)
                if main and shifted:
                    at(act, pT_psum[0], n)
                    act.activation(PTs[p][:, 0:HJ], scores[0:K, 0:HJ].rearrange("k j (c t) -> k j c t", t=T),
                                   ACT.Copy).then_inc(pT_ready[0], 1)
                if tail and small:
                    at(act, outT_psum, t)
                    act.activation(outT[:], outT_ps.rearrange("p (c t) -> p c t", c=C), ACT.Copy).then_inc(outT_ready, 1)
                if front and not small:
                    if tail:
                        at(act, o_psum, t)
                    act.activation(V[1 - p][0:K, :, 0:Dh], proj_ps[0:K].rearrange("k (h d) -> k h d", h=H),
                                   ACT.Copy).then_inc(v_ready, 1)
            steps(act, step)

        @block.vector
        def _(dve):
            dve.wait_ge(zeroed, 4)
            dve.wait_ge(weights_in, 16 * len(loads))
            if scaled:
                dve.tensor_tensor(wx[:], wx[:], grow[:], ALU.mult).then_inc(setup, 1)
                dve.tensor_tensor(brow[:, 0:3, :], brow[:, 0:3, :], grow[:], ALU.mult).then_inc(setup, 1)
                dve.tensor_tensor(bor[:], bor[:], lgam[:], ALU.mult).then_inc(setup, 1)
                dve.tensor_tensor(wo[:, 0, :], wo[:, 0, :], lgam[:], ALU.mult).then_inc(setup, 1)
                dve.wait_ge(setup, 4)
                dve.tensor_scalar(wo[:, 0, :], wo[:, 0, :], alpha[:, 0:1], None, ALU.mult).then_inc(setup, 1)
            if post == "l1x":
                dve.tensor_tensor(brow[:, 3, :], brow[:, 3, :], brow[:, 0, :], ALU.add).then_inc(setup, 1)
            if mask and shifted:
                dve.tensor_copy(msk[:], mask_in[:].unsqueeze(1).to_broadcast([T, C, T])).then_inc(setup, 1)
            if setups:
                dve.wait_ge(setup, setups)
            dve.sem_inc(y_read, 1)
            dve.sem_inc(finished, 1)

            def norm(src, n, bufs, done):
                st_, mv_, ve_ = bufs
                dve.bn_stats(st_[:], src).then_inc(done[0], 1)
                at_alone(dve, done[0], n, s.passed)
                dve.bn_aggr(mv_[:], st_[:]).then_inc(done[1], 1)
                at(dve, done[1], n)
                dve.tensor_scalar(ve_[:], mv_[:, 1:2], LN_EPS, None, ALU.add).then_inc(done[2], 1)

            def step(n, p, fetch=False, front=False, main=False, tail=False, output=False):
                f, t, d = n + 1, n - 1, n - 2

                def output_read():
                    at(dve, y_psum, d)
                    at(dve, kept_ready, d)
                    if post == "gate":
                        dve.tensor_tensor(gt[:], y_ps, tile(kept, d), ALU.add).then_inc(gate_in, 1)
                        at(dve, gate_in, d)
                        dve.sem_inc(y_read, 1)
                    elif post == "l3ffn":
                        dve.tensor_tensor(tile(x_after, d), y_ps, tile(kept, d), ALU.add).then_inc(y_read, 1)
                    else:
                        at(dve, finished, d)
                        dve.tensor_tensor(r[:], y_ps, tile(kept, d), ALU.add).then_inc(y_read, 1)

                def shift(half):
                    own = slice(half * HJ, (half + 1) * HJ)
                    at(dve, s_psum[half], n)
                    if shifted:
                        sc = scores[:, own, 0:C * K].rearrange("t j (c k) -> t j c k", c=C)
                        dve.tensor_reduce(mx[:, own], sc, AX.X, ALU.max).then_inc(max_ready[half], 1)
                        if half == 1 and output:
                            output_read()
                        at(dve, max_ready[half], n)
                        dve.tensor_tensor(S[:, own], sc, mx[:, own].unsqueeze(3).to_broadcast([T, HJ, C, K]),
                                          ALU.subtract).then_inc(shifted_ready[half], 1)
                    else:
                        dve.tensor_tensor(PTs[p][:, own].rearrange("k j c t -> k (j c) t"), scores[0:K, own].rearrange("k j (c t) -> k (j c) t", t=T),
                                          msk[:].unsqueeze(1).to_broadcast([K, HJ * C, T]), ALU.mult).then_inc(pT_ready[half], 1)

                if fetch and post == "l3ffn":
                    a = n + 2
                    if not (isinstance(a, int) and a < 1):
                        dve.wait_ge(x_ready, a)
                    norm(tile(X, a), a, (st1, mv1, ve1), (i_stats, i_mv, i_ve))
                if output:
                    at(dve, o_psum, d)
                    po = o_ps.rearrange("t n (g d) -> t n g d", g=G)
                    ov = oS[:].rearrange("t (n g) d -> t n g d", g=G)
                    if form == "linear":
                        dve.tensor_copy(ov, po[:, :, :, 0:Dh]).then_inc(o_ready, 1)
                    else:
                        rv = rz[:].rearrange("t (n g) -> t n g", g=G)
                        dve.reciprocal(rv.unsqueeze(3), po[:, :, :, Dh:Dh + 1]).then_inc(z_ready, 1)
                        at(dve, z_ready, d)
                        dve.tensor_tensor(ov, po[:, :, :, 0:Dh], rv.unsqueeze(3).to_broadcast([T, H // G, G, Dh]),
                                          ALU.mult).then_inc(o_ready, 1)
                if main and form != "bounded":
                    shift(0)
                if front and small:
                    at(dve, proj_psum, f)
                    u = U[1 - p]
                    pp = proj_ps.rearrange("t (a h d) -> t a h d", a=4, h=H)
                    bb = brow[:].rearrange("t a (h d) -> t a h d", h=H)
                    if post in ("gate", "l1x"):
                        a = 3 if post == "gate" else 0
                        dve.tensor_tensor(tile(kept, f), proj_ps[:, a * HD:(a + 1) * HD], brow[:, 3, :], ALU.add).then_inc(kept_ready, 1)
                    if form == "linear":
                        dve.tensor_tensor(sq[:], pp[:, 0:2], bb[:, 0:2], ALU.add).then_inc(raw, 1)
                        at(dve, raw, f)
                        dve.tensor_scalar(rl[:], sq[:], 0.0, None, ALU.max).then_inc(low, 1)
                    elif form == "bounded":
                        dve.tensor_tensor(u[:, 0, :, 0:Dh], pp[:, 0], bb[:, 0], ALU.add).then_inc(raw, 1)
                        dve.tensor_tensor(u[0:K, 1, :, 0:Dh], pp[0:K, 1], bb[0:K, 1], ALU.add).then_inc(raw, 1)
                        at(dve, raw, f, 2)
                        dve.tensor_tensor(sq[:], u[:, 0:2, :, 0:Dh], u[:, 0:2, :, 0:Dh], ALU.mult).then_inc(squares, 1)
                        at(dve, squares, f)
                        dve.tensor_reduce(ss[:], sq[:].rearrange("t a h d -> t a (h d)"), AX.X, ALU.add).then_inc(square_sum, 1)
                        at(dve, square_sum, f)
                        dve.tensor_scalar(ss[:], ss[:], 1e-24, None, ALU.max).then_inc(norm_safe, 1)
                    elif flow:
                        dve.tensor_tensor(u[:, 0:2, :, 0:Dh], pp[:, 0:2], bb[:, 0:2], ALU.add).then_inc(raw, 1)
                        at(dve, raw, f)
                        dve.tensor_scalar(u[:, 0, :, Dh:Q], u[:, 1, :, 0:Dh], -1.0, None, ALU.mult).then_inc(q_biased, 1)
                        dve.tensor_copy(u[:, 1, :, Dh:Q], u[:, 0, :, 0:Dh]).then_inc(u_ready, 1)
                    elif context:
                        dve.tensor_tensor(u[:, 0, :, 0:Dh], pp[:, 0], bb[:, 0], ALU.add).then_inc(q_biased, 1)
                        dve.tensor_tensor(u[0:K, 1, :, 0:Dh], pp[0:K, 1], bb[0:K, 1], ALU.add).then_inc(u_ready, 1)
                    else:
                        dve.tensor_tensor(u[:, 0:2, :, 0:Dh], pp[:, 0:2], bb[:, 0:2], ALU.add).then_inc(u_ready, 1)
                if front and form == "bounded":
                    u = U[1 - p]
                    at(dve, norm_ready, f)
                    dve.tensor_tensor(u[:, 0:2, :, 0:Dh], u[:, 0:2, :, 0:Dh],
                                      ss[:].unsqueeze(2).unsqueeze(3).to_broadcast([T, 2, H, Dh]), ALU.mult).then_inc(u_ready, 1)
                if front and form == "linear":
                    u = U[1 - p]
                    at(dve, expd, f)
                    at(dve, low, f)
                    dve.scalar_tensor_tensor(out=u[:, 0:2, :, 0:Dh], in0=ef[:], scalar=1.0, in1=rl[:],
                                             op0=ALU.min, op1=ALU.add).then_inc(u_ready, 1)
                if main and form != "bounded":
                    shift(1)
                if output and not (main and shifted):
                    output_read()
                if front and not small:
                    at(dve, proj_psum, f)
                    if main:
                        at(dve, s_psum[1], n)
                    dve.tensor_copy(k4[:], k_ps[:, 0:C * K].rearrange("p (c t) -> p c t", c=C)).then_inc(k_ready, 1)
                if output:
                    if post == "gate":
                        at(dve, gate_exp, d)
                        dve.tensor_scalar(gt[:], gt[:], 1.0, None, ALU.add).then_inc(gate_plus1, 1)
                        at(dve, gate_plus1, d)
                        dve.reciprocal(gt[:], gt[:]).then_inc(gate_ready, 1)
                        at(dve, gate_ready, d)
                        dve.tensor_tensor(gt[:], gt[:], oS[:].rearrange("t h d -> t (h d)"), ALU.mult).then_inc(gated, 1)
                        at(dve, gated, d)
                        at(dve, finished, d)
                        dve.tensor_tensor(r[:], gt[:], tile(X, d), ALU.add).then_inc(r1_ready, 1)
                        at(dve, r1_ready, d)
                        norm(r[:], d, (st1, mv1, ve1), (stats1, mean_var1, var_eps1))
                    elif post != "l3ffn":
                        at_alone(dve, y_read, d + 1, s.passed)
                        if post == "l1x":
                            norm(r[:], d, (st1, mv1, ve1), (stats1, mean_var1, var_eps1))
                        else:
                            norm(r[:], d, (st, mv, ve), (stats, mean_var, var_eps))
                if output and two_norms:
                    at(dve, mean_var1, d)
                    dve.scalar_tensor_tensor(out=rm[:], in0=r[:], scalar=mv1[:, 0:1], in1=gam[:], op0=ALU.subtract, op1=ALU.mult).then_inc(scaled1, 1)
                if front and small:
                    if tail:
                        at(dve, outT_psum, t)
                    else:
                        at(dve, proj_psum, f)
                    dve.tensor_tensor(U[1 - p][0:K, 2, :, 0:Dh], proj_ps[0:K, 2 * HD:3 * HD].rearrange("t (h d) -> t h d", h=H),
                                      brow[0:K, 2, :].rearrange("t (h d) -> t h d", h=H), ALU.add).then_inc(v_ready, 1)
                if main and shifted:
                    at(dve, pT_psum[1], n)
                    dve.tensor_copy(PTs[p][:, HJ:J], scores[0:K, HJ:J].rearrange("k j (c t) -> k j c t", t=T)).then_inc(pT_ready[1], 1)
                if output and two_norms:
                    at(dve, rstd1, d)
                    at(dve, scaled1, d)
                    at(dve, xb_ready, d)
                    dve.scalar_tensor_tensor(out=rm[:], in0=rm[:], scalar=rs1[:, 0:1], in1=xb[:], op0=ALU.mult, op1=ALU.add).then_inc(r_ready, 1)
                    at_alone(dve, r_ready, d, s.passed)
                    norm(rm[:], d, (st, mv, ve), (stats, mean_var, var_eps))
            steps(dve, step)
    s.close()


def batch_axis_attention(core):
    nc, X = core.nc, core.X
    before = nc.dram_tensor("x_by_position", (T, B, D), F32, kind="Internal").ap()
    after = nc.dram_tensor("x_by_batch", (T, B, D), F32, kind="Internal").ap()

    def reorder(name, order_out, order_in):
        s = Scope(nc, name)
        moved = s.sem("moved")
        with nc.Block() as block:
            @block.sync
            def _(sp):
                sp.dma_start(order_out, X[:]).then_inc(moved, 16)
                sp.wait_ge(moved, 16)
                sp.dma_start(X[:], order_in).then_inc(moved, 16)
                sp.wait_ge(moved, 32)
        s.close()

    def by_tile(a):
        return a.rearrange("(n g) b d -> (g b) n d", g=T // B)
    reorder("L2out", before, by_tile(before))
    attention(core, "L2self", H=16, Dh=8, Wq="L2_attn_Wq", Wk="L2_attn_Wk", Wv="L2_attn_Wv", Wo="L2_attn_WoT",
              bq="L2_attn_bq", bk="L2_attn_bk", bv="L2_attn_bv", bo="L2_attn_out_proj_bias",
              mask="mask_within", post="l2self")
    reorder("L2back", by_tile(after), after)


def expert_pass(core, name, *, w1, b1, w2, act, xT, gates):
    nc, I, X = core.nc, core.I, core.X
    s = Scope(nc, name)
    CH = 4
    N = B // CH
    w1s, w2s, b1s = s.lanes("w1", [D, F]), s.lanes("w2", [128, FC, D]), s.lanes("b1", [128, FC])
    hT = s.lanes("hT", [128, FC, CH * T])
    gy = s.lanes("gy", [T, CH, D])
    ph = s.psum("ph", [128, FC, 512])
    py = s.psum("py", [128, 2, 512])
    w_in = [s.sem(f"weights_in{k}") for k in range(LANES)]
    h_psum, h_ready, y_psum, y_gated, added = [s.sem(n) for n in ("h_psum", "h_ready", "y_psum", "y_gated", "added")]
    H0, Y0, G0, A0 = FC, 2 * N, 2, 1
    st, mv = s.sb("st", [T, N, CH, 6]), s.sb("mv", [T, N, CH, 2])
    ve, rs = s.sb("ve", [T, N, CH]), s.sb("rs", [T, N, CH])
    stats, mean_var, var_eps, rstd, finished = [s.sem(n) for n in ("stats", "mean_var", "var_eps", "rstd", "finished")]
    Xf, xTf = X[:].rearrange("t b d -> t (b d)"), xT[:]

    with nc.Block() as block:
        @block.sync
        def _(sp):
            with sp.Fori(0, E // LANES) as i:
                for lane in range(LANES):
                    e = i * LANES + lane
                    sp.wait_ge(y_psum, (e + 1) * N)
                    with nc.allow_non_contiguous_dma(reason="a bias column"):
                        sp.dma_start(w1s[lane][:], I[w1][bass.ds(e, 1)].rearrange("a d f -> d (a f)")).then_inc(w_in[lane], 16)
                        sp.dma_start(w2s[lane][:], I[w2][bass.ds(e, 1)].rearrange("a (c p) d -> p (a c) d", p=128)).then_inc(w_in[lane], 16)
                        sp.dma_start(b1s[lane][:], I[b1][bass.ds(e, 1)].rearrange("a (c p) -> p (a c)", p=128)).then_inc(w_in[lane], 16)

        @block.gpsimd
        def _(pool):
            for k in range(N):
                pool.wait_ge(var_eps, k + 1)
                pool.tensor_tensor(rs[:, k, :], ve[:, k, :], core.neghalf[:, 0:CH], ALU.pow).then_inc(rstd, 1)

        @block.tensor
        def _(pe):
            pe.sem_inc(y_psum, Y0)
            pe.sem_inc(h_ready, H0)
            with pe.Fori(0, E // LANES) as i:
                for lane in range(LANES):
                    e = i * LANES + lane
                    with pe.Fori(0, N // 2) as c2:
                        at(pe, w_in[lane], i, 48)
                        for par in range(2):
                            m = e * N + c2 * 2 + par
                            for f in range(FC):
                                pe.wait_ge(h_ready, m * FC + f + 1)
                                pe.matmul(ph[:, f, :], w1s[lane][:, f * 128:(f + 1) * 128],
                                          xTf[:, bass.ds((c2 * 2 + par) * (CH * T), CH * T)], start=True, stop=True).then_inc(h_psum, 1)
                        for par in range(2):
                            m = e * N + c2 * 2 + par
                            pe.wait_ge(h_ready, m * FC + FC + H0)
                            pe.wait_ge(y_gated, m + 1)
                            for b in range(CH):
                                for f in range(FC):
                                    last = pe.matmul(py[:, par, b * D:(b + 1) * D], hT[par][:, f, b * T:(b + 1) * T],
                                                     w2s[lane][:, f, :], start=f == 0, stop=f == FC - 1)
                            last.then_inc(y_psum, 1)

        @block.scalar
        def _(act_eng):
            with act_eng.Fori(0, E // LANES) as i:
                for lane in range(LANES):
                    e = i * LANES + lane
                    with act_eng.Fori(0, N // 2) as c2:
                        at(act_eng, w_in[lane], i, 48)
                        for par in range(2):
                            m = e * N + c2 * 2 + par
                            act_eng.wait_ge(y_psum, m - 1 + Y0)
                            for f in range(FC):
                                act_eng.wait_ge(h_psum, m * FC + f + 1)
                                act_eng.activation(hT[par][:, f, :], ph[:, f, :], act, bias=b1s[lane][:, f:f + 1]).then_inc(h_ready, 1)

        @block.vector
        def _(dve):
            dve.sem_inc(y_gated, G0)
            dve.sem_inc(added, A0)
            gates_f = gates[:].rearrange("t e b -> t (e b)")

            def chunk(m, k):
                par = k % 2
                dve.wait_ge(y_psum, m + 1 + Y0)
                dve.wait_ge(added, m + A0)
                g = gates_f[:, m * CH:(m + 1) * CH] if isinstance(m, int) else gates_f[:, bass.ds(m * CH, CH)]
                dve.tensor_tensor(gy[par][:], py[:, par, :].rearrange("t (b d) -> t b d", b=CH),
                                  g.unsqueeze(2).to_broadcast([T, CH, D]), ALU.mult).then_inc(y_gated, 1)
                dve.wait_ge(y_gated, m + 1 + G0)
                xc = Xf[:, k * CH * D:(k + 1) * CH * D]
                dve.tensor_tensor(xc, xc, gy[par][:].rearrange("t b d -> t (b d)"), ALU.add).then_inc(added, 1)

            def statistics(k):
                dve.wait_ge(added, (E - 1) * N + k + 1 + A0)
                for b in range(CH):
                    dve.bn_stats(st[:, k, b, :], X[:, k * CH + b, :]).then_inc(stats, 1)
                dve.wait_ge(stats, (k + 1) * CH)
                for b in range(CH):
                    dve.bn_aggr(mv[:, k, b, :], st[:, k, b, :]).then_inc(mean_var, 1)
                dve.wait_ge(mean_var, (k + 1) * CH)
                dve.tensor_scalar(ve[:, k, :].unsqueeze(2), mv[:, k, :, 1:2], LN_EPS, None, ALU.add).then_inc(var_eps, 1)

            def normed(k):
                dve.wait_ge(rstd, k + 1)
                for b in range(CH):
                    dve.tensor_scalar(X[:, k * CH + b, :], X[:, k * CH + b, :], mv[:, k, b, 0:1], rs[:, k, b:b + 1],
                                      ALU.subtract, ALU.mult).then_inc(finished, 1)

            with dve.Fori(0, E - 1) as i:
                for k in range(N):
                    chunk(i * N + k, k)
            for k in range(N):
                chunk((E - 1) * N + k, k)
                if k:
                    normed(k - 1)
                statistics(k)
            normed(N - 1)
            dve.wait_ge(finished, B)
    s.close()


def route(core, name, xT, gates, *, kind, top, X1=None):
    nc, I, X = core.nc, core.I, core.X
    s = Scope(nc, name)
    NK = E if top == 1 else 2

    def lanes(tag, shape, dtype=F32):
        return s.lanes(tag, shape, dtype, n=MANY)

    loads = []

    def tile(tag, shape, src):
        t = s.sb(tag, shape)
        loads.append((t[:], src))
        return t

    b2 = tile("b2", [E, D], I[{"L0": "L0_ffn_b2", "L1": "L1_ffn_b2", "L3": "L3_ffn_fc2_b"}[kind]])
    iota = tile("iota", [T, E], row_bc(I["iota8"]))
    normed_input = kind != "L0"
    if kind == "L0":
        w_red = tile("w_red", [D, 16], I["L0_ffn_w_red"])
        wgT = tile("wgT", [16, E], I["L0_ffn_wg"].rearrange("e g -> g e"))
        wsq, wnorm, wgn = s.sb("wsq", [16, E]), s.sb("wnorm", [16, E]), s.sb("wgn", [16, E])
        redT = lanes("redT", [16, T])
    elif kind == "L1":
        wr = tile("wr", [D, E], I["L1_ffn_Wr"])
        br = tile("br", [T, E], row_bc(I["L1_ffn_br"]))
        gam, bet = tile("gam", [T, D], row_bc(I["L1_ffn_ln_g"])), tile("bet", [T, D], row_bc(I["L1_ffn_ln_b"]))
    else:
        wr = tile("wr", [D, E], I["L3_ffn_gate_W"])
        gam, bet = tile("gam", [T, D], row_bc(I["L3_ffn_ln2_w"])), tile("bet", [T, D], row_bc(I["L3_ffn_ln2_b"]))
    xs, xn, xTs, gT = lanes("xs", [T, D]), lanes("xn", [T, D]), lanes("xTs", [D, T]), lanes("gT", [E, T])
    lg, m8, nmx = lanes("lg", [T, E]), lanes("m8", [T, 8]), lanes("nmx", [T, 1])
    idx, idf, ex = lanes("idx", [T, 8], U32), lanes("idf", [T, 8]), lanes("ex", [T, 8])
    sm, pr, g8, g8b = lanes("sm", [T, 1]), lanes("pr", [T, 8]), lanes("g8", [T, E]), lanes("g8b", [T, E])
    st, mv, ve, rs, xb = lanes("st", [T, 6]), lanes("mv", [T, 2]), lanes("ve", [T, 1]), lanes("rs", [T, 1]), lanes("xb", [T, D])
    ps = [s.psum(f"ps{lane}", [128, 2, 512]) for lane in range(MANY)]
    names = ("weights_in lane_free x_copied x_psum xT_ready xnT_ready red_psum red_ready logits_psum logits_ready sorted negmax "
             "index_ready index_float exp_ready recip_ready prob_ready gate1 gate2 gate_ready gT_psum gT_ready bias_psum "
             "biased stats mean_var var_eps rstd normed scaled offset wsq_ready wnorm_psum wnorm_safe wnorm_pow wg_ready gate_stored")
    S_ = type("Ready", (), {n: s.sem(n) for n in names.split()})
    with nc.Block() as block:
        @block.sync
        def _(sp):
            with nc.allow_non_contiguous_dma(reason="small weights, once"):
                for dst, src in loads:
                    sp.dma_start(dst, src).then_inc(S_.weights_in, 16)

        @block.gpsimd
        def _(pool):
            if kind == "L0":
                pool.wait_ge(S_.wnorm_safe, 1)
                pool.tensor_tensor(wnorm[:], wnorm[:], core.neghalf[0:16, 0:E], ALU.pow).then_inc(S_.wnorm_pow, 1)
            pool.sem_inc(S_.lane_free, MANY)
            with pool.Fori(0, B // MANY) as i:
                for lane in range(MANY):
                    n = i * MANY + lane
                    at(pool, S_.lane_free, n)
                    pool.tensor_copy(xs[lane][:], (X1 or X)[:, bass.ds(n, 1), :].rearrange("t a d -> t (a d)")).then_inc(S_.x_copied, 1)
                if normed_input:
                    for lane in range(MANY):
                        at(pool, S_.var_eps, i * MANY + lane)
                        pool.tensor_tensor(rs[lane][:], ve[lane][:], core.neghalf[:, 0:1], ALU.pow).then_inc(S_.rstd, 1)

        @block.tensor
        def _(pe):
            pe.wait_ge(S_.weights_in, 16 * len(loads))
            if kind == "L0":
                pe.wait_ge(S_.wsq_ready, 1)
                pe.matmul(ps[0][0:16, 0, 0:E], core.ones[0:16, 0:16], wsq[:], start=True, stop=True).then_inc(S_.wnorm_psum, 1)
                pe.wait_ge(S_.wg_ready, 1)
            with pe.Fori(0, B // MANY) as i:
                for lane in range(MANY):
                    n = i * MANY + lane
                    if normed_input:
                        at(pe, S_.offset, n)
                        pe.transpose(ps[lane][:, 0, 128:256], xn[lane][:], core.ident[:])
                    at(pe, S_.x_copied, n)
                    pe.transpose(ps[lane][:, 0, 0:T], xs[lane][:], core.ident[:]).then_inc(S_.x_psum, 1)
                if kind == "L0":
                    for lane in range(MANY):
                        at(pe, S_.xT_ready, i * MANY + lane)
                        pe.matmul(ps[lane][0:16, 1, 384:512], w_red[:], xTs[lane][:], start=True, stop=True).then_inc(S_.red_psum, 1)
                for lane in range(MANY):
                    n = i * MANY + lane
                    if kind == "L0":
                        at(pe, S_.red_ready, n)
                        pe.matmul(ps[lane][:, 1, 0:E], redT[lane][:], wgn[:], start=True, stop=True).then_inc(S_.logits_psum, 1)
                    else:
                        at(pe, S_.xT_ready, n)
                        pe.matmul(ps[lane][:, 1, 0:E], xTs[lane][:], wr[:], start=True, stop=True).then_inc(S_.logits_psum, 1)
                for lane in range(MANY):
                    at(pe, S_.gate_ready, i * MANY + lane)
                    pe.transpose(ps[lane][0:E, 1, 128:256], g8[lane][:], core.ident[:]).then_inc(S_.gT_psum, 1)
                for lane in range(MANY):
                    at(pe, S_.gT_ready, i * MANY + lane)
                    pe.matmul(ps[lane][:, 1, 256:384], gT[lane][:], b2[:], start=True, stop=True).then_inc(S_.bias_psum, 1)

        @block.scalar
        def _(act):
            with act.Fori(0, B // MANY) as i:
                for lane in range(MANY):
                    n = i * MANY + lane
                    at(act, S_.x_psum, n)
                    logits_of = ps[lane][:, 0, 128:256] if kind == "L3" else ps[lane][:, 0, 0:T]
                    experts_of = ps[lane][:, 0, 128:256] if normed_input else ps[lane][:, 0, 0:T]
                    act.activation(xTs[lane][:], logits_of, ACT.Copy).then_inc(S_.xT_ready, 1)
                    act.activation(xT[:, bass.ds(n * T, T)], experts_of, ACT.Copy).then_inc(S_.xnT_ready, 1)
                if kind == "L0":
                    for lane in range(MANY):
                        at(act, S_.red_psum, i * MANY + lane)
                        act.activation(redT[lane][:], ps[lane][0:16, 1, 384:512], ACT.Copy).then_inc(S_.red_ready, 1)
                for lane in range(MANY):
                    at(act, S_.negmax, i * MANY + lane)
                    act.activation(ex[lane][:, 0:NK], m8[lane][:, 0:NK], ACT.Exp, bias=nmx[lane][:, 0:1],
                                   accum_out=sm[lane][:]).then_inc(S_.exp_ready, 1)
                for lane in range(MANY):
                    at(act, S_.gT_psum, i * MANY + lane)
                    act.activation(gT[lane][:], ps[lane][0:E, 1, 128:256], ACT.Copy).then_inc(S_.gT_ready, 1)

        @block.vector
        def _(dve):
            dve.wait_ge(S_.weights_in, 16 * len(loads))
            if kind == "L0":
                dve.tensor_tensor(wsq[:], wgT[:], wgT[:], ALU.mult).then_inc(S_.wsq_ready, 1)
                dve.wait_ge(S_.wnorm_psum, 1)
                dve.tensor_scalar(wnorm[:], ps[0][0:16, 0, 0:E], 1e-8, None, ALU.max).then_inc(S_.wnorm_safe, 1)
                dve.wait_ge(S_.wnorm_pow, 1)
                dve.tensor_tensor(wgn[:], wgT[:], wnorm[:], ALU.mult).then_inc(S_.wg_ready, 1)
            with dve.Fori(0, B // MANY) as i:
                if normed_input:
                    for lane in range(MANY):
                        n = i * MANY + lane
                        at(dve, S_.x_copied, n)
                        dve.bn_stats(st[lane][:], xs[lane][:]).then_inc(S_.stats, 1)
                    for lane in range(MANY):
                        n = i * MANY + lane
                        at_alone(dve, S_.stats, n, s.passed)
                        dve.bn_aggr(mv[lane][:], st[lane][:]).then_inc(S_.mean_var, 1)
                    for lane in range(MANY):
                        n = i * MANY + lane
                        at(dve, S_.mean_var, n)
                        dve.tensor_scalar(ve[lane][:], mv[lane][:, 1:2], LN_EPS, None, ALU.add).then_inc(S_.var_eps, 1)
                    for lane in range(MANY):
                        n = i * MANY + lane
                        at(dve, S_.rstd, n)
                        dve.tensor_scalar(xn[lane][:], xs[lane][:], mv[lane][:, 0:1], rs[lane][:, 0:1], ALU.subtract, ALU.mult).then_inc(S_.normed, 1)
                    for lane in range(MANY):
                        n = i * MANY + lane
                        at(dve, S_.normed, n)
                        dve.tensor_tensor(xn[lane][:], xn[lane][:], gam[:], ALU.mult).then_inc(S_.scaled, 1)
                    for lane in range(MANY):
                        n = i * MANY + lane
                        at(dve, S_.scaled, n)
                        dve.tensor_tensor(xn[lane][:], xn[lane][:], bet[:], ALU.add).then_inc(S_.offset, 1)
                for lane in range(MANY):
                    n = i * MANY + lane
                    at(dve, S_.logits_psum, n)
                    if kind == "L1":
                        dve.tensor_tensor(lg[lane][:], ps[lane][:, 1, 0:E], br[:], ALU.add).then_inc(S_.logits_ready, 1)
                    else:
                        dve.tensor_copy(lg[lane][:], ps[lane][:, 1, 0:E]).then_inc(S_.logits_ready, 1)
                for lane in range(MANY):
                    n = i * MANY + lane
                    at_alone(dve, S_.logits_ready, n, s.passed)
                    dve.max(m8[lane][:], lg[lane][:]).then_inc(S_.sorted, 1)
                for lane in range(MANY):
                    n = i * MANY + lane
                    at(dve, S_.sorted, n)
                    dve.tensor_scalar(nmx[lane][:], m8[lane][:, 0:1], -1.0, None, ALU.mult).then_inc(S_.negmax, 1)
                for lane in range(MANY):
                    dve.max_index(idx[lane][:], m8[lane][:], lg[lane][:]).then_inc(S_.index_ready, 1)
                for lane in range(MANY):
                    n = i * MANY + lane
                    at(dve, S_.index_ready, n)
                    dve.tensor_copy(idf[lane][:], idx[lane][:]).then_inc(S_.index_float, 1)
                for lane in range(MANY):
                    n = i * MANY + lane
                    at(dve, S_.exp_ready, n)
                    dve.reciprocal(sm[lane][:], sm[lane][:]).then_inc(S_.recip_ready, 1)
                for lane in range(MANY):
                    n = i * MANY + lane
                    at(dve, S_.recip_ready, n)
                    dve.tensor_scalar(pr[lane][:, 0:top], ex[lane][:, 0:top], sm[lane][:, 0:1], None, ALU.mult).then_inc(S_.prob_ready, 1)
                for lane in range(MANY):
                    n = i * MANY + lane
                    at(dve, S_.prob_ready, n)
                    dve.tensor_scalar(g8[lane][:], iota[:], idf[lane][:, 0:1], pr[lane][:, 0:1], ALU.is_equal, ALU.mult).then_inc(S_.gate_ready if top == 1 else S_.gate1, 1)
                for lane in range(MANY):
                    n = i * MANY + lane
                    if top == 2:
                        dve.tensor_scalar(g8b[lane][:], iota[:], idf[lane][:, 1:2], pr[lane][:, 1:2], ALU.is_equal, ALU.mult).then_inc(S_.gate2, 1)
                        at(dve, S_.gate2, n)
                        dve.tensor_tensor(g8[lane][:], g8[lane][:], g8b[lane][:], ALU.add).then_inc(S_.gate_ready, 1)
                for lane in range(MANY):
                    n = i * MANY + lane
                    at(dve, S_.gate_ready, n)
                    dve.tensor_copy(gates[:, :, bass.ds(n, 1)], g8[lane][:].unsqueeze(2)).then_inc(S_.gate_stored, 1)
                for lane in range(MANY):
                    n = i * MANY + lane
                    at(dve, S_.bias_psum, n)
                    dve.tensor_tensor(xb[lane][:], ps[lane][:, 1, 256:384], xs[lane][:], ALU.add).then_inc(S_.biased, 1)
                for lane in range(MANY):
                    n = i * MANY + lane
                    at(dve, S_.biased, n)
                    row = X[:, bass.ds(n, 1), :].rearrange("t a d -> t (a d)")
                    if X1 is None:
                        dve.tensor_copy(row, xb[lane][:]).then_inc(S_.lane_free, 1)
                    else:
                        dve.tensor_tensor(row, row, xb[lane][:], ALU.add).then_inc(S_.lane_free, 1)
    s.close()


def experts_top1(core, name):
    nc = core.nc
    kind = name[:2]
    with ExitStack() as stack:
        xT = stack.enter_context(nc.sbuf_tensor(f"{name}_xT", [D, B * T], F32))
        gates = stack.enter_context(nc.sbuf_tensor(f"{name}_gates", [T, E, B], F32))
        route(core, f"{name}_route", xT, gates, kind=kind, top=1)
        w = ("w1", "b1", "w2") if kind == "L0" else ("W1", "b1", "W2")
        expert_pass(core, f"{name}_pass", w1=f"{kind}_ffn_{w[0]}", b1=f"{kind}_ffn_{w[1]}", w2=f"{kind}_ffn_{w[2]}",
                    act=ACT.Gelu if kind == "L0" else ACT.Relu, xT=xT, gates=gates)


def block_experts(core):
    nc = core.nc
    with ExitStack() as stack:
        X1 = stack.enter_context(nc.sbuf_tensor("X1", [T, B, D], F32))
        attention(core, "L3self", H=16, Dh=8, Wq="L3_ffn_Wq", Wk="L3_ffn_Wk", Wv="L3_ffn_Wv", Wo="L3_ffn_Wo",
                  bq="L3_ffn_bq", bk="L3_ffn_bk", bv="L3_ffn_bv", bo="L3_ffn_bo", mask="mask_causal",
                  post="l3ffn", x_after=X1)
        xT = stack.enter_context(nc.sbuf_tensor("L3ffn_xT", [D, B * T], F32))
        gates = stack.enter_context(nc.sbuf_tensor("L3ffn_gates", [T, E, B], F32))
        route(core, "L3ffn_route", xT, gates, kind="L3", top=2, X1=X1)
        expert_pass(core, "L3ffn_pass", w1="L3_ffn_fc1T", b1="L3_ffn_fc1_b", w2="L3_ffn_fc2T", act=ACT.Gelu,
                    xT=xT, gates=gates)


def wkv_mix(core):
    nc, I, X = core.nc, core.I, core.X
    s = Scope(nc, "wkv")

    def lanes(tag, shape, dtype=F32):
        return s.lanes(tag, shape, dtype, n=MANY)

    loads = []

    def tile(tag, shape, src):
        t = s.sb(tag, shape)
        loads.append((t[:], src))
        return t

    mix = {c: tile(f"mix_{c}", [D, 1], col(I[f"L1_attn_time_mix_{c}"])) for c in "kvr"}
    W = {c: tile(f"W{c}", [D, D], I[f"L1_attn_W{c}T"]) for c in "kvr"}
    Wo = tile("Wo", [D, D], I["L1_attn_WoT"])
    decay_in = tile("decay_in", [D, 1], col(I["L1_attn_time_decay"]))
    first = tile("first", [D, 1], col(I["L1_attn_time_first"]))
    decay, decays = s.sb("decay", [D, 1]), s.sb("decays", [D, T])
    rest = {c: s.sb(f"rest_{c}", [D, 1]) for c in "kvr"}
    START = -1e38

    xs, r = lanes("xs", [T, D]), lanes("r", [T, D])
    xT = lanes("xT", [D, T + 1])
    mixed = {c: lanes(f"mixed_{c}", [D, T]) for c in "kvr"}
    shifted = {c: lanes(f"shifted_{c}", [D, T]) for c in "kvr"}
    k, v, sr = lanes("k", [D, T]), lanes("v", [D, T]), lanes("sr", [D, T])
    pp, aa, bb = lanes("pp", [D, T + 1]), lanes("aa", [D, T + 1]), lanes("bb", [D, T + 1])
    ex = lanes("ex", [D, 4, T])
    ww, p = lanes("ww", [D, T]), lanes("p", [D, T])
    ev, num, den, y = lanes("ev", [D, 2, T]), lanes("num", [D, T]), lanes("den", [D, T]), lanes("y", [D, T])
    st, mv, ve, rs = lanes("st", [T, 6]), lanes("mv", [T, 2]), lanes("ve", [T, 1]), lanes("rs", [T, 1])
    ps = [s.psum(f"ps{lane}", [128, 2, 512]) for lane in range(MANY)]
    names = ("weights_in lane_free starts_set decay_exp decay_neg decays_ready rests_ready x_copied x_psum xT_ready mixed_ready "
             "rest_mixed kvr_psum kv_ready r_exp max_scanned exps_in exps_ready ev_ready sums_scanned ww_ready "
             "p_ready num1 num2 den1 den2 den_scaled den_inv y_ready out_psum sum_ready stats mean_var var_eps rstd")
    S_ = type("Ready", (), {n: s.sem(n) for n in names.split()})
    with nc.Block() as block:
        @block.sync
        def _(sp):
            with nc.allow_non_contiguous_dma(reason="small weights, once"):
                for dst, src in loads:
                    sp.dma_start(dst, src).then_inc(S_.weights_in, 16)

        @block.gpsimd
        def _(pool):
            for lane in range(MANY):
                pool.memset(xT[lane][:, 0:1], 0.0).then_inc(S_.starts_set, 1)
                pool.memset(pp[lane][:, 0:1], START).then_inc(S_.starts_set, 1)
                pool.memset(aa[lane][:, 0:1], 0.0).then_inc(S_.starts_set, 1)
                pool.memset(bb[lane][:, 0:1], 0.0).then_inc(S_.starts_set, 1)
            pool.sem_inc(S_.lane_free, MANY)
            with pool.Fori(0, B // MANY) as i:
                for lane in range(MANY):
                    n = i * MANY + lane
                    at(pool, S_.lane_free, n)
                    pool.tensor_copy(xs[lane][:], X[:, bass.ds(n, 1), :].rearrange("t a d -> t (a d)")).then_inc(S_.x_copied, 1)
                for lane in range(MANY):
                    at(pool, S_.var_eps, i * MANY + lane)
                    pool.tensor_tensor(rs[lane][:], ve[lane][:], core.neghalf[:, 0:1], ALU.pow).then_inc(S_.rstd, 1)

        @block.tensor
        def _(pe):
            pe.wait_ge(S_.weights_in, 16 * len(loads))
            with pe.Fori(0, B // MANY) as i:
                for lane in range(MANY):
                    at(pe, S_.x_copied, i * MANY + lane)
                    pe.transpose(ps[lane][:, 0, 0:T], xs[lane][:], core.ident[:]).then_inc(S_.x_psum, 1)
                for lane in range(MANY):
                    at(pe, S_.mixed_ready, i * MANY + lane, 3)
                    for j, c in enumerate("kvr"):
                        last = pe.matmul(ps[lane][:, 1, j * T:(j + 1) * T], W[c][:], mixed[c][lane][:], start=True, stop=True)
                    last.then_inc(S_.kvr_psum, 1)
                for lane in range(MANY):
                    at(pe, S_.y_ready, i * MANY + lane)
                    pe.matmul(ps[lane][:, 0, 128:256], y[lane][:], Wo[:], start=True, stop=True).then_inc(S_.out_psum, 1)

        @block.scalar
        def _(act):
            act.wait_ge(S_.weights_in, 16 * len(loads))
            act.activation(decay[:], decay_in[:], ACT.Exp).then_inc(S_.decay_exp, 1)
            act.wait_ge(S_.starts_set, 4 * MANY)
            with act.Fori(0, B // MANY) as i:
                for lane in range(MANY):
                    at(act, S_.x_psum, i * MANY + lane)
                    act.activation(xT[lane][:, 1:T + 1], ps[lane][:, 0, 0:T], ACT.Copy).then_inc(S_.xT_ready, 1)
                for lane in range(MANY):
                    at(act, S_.kvr_psum, i * MANY + lane)
                    act.activation(k[lane][:], ps[lane][:, 1, 0:T], ACT.Copy).then_inc(S_.kv_ready, 1)
                    act.activation(v[lane][:], ps[lane][:, 1, T:2 * T], ACT.Copy).then_inc(S_.kv_ready, 1)
                    act.activation(sr[lane][:], ps[lane][:, 1, 2 * T:3 * T], ACT.Exp, scale=-1.0).then_inc(S_.r_exp, 1)
                for lane in range(MANY):
                    at(act, S_.exps_in, i * MANY + lane, 4)
                    act.activation(ex[lane][:], ex[lane][:], ACT.Exp).then_inc(S_.exps_ready, 1)

        @block.vector
        def _(dve):
            dve.wait_ge(S_.starts_set, 4 * MANY)
            dve.wait_ge(S_.decay_exp, 1)
            dve.tensor_scalar(decay[:], decay[:], -1.0, None, ALU.mult).then_inc(S_.decay_neg, 1)
            dve.wait_ge(S_.decay_neg, 1)
            dve.tensor_scalar(decays[:], core.ones[:], decay[:, 0:1], None, ALU.mult).then_inc(S_.decays_ready, 1)
            for c in "kvr":
                dve.tensor_scalar(rest[c][:], mix[c][:], -1.0, 1.0, ALU.mult, ALU.add).then_inc(S_.rests_ready, 1)
            dve.wait_ge(S_.decays_ready, 1)
            dve.wait_ge(S_.rests_ready, 3)
            with dve.Fori(0, B // MANY) as i:
                for lane in range(MANY):
                    n = i * MANY + lane
                    at(dve, S_.xT_ready, n)
                    for c in "kvr":
                        dve.tensor_scalar(shifted[c][lane][:], xT[lane][:, 0:T], rest[c][:, 0:1], None, ALU.mult).then_inc(S_.rest_mixed, 1)
                    at(dve, S_.rest_mixed, n, 3)
                    for c in "kvr":
                        dve.scalar_tensor_tensor(out=mixed[c][lane][:], in0=xT[lane][:, 1:T + 1], scalar=mix[c][:, 0:1],
                                                 in1=shifted[c][lane][:], op0=ALU.mult, op1=ALU.add).then_inc(S_.mixed_ready, 1)
                for lane in range(MANY):
                    n = i * MANY + lane
                    at(dve, S_.kv_ready, n, 2)
                    dve.tensor_tensor_scan(pp[lane][:, 1:T + 1], decays[:], k[lane][:], START, ALU.add, ALU.max).then_inc(S_.max_scanned, 1)
                    dve.tensor_scalar(ww[lane][:], k[lane][:], first[:, 0:1], None, ALU.add).then_inc(S_.ww_ready, 1)
                    at(dve, S_.ww_ready, n)
                    at(dve, S_.max_scanned, n)
                    dve.tensor_tensor(p[lane][:], pp[lane][:, 0:T], ww[lane][:], ALU.max).then_inc(S_.p_ready, 1)
                    dve.scalar_tensor_tensor(out=ex[lane][:, 0, :], in0=pp[lane][:, 0:T], scalar=decay[:, 0:1],
                                             in1=pp[lane][:, 1:T + 1], op0=ALU.add, op1=ALU.subtract).then_inc(S_.exps_in, 1)
                    dve.tensor_tensor(ex[lane][:, 1, :], k[lane][:], pp[lane][:, 1:T + 1], ALU.subtract).then_inc(S_.exps_in, 1)
                    at(dve, S_.p_ready, n)
                    dve.tensor_tensor(ex[lane][:, 2, :], pp[lane][:, 0:T], p[lane][:], ALU.subtract).then_inc(S_.exps_in, 1)
                    dve.tensor_tensor(ex[lane][:, 3, :], ww[lane][:], p[lane][:], ALU.subtract).then_inc(S_.exps_in, 1)
                for lane in range(MANY):
                    n = i * MANY + lane
                    at(dve, S_.exps_ready, n)
                    dve.tensor_tensor(ev[lane][:, 0, :], ex[lane][:, 1, :], v[lane][:], ALU.mult).then_inc(S_.ev_ready, 1)
                    dve.tensor_tensor(ev[lane][:, 1, :], ex[lane][:, 3, :], v[lane][:], ALU.mult).then_inc(S_.ev_ready, 1)
                    dve.tensor_tensor_scan(bb[lane][:, 1:T + 1], ex[lane][:, 0, :], ex[lane][:, 1, :], 0.0, ALU.mult, ALU.add).then_inc(S_.sums_scanned, 1)
                    at(dve, S_.ev_ready, n, 2)
                    dve.tensor_tensor_scan(aa[lane][:, 1:T + 1], ex[lane][:, 0, :], ev[lane][:, 0, :], 0.0, ALU.mult, ALU.add).then_inc(S_.sums_scanned, 1)
                    at(dve, S_.sums_scanned, n, 2)
                    dve.tensor_tensor(den[lane][:], ex[lane][:, 2, :], bb[lane][:, 0:T], ALU.mult).then_inc(S_.den1, 1)
                    dve.tensor_tensor(num[lane][:], ex[lane][:, 2, :], aa[lane][:, 0:T], ALU.mult).then_inc(S_.num1, 1)
                    at(dve, S_.den1, n)
                    dve.tensor_tensor(den[lane][:], den[lane][:], ex[lane][:, 3, :], ALU.add).then_inc(S_.den2, 1)
                    at(dve, S_.num1, n)
                    dve.tensor_tensor(num[lane][:], num[lane][:], ev[lane][:, 1, :], ALU.add).then_inc(S_.num2, 1)
                    at(dve, S_.r_exp, n)
                    at(dve, S_.den2, n)
                    dve.scalar_tensor_tensor(out=den[lane][:], in0=sr[lane][:], scalar=1.0, in1=den[lane][:],
                                             op0=ALU.add, op1=ALU.mult).then_inc(S_.den_scaled, 1)
                    at(dve, S_.den_scaled, n)
                    dve.reciprocal(den[lane][:], den[lane][:]).then_inc(S_.den_inv, 1)
                    at(dve, S_.den_inv, n)
                    at(dve, S_.num2, n)
                    dve.tensor_tensor(y[lane][:], num[lane][:], den[lane][:], ALU.mult).then_inc(S_.y_ready, 1)
                for lane in range(MANY):
                    n = i * MANY + lane
                    at(dve, S_.out_psum, n)
                    dve.tensor_tensor(r[lane][:], ps[lane][:, 0, 128:256], xs[lane][:], ALU.add).then_inc(S_.sum_ready, 1)
                    at(dve, S_.sum_ready, n)
                    dve.bn_stats(st[lane][:], r[lane][:]).then_inc(S_.stats, 1)
                    at_alone(dve, S_.stats, n, s.passed)
                    dve.bn_aggr(mv[lane][:], st[lane][:]).then_inc(S_.mean_var, 1)
                    at(dve, S_.mean_var, n)
                    dve.tensor_scalar(ve[lane][:], mv[lane][:, 1:2], LN_EPS, None, ALU.add).then_inc(S_.var_eps, 1)
                for lane in range(MANY):
                    n = i * MANY + lane
                    at(dve, S_.rstd, n)
                    dve.tensor_scalar(X[:, bass.ds(n, 1), :].rearrange("t a d -> t (a d)"), r[lane][:], mv[lane][:, 0:1],
                                      rs[lane][:, 0:1], ALU.subtract, ALU.mult).then_inc(S_.lane_free, 1)
    s.close()


def soft_experts(core):
    nc, I, X = core.nc, core.I, core.X
    NS = I["L2_ffn_slot_embeds"].shape[1]
    SC = E * NS // 128
    with ExitStack() as stack:
        snT = stack.enter_context(nc.sbuf_tensor("snT", [D, E * NS], F32))
        slots = stack.enter_context(nc.sbuf_tensor("slotsT", [D, E, B, NS], F32))
        slot_keys(core, snT, SC)
        dispatch_or_combine(core, "dispatch", snT, slots, SC, NS, combine=False)
        slot_pass(core, slots, NS)
        dispatch_or_combine(core, "combine", snT, slots, SC, NS, combine=True)


def slot_keys(core, snT, SC):
    nc, I = core.nc, core.I
    s = Scope(nc, "slotkeys")
    emb, sq = s.sb("emb", [128, SC, D]), s.sb("sq", [128, SC, D])
    gam = s.sb("gam", [128, D])
    ss = s.sb("ss", [128, SC])
    ps = s.psum("ps", [128, SC, 128])
    loaded, step, safe, inv, scaled, turned, done = [s.sem(n) for n in ("loaded", "step", "safe", "inverse", "scaled", "turned", "done")]
    with nc.Block() as block:
        @block.sync
        def _(sp):
            sp.dma_start(emb[:], I["L2_ffn_slot_embeds"].rearrange("e s d -> (e s) d").rearrange("(c p) d -> p c d", p=128)).then_inc(loaded, 16)
            sp.dma_start(gam[:], row_bc(I["L2_ffn_slot_norm_gamma"])).then_inc(loaded, 16)

        @block.gpsimd
        def _(pool):
            pool.wait_ge(safe, 1)
            pool.tensor_tensor(ss[:], ss[:], core.neghalf[:, 0:SC], ALU.pow).then_inc(inv, 1)

        @block.tensor
        def _(pe):
            pe.wait_ge(scaled, 1)
            for c in range(SC):
                last = pe.transpose(ps[:, c, :], emb[:, c, :], core.ident[:])
            last.then_inc(turned, 1)

        @block.vector
        def _(dve):
            dve.wait_ge(loaded, 32)
            dve.tensor_tensor(sq[:], emb[:], emb[:], ALU.mult).then_inc(step, 1)
            dve.wait_ge(step, 1)
            dve.tensor_reduce(ss[:], sq[:], AX.X, ALU.add).then_inc(step, 1)
            dve.wait_ge(step, 2)
            dve.tensor_scalar(ss[:], ss[:], 1e-24, None, ALU.max).then_inc(safe, 1)
            dve.wait_ge(inv, 1)
            dve.tensor_tensor(emb[:], emb[:], ss[:].unsqueeze(2).to_broadcast([128, SC, D]), ALU.mult).then_inc(step, 1)
            dve.wait_ge(step, 3)
            dve.tensor_scalar(emb[:], emb[:], float(D) ** 0.5, None, ALU.mult).then_inc(step, 1)
            dve.wait_ge(step, 4)
            dve.tensor_tensor(emb[:], emb[:], gam[:].unsqueeze(1).to_broadcast([128, SC, D]), ALU.mult).then_inc(scaled, 1)

        @block.scalar
        def _(act):
            act.wait_ge(turned, 1)
            act.activation(snT[:], ps[:].rearrange("p c s -> p (c s)"), ACT.Copy).then_inc(done, 1)
            act.wait_ge(done, 1)
    s.close()


def dispatch_or_combine(core, name, snT, slots, SC, NS, *, combine):
    nc, I, X = core.nc, core.I, core.X
    s = Scope(nc, name)

    def tile(buffer, n):
        return buffer[:, bass.ds(n, 1), :].rearrange("t a d -> t (a d)")

    def lanes(tag, shape, dtype=F32):
        return s.lanes(tag, shape, dtype, n=MANY)

    gam = s.sb("gam", [T, D])
    sq, xn, xnT = lanes("sq", [T, D]), lanes("xn", [T, D]), lanes("xnT", [D, T])
    ss = lanes("ss", [T, 1])
    rs = lanes("rs", [T, 1])
    mx, zz = lanes("mx", [128, SC]), lanes("zz", [128, SC])
    P = lanes("P", [128, SC, 128])
    PT = lanes("PT", [128, SC, 128])
    ps = [s.psum(f"ps{lane}", [128, 2, 512]) for lane in range(MANY)]
    r, st, mv, ve = lanes("r", [T, D]), lanes("st", [T, 6]), lanes("mv", [T, 2]), lanes("ve", [T, 1])
    eT, eo = (lanes("eT", [D, E, NS]), lanes("eo", [128, SC, D])) if combine else (None, None)
    names = ("gamma_in lane_free squared square_sum sum_safe inv_norm unit scaled x_normed x_psum xT_ready logits_psum "
             "max_ready shifted exp_ready sum_ready recip_ready weights_ready turned_psum turned_ready out_psum slots_copied "
             "eo_psum eo_ready out_scaled r_ready stats mean_var var_eps rstd")
    S_ = type("Ready", (), {n: s.sem(n) for n in names.split()})
    with nc.Block() as block:
        @block.sync
        def _(sp):
            sp.dma_start(gam[:], row_bc(I["L2_ffn_norm_gamma"])).then_inc(S_.gamma_in, 16)

        @block.gpsimd
        def _(pool):
            pool.sem_inc(S_.eo_psum, MANY)
            with pool.Fori(0, B // MANY) as i:
                if combine:
                    for lane in range(MANY):
                        n = i * MANY + lane
                        at_alone(pool, S_.eo_psum, n, s.passed)
                        pool.tensor_copy(eT[lane][:], slots[:, :, bass.ds(n, 1), :].rearrange("d e a s -> d e (a s)")).then_inc(S_.slots_copied, 1)
                for lane in range(MANY):
                    at(pool, S_.sum_safe, i * MANY + lane)
                    pool.tensor_tensor(rs[lane][:], ss[lane][:], core.neghalf[:, 0:1], ALU.pow).then_inc(S_.inv_norm, 1)
                if combine:
                    for lane in range(MANY):
                        at(pool, S_.var_eps, i * MANY + lane)
                        pool.tensor_tensor(rs[lane][:], ve[lane][:], core.neghalf[:, 0:1], ALU.pow).then_inc(S_.rstd, 1)

        @block.tensor
        def _(pe):
            with pe.Fori(0, B // MANY) as i:
                for lane in range(MANY):
                    at(pe, S_.x_normed, i * MANY + lane)
                    pe.transpose(ps[lane][:, 0, 0:T], xn[lane][:], core.ident[:]).then_inc(S_.x_psum, 1)
                for lane in range(MANY):
                    at(pe, S_.xT_ready, i * MANY + lane)
                    if combine:
                        pe.matmul(ps[lane][:, 1, :], xnT[lane][:], snT[:], start=True, stop=True).then_inc(S_.logits_psum, 1)
                    else:
                        for c in range(SC):
                            last = pe.matmul(ps[lane][:, 1, c * T:(c + 1) * T], snT[:, c * 128:(c + 1) * 128], xnT[lane][:], start=True, stop=True)
                        last.then_inc(S_.logits_psum, 1)
                if combine:
                    for lane in range(MANY):
                        at(pe, S_.slots_copied, i * MANY + lane)
                        ef = eT[lane][:].rearrange("d e s -> d (e s)")
                        for c in range(SC):
                            last = pe.transpose(ps[lane][:, 0, c * D:(c + 1) * D], ef[:, c * 128:(c + 1) * 128], core.ident[:])
                        last.then_inc(S_.eo_psum, 1)
                for lane in range(MANY):
                    at(pe, S_.weights_ready, i * MANY + lane)
                    if combine:
                        at(pe, S_.eo_ready, i * MANY + lane)
                    for c in range(SC):
                        last = pe.transpose(ps[lane][:, 0, c * 128:(c + 1) * 128], P[lane][:, c, :], core.ident[:])
                    last.then_inc(S_.turned_psum, 1)
                for lane in range(MANY):
                    n = i * MANY + lane
                    at(pe, S_.turned_ready, n)
                    if combine:
                        for c in range(SC):
                            last = pe.matmul(ps[lane][:, 1, 0:D], PT[lane][:, c, :], eo[lane][:, c, :], start=c == 0, stop=c == SC - 1)
                        last.then_inc(S_.out_psum, 1)
                    else:
                        pe.matmul(ps[lane][:, 1, :], xn[lane][:], PT[lane][:].rearrange("t c s -> t (c s)"), start=True, stop=True).then_inc(S_.out_psum, 1)

        @block.scalar
        def _(act):
            with act.Fori(0, B // MANY) as i:
                for lane in range(MANY):
                    at(act, S_.x_psum, i * MANY + lane)
                    act.activation(xnT[lane][:], ps[lane][:, 0, 0:T], ACT.Copy).then_inc(S_.xT_ready, 1)
                if combine:
                    for lane in range(MANY):
                        at(act, S_.eo_psum, (i + 1) * MANY + lane)
                        act.activation(eo[lane][:].rearrange("m c d -> m (c d)"), ps[lane][:, 0, :], ACT.Copy).then_inc(S_.eo_ready, 1)
                for lane in range(MANY):
                    at(act, S_.shifted, i * MANY + lane)
                    if combine:
                        act.activation(P[lane][:].rearrange("t c s -> t (c s)"), ps[lane][:, 1, :], ACT.Exp, bias=mx[lane][:, 0:1],
                                       accum_out=zz[lane][:, 0:1]).then_inc(S_.exp_ready, 1)
                    else:
                        act.activation(P[lane][:], P[lane][:], ACT.Exp).then_inc(S_.exp_ready, 1)
                for lane in range(MANY):
                    at(act, S_.turned_psum, i * MANY + lane)
                    act.activation(PT[lane][:].rearrange("t c s -> t (c s)"), ps[lane][:, 0, :], ACT.Copy).then_inc(S_.turned_ready, 1)

        @block.vector
        def _(dve):
            dve.wait_ge(S_.gamma_in, 16)
            with dve.Fori(0, B // MANY) as i:
                for lane in range(MANY):
                    x = tile(X, i * MANY + lane)
                    dve.tensor_tensor(sq[lane][:], x, x, ALU.mult).then_inc(S_.squared, 1)
                for lane in range(MANY):
                    at(dve, S_.squared, i * MANY + lane)
                    dve.tensor_reduce(ss[lane][:], sq[lane][:], AX.X, ALU.add).then_inc(S_.square_sum, 1)
                for lane in range(MANY):
                    at(dve, S_.square_sum, i * MANY + lane)
                    dve.tensor_scalar(ss[lane][:], ss[lane][:], 1e-24, None, ALU.max).then_inc(S_.sum_safe, 1)
                for lane in range(MANY):
                    n = i * MANY + lane
                    at(dve, S_.inv_norm, n)
                    dve.tensor_scalar(xn[lane][:], tile(X, n), rs[lane][:, 0:1], float(D) ** 0.5, ALU.mult, ALU.mult).then_inc(S_.unit, 1)
                for lane in range(MANY):
                    at(dve, S_.unit, i * MANY + lane)
                    dve.tensor_tensor(xn[lane][:], xn[lane][:], gam[:], ALU.mult).then_inc(S_.x_normed, 1)
                for lane in range(MANY):
                    n = i * MANY + lane
                    at(dve, S_.logits_psum, n)
                    if combine:
                        dve.tensor_reduce(mx[lane][:, 1:2], ps[lane][:, 1, :], AX.X, ALU.max).then_inc(S_.max_ready, 1)
                        at(dve, S_.max_ready, n)
                        dve.tensor_scalar(mx[lane][:, 0:1], mx[lane][:, 1:2], -1.0, None, ALU.mult).then_inc(S_.shifted, 1)
                    else:
                        lt = ps[lane][:, 1, :].rearrange("m (c t) -> m c t", c=SC)
                        dve.tensor_reduce(mx[lane][:], lt, AX.X, ALU.max).then_inc(S_.max_ready, 1)
                        at(dve, S_.max_ready, n)
                        dve.tensor_tensor(P[lane][:], lt, mx[lane][:].unsqueeze(2).to_broadcast([128, SC, T]), ALU.subtract).then_inc(S_.shifted, 1)
                for lane in range(MANY):
                    n = i * MANY + lane
                    at(dve, S_.exp_ready, n)
                    if combine:
                        dve.reciprocal(zz[lane][:, 1:2], zz[lane][:, 0:1]).then_inc(S_.recip_ready, 1)
                        at(dve, S_.recip_ready, n)
                        dve.tensor_scalar(P[lane][:], P[lane][:], zz[lane][:, 1:2], None, ALU.mult).then_inc(S_.weights_ready, 1)
                    else:
                        dve.tensor_reduce(zz[lane][:], P[lane][:], AX.X, ALU.add).then_inc(S_.sum_ready, 1)
                        at(dve, S_.sum_ready, n)
                        dve.reciprocal(mx[lane][:], zz[lane][:]).then_inc(S_.recip_ready, 1)
                        at(dve, S_.recip_ready, n)
                        dve.tensor_tensor(P[lane][:], P[lane][:], mx[lane][:].unsqueeze(2).to_broadcast([128, SC, T]), ALU.mult).then_inc(S_.weights_ready, 1)
                if not combine:
                    for lane in range(MANY):
                        n = i * MANY + lane
                        at(dve, S_.out_psum, n)
                        dve.tensor_copy(slots[:, :, bass.ds(n, 1), :], ps[lane][:, 1, :].rearrange("d (e a s) -> d e a s", e=E, a=1)).then_inc(S_.lane_free, 1)
                else:
                    for lane in range(MANY):
                        n = i * MANY + lane
                        at(dve, S_.out_psum, n)
                        dve.tensor_tensor(r[lane][:], ps[lane][:, 1, 0:D], tile(X, n), ALU.add).then_inc(S_.r_ready, 1)
                    for lane in range(MANY):
                        at_alone(dve, S_.r_ready, i * MANY + lane, s.passed)
                        dve.bn_stats(st[lane][:], r[lane][:]).then_inc(S_.stats, 1)
                    for lane in range(MANY):
                        at_alone(dve, S_.stats, i * MANY + lane, s.passed)
                        dve.bn_aggr(mv[lane][:], st[lane][:]).then_inc(S_.mean_var, 1)
                    for lane in range(MANY):
                        at(dve, S_.mean_var, i * MANY + lane)
                        dve.tensor_scalar(ve[lane][:], mv[lane][:, 1:2], LN_EPS, None, ALU.add).then_inc(S_.var_eps, 1)
                    for lane in range(MANY):
                        n = i * MANY + lane
                        at(dve, S_.rstd, n)
                        dve.tensor_scalar(X[:, bass.ds(n, 1), :].rearrange("t a d -> t (a d)"), r[lane][:], mv[lane][:, 0:1],
                                          rs[lane][:, 0:1], ALU.subtract, ALU.mult).then_inc(S_.lane_free, 1)
    s.close()


def slot_pass(core, slots, NS):
    nc, I = core.nc, core.I
    s = Scope(nc, "slotpass")
    CW = 512
    N = B * NS // CW
    w1s, w2s, b1s, b2s = (s.lanes("w1", [D, F]), s.lanes("w2", [128, FC, D]), s.lanes("b1", [128, FC]), s.lanes("b2", [D, 1]))
    hT = s.lanes("hT", [128, FC, CW])
    ph = s.psum("ph", [128, FC, 512])
    py = s.psum("py", [128, 2, 512])
    w_in = [s.sem(f"weights_in{k}") for k in range(LANES)]
    h_psum, h_ready, y_psum, y_stored = [s.sem(n) for n in ("h_psum", "h_ready", "y_psum", "y_stored")]
    H0, Y0 = FC, 2
    S0 = 2 * N
    sf = slots[:].rearrange("d e b s -> d (e b s)")
    with nc.Block() as block:
        @block.sync
        def _(sp):
            with sp.Fori(0, E // LANES) as i:
                for lane in range(LANES):
                    e = i * LANES + lane
                    sp.wait_ge(y_stored, (e + 1) * N)
                    with nc.allow_non_contiguous_dma(reason="bias columns"):
                        sp.dma_start(w1s[lane][:], I["L2_ffn_w1"][bass.ds(e, 1)].rearrange("a d f -> d (a f)")).then_inc(w_in[lane], 16)
                        sp.dma_start(w2s[lane][:], I["L2_ffn_w2"][bass.ds(e, 1)].rearrange("a (c p) d -> p (a c) d", p=128)).then_inc(w_in[lane], 16)
                        sp.dma_start(b1s[lane][:], I["L2_ffn_b1"][bass.ds(e, 1)].rearrange("a (c p) -> p (a c)", p=128)).then_inc(w_in[lane], 16)
                        sp.dma_start(b2s[lane][:], I["L2_ffn_b2"][bass.ds(e, 1)].rearrange("a d -> d a")).then_inc(w_in[lane], 16)

        @block.tensor
        def _(pe):
            pe.sem_inc(y_psum, Y0)
            pe.sem_inc(h_ready, H0)
            with pe.Fori(0, E // LANES) as i:
                for lane in range(LANES):
                    e = i * LANES + lane
                    with pe.Fori(0, N // 2) as c2:
                        at(pe, w_in[lane], i, 64)
                        for par in range(2):
                            m = e * N + c2 * 2 + par
                            for f in range(FC):
                                pe.wait_ge(h_ready, m * FC + f + 1)
                                pe.matmul(ph[:, f, :], w1s[lane][:, f * 128:(f + 1) * 128], sf[:, bass.ds(m * CW, CW)],
                                          start=True, stop=True).then_inc(h_psum, 1)
                        for par in range(2):
                            m = e * N + c2 * 2 + par
                            pe.wait_ge(h_ready, m * FC + FC + H0)
                            pe.wait_ge(y_stored, m - 1 + S0)
                            for f in range(FC):
                                last = pe.matmul(py[:, par, :], w2s[lane][:, f, :], hT[par][:, f, :], start=f == 0, stop=f == FC - 1)
                            last.then_inc(y_psum, 1)

        @block.scalar
        def _(act):
            with act.Fori(0, E // LANES) as i:
                for lane in range(LANES):
                    e = i * LANES + lane
                    with act.Fori(0, N // 2) as c2:
                        at(act, w_in[lane], i, 64)
                        for par in range(2):
                            m = e * N + c2 * 2 + par
                            act.wait_ge(y_psum, m - 1 + Y0)
                            for f in range(FC):
                                act.wait_ge(h_psum, m * FC + f + 1)
                                act.activation(hT[par][:, f, :], ph[:, f, :], ACT.Gelu, bias=b1s[lane][:, f:f + 1]).then_inc(h_ready, 1)

        @block.vector
        def _(dve):
            dve.sem_inc(y_stored, S0)
            with dve.Fori(0, E // LANES) as i:
                for lane in range(LANES):
                    e = i * LANES + lane
                    with dve.Fori(0, N // 2) as c2:
                        at(dve, w_in[lane], i, 64)
                        for par in range(2):
                            m = e * N + c2 * 2 + par
                            dve.wait_ge(y_psum, m + 1 + Y0)
                            dve.tensor_scalar(sf[:, bass.ds(m * CW, CW)], py[:, par, :], b2s[lane][:, 0:1], None, ALU.add).then_inc(y_stored, 1)
    s.close()


def text_vision(core):
    nc = core.nc
    with ExitStack() as stack:
        Y = stack.enter_context(nc.sbuf_tensor("Y", [T, B, D], F32))
        FO = stack.enter_context(nc.sbuf_tensor("FO", [T, B, 2 * D], F32))
        kernel_dram = nc.dram_tensor("s4d_kernel", (D, 2 * T), F32, kind="Internal").ap()
        topk_film(core, Y, FO)
        s4d_kernel(core, kernel_dram)
        s4d_convolve(core, Y, kernel_dram)
        film_ffn(core, Y, FO)


def topk_film(core, Y, FO):
    nc, I, X = core.nc, core.I, core.X
    s = Scope(nc, "topk")
    H, Dh, TOP = 4, 32, 32
    ROUNDS = TOP // 8
    scale = 1.0 / float(np.sqrt(Dh).astype(np.float32))
    TAKEN = -3e38
    loads = []

    def loaded(tag, shape, src, dtype=F32):
        t = s.sb(tag, shape, dtype)
        loads.append((t[:], src))
        return t

    wq = loaded("wq", [D, D], I["L0_xattn_Wq"])
    wk, wv = loaded("wk", [DC, D], I["L0_xattn_Wk"]), loaded("wv", [DC, D], I["L0_xattn_Wv"])
    gam, bet = loaded("gam", [T, D], row_bc(I["L0_xattn_g_norm_in"])), loaded("bet", [T, D], row_bc(I["L0_xattn_b_norm_in"]))
    mg = loaded("mg", [T, 1], row_bc(I["L0_xattn_mod_gate"]))
    wf, bf = s.sb("wf", [D, 4 * D]), s.sb("bf", [T, 4 * D])
    for j, side in enumerate(("in", "out")):
        loads.append((wf[:, 2 * D * j:2 * D * (j + 1)], I[f"L0_xattn_W_film_{side}"]))
        loads.append((bf[:, 2 * D * j:2 * D * (j + 1)], row_bc(I[f"L0_xattn_b_film_{side}"])))
    tm8 = loaded("tm8", [T, B], I["text_mask_T"], U8)
    vm8 = loaded("vm8", [T, B * TC], row_bc(I["mask_BxS2_bf1"].rearrange("b k -> (b k)")), U8)
    tmask, vbias = s.sb("tmask", [T, B]), s.sb("vbias", [T, B * TC])

    def pair(tag, shape):
        return [s.sb(f"{tag}{p}", shape) for p in (0, 1)]

    xs, cs, V = pair("xs", [T, D]), pair("cs", [DC, TC]), pair("V", [TC, D])
    xT, qT, kT = s.sb("xT", [D, T]), s.sb("qT", [D, T]), s.sb("kT", [D, TC])
    S, W, ex, P = (s.sb(tag, [T, H, TC]) for tag in ("S", "W", "ex", "P"))
    m8, nmx = s.sb("m8", [T, ROUNDS, H, 8]), s.sb("nmx", [T, H])
    sm, rz, diag = s.sb("sm", [T, H]), s.sb("rz", [T, H]), s.sb("diag", [T, H, T])
    aT, cT = s.sb("aT", [TC, T]), s.sb("cT", [D, T])
    film, xn, tm = s.sb("film", [T, 2 * D]), s.sb("xn", [T, D]), s.sb("tm", [T, 1])
    st, mv, ve, rs = s.sb("st", [T, 6]), s.sb("mv", [T, 2]), s.sb("ve", [T, 1]), s.sb("rs", [T, 1])
    bank = s.psum("bank", [128, 8, 512])
    scores, xT_ps, film_ps = bank[:, 0:H, 0:TC], bank[:, 4, 0:T], bank[:, 7, :]
    q_ps, k_ps, v_ps = bank[:, 5, 0:T], bank[:, 5, T:T + TC], bank[0:TC, 5, 256:256 + D]
    aT_ps, cT_ps = bank[0:TC, 6, 0:T], bank[:, 6, 128:128 + T]
    names = ("weights_in setup x_copied xT_psum xT_ready proj_psum qk_ready v_ready scores_psum scores_ready negmax sorted_ taken "
             "exp_ready kept sum_ready recip_ready rz_ready diag_ready attnT_psum attnT_ready c_psum c_ready film_psum film_ready "
             "film_out stats mean_var var_eps rstd x_again normed scaled offset modulated y_ready tm_ready")
    R = type("Ready", (), {n: s.sem(n) for n in names.split()})
    ctx_in = [s.sem(f"ctx_in{k}") for k in (0, 1)]
    SETUPS = 5

    def tile(buffer, n):
        return buffer[:, n, :] if isinstance(n, int) else buffer[:, bass.ds(n, 1), :].rearrange("t a d -> t (a d)")

    def steps(step):
        def run(eng):
            step(-2, 0, fetch=True)
            step(-1, 1, fetch=True, front=True)
            step(0, 0, fetch=True, front=True, main=True)
            with eng.Fori(0, (B - 4) // 2) as i:
                step(i * 2 + 1, 1, fetch=True, front=True, main=True, output=True)
                step(i * 2 + 2, 0, fetch=True, front=True, main=True, output=True)
            step(B - 3, 1, fetch=True, front=True, main=True, output=True)
            step(B - 2, 0, front=True, main=True, output=True)
            step(B - 1, 1, main=True, output=True)
            step(B, 0, output=True)
        return run

    with nc.Block() as block:
        @block.sync
        def _(sp):
            with nc.allow_non_contiguous_dma(reason="small weights, once"):
                for dst, src in loads:
                    sp.dma_start(dst, src).then_inc(R.weights_in, 16)
            for p in (0, 1):
                sp.dma_start(cs[p][:], I["ctxT"][:, p * TC:(p + 1) * TC]).then_inc(ctx_in[p], 16)
            with sp.Fori(0, (B - 2) // 2) as i:
                for p in (0, 1):
                    n = i * 2 + p
                    at(sp, R.proj_psum, n)
                    sp.dma_start(cs[p][:], I["ctxT"][:, bass.ds(n * TC + 2 * TC, TC)]).then_inc(ctx_in[p], 16)

        @block.gpsimd
        def _(pool):
            pool.wait_ge(R.setup, SETUPS)
            pool.tensor_copy(tm[:], tmask[:, 0:1]).then_inc(R.tm_ready, 1)

            def step(n, p, fetch=False, front=False, main=False, output=False):
                a, d = n + 2, n - 1
                if output:
                    at(pool, R.rz_ready, d)
                    pool.tensor_tensor(diag[:], core.ident[:].unsqueeze(1).to_broadcast([T, H, T]),
                                       rz[:].unsqueeze(2).to_broadcast([T, H, T]), ALU.mult).then_inc(R.diag_ready, 1)
                if fetch:
                    if not (isinstance(a, int) and a < 2):
                        at_alone(pool, R.xT_psum, a - 2, s.passed)
                    pool.tensor_copy(xs[p][:], tile(X, a)).then_inc(R.x_copied, 1)
                if output:
                    at(pool, R.var_eps, d)
                    pool.tensor_tensor(rs[:], ve[:], core.neghalf[:, 0:1], ALU.pow).then_inc(R.rstd, 1)
                    if not (isinstance(d, int) and d < 1):
                        at_alone(pool, R.y_ready, d - 1, s.passed)
                    pool.tensor_copy(xn[:], tile(X, d)).then_inc(R.x_again, 1)
                    at_alone(pool, R.rstd, d, s.passed)
                    at_alone(pool, R.x_again, d, s.passed)
                    pool.tensor_scalar(xn[:], xn[:], mv[:, 0:1], rs[:, 0:1], ALU.subtract, ALU.mult).then_inc(R.normed, 1)
                    at(pool, R.normed, d)
                    pool.tensor_tensor(xn[:], xn[:], gam[:], ALU.mult).then_inc(R.scaled, 1)
                    at(pool, R.scaled, d)
                    pool.tensor_tensor(xn[:], xn[:], bet[:], ALU.add).then_inc(R.offset, 1)
                    at(pool, R.offset, d)
                    at(pool, R.film_ready, d)
                    pool.tensor_tensor(xn[:], xn[:], film[:, 0:D], ALU.mult).then_inc(R.modulated, 1)
                    at(pool, R.modulated, d)
                    pool.tensor_tensor(tile(Y, d), xn[:], film[:, D:2 * D], ALU.add).then_inc(R.y_ready, 1)
                    if not (isinstance(n, int) and n >= B):
                        at_alone(pool, R.film_out, d, s.passed)
                        pool.tensor_copy(tm[:], tmask[:, n:n + 1] if isinstance(n, int) else tmask[:, bass.ds(n, 1)]).then_inc(R.tm_ready, 1)
            steps(step)(pool)
            pool.wait_ge(R.y_ready, B)

        @block.tensor
        def _(pe):
            pe.wait_ge(R.weights_in, 16 * len(loads))
            pe.wait_ge(R.setup, SETUPS)

            def step(n, p, fetch=False, front=False, main=False, output=False):
                f, d = n + 1, n - 1
                if front:
                    at(pe, R.x_copied, f)
                    if main:
                        at(pe, R.xT_ready, n)
                    pe.transpose(xT_ps, xs[1 - p][:], core.ident[:]).then_inc(R.xT_psum, 1)
                    at(pe, R.xT_ready, f)
                    if main:
                        at(pe, R.v_ready, n)
                    pe.wait_ge(ctx_in[1 - p], (f // 2 + 1) * 16 if isinstance(f, int) else f * 8 + 16 - 8 * (1 - p))
                    pe.matmul(q_ps, wq[:], xT[:], start=True, stop=True)
                    pe.matmul(k_ps, wk[:], cs[1 - p][:], start=True, stop=True)
                    pe.matmul(v_ps, cs[1 - p][:], wv[:], start=True, stop=True).then_inc(R.proj_psum, 1)
                if output:
                    at(pe, R.diag_ready, d)
                    for h in range(H):
                        last = pe.matmul(aT_ps, P[:, h, :], diag[:, h, :], start=h == 0, stop=h == H - 1)
                    last.then_inc(R.attnT_psum, 1)
                    at(pe, R.attnT_ready, d)
                    pe.matmul(cT_ps, V[1 - p][:], aT[:], start=True, stop=True).then_inc(R.c_psum, 1)
                    at(pe, R.c_ready, d)
                    if not (isinstance(d, int) and d < 1):
                        pe.wait_ge(R.film_out, d)
                    pe.matmul(film_ps, cT[:], wf[:], start=True, stop=True).then_inc(R.film_psum, 1)
                if front:
                    at(pe, R.qk_ready, f, 2)
                    if main:
                        at(pe, R.scores_ready, n)
                    for h in range(H):
                        rows = slice(h * Dh, (h + 1) * Dh)
                        last = pe.matmul(scores[:, h, :], qT[rows, :], kT[rows, :], start=True, stop=True)
                    last.then_inc(R.scores_psum, 1)
            steps(step)(pe)

        @block.scalar
        def _(act):
            def step(n, p, fetch=False, front=False, main=False, output=False):
                f, d = n + 1, n - 1
                if front:
                    at(act, R.xT_psum, f)
                    act.activation(xT[:], xT_ps, ACT.Copy).then_inc(R.xT_ready, 1)
                if main:
                    at(act, R.negmax, n)
                    for h in range(H):
                        act.activation(ex[:, h, :], S[:, h, :], ACT.Exp, bias=nmx[:, h:h + 1], scale=scale).then_inc(R.exp_ready, 1)
                if output:
                    at(act, R.attnT_psum, d)
                    act.activation(aT[:], aT_ps, ACT.Copy).then_inc(R.attnT_ready, 1)
                    at(act, R.c_psum, d)
                    act.activation(cT[:], cT_ps, ACT.Copy).then_inc(R.c_ready, 1)
                if front:
                    at(act, R.proj_psum, f)
                    act.activation(qT[:], q_ps, ACT.Copy).then_inc(R.qk_ready, 1)
                    act.activation(kT[:], k_ps, ACT.Copy).then_inc(R.qk_ready, 1)
                    act.activation(V[1 - p][:], v_ps, ACT.Copy).then_inc(R.v_ready, 1)
            steps(step)(act)

        @block.vector
        def _(dve):
            dve.wait_ge(R.weights_in, 16 * len(loads))
            dve.tensor_copy(tmask[:], tm8[:]).then_inc(R.setup, 1)
            dve.tensor_scalar(vbias[:], vm8[:], -NEG, NEG, ALU.mult, ALU.add).then_inc(R.setup, 1)
            dve.tensor_scalar(wf[:], wf[:], mg[:, 0:1], None, ALU.mult).then_inc(R.setup, 1)
            dve.tensor_scalar(bf[:], bf[:], mg[:, 0:1], None, ALU.mult).then_inc(R.setup, 1)
            dve.wait_ge(R.setup, 4)
            b4 = bf[:].rearrange("t (a b d) -> t a b d", a=2, b=2)
            dve.tensor_scalar(b4[:, :, 0, :], b4[:, :, 0, :], 1.0, None, ALU.add).then_inc(R.setup, 1)
            dve.wait_ge(R.setup, SETUPS)

            def step(n, p, fetch=False, front=False, main=False, output=False):
                d = n - 1

                def chosen(q):
                    if q:
                        at_alone(dve, R.taken, n * (ROUNDS * H) + q * H - 1, s.passed)
                    src = W if q else S
                    for h in range(H):
                        dve.max(m8[:, q, h, :], src[:, h, :]).then_inc(R.sorted_, 1)
                    at_alone(dve, R.sorted_, n * (ROUNDS * H) + (q + 1) * H - 1, s.passed)
                    if q == 0:
                        dve.tensor_scalar(nmx[:].unsqueeze(2), m8[:, 0, :, 0:1], -scale, None, ALU.mult).then_inc(R.negmax, 1)
                    for h in range(H):
                        dve.match_replace(W[:, h, :], m8[:, q, h, :], src[:, h, :], TAKEN).then_inc(R.taken, 1)

                if main:
                    at(dve, R.scores_psum, n)
                    vb = vbias[:, n * TC:(n + 1) * TC] if isinstance(n, int) else vbias[:, bass.ds(n * TC, TC)]
                    dve.tensor_tensor(S[:], scores, vb.unsqueeze(1).to_broadcast([T, H, TC]), ALU.add).then_inc(R.scores_ready, 1)
                    at_alone(dve, R.scores_ready, n, s.passed)
                    chosen(0)
                    chosen(1)
                    chosen(2)
                if output:
                    at(dve, R.film_psum, d)
                    at(dve, R.tm_ready, d)
                    if not (isinstance(d, int) and d < 1):
                        dve.wait_ge(R.y_ready, d)
                    dve.scalar_tensor_tensor(out=film[:], in0=film_ps[:, 0:2 * D], scalar=tm[:, 0:1], in1=bf[:, 0:2 * D],
                                             op0=ALU.mult, op1=ALU.add).then_inc(R.film_ready, 1)
                    dve.scalar_tensor_tensor(out=tile(FO, d), in0=film_ps[:, 2 * D:4 * D], scalar=tm[:, 0:1], in1=bf[:, 2 * D:4 * D],
                                             op0=ALU.mult, op1=ALU.add).then_inc(R.film_out, 1)
                if main:
                    chosen(3)
                    at(dve, R.exp_ready, n, H)
                    at(dve, R.taken, n, ROUNDS * H)
                    if output:
                        at(dve, R.attnT_psum, d)
                    dve.scalar_tensor_tensor(out=P[:], in0=W[:], scalar=-2e38, in1=ex[:], op0=ALU.is_lt, op1=ALU.mult).then_inc(R.kept, 1)
                    at(dve, R.kept, n)
                    dve.tensor_reduce(sm[:], P[:], AX.X, ALU.add).then_inc(R.sum_ready, 1)
                    at(dve, R.sum_ready, n)
                    dve.reciprocal(rz[:], sm[:]).then_inc(R.recip_ready, 1)
                    at(dve, R.recip_ready, n)
                    dve.tensor_scalar(rz[:], rz[:], 1.0 / H, None, ALU.mult).then_inc(R.rz_ready, 1)
                    if output:
                        at_alone(dve, R.normed, d, s.passed)
                    dve.bn_stats(st[:], tile(X, n)).then_inc(R.stats, 1)
                    at_alone(dve, R.stats, n, s.passed)
                    dve.bn_aggr(mv[:], st[:]).then_inc(R.mean_var, 1)
                    at(dve, R.mean_var, n)
                    dve.tensor_scalar(ve[:], mv[:, 1:2], LN_EPS, None, ALU.add).then_inc(R.var_eps, 1)
            steps(step)(dve)
    s.close()


def s4d_kernel(core, kernel_dram):
    nc, I = core.nc, core.I
    s = Scope(nc, "s4d")
    NSt = I["L0_xattn_A_re"].shape[1]
    NA_, NB_ = 8, 16
    TWO_PI = (6.28125, 1.9350051879882812e-3, 3.0199159795e-7)
    ROUND = 1.5 * 2.0 ** 23
    PI = 3.1415925
    Are, Aim, Cre, Cim = (s.sb(n, [D, NSt]) for n in ("Are", "Aim", "Cre", "Cim"))
    ldt, dt, skip = s.sb("ldt", [D, 1]), s.sb("dt", [D, 1]), s.sb("skip", [D, 1])
    mag, ang, turn, snh, sn_, cs_ = (s.sb(n, [D, NSt]) for n in ("mag", "ang", "turn", "snh", "sin", "cos"))
    U = s.sb("U", [D, 2, NSt, NA_])
    V = s.sb("V", [D, 2, NSt, NB_])
    w = s.sb("w", [D, 7, 2, NSt])
    dC, den = s.sb("dC", [D, 2, NSt]), s.sb("den", [D, NSt])
    ta, tb = s.sb("ta", [D, NSt, 8]), s.sb("tb", [D, NSt, 8])
    zm, cz = s.sb("zm", [D, 2, NSt]), s.sb("cz", [D, 2, NSt])
    prod = s.sb("prod", [D, 2, NSt, NB_])
    K, Kp = s.sb("K", [D, T]), s.sb("Kp", [D, 2 * T])
    loaded, step, dt_ready, angle_ready, sines_ready, padded, kernel_ready, stored = [
        s.sem(n) for n in ("loaded", "step", "dt_ready", "angle_ready", "sines_ready", "padded", "kernel_ready", "stored")]
    with nc.Block() as block:
        @block.sync
        def _(sp):
            loads = [(Are, "A_re"), (Aim, "A_im"), (Cre, "C_re"), (Cim, "C_im")]
            for t, key in loads:
                sp.dma_start(t[:], I[f"L0_xattn_{key}"]).then_inc(loaded, 16)
            with nc.allow_non_contiguous_dma(reason="two columns"):
                sp.dma_start(ldt[:], col(I["L0_xattn_log_dt"])).then_inc(loaded, 16)
                sp.dma_start(skip[:], col(I["L0_xattn_D_skip"])).then_inc(loaded, 16)
            sp.wait_ge(kernel_ready, 1)
            sp.wait_ge(padded, 1)
            sp.dma_start(kernel_dram, Kp[:]).then_inc(stored, 16)
            sp.wait_ge(stored, 16)

        @block.gpsimd
        def _(pool):
            pool.memset(Kp[:], 0.0).then_inc(padded, 1)

        @block.scalar
        def _(act):
            act.wait_ge(loaded, 96)
            act.activation(dt[:], ldt[:], ACT.Exp).then_inc(dt_ready, 1)
            act.wait_ge(dt_ready, 1)
            act.activation(mag[:], Are[:], ACT.Exp, scale=dt[:, 0:1]).then_inc(dt_ready, 1)
            act.wait_ge(angle_ready, 1)
            act.activation(sn_[:], ang[:], ACT.Sin).then_inc(sines_ready, 1)
            act.activation(snh[:], ang[:], ACT.Sin, scale=0.5).then_inc(sines_ready, 1)

        @block.vector
        def _(dve):
            links = [0]

            def link(ins):
                links[0] += 1
                ins.then_inc(step, 1)
                dve.wait_ge(step, links[0])

            def product(out, a, b, shape):
                n, m = shape
                x, y = ta[:, :, 0:m], tb[:, :, 0:m]
                for k, (p, q, op) in enumerate((((0, 0), (1, 1), ALU.subtract), ((0, 1), (1, 0), ALU.add))):
                    link(dve.tensor_tensor(x, a[p[0]], b[p[1]], ALU.mult))
                    link(dve.tensor_tensor(y, a[q[0]], b[q[1]], ALU.mult))
                    link(dve.tensor_tensor(out[k], x, y, op))

            def pair(t):
                return t[:, 0, :].unsqueeze(2), t[:, 1, :].unsqueeze(2)

            def wide(t, m):
                return tuple(v.to_broadcast([D, NSt, m]) for v in pair(t))

            dve.wait_ge(loaded, 96)
            dve.wait_ge(dt_ready, 2)
            link(dve.tensor_scalar(ang[:], Aim[:], dt[:, 0:1], None, ALU.mult))
            link(dve.tensor_scalar(turn[:], ang[:], float(1.0 / (2.0 * np.pi)), None, ALU.mult))
            link(dve.tensor_scalar(turn[:], turn[:], ROUND, None, ALU.add))
            link(dve.tensor_scalar(turn[:], turn[:], -ROUND, None, ALU.add))
            for part in TWO_PI:
                link(dve.scalar_tensor_tensor(out=ang[:], in0=turn[:], scalar=-part, in1=ang[:], op0=ALU.mult, op1=ALU.add))
            link(dve.tensor_scalar(ang[:], ang[:], PI, None, ALU.min))
            dve.tensor_scalar(ang[:], ang[:], -PI, None, ALU.max).then_inc(angle_ready, 1)
            dve.wait_ge(sines_ready, 2)
            link(dve.tensor_tensor(cs_[:], snh[:], snh[:], ALU.mult))
            link(dve.tensor_scalar(cs_[:], cs_[:], -2.0, 1.0, ALU.mult, ALU.add))
            link(dve.tensor_tensor(w[:, 0, 0, :], mag[:], cs_[:], ALU.mult))
            link(dve.tensor_tensor(w[:, 0, 1, :], mag[:], sn_[:], ALU.mult))
            for k in range(6):
                product(pair(w[:, k + 1]), pair(w[:, k]), pair(w[:, k]), (NSt, 1))
            link(dve.tensor_scalar(zm[:, 0, :], w[:, 0, 0, :], -1.0, None, ALU.add))
            link(dve.tensor_copy(zm[:, 1, :], w[:, 0, 1, :]))
            product(pair(cz), (Cre[:].unsqueeze(2), Cim[:].unsqueeze(2)), pair(zm), (NSt, 1))
            link(dve.tensor_tensor(den[:], Are[:], Are[:], ALU.mult))
            link(dve.tensor_tensor(snh[:], Aim[:], Aim[:], ALU.mult))
            link(dve.tensor_tensor(den[:], den[:], snh[:], ALU.add))
            link(dve.reciprocal(den[:], den[:]))
            link(dve.tensor_scalar(turn[:], Aim[:], -1.0, None, ALU.mult))
            product(pair(dC), pair(cz), (Are[:].unsqueeze(2), turn[:].unsqueeze(2)), (NSt, 1))
            for k in range(2):
                link(dve.scalar_tensor_tensor(out=U[:, k, :, 0], in0=dC[:, k, :], scalar=2.0, in1=den[:], op0=ALU.mult, op1=ALU.mult))
            for j in range(3):
                m = 1 << j
                product((U[:, 0, :, m:2 * m], U[:, 1, :, m:2 * m]), (U[:, 0, :, 0:m], U[:, 1, :, 0:m]), wide(w[:, 4 + j], m), (NSt, m))
            link(dve.memset(V[:, 0, :, 0:1], 1.0))
            link(dve.memset(V[:, 1, :, 0:1], 0.0))
            for j in range(4):
                m = 1 << j
                product((V[:, 0, :, m:2 * m], V[:, 1, :, m:2 * m]), (V[:, 0, :, 0:m], V[:, 1, :, 0:m]), wide(w[:, j], m), (NSt, m))
            link(dve.tensor_scalar(V[:, 1], V[:, 1], -1.0, None, ALU.mult))
            for a in range(NA_):
                link(dve.tensor_tensor(prod[:], V[:], U[:, :, :, a:a + 1].to_broadcast([D, 2, NSt, NB_]), ALU.mult))
                link(dve.tensor_reduce(K[:, a * NB_:(a + 1) * NB_], prod[:].rearrange("d c n b -> d b (c n)"), AX.X, ALU.add))
            link(dve.tensor_tensor(K[:, 0:1], K[:, 0:1], skip[:], ALU.add))
            dve.wait_ge(padded, 1)
            dve.tensor_copy(Kp[:, 0:T], K[:, ::-1]).then_inc(kernel_ready, 1)
    s.close()


def s4d_convolve(core, Y, kernel_dram):
    nc = core.nc
    s = Scope(nc, "conv")
    CH = 16
    N = D // CH
    tz = s.lanes("toeplitz", [T, CH, T])
    ps = [s.psum(f"ps{k}", [T, CH, B]) for k in range(LANES)]
    toeplitz_in = [s.sem(f"toeplitz_in{k}") for k in range(LANES)]
    y_psum, y_stored = s.sem("y_psum"), s.sem("y_stored")
    Yd = Y[:].rearrange("t b d -> t d b")
    with nc.Block() as block:
        @block.sync
        def _(sp):
            for c in range(N):
                lane = c % LANES
                if c >= LANES:
                    sp.wait_ge(y_psum, c - LANES + 1)
                base = kernel_dram[c * CH:(c + 1) * CH, :]
                src = bass.AP(base.tensor, c * CH * 2 * T, [[1, T], [2 * T, CH], [1, T]])
                sp.dma_start(tz[lane][:], src).then_inc(toeplitz_in[lane], 16)

        @block.tensor
        def _(pe):
            for c in range(N):
                lane = c % LANES
                pe.wait_ge(toeplitz_in[lane], 16 * (c // LANES + 1))
                if c >= LANES:
                    pe.wait_ge(y_stored, c - LANES + 1)
                for k in range(CH):
                    last = pe.matmul(ps[lane][:, k, :], tz[lane][:, k, :], Yd[:, c * CH + k, :], start=True, stop=True)
                last.then_inc(y_psum, 1)

        @block.vector
        def _(dve):
            for c in range(N):
                dve.wait_ge(y_psum, c + 1)
                dve.tensor_copy(Yd[:, c * CH:(c + 1) * CH, :], ps[c % LANES][:]).then_inc(y_stored, 1)
    s.close()


def film_ffn(core, Y, FO):
    nc, I, X = core.nc, core.I, core.X
    s = Scope(nc, "filmffn")

    def tile_of(buffer, n):
        return buffer[:, bass.ds(n, 1), :].rearrange("t a d -> t (a d)")

    def lanes(tag, shape, dtype=F32):
        return s.lanes(tag, shape, dtype, n=MANY)

    loads = []

    def tile(tag, shape, src):
        t = s.sb(tag, shape)
        loads.append((t[:], src))
        return t

    p = "L0_xattn_"
    w1, w2 = tile("w1", [D, F], I[p + "W1"]), tile("w2", [128, FC, D], I[p + "W2"].rearrange("(c p) d -> p c d", p=128))
    b1, b2 = tile("b1", [128, FC], I[p + "b1"].rearrange("(c p) -> p c", p=128)), tile("b2", [T, D], row_bc(I[p + "b2"]))
    gf, bf = tile("gf", [T, D], row_bc(I[p + "g_ffn"])), tile("bf", [T, D], row_bc(I[p + "b_ffn"]))
    go, bo = tile("go", [T, D], row_bc(I[p + "g_norm_out"])), tile("bo", [T, D], row_bc(I[p + "b_norm_out"]))
    ys = lanes("ys", [T, D])
    xt, xn, xT, hT = lanes("xt", [T, D]), lanes("xn", [T, D]), lanes("xT", [D, T]), lanes("hT", [128, FC, T])
    st, mv, ve, rs = lanes("st", [T, 6]), lanes("mv", [T, 2]), lanes("ve", [T, 1]), lanes("rs", [T, 1])
    ps = [s.psum(f"ps{lane}", [128, 2, 512]) for lane in range(MANY)]
    names = ("weights_in lane_free turned modulated shifted xt_ready n_psum nT_ready h_psum h_ready y_psum y_biased xt2_ready sum_ready"
             + "".join(f" stats{k} mean_var{k} var_eps{k} rstd{k} normed{k} scaled{k} offset{k}" for k in range(3)))
    sems = {n: s.sem(n) for n in names.split()}
    S_ = type("Ready", (), sems)
    stats, mean_var, var_eps, rstd, normed, scaled, offset = (
        [sems[f"{n}{k}"] for k in range(3)] for n in ("stats", "mean_var", "var_eps", "rstd", "normed", "scaled", "offset"))
    with nc.Block() as block:
        @block.sync
        def _(sp):
            with nc.allow_non_contiguous_dma(reason="small weights, once"):
                for dst, src in loads:
                    sp.dma_start(dst, src).then_inc(S_.weights_in, 16)

        @block.gpsimd
        def _(pool):
            with pool.Fori(0, B // MANY) as i:
                for k in range(3):
                    for lane in range(MANY):
                        at(pool, var_eps[k], i * MANY + lane)
                        pool.tensor_tensor(rs[lane][:], ve[lane][:], core.neghalf[:, 0:1], ALU.pow).then_inc(rstd[k], 1)

        @block.tensor
        def _(pe):
            pe.sem_inc(S_.lane_free, MANY)
            pe.wait_ge(S_.weights_in, 16 * len(loads))
            with pe.Fori(0, B // MANY) as i:
                for lane in range(MANY):
                    n = i * MANY + lane
                    at(pe, S_.lane_free, n)
                    pe.matmul(ps[lane][:, 0, 256:384], core.anti[:], Y[:, bass.ds(n, 1), :].rearrange("t a d -> t (a d)"), start=True, stop=True).then_inc(S_.turned, 1)
                for lane in range(MANY):
                    at(pe, offset[0], i * MANY + lane)
                    pe.transpose(ps[lane][:, 0, 0:T], xn[lane][:], core.ident[:]).then_inc(S_.n_psum, 1)
                for lane in range(MANY):
                    at(pe, S_.nT_ready, i * MANY + lane)
                    for f in range(FC):
                        last = pe.matmul(ps[lane][:, 1, f * T:(f + 1) * T], w1[:, f * 128:(f + 1) * 128], xT[lane][:], start=True, stop=True)
                    last.then_inc(S_.h_psum, 1)
                for lane in range(MANY):
                    at(pe, S_.h_ready, i * MANY + lane, FC)
                    for f in range(FC):
                        last = pe.matmul(ps[lane][:, 0, 384:512], hT[lane][:, f, :], w2[:, f, :], start=f == 0, stop=f == FC - 1)
                    last.then_inc(S_.y_psum, 1)

        @block.scalar
        def _(act):
            act.wait_ge(S_.weights_in, 16 * len(loads))
            with act.Fori(0, B // MANY) as i:
                for lane in range(MANY):
                    at(act, S_.n_psum, i * MANY + lane)
                    act.activation(xT[lane][:], ps[lane][:, 0, 0:T], ACT.Copy).then_inc(S_.nT_ready, 1)
                for lane in range(MANY):
                    at(act, S_.h_psum, i * MANY + lane)
                    for f in range(FC):
                        act.activation(hT[lane][:, f, :], ps[lane][:, 1, f * T:(f + 1) * T], ACT.Gelu, bias=b1[:, f:f + 1]).then_inc(S_.h_ready, 1)

        @block.vector
        def _(dve):
            dve.wait_ge(S_.weights_in, 16 * len(loads))

            def norm_stats(i, k):
                for lane in range(MANY):
                    dve.bn_stats(st[lane][:], xt[lane][:]).then_inc(stats[k], 1)
                for lane in range(MANY):
                    at_alone(dve, stats[k], i * MANY + lane, s.passed)
                    dve.bn_aggr(mv[lane][:], st[lane][:]).then_inc(mean_var[k], 1)
                for lane in range(MANY):
                    at(dve, mean_var[k], i * MANY + lane)
                    dve.tensor_scalar(ve[lane][:], mv[lane][:, 1:2], LN_EPS, None, ALU.add).then_inc(var_eps[k], 1)

            def norm_apply(dst, src, n, lane, k):
                at(dve, rstd[k], n)
                return dve.tensor_scalar(dst, src, mv[lane][:, 0:1], rs[lane][:, 0:1], ALU.subtract, ALU.mult)

            def affine(i, k, g, b):
                for lane in range(MANY):
                    at(dve, normed[k], i * MANY + lane)
                    dve.tensor_tensor(xn[lane][:], xn[lane][:], g[:], ALU.mult).then_inc(scaled[k], 1)
                for lane in range(MANY):
                    at(dve, scaled[k], i * MANY + lane)
                    dve.tensor_tensor(xn[lane][:], xn[lane][:], b[:], ALU.add).then_inc(offset[k], 1)

            with dve.Fori(0, B // MANY) as i:
                for lane in range(MANY):
                    n = i * MANY + lane
                    at(dve, S_.turned, n)
                    dve.tensor_tensor(xt[lane][:], ps[lane][:, 0, 256:384], tile_of(FO, n)[:, 0:D], ALU.mult).then_inc(S_.modulated, 1)
                for lane in range(MANY):
                    n = i * MANY + lane
                    at(dve, S_.modulated, n)
                    dve.tensor_tensor(xt[lane][:], xt[lane][:], tile_of(FO, n)[:, D:2 * D], ALU.add).then_inc(S_.shifted, 1)
                for lane in range(MANY):
                    n = i * MANY + lane
                    at(dve, S_.shifted, n)
                    dve.tensor_tensor(xt[lane][:], xt[lane][:], tile_of(X, n), ALU.add).then_inc(S_.xt_ready, 1)
                for lane in range(MANY):
                    at_alone(dve, S_.xt_ready, i * MANY + lane, s.passed)
                norm_stats(i, 0)
                for lane in range(MANY):
                    n = i * MANY + lane
                    norm_apply(xn[lane][:], xt[lane][:], n, lane, 0).then_inc(normed[0], 1)
                affine(i, 0, gf, bf)
                for lane in range(MANY):
                    n = i * MANY + lane
                    at(dve, S_.y_psum, n)
                    dve.tensor_tensor(ys[lane][:], ps[lane][:, 0, 384:512], b2[:], ALU.add).then_inc(S_.y_biased, 1)
                for lane in range(MANY):
                    n = i * MANY + lane
                    at(dve, S_.y_biased, n)
                    dve.tensor_tensor(xt[lane][:], xt[lane][:], ys[lane][:], ALU.add).then_inc(S_.xt2_ready, 1)
                for lane in range(MANY):
                    at_alone(dve, S_.xt2_ready, i * MANY + lane, s.passed)
                norm_stats(i, 1)
                for lane in range(MANY):
                    n = i * MANY + lane
                    norm_apply(xn[lane][:], xt[lane][:], n, lane, 1).then_inc(normed[1], 1)
                affine(i, 1, go, bo)
                for lane in range(MANY):
                    n = i * MANY + lane
                    at(dve, offset[1], n)
                    dve.tensor_tensor(xt[lane][:], xn[lane][:], tile_of(X, n), ALU.add).then_inc(S_.sum_ready, 1)
                for lane in range(MANY):
                    at_alone(dve, S_.sum_ready, i * MANY + lane, s.passed)
                norm_stats(i, 2)
                for lane in range(MANY):
                    n = i * MANY + lane
                    norm_apply(X[:, bass.ds(n, 1), :].rearrange("t a d -> t (a d)"), xt[lane][:], n, lane, 2).then_inc(S_.lane_free, 1)
    s.close()


def lay_out(inputs):
    a = {k: np.ascontiguousarray(v) for k, v in inputs.items()}
    for key in ("mask_BxS_bf1", "mask_BxS2_bf1"):
        a[key] = a[key].view(np.uint8)
    a["text_mask_T"] = a.pop("mask_BxS_bf1").T
    a["L0_xattn_mod_gate"] = a["L0_xattn_mod_gate"].reshape(1)
    a["ctxT"] = a.pop("ctx_768").transpose(2, 0, 1).reshape(DC, B * TC)
    w, b, g = a.pop("L2_attn_in_proj_weight"), a.pop("L2_attn_in_proj_bias"), a.pop("L2_attn_gamma").reshape(-1)
    w3, b3 = a.pop("L3_ffn_Wqkv"), a.pop("L3_ffn_bqkv")
    for n, c in enumerate("qkv"):
        part = slice(n * D, (n + 1) * D)
        a[f"L2_attn_W{c}"], a[f"L2_attn_b{c}"], a[f"L2_attn_gamma_{c}"] = w[part].T, b[part], g[part]
        a[f"L3_ffn_W{c}"], a[f"L3_ffn_b{c}"] = w3[:, part], b3[part]
        a[f"L3_attn_W{c}T"] = a.pop(f"L3_attn_W{c}").T
    a["L3_attn_WoT"] = a.pop("L3_attn_Wo").T
    a["L2_attn_WoT"] = a.pop("L2_attn_out_proj_weight").T
    a["L2_attn_alpha"] = a.pop("L2_attn_linear_alpha").reshape(-1)
    a["L2_attn_lgamma"] = a.pop("L2_attn_linear_gamma").reshape(-1)
    for c in "kvr":
        a[f"L1_attn_time_mix_{c}"] = a[f"L1_attn_time_mix_{c}"].reshape(-1)
        a[f"L1_attn_W{c}T"] = a.pop(f"L1_attn_W{c}").T
    a["L1_attn_WoT"] = a.pop("L1_attn_Wo").T
    a["L3_ffn_fc1T"] = a.pop("L3_ffn_fc1_w").transpose(0, 2, 1)
    a["L3_ffn_fc2T"] = a.pop("L3_ffn_fc2_w").transpose(0, 2, 1)
    i, j = np.arange(T)[:, None], np.arange(T)[None, :]
    causal, within = j <= i, (j <= i) & (i // B == j // B)
    for name, sees in (("mask_causal", causal), ("mask_within", within)):
        a[name] = np.where(sees, 0.0, NEG).astype(np.float32)
    a["iota8"] = np.arange(E, dtype=np.float32)
    a["mask_causal_T"] = causal.T.astype(np.float32)
    return {k: np.ascontiguousarray(v) for k, v in a.items()}


def build(nc, I, out, stages=tuple(range(12))):
    I = dict(I)
    with ExitStack() as stack:
        core = Core(nc, stack, I)
        load_block(core)
        if 0 in stages:
            attention(core, "L0self", H=16, Dh=8, Wq="L0_attn_Wq", Wk="L0_attn_Wk", Wv="L0_attn_Wv", Wo="L0_attn_Wq",
                      bq="L0_attn_bq", bk="L0_attn_bk", bv="L0_attn_bv", flow=True, post="gate")
        if 1 in stages:
            text_vision(core)
        if 2 in stages:
            experts_top1(core, "L0ffn")
        if 3 in stages:
            wkv_mix(core)
        if 4 in stages:
            attention(core, "L1x", H=16, Dh=8, Wq="L1_xattn_Wq", Wk="L1_xattn_Wk", Wv="L1_xattn_Wv", Wo="L1_xattn_Wo",
                      bq="L1_xattn_bq", bk="L1_xattn_bk", bv="L1_xattn_bv", bo="L1_xattn_bo", context=True,
                      form="bounded", post="l1x")
        if 5 in stages:
            experts_top1(core, "L1ffn")
        if 6 in stages:
            batch_axis_attention(core)
        if 7 in stages:
            attention(core, "L2x", H=16, Dh=8, Wq="L2_xattn_wq", Wk="L2_xattn_wk", Wv="L2_xattn_wv", Wo="L2_xattn_wo",
                      bq="L2_xattn_bq", bk="L2_xattn_bk", bv="L2_xattn_bv", bo="L2_xattn_bo", context=True)
        if 8 in stages:
            soft_experts(core)
        if 9 in stages:
            attention(core, "L3lin", H=16, Dh=8, Wq="L3_attn_WqT", Wk="L3_attn_WkT", Wv="L3_attn_WvT", Wo="L3_attn_WoT",
                      bq="L3_attn_bq", bk="L3_attn_bk", bv="L3_attn_bv", bo="L3_attn_bo", form="linear",
                      mask="mask_causal_T")
        if 10 in stages:
            attention(core, "L3x", H=8, Dh=64, Wq="L3_xattn_Wq", Wk="L3_xattn_Wk", Wv="L3_xattn_Wv", Wo="L3_xattn_Wo",
                      bo="L3_xattn_bo", context=True)
        if 11 in stages:
            block_experts(core)
        store_block(core, out)


STAGES = tuple(range(12))


def kernel(**inputs):
    from concourse import bacc
    from concourse.bass_utils import run_bass_kernel_spmd

    nc = bacc.Bacc("TRN2", target_bir_lowering=False, num_devices=1)
    arrays = lay_out(inputs)
    I = {k: nc.dram_tensor(f"in_{k}", v.shape, mybir.dt.from_np(v.dtype), kind="ExternalInput").ap()
         for k, v in arrays.items()}
    out = nc.dram_tensor("out_x", (B, T, D), F32, kind="ExternalOutput").ap()
    build(nc, I, out, STAGES)
    r = run_bass_kernel_spmd(nc, [{f"in_{k}": v for k, v in arrays.items()}], core_ids=[0])
    return r.results[0]["out_x"]
```
